# Optimizing a Trainium2 kernel written in Bass

```python
import numpy as np
import jax
import jax.numpy as jnp

def _softmax(x, axis=-1):
    return jax.nn.softmax(x, axis=axis)

def _gelu(x):
    return jax.nn.gelu(x, approximate=True)

def _silu(x):
    return jax.nn.silu(x)

def _sigmoid(x):
    return jax.nn.sigmoid(x)

def _layernorm(x, axis=-1, eps=1e-05):
    m = jnp.mean(x, axis=axis, keepdims=True)
    v = jnp.var(x, axis=axis, keepdims=True)
    return (x - m) / jnp.sqrt(v + eps)

def _scatter_add(tgt, idx, src, axis=0):
    return tgt.at[idx].add(src)

def _segment_sum(src, seg, n):
    return jax.ops.segment_sum(src, seg, n)
kernel_name = 'mk_sandwich_d4_jaxref_r8_dcb2ca'

def setup_inputs(seed: int=0):
    np.random.seed(seed)
    _w = jnp.asarray

    def _L0_attn_setup():
        import jax, jax.numpy as jnp
        import numpy as np
        BSZ, T, D, H, WIN, N = (2, 256, 128, 16, 128, 64)
        DH = D // H
        DFF = 4 * D

        def _layernorm(x, g, b, eps=1e-05):
            mu = jnp.mean(x, axis=-1, keepdims=True)
            var = jnp.mean((x - mu) ** 2, axis=-1, keepdims=True)
            return (x - mu) * jax.lax.rsqrt(var + eps) * g + b
        key = jax.random.key(seed)
        ks = jax.random.split(key, 16)
        w = lambda k, shape: (jax.random.normal(k, shape) * 0.02).astype(jnp.float32)
        return {'x': jax.random.normal(ks[0], (BSZ, T, D), dtype=jnp.float32), 'ln1_g': jnp.ones((D,), jnp.float32), 'ln1_b': jnp.zeros((D,), jnp.float32), 'WQ': w(ks[1], (D, D)), 'bQ': jnp.zeros((D,), jnp.float32), 'WK': w(ks[2], (D, D)), 'bK': jnp.zeros((D,), jnp.float32), 'WV': w(ks[3], (D, D)), 'bV': jnp.zeros((D,), jnp.float32), 'WO': w(ks[4], (D, D)), 'bO': jnp.zeros((D,), jnp.float32), 'Wg': w(ks[5], (D, D)), 'bg': jnp.zeros((D,), jnp.float32), 'A': jax.random.uniform(ks[6], (N,), jnp.float32, -0.1, 0.1), 'Bw': w(ks[7], (D, N)), 'Cw': w(ks[8], (N, D)), 'ln2_g': jnp.ones((D,), jnp.float32), 'ln2_b': jnp.zeros((D,), jnp.float32), 'W1': w(ks[9], (D, DFF)), 'b1': jnp.zeros((DFF,), jnp.float32), 'W2': w(ks[10], (DFF, D)), 'b2': jnp.zeros((D,), jnp.float32)}
    _L0_attn_in = _L0_attn_setup()

    def _L0_ffn_setup():
        import jax, jax.numpy as jnp
        import numpy as np
        DIM = 128
        DEPTH = 6
        HEADS = 16
        DIM_HEAD = 64
        WINDOW = 32
        INNER = HEADS * DIM_HEAD
        DIM_INNER = int(DIM * 4 * 2 / 3)
        QK_SCALE = 8.0

        def shift_tokens(t):
            a, s = jnp.split(t, 2, -1)
            s = jnp.pad(s, ((0, 0), (1, 0), (0, 0)))[:, :-1]
            return jnp.concatenate([a, s], -1)

        def l2norm(t):
            return t / jnp.maximum(jnp.linalg.norm(t, axis=-1, keepdims=True), 1e-12)

        def rotate_half(x):
            x1, x2 = jnp.split(x, 2, -1)
            return jnp.concatenate([-x2, x1], -1)

        def rotary_tables(n):
            half = jnp.arange(0, DIM_HEAD, 2, dtype=jnp.float32)
            inv_freq = 1.0 / 10000.0 ** (half / DIM_HEAD)
            t = jnp.arange(n, dtype=jnp.float32)
            freqs = t[:, None] * inv_freq[None, :]
            freqs = jnp.concatenate([freqs, freqs], -1)
            base_scale = (half + 0.4 * DIM_HEAD) / (1.4 * DIM_HEAD)
            power = (t - n // 2) / (WINDOW // 2)
            scale = base_scale[None, :] ** power[:, None]
            scale = jnp.concatenate([scale, scale], -1)
            return (freqs, scale)

        def local_attention(q, k, v):
            b, h, n, d = q.shape
            w = WINDOW
            nw = n // w
            bq = q.reshape(b, h, nw, w, d)
            bk = k.reshape(b, h, nw, w, d)
            bv = v.reshape(b, h, nw, w, d)

            def look(t):
                p = jnp.pad(t, ((0, 0), (0, 0), (1, 0), (0, 0), (0, 0)))
                return jnp.concatenate([p[:, :, :nw], p[:, :, 1:]], axis=3)
            bk2, bv2 = (look(bk), look(bv))
            seq = jnp.arange(n).reshape(nw, w)
            seq_p = jnp.pad(seq, ((1, 0), (0, 0)), constant_values=-1)
            jt = jnp.concatenate([seq_p[:nw], seq_p[1:]], axis=1)
            it = seq[:, :, None]
            jb = jt[:, None, :]
            mask = (it < jb) | (it > jb + w) | (jb == -1)
            sim = jnp.einsum('bhwie,bhwje->bhwij', bq, bk2) * QK_SCALE
            sim = jnp.where(mask, -jnp.finfo(sim.dtype).max, sim)
            attn = jax.nn.softmax(sim, -1)
            out = jnp.einsum('bhwij,bhwje->bhwie', attn, bv2)
            return out.reshape(b, h, n, d)

        def attn_layer(x, Wqkv, qs, ksc, Wo):
            b, n, _ = x.shape
            qkv = x @ Wqkv
            q, k, v = jnp.split(qkv, 3, -1)
            sh = lambda t: t.reshape(b, n, HEADS, DIM_HEAD).transpose(0, 2, 1, 3)
            q, k, v = (sh(q), sh(k), sh(v))
            q = l2norm(q) * qs
            k = l2norm(k) * ksc
            freqs, scale = rotary_tables(n)
            cos, sin = (jnp.cos(freqs), jnp.sin(freqs))
            q = q * cos * scale + rotate_half(q) * sin * scale
            inv = 1.0 / scale
            k = k * cos * inv + rotate_half(k) * sin * inv
            out = local_attention(q, k, v)
            out = out.transpose(0, 2, 1, 3).reshape(b, n, INNER)
            return out @ Wo

        def ffn_layer(x, g, bln, W1, b1, W2, b2):
            mu = x.mean(-1, keepdims=True)
            var = ((x - mu) ** 2).mean(-1, keepdims=True)
            xn = (x - mu) / jnp.sqrt(var + 1e-05) * g + bln
            hg = xn @ W1 + b1
            a, gate = jnp.split(hg, 2, -1)
            return a * jax.nn.gelu(gate, approximate=False) @ W2 + b2
        key = jax.random.key(seed)
        ks = jax.random.split(key, 8)
        B, N = (2, 256)
        init = lambda k, shape: jax.random.normal(k, shape, jnp.float32) * 0.02
        return {'x': jax.random.normal(ks[0], (B, N, DIM), jnp.float32), 'Wqkv': init(ks[1], (DEPTH, DIM, 3 * INNER)), 'q_scale': jnp.ones((DEPTH, DIM_HEAD), jnp.float32), 'k_scale': jnp.ones((DEPTH, DIM_HEAD), jnp.float32), 'Wo': init(ks[2], (DEPTH, INNER, DIM)), 'ln_g': jnp.ones((DEPTH, DIM), jnp.float32), 'ln_b': jnp.zeros((DEPTH, DIM), jnp.float32), 'W1': init(ks[3], (DEPTH, DIM, 2 * DIM_INNER)), 'b1': jnp.zeros((DEPTH, 2 * DIM_INNER), jnp.float32), 'W2': init(ks[4], (DEPTH, DIM_INNER, DIM)), 'b2': jnp.zeros((DEPTH, DIM), jnp.float32)}
    _L0_ffn_in = _L0_ffn_setup()

    def _L1_attn_setup():
        import jax, jax.numpy as jnp
        import numpy as np
        H = 8
        LN_EPS = 1e-05
        key = jax.random.key(seed)
        ks = jax.random.split(key, 4)
        B, S, D = (4, 256, 128)
        x = jax.random.normal(ks[0], (B, S, D), dtype=jnp.float32)
        sc = 1.0 / np.sqrt(D)
        Wq = jax.random.normal(ks[1], (D, D), dtype=jnp.float32) * sc
        Wk = jax.random.normal(ks[2], (D, D), dtype=jnp.float32) * sc
        Wv = jax.random.normal(ks[3], (D, D * H), dtype=jnp.float32) * sc
        return {'x': x, 'Wq': Wq, 'bq': jnp.zeros((D,), jnp.float32), 'Wk': Wk, 'bk': jnp.zeros((D,), jnp.float32), 'Wv': Wv, 'bv': jnp.zeros((D * H,), jnp.float32), 'gamma': jnp.ones((D,), jnp.float32), 'beta': jnp.zeros((D,), jnp.float32)}
    _L1_attn_in = _L1_attn_setup()

    def _L1_ffn_setup():
        import jax, jax.numpy as jnp
        import numpy as np
        DIM = 128
        DEPTH = 2
        HEADS = 8
        DIM_HEAD = 64
        WINDOW = 64
        INNER = HEADS * DIM_HEAD
        HID = int(DIM * 4 * 2 / 3)
        B, N = (2, 1024)
        QK_SCALE = 8.0

        def shift_token(t):
            t1, t2 = jnp.split(t, 2, axis=-1)
            t2 = jnp.pad(t2, ((0, 0), (1, 0), (0, 0)))[:, :-1]
            return jnp.concatenate([t1, t2], axis=-1)

        def l2norm(t):
            return t / jnp.clip(jnp.linalg.norm(t, axis=-1, keepdims=True), 1e-12)

        def rotate_half(x):
            x1, x2 = jnp.split(x, 2, axis=-1)
            return jnp.concatenate([-x2, x1], axis=-1)

        def rotary_xpos(q, k):
            n = q.shape[-2]
            half_idx = jnp.arange(0, DIM_HEAD, 2, dtype=jnp.float32)
            inv_freq = 1.0 / 10000.0 ** (half_idx / DIM_HEAD)
            t = jnp.arange(n, dtype=jnp.float32)
            freqs = t[:, None] * inv_freq[None, :]
            freqs = jnp.concatenate([freqs, freqs], axis=-1)
            base = (half_idx + 0.4 * DIM_HEAD) / (1.4 * DIM_HEAD)
            power = (t - n // 2) / float(WINDOW // 2)
            scale = base[None, :] ** power[:, None]
            scale = jnp.concatenate([scale, scale], axis=-1)
            cos, sin = (jnp.cos(freqs), jnp.sin(freqs))
            q = q * cos * scale + rotate_half(q) * sin * scale
            k = k * cos / scale + rotate_half(k) * sin / scale
            return (q, k)

        def local_attention(q, k, v):
            b, h, n, d = q.shape
            w = n // WINDOW
            bq = q.reshape(b, h, w, WINDOW, d) * QK_SCALE
            bk = k.reshape(b, h, w, WINDOW, d)
            bv = v.reshape(b, h, w, WINDOW, d)

            def look_around(t):
                p = jnp.pad(t, ((0, 0), (0, 0), (1, 0), (0, 0), (0, 0)))
                return jnp.concatenate([p[:, :, :w], p[:, :, 1:]], axis=3)
            bk, bv = (look_around(bk), look_around(bv))
            bt = jnp.arange(n).reshape(w, WINDOW)
            btp = jnp.pad(bt, ((1, 0), (0, 0)), constant_values=-1)
            btk = jnp.concatenate([btp[:w], btp[1:]], axis=1)
            sim = jnp.einsum('bhwid,bhwjd->bhwij', bq, bk)
            i = bt[:, :, None]
            j = btk[:, None, :]
            mask = (i < j) | (i > j + WINDOW) | (j == -1)
            sim = jnp.where(mask, -jnp.finfo(sim.dtype).max, sim)
            attn = jax.nn.softmax(sim, axis=-1)
            out = jnp.einsum('bhwij,bhwjd->bhwid', attn, bv)
            return out.reshape(b, h, n, d)

        def _layer(x, wqkv, qs, ksc, wo, lg, lb, w1, b1, w2, b2):
            b, n, _ = x.shape
            h = shift_token(x)
            qkv = h @ wqkv
            q, k, v = jnp.split(qkv, 3, axis=-1)
            to_heads = lambda t: t.reshape(b, n, HEADS, DIM_HEAD).transpose(0, 2, 1, 3)
            q, k, v = (to_heads(q), to_heads(k), to_heads(v))
            q = l2norm(q) * qs
            k = l2norm(k) * ksc
            q, k = rotary_xpos(q, k)
            o = local_attention(q, k, v)
            o = o.transpose(0, 2, 1, 3).reshape(b, n, INNER)
            x = x + o @ wo
            h = shift_token(x)
            mu = h.mean(-1, keepdims=True)
            var = h.var(-1, keepdims=True)
            h = (h - mu) / jnp.sqrt(var + 1e-05) * lg + lb
            h = h @ w1 + b1
            a, g = jnp.split(h, 2, axis=-1)
            h = a * jax.nn.gelu(g, approximate=False)
            x = x + h @ w2 + b2
            return x
        key = jax.random.key(seed)
        ks = jax.random.split(key, 6)
        return {'x': jax.random.normal(ks[0], (B, N, DIM), jnp.float32), 'wqkv': jax.random.normal(ks[1], (DEPTH, DIM, 3 * INNER), jnp.float32) * 0.02, 'q_scale': jnp.ones((DEPTH, DIM_HEAD), jnp.float32), 'k_scale': jnp.ones((DEPTH, DIM_HEAD), jnp.float32), 'wo': jax.random.normal(ks[2], (DEPTH, INNER, DIM), jnp.float32) * 0.02, 'ln_g': jnp.ones((DEPTH, DIM), jnp.float32), 'ln_b': jnp.zeros((DEPTH, DIM), jnp.float32), 'w1': jax.random.normal(ks[3], (DEPTH, DIM, 2 * HID), jnp.float32) * 0.02, 'b1': jnp.zeros((DEPTH, 2 * HID), jnp.float32), 'w2': jax.random.normal(ks[4], (DEPTH, HID, DIM), jnp.float32) * 0.02, 'b2': jnp.zeros((DEPTH, DIM), jnp.float32)}
    _L1_ffn_in = _L1_ffn_setup()

    def _L2_attn_setup():
        import jax, jax.numpy as jnp
        import numpy as np
        HIDDEN = 128
        INNER = 256
        STATE = 64
        K = 4
        BATCH, SEQ = (2, 256)
        key = jax.random.key(seed)
        ks = jax.random.split(key, 8)

        def w(k, shape, scale=0.02):
            return jax.random.normal(k, shape, jnp.float32) * scale
        return {'x': jax.random.normal(ks[0], (BATCH, SEQ, HIDDEN), jnp.float32), 'W_in': w(ks[1], (HIDDEN, 2 * INNER)), 'conv_w': w(ks[2], (INNER, 1, K), 0.2), 'conv_b': jnp.zeros((INNER,), jnp.float32), 'W_dt': w(ks[3], (INNER, INNER)), 'b_dt': jnp.linspace(-4.0, -2.0, INNER).astype(jnp.float32), 'W_B': w(ks[4], (INNER, STATE)), 'W_C': w(ks[5], (INNER, STATE)), 'D': jnp.ones((INNER,), jnp.float32), 'W_out': w(ks[6], (INNER, HIDDEN))}
    _L2_attn_in = _L2_attn_setup()

    def _L2_ffn_setup():
        import jax, jax.numpy as jnp
        import numpy as np
        D_MODEL = 128
        N_EXPERTS = 8
        TOP_K = 2
        LN_EPS = 1e-05
        key = jax.random.key(seed)
        ks = jax.random.split(key, 8)
        B, S, d, E = (2, 256, D_MODEL, N_EXPERTS)
        f = 2 * d
        s_in = 0.02
        return {'x': jax.random.normal(ks[0], (B, S, d), jnp.float32), 'Wg': jax.random.normal(ks[1], (d, E), jnp.float32) * s_in, 'bg': jnp.zeros((E,), jnp.float32), 'W1': jax.random.normal(ks[2], (E, d, f), jnp.float32) * s_in, 'b1': jnp.zeros((E, f), jnp.float32), 'W2': jax.random.normal(ks[3], (E, f, d), jnp.float32) * s_in, 'b2': jnp.zeros((E, d), jnp.float32), 'gamma': jnp.ones((d,), jnp.float32), 'beta': jnp.zeros((d,), jnp.float32)}
    _L2_ffn_in = _L2_ffn_setup()

    def _L3_attn_setup():
        import jax, jax.numpy as jnp
        import numpy as np
        B, T, HS, H, R = (4, 256, 128, 16, 16)
        D = HS // H
        LOGIT_01 = float(np.log(0.1 / 0.9))
        LOGIT_098 = float(np.log(0.98 / 0.02))

        def _rope_cos_sin(seq_len, dim, base=10000.0):
            half = dim // 2
            inv_freq = 1.0 / base ** (jnp.arange(half, dtype=jnp.float32) / half)
            freqs = jnp.arange(seq_len, dtype=jnp.float32)[:, None] * inv_freq[None, :]
            return (jnp.cos(freqs), jnp.sin(freqs))

        def _apply_rope(x, cos, sin):
            c = cos[None, :, None, :]
            s = sin[None, :, None, :]
            x1 = x[..., 0::2]
            x2 = x[..., 1::2]
            r1 = x1 * c - x2 * s
            r2 = x1 * s + x2 * c
            return jnp.stack((r1, r2), axis=-1).reshape(x.shape)
        key = jax.random.key(seed)
        ks = jax.random.split(key, 10)

        def rn(k, shape, s=0.02):
            return jax.random.normal(k, shape, dtype=jnp.float32) * s
        return {'x': jax.random.normal(ks[0], (B, T, HS), dtype=jnp.float32), 'q_w': rn(ks[1], (HS, HS)), 'k_w': rn(ks[2], (HS, HS)), 'v_w': rn(ks[3], (HS, HS)), 'Wq': rn(ks[4], (H, R, D), 0.05), 'Wk': rn(ks[5], (H, R, D), 0.05), 'g_w': rn(ks[6], (H * R, HS)), 'g_b': jnp.full((H * R,), LOGIT_01, dtype=jnp.float32), 'base_decay_logits': jnp.full((H, R), LOGIT_098, dtype=jnp.float32), 'out_w': rn(ks[7], (HS, HS)), 'out_b': jnp.zeros((HS,), dtype=jnp.float32), 'ln_g': jnp.ones((HS,), dtype=jnp.float32), 'ln_b': jnp.zeros((HS,), dtype=jnp.float32)}
    _L3_attn_in = _L3_attn_setup()

    def _L3_ffn_setup():
        import jax, jax.numpy as jnp
        import numpy as np
        BLOCK = 16
        _GRID = jnp.array([0.0, 0.5, 1.0, 1.5, 2.0, 3.0, 4.0, 6.0], dtype=jnp.float32)
        _MID = jnp.array([0.25, 0.75, 1.25, 1.75, 2.5, 3.5, 5.0], dtype=jnp.float32)

        def fp4_quant_dequant(x):
            shape = x.shape
            xb = x.reshape(shape[:-1] + (shape[-1] // BLOCK, BLOCK))
            scale = jnp.max(jnp.abs(xb), axis=-1, keepdims=True) / 6.0
            scale = jnp.maximum(scale, jnp.float32(1e-12))
            xn = xb / scale
            idx = jnp.searchsorted(_MID, jnp.abs(xn))
            q = _GRID[idx] * jnp.sign(xn) * scale
            return q.reshape(shape)

        def fp4_linear(x, w):
            xq = fp4_quant_dequant(x)
            wq = fp4_quant_dequant(w)
            return jnp.einsum('bsk,nk->bsn', xq, wq)
        key = jax.random.key(seed)
        k1, k2, k3, k4 = jax.random.split(key, 4)
        H, I = (128, 352)
        x = jax.random.normal(k1, (4, 512, H), dtype=jnp.float32)
        w_gate = jax.random.normal(k2, (I, H), dtype=jnp.float32) * 0.02
        w_up = jax.random.normal(k3, (I, H), dtype=jnp.float32) * 0.02
        w_down = jax.random.normal(k4, (H, I), dtype=jnp.float32) * 0.02
        return {'x': x, 'w_gate': w_gate, 'w_up': w_up, 'w_down': w_down}
    _L3_ffn_in = _L3_ffn_setup()
    _d = {'L0_attn_x': _L0_attn_in['x'], 'L0_attn_ln1_g': _L0_attn_in['ln1_g'], 'L0_attn_ln1_b': _L0_attn_in['ln1_b'], 'L0_attn_WQ': _L0_attn_in['WQ'], 'L0_attn_bQ': _L0_attn_in['bQ'], 'L0_attn_WK': _L0_attn_in['WK'], 'L0_attn_bK': _L0_attn_in['bK'], 'L0_attn_WV': _L0_attn_in['WV'], 'L0_attn_bV': _L0_attn_in['bV'], 'L0_attn_WO': _L0_attn_in['WO'], 'L0_attn_bO': _L0_attn_in['bO'], 'L0_attn_Wg': _L0_attn_in['Wg'], 'L0_attn_bg': _L0_attn_in['bg'], 'L0_attn_A': _L0_attn_in['A'], 'L0_attn_Bw': _L0_attn_in['Bw'], 'L0_attn_Cw': _L0_attn_in['Cw'], 'L0_attn_ln2_g': _L0_attn_in['ln2_g'], 'L0_attn_ln2_b': _L0_attn_in['ln2_b'], 'L0_attn_W1': _L0_attn_in['W1'], 'L0_attn_b1': _L0_attn_in['b1'], 'L0_attn_W2': _L0_attn_in['W2'], 'L0_attn_b2': _L0_attn_in['b2'], 'L0_ffn_Wqkv': _L0_ffn_in['Wqkv'], 'L0_ffn_q_scale': _L0_ffn_in['q_scale'], 'L0_ffn_k_scale': _L0_ffn_in['k_scale'], 'L0_ffn_Wo': _L0_ffn_in['Wo'], 'L0_ffn_ln_g': _L0_ffn_in['ln_g'], 'L0_ffn_ln_b': _L0_ffn_in['ln_b'], 'L0_ffn_W1': _L0_ffn_in['W1'], 'L0_ffn_b1': _L0_ffn_in['b1'], 'L0_ffn_W2': _L0_ffn_in['W2'], 'L0_ffn_b2': _L0_ffn_in['b2'], 'L1_attn_Wq': _L1_attn_in['Wq'], 'L1_attn_bq': _L1_attn_in['bq'], 'L1_attn_Wk': _L1_attn_in['Wk'], 'L1_attn_bk': _L1_attn_in['bk'], 'L1_attn_Wv': _L1_attn_in['Wv'], 'L1_attn_bv': _L1_attn_in['bv'], 'L1_attn_gamma': _L1_attn_in['gamma'], 'L1_attn_beta': _L1_attn_in['beta'], 'L1_ffn_wqkv': _L1_ffn_in['wqkv'], 'L1_ffn_q_scale': _L1_ffn_in['q_scale'], 'L1_ffn_k_scale': _L1_ffn_in['k_scale'], 'L1_ffn_wo': _L1_ffn_in['wo'], 'L1_ffn_ln_g': _L1_ffn_in['ln_g'], 'L1_ffn_ln_b': _L1_ffn_in['ln_b'], 'L1_ffn_w1': _L1_ffn_in['w1'], 'L1_ffn_b1': _L1_ffn_in['b1'], 'L1_ffn_w2': _L1_ffn_in['w2'], 'L1_ffn_b2': _L1_ffn_in['b2'], 'L2_attn_W_in': _L2_attn_in['W_in'], 'L2_attn_conv_w': _L2_attn_in['conv_w'], 'L2_attn_conv_b': _L2_attn_in['conv_b'], 'L2_attn_W_dt': _L2_attn_in['W_dt'], 'L2_attn_b_dt': _L2_attn_in['b_dt'], 'L2_attn_W_B': _L2_attn_in['W_B'], 'L2_attn_W_C': _L2_attn_in['W_C'], 'L2_attn_D': _L2_attn_in['D'], 'L2_attn_W_out': _L2_attn_in['W_out'], 'L2_ffn_Wg': _L2_ffn_in['Wg'], 'L2_ffn_bg': _L2_ffn_in['bg'], 'L2_ffn_W1': _L2_ffn_in['W1'], 'L2_ffn_b1': _L2_ffn_in['b1'], 'L2_ffn_W2': _L2_ffn_in['W2'], 'L2_ffn_b2': _L2_ffn_in['b2'], 'L2_ffn_gamma': _L2_ffn_in['gamma'], 'L2_ffn_beta': _L2_ffn_in['beta'], 'L3_attn_q_w': _L3_attn_in['q_w'], 'L3_attn_k_w': _L3_attn_in['k_w'], 'L3_attn_v_w': _L3_attn_in['v_w'], 'L3_attn_Wq': _L3_attn_in['Wq'], 'L3_attn_Wk': _L3_attn_in['Wk'], 'L3_attn_g_w': _L3_attn_in['g_w'], 'L3_attn_g_b': _L3_attn_in['g_b'], 'L3_attn_base_decay_logits': _L3_attn_in['base_decay_logits'], 'L3_attn_out_w': _L3_attn_in['out_w'], 'L3_attn_out_b': _L3_attn_in['out_b'], 'L3_attn_ln_g': _L3_attn_in['ln_g'], 'L3_attn_ln_b': _L3_attn_in['ln_b'], 'L3_ffn_w_gate': _L3_ffn_in['w_gate'], 'L3_ffn_w_up': _L3_ffn_in['w_up'], 'L3_ffn_w_down': _L3_ffn_in['w_down']}
    _x0 = _d['L0_attn_x']
    _d['L0_attn_x'] = jax.random.normal(jax.random.fold_in(jax.random.key(seed), 1), (8, 512, 128), dtype=_x0.dtype)
    del _x0
    return _d

def reference(L0_attn_x, L0_attn_ln1_g, L0_attn_ln1_b, L0_attn_WQ, L0_attn_bQ, L0_attn_WK, L0_attn_bK, L0_attn_WV, L0_attn_bV, L0_attn_WO, L0_attn_bO, L0_attn_Wg, L0_attn_bg, L0_attn_A, L0_attn_Bw, L0_attn_Cw, L0_attn_ln2_g, L0_attn_ln2_b, L0_attn_W1, L0_attn_b1, L0_attn_W2, L0_attn_b2, L0_ffn_Wqkv, L0_ffn_q_scale, L0_ffn_k_scale, L0_ffn_Wo, L0_ffn_ln_g, L0_ffn_ln_b, L0_ffn_W1, L0_ffn_b1, L0_ffn_W2, L0_ffn_b2, L1_attn_Wq, L1_attn_bq, L1_attn_Wk, L1_attn_bk, L1_attn_Wv, L1_attn_bv, L1_attn_gamma, L1_attn_beta, L1_ffn_wqkv, L1_ffn_q_scale, L1_ffn_k_scale, L1_ffn_wo, L1_ffn_ln_g, L1_ffn_ln_b, L1_ffn_w1, L1_ffn_b1, L1_ffn_w2, L1_ffn_b2, L2_attn_W_in, L2_attn_conv_w, L2_attn_conv_b, L2_attn_W_dt, L2_attn_b_dt, L2_attn_W_B, L2_attn_W_C, L2_attn_D, L2_attn_W_out, L2_ffn_Wg, L2_ffn_bg, L2_ffn_W1, L2_ffn_b1, L2_ffn_W2, L2_ffn_b2, L2_ffn_gamma, L2_ffn_beta, L3_attn_q_w, L3_attn_k_w, L3_attn_v_w, L3_attn_Wq, L3_attn_Wk, L3_attn_g_w, L3_attn_g_b, L3_attn_base_decay_logits, L3_attn_out_w, L3_attn_out_b, L3_attn_ln_g, L3_attn_ln_b, L3_ffn_w_gate, L3_ffn_w_up, L3_ffn_w_down):

    def _L0_attn_ref(x, ln1_g, ln1_b, WQ, bQ, WK, bK, WV, bV, WO, bO, Wg, bg, A, Bw, Cw, ln2_g, ln2_b, W1, b1, W2, b2):
        import jax, jax.numpy as jnp
        import numpy as np
        BSZ, T, D, H, WIN, N = (2, 256, 128, 16, 128, 64)
        DH = D // H
        DFF = 4 * D

        def _layernorm(x, g, b, eps=1e-05):
            mu = jnp.mean(x, axis=-1, keepdims=True)
            var = jnp.mean((x - mu) ** 2, axis=-1, keepdims=True)
            return (x - mu) * jax.lax.rsqrt(var + eps) * g + b
        B, Tlen, d = x.shape
        h = _layernorm(x, ln1_g, ln1_b)

        def heads(t):
            return t.reshape(B, Tlen, H, DH).transpose(0, 2, 1, 3)
        q = heads(h @ WQ + bQ)
        k = heads(h @ WK + bK)
        v = heads(h @ WV + bV)
        scores = jnp.einsum('bhqd,bhkd->bhqk', q, k) / jnp.sqrt(jnp.float32(DH))
        i = jnp.arange(Tlen)
        diff = i[:, None] - i[None, :]
        allowed = (diff >= 0) & (diff < WIN)
        scores = jnp.where(allowed, scores, -jnp.inf)
        attn = jax.nn.softmax(scores, axis=-1)
        ao = jnp.einsum('bhqk,bhkd->bhqd', attn, v)
        ao = ao.transpose(0, 2, 1, 3).reshape(B, Tlen, d)
        attn_out = ao @ WO + bO
        u = h @ Bw

        def step(s, u_t):
            s = A * s + u_t
            return (s, s)
        _, states = jax.lax.scan(step, jnp.zeros((B, N), x.dtype), jnp.swapaxes(u, 0, 1))
        ssm_out = jnp.swapaxes(states, 0, 1) @ Cw
        g = jax.nn.sigmoid(h @ Wg + bg)
        x1 = x + g * attn_out + (1.0 - g) * ssm_out
        h2 = _layernorm(x1, ln2_g, ln2_b)
        mlp = jax.nn.gelu(h2 @ W1 + b1, approximate=False) @ W2 + b2
        return x1 + mlp

    def _L0_ffn_ref(x, Wqkv, q_scale, k_scale, Wo, ln_g, ln_b, W1, b1, W2, b2):
        import jax, jax.numpy as jnp
        import numpy as np
        DIM = 128
        DEPTH = 6
        HEADS = 16
        DIM_HEAD = 64
        WINDOW = 32
        INNER = HEADS * DIM_HEAD
        DIM_INNER = int(DIM * 4 * 2 / 3)
        QK_SCALE = 8.0

        def shift_tokens(t):
            a, s = jnp.split(t, 2, -1)
            s = jnp.pad(s, ((0, 0), (1, 0), (0, 0)))[:, :-1]
            return jnp.concatenate([a, s], -1)

        def l2norm(t):
            return t / jnp.maximum(jnp.linalg.norm(t, axis=-1, keepdims=True), 1e-12)

        def rotate_half(x):
            x1, x2 = jnp.split(x, 2, -1)
            return jnp.concatenate([-x2, x1], -1)

        def rotary_tables(n):
            half = jnp.arange(0, DIM_HEAD, 2, dtype=jnp.float32)
            inv_freq = 1.0 / 10000.0 ** (half / DIM_HEAD)
            t = jnp.arange(n, dtype=jnp.float32)
            freqs = t[:, None] * inv_freq[None, :]
            freqs = jnp.concatenate([freqs, freqs], -1)
            base_scale = (half + 0.4 * DIM_HEAD) / (1.4 * DIM_HEAD)
            power = (t - n // 2) / (WINDOW // 2)
            scale = base_scale[None, :] ** power[:, None]
            scale = jnp.concatenate([scale, scale], -1)
            return (freqs, scale)

        def local_attention(q, k, v):
            b, h, n, d = q.shape
            w = WINDOW
            nw = n // w
            bq = q.reshape(b, h, nw, w, d)
            bk = k.reshape(b, h, nw, w, d)
            bv = v.reshape(b, h, nw, w, d)

            def look(t):
                p = jnp.pad(t, ((0, 0), (0, 0), (1, 0), (0, 0), (0, 0)))
                return jnp.concatenate([p[:, :, :nw], p[:, :, 1:]], axis=3)
            bk2, bv2 = (look(bk), look(bv))
            seq = jnp.arange(n).reshape(nw, w)
            seq_p = jnp.pad(seq, ((1, 0), (0, 0)), constant_values=-1)
            jt = jnp.concatenate([seq_p[:nw], seq_p[1:]], axis=1)
            it = seq[:, :, None]
            jb = jt[:, None, :]
            mask = (it < jb) | (it > jb + w) | (jb == -1)
            sim = jnp.einsum('bhwie,bhwje->bhwij', bq, bk2) * QK_SCALE
            sim = jnp.where(mask, -jnp.finfo(sim.dtype).max, sim)
            attn = jax.nn.softmax(sim, -1)
            out = jnp.einsum('bhwij,bhwje->bhwie', attn, bv2)
            return out.reshape(b, h, n, d)

        def attn_layer(x, Wqkv, qs, ksc, Wo):
            b, n, _ = x.shape
            qkv = x @ Wqkv
            q, k, v = jnp.split(qkv, 3, -1)
            sh = lambda t: t.reshape(b, n, HEADS, DIM_HEAD).transpose(0, 2, 1, 3)
            q, k, v = (sh(q), sh(k), sh(v))
            q = l2norm(q) * qs
            k = l2norm(k) * ksc
            freqs, scale = rotary_tables(n)
            cos, sin = (jnp.cos(freqs), jnp.sin(freqs))
            q = q * cos * scale + rotate_half(q) * sin * scale
            inv = 1.0 / scale
            k = k * cos * inv + rotate_half(k) * sin * inv
            out = local_attention(q, k, v)
            out = out.transpose(0, 2, 1, 3).reshape(b, n, INNER)
            return out @ Wo

        def ffn_layer(x, g, bln, W1, b1, W2, b2):
            mu = x.mean(-1, keepdims=True)
            var = ((x - mu) ** 2).mean(-1, keepdims=True)
            xn = (x - mu) / jnp.sqrt(var + 1e-05) * g + bln
            hg = xn @ W1 + b1
            a, gate = jnp.split(hg, 2, -1)
            return a * jax.nn.gelu(gate, approximate=False) @ W2 + b2
        for i in range(DEPTH):
            x = attn_layer(shift_tokens(x), Wqkv[i], q_scale[i], k_scale[i], Wo[i]) + x
            x = ffn_layer(shift_tokens(x), ln_g[i], ln_b[i], W1[i], b1[i], W2[i], b2[i]) + x
        return x

    def _L1_attn_ref(x, Wq, bq, Wk, bk, Wv, bv, gamma, beta):
        import jax, jax.numpy as jnp
        import numpy as np
        H = 8
        LN_EPS = 1e-05
        B, S, D = x.shape
        dk = D // H
        mu = jnp.mean(x, axis=-1, keepdims=True)
        var = jnp.mean(jnp.square(x - mu), axis=-1, keepdims=True)
        xn = (x - mu) * jax.lax.rsqrt(var + LN_EPS) * gamma + beta
        q = (xn @ Wq + bq).reshape(B, S, H, dk).transpose(0, 2, 1, 3)
        k = (xn @ Wk + bk).reshape(B, S, H, dk).transpose(0, 2, 1, 3)
        v = (xn @ Wv + bv).reshape(B, S, H, D).transpose(0, 2, 1, 3)
        scores = jnp.einsum('bhsd,bhtd->bhst', q, k) / jnp.sqrt(jnp.asarray(dk, x.dtype))
        p = jax.nn.softmax(scores, axis=-1)
        att = jnp.einsum('bhst,bhtd->bhsd', p, v)
        out = att.reshape(S, B, D, H).sum(axis=-1).reshape(B, S, D)
        return out

    def _L1_ffn_ref(x, wqkv, q_scale, k_scale, wo, ln_g, ln_b, w1, b1, w2, b2):
        import jax, jax.numpy as jnp
        import numpy as np
        DIM = 128
        DEPTH = 2
        HEADS = 8
        DIM_HEAD = 64
        WINDOW = 64
        INNER = HEADS * DIM_HEAD
        HID = int(DIM * 4 * 2 / 3)
        B, N = (2, 1024)
        QK_SCALE = 8.0

        def shift_token(t):
            t1, t2 = jnp.split(t, 2, axis=-1)
            t2 = jnp.pad(t2, ((0, 0), (1, 0), (0, 0)))[:, :-1]
            return jnp.concatenate([t1, t2], axis=-1)

        def l2norm(t):
            return t / jnp.clip(jnp.linalg.norm(t, axis=-1, keepdims=True), 1e-12)

        def rotate_half(x):
            x1, x2 = jnp.split(x, 2, axis=-1)
            return jnp.concatenate([-x2, x1], axis=-1)

        def rotary_xpos(q, k):
            n = q.shape[-2]
            half_idx = jnp.arange(0, DIM_HEAD, 2, dtype=jnp.float32)
            inv_freq = 1.0 / 10000.0 ** (half_idx / DIM_HEAD)
            t = jnp.arange(n, dtype=jnp.float32)
            freqs = t[:, None] * inv_freq[None, :]
            freqs = jnp.concatenate([freqs, freqs], axis=-1)
            base = (half_idx + 0.4 * DIM_HEAD) / (1.4 * DIM_HEAD)
            power = (t - n // 2) / float(WINDOW // 2)
            scale = base[None, :] ** power[:, None]
            scale = jnp.concatenate([scale, scale], axis=-1)
            cos, sin = (jnp.cos(freqs), jnp.sin(freqs))
            q = q * cos * scale + rotate_half(q) * sin * scale
            k = k * cos / scale + rotate_half(k) * sin / scale
            return (q, k)

        def local_attention(q, k, v):
            b, h, n, d = q.shape
            w = n // WINDOW
            bq = q.reshape(b, h, w, WINDOW, d) * QK_SCALE
            bk = k.reshape(b, h, w, WINDOW, d)
            bv = v.reshape(b, h, w, WINDOW, d)

            def look_around(t):
                p = jnp.pad(t, ((0, 0), (0, 0), (1, 0), (0, 0), (0, 0)))
                return jnp.concatenate([p[:, :, :w], p[:, :, 1:]], axis=3)
            bk, bv = (look_around(bk), look_around(bv))
            bt = jnp.arange(n).reshape(w, WINDOW)
            btp = jnp.pad(bt, ((1, 0), (0, 0)), constant_values=-1)
            btk = jnp.concatenate([btp[:w], btp[1:]], axis=1)
            sim = jnp.einsum('bhwid,bhwjd->bhwij', bq, bk)
            i = bt[:, :, None]
            j = btk[:, None, :]
            mask = (i < j) | (i > j + WINDOW) | (j == -1)
            sim = jnp.where(mask, -jnp.finfo(sim.dtype).max, sim)
            attn = jax.nn.softmax(sim, axis=-1)
            out = jnp.einsum('bhwij,bhwjd->bhwid', attn, bv)
            return out.reshape(b, h, n, d)

        def _layer(x, wqkv, qs, ksc, wo, lg, lb, w1, b1, w2, b2):
            b, n, _ = x.shape
            h = shift_token(x)
            qkv = h @ wqkv
            q, k, v = jnp.split(qkv, 3, axis=-1)
            to_heads = lambda t: t.reshape(b, n, HEADS, DIM_HEAD).transpose(0, 2, 1, 3)
            q, k, v = (to_heads(q), to_heads(k), to_heads(v))
            q = l2norm(q) * qs
            k = l2norm(k) * ksc
            q, k = rotary_xpos(q, k)
            o = local_attention(q, k, v)
            o = o.transpose(0, 2, 1, 3).reshape(b, n, INNER)
            x = x + o @ wo
            h = shift_token(x)
            mu = h.mean(-1, keepdims=True)
            var = h.var(-1, keepdims=True)
            h = (h - mu) / jnp.sqrt(var + 1e-05) * lg + lb
            h = h @ w1 + b1
            a, g = jnp.split(h, 2, axis=-1)
            h = a * jax.nn.gelu(g, approximate=False)
            x = x + h @ w2 + b2
            return x
        for l in range(DEPTH):
            x = _layer(x, wqkv[l], q_scale[l], k_scale[l], wo[l], ln_g[l], ln_b[l], w1[l], b1[l], w2[l], b2[l])
        return x

    def _L2_attn_ref(x, W_in, conv_w, conv_b, W_dt, b_dt, W_B, W_C, D, W_out):
        import jax, jax.numpy as jnp
        import numpy as np
        HIDDEN = 128
        INNER = 256
        STATE = 64
        K = 4
        BATCH, SEQ = (2, 256)
        batch, seq_len, _ = x.shape
        inner = W_dt.shape[0]
        state_dim = W_B.shape[1]
        xz = x @ W_in
        x_inner, z = jnp.split(xz, 2, axis=-1)
        xc = jnp.transpose(x_inner, (0, 2, 1))
        k = conv_w.shape[-1]
        xc = jax.lax.conv_general_dilated(xc, conv_w, window_strides=(1,), padding=[(k - 1, 0)], dimension_numbers=('NCH', 'OIH', 'NCH'), feature_group_count=inner)
        xc = xc + conv_b[None, :, None]
        xc = jax.nn.silu(jnp.transpose(xc, (0, 2, 1)))
        dt = jax.nn.softplus(xc @ W_dt + b_dt)
        Bm = xc @ W_B
        Cm = xc @ W_C
        a = jnp.exp(-dt)
        dtx = dt * xc

        def step(state, inp):
            a_t, dtx_t, b_t, c_t = inp
            state = a_t[..., None] * state + dtx_t[..., None] * b_t[:, None, :]
            y_t = jnp.einsum('bin,bn->bi', state, c_t)
            return (state, y_t)
        init = jnp.zeros((batch, inner, state_dim), x.dtype)
        xs = (jnp.swapaxes(a, 0, 1), jnp.swapaxes(dtx, 0, 1), jnp.swapaxes(Bm, 0, 1), jnp.swapaxes(Cm, 0, 1))
        _, ys = jax.lax.scan(step, init, xs)
        y = jnp.swapaxes(ys, 0, 1) + D * xc
        y = y * jax.nn.silu(z)
        return y @ W_out

    def _L2_ffn_ref(x, Wg, bg, W1, b1, W2, b2, gamma, beta):
        import jax, jax.numpy as jnp
        import numpy as np
        D_MODEL = 128
        N_EXPERTS = 8
        TOP_K = 2
        LN_EPS = 1e-05
        logits = jnp.einsum('bsd,de->bse', x, Wg) + bg
        topk_vals, topk_idx = jax.lax.top_k(logits, TOP_K)
        topk_w = jax.nn.softmax(topk_vals, axis=-1)
        h = jax.nn.relu(jnp.einsum('bsd,edf->bsef', x, W1) + b1)
        eo = jnp.einsum('bsef,efd->bsed', h, W2) + b2
        sel = jnp.take_along_axis(eo, topk_idx[..., None], axis=2)
        mixed = jnp.sum(sel * topk_w[..., None], axis=2)
        y = mixed + x
        mu = jnp.mean(y, axis=-1, keepdims=True)
        var = jnp.mean(jnp.square(y - mu), axis=-1, keepdims=True)
        return gamma * (y - mu) * jax.lax.rsqrt(var + LN_EPS) + beta

    def _L3_attn_ref(x, q_w, k_w, v_w, Wq, Wk, g_w, g_b, base_decay_logits, out_w, out_b, ln_g, ln_b):
        import jax, jax.numpy as jnp
        import numpy as np
        B, T, HS, H, R = (4, 256, 128, 16, 16)
        D = HS // H
        LOGIT_01 = float(np.log(0.1 / 0.9))
        LOGIT_098 = float(np.log(0.98 / 0.02))

        def _rope_cos_sin(seq_len, dim, base=10000.0):
            half = dim // 2
            inv_freq = 1.0 / base ** (jnp.arange(half, dtype=jnp.float32) / half)
            freqs = jnp.arange(seq_len, dtype=jnp.float32)[:, None] * inv_freq[None, :]
            return (jnp.cos(freqs), jnp.sin(freqs))

        def _apply_rope(x, cos, sin):
            c = cos[None, :, None, :]
            s = sin[None, :, None, :]
            x1 = x[..., 0::2]
            x2 = x[..., 1::2]
            r1 = x1 * c - x2 * s
            r2 = x1 * s + x2 * c
            return jnp.stack((r1, r2), axis=-1).reshape(x.shape)
        b, t, hs = x.shape
        h, r, d = Wq.shape
        q = (x @ q_w.T).reshape(b, t, h, d)
        k = (x @ k_w.T).reshape(b, t, h, d)
        v = (x @ v_w.T).reshape(b, t, h, d)
        cos, sin = _rope_cos_sin(t, d)
        q = _apply_rope(q, cos, sin)
        k = _apply_rope(k, cos, sin)
        q_r = jnp.einsum('bthd,hrd->bthr', q, Wq)
        k_r = jnp.einsum('bthd,hrd->bthr', k, Wk)
        g = jax.nn.sigmoid((x @ g_w.T + g_b).reshape(b, t, h, r))
        decay = jax.nn.sigmoid(base_decay_logits)[None, :, :, None]
        scale = 1.0 / jnp.sqrt(jnp.asarray(d, dtype=x.dtype))

        def step(M, inp):
            q_t, k_t, v_t, g_t = inp
            M = M * decay + jnp.einsum('bhr,bhd->bhrd', g_t * k_t * scale, v_t)
            y = jnp.einsum('bhr,bhrd->bhd', q_t, M)
            return (M, y)
        xs = (q_r.transpose(1, 0, 2, 3), k_r.transpose(1, 0, 2, 3), v.transpose(1, 0, 2, 3), g.transpose(1, 0, 2, 3))
        M0 = jnp.zeros((b, h, r, d), dtype=x.dtype)
        _, Y = jax.lax.scan(step, M0, xs)
        Y = Y.transpose(1, 0, 2, 3).reshape(b, t, hs)
        out = Y @ out_w.T + out_b
        hres = x + out
        mu = jnp.mean(hres, axis=-1, keepdims=True)
        var = jnp.mean((hres - mu) ** 2, axis=-1, keepdims=True)
        return (hres - mu) / jnp.sqrt(var + 1e-05) * ln_g + ln_b

    def _L3_ffn_ref(x, w_gate, w_up, w_down):
        import jax, jax.numpy as jnp
        import numpy as np
        BLOCK = 16
        _GRID = jnp.array([0.0, 0.5, 1.0, 1.5, 2.0, 3.0, 4.0, 6.0], dtype=jnp.float32)
        _MID = jnp.array([0.25, 0.75, 1.25, 1.75, 2.5, 3.5, 5.0], dtype=jnp.float32)

        def fp4_quant_dequant(x):
            shape = x.shape
            xb = x.reshape(shape[:-1] + (shape[-1] // BLOCK, BLOCK))
            scale = jnp.max(jnp.abs(xb), axis=-1, keepdims=True) / 6.0
            scale = jnp.maximum(scale, jnp.float32(1e-12))
            xn = xb / scale
            idx = jnp.searchsorted(_MID, jnp.abs(xn))
            q = _GRID[idx] * jnp.sign(xn) * scale
            return q.reshape(shape)

        def fp4_linear(x, w):
            xq = fp4_quant_dequant(x)
            wq = fp4_quant_dequant(w)
            return jnp.einsum('bsk,nk->bsn', xq, wq)
        gate = fp4_linear(x, w_gate)
        y = fp4_linear(x, w_up)
        h = jax.nn.silu(gate) * y
        return fp4_linear(h, w_down)
    x = L0_attn_x
    x = x + _layernorm(_L0_attn_ref(_layernorm(x, axis=-1), L0_attn_ln1_g, L0_attn_ln1_b, L0_attn_WQ, L0_attn_bQ, L0_attn_WK, L0_attn_bK, L0_attn_WV, L0_attn_bV, L0_attn_WO, L0_attn_bO, L0_attn_Wg, L0_attn_bg, L0_attn_A, L0_attn_Bw, L0_attn_Cw, L0_attn_ln2_g, L0_attn_ln2_b, L0_attn_W1, L0_attn_b1, L0_attn_W2, L0_attn_b2), axis=-1)
    x = x + _layernorm(_L0_ffn_ref(_layernorm(x, axis=-1), L0_ffn_Wqkv, L0_ffn_q_scale, L0_ffn_k_scale, L0_ffn_Wo, L0_ffn_ln_g, L0_ffn_ln_b, L0_ffn_W1, L0_ffn_b1, L0_ffn_W2, L0_ffn_b2), axis=-1)
    x = x + _layernorm(_L1_attn_ref(_layernorm(x, axis=-1), L1_attn_Wq, L1_attn_bq, L1_attn_Wk, L1_attn_bk, L1_attn_Wv, L1_attn_bv, L1_attn_gamma, L1_attn_beta), axis=-1)
    x = x + _layernorm(_L1_ffn_ref(_layernorm(x, axis=-1), L1_ffn_wqkv, L1_ffn_q_scale, L1_ffn_k_scale, L1_ffn_wo, L1_ffn_ln_g, L1_ffn_ln_b, L1_ffn_w1, L1_ffn_b1, L1_ffn_w2, L1_ffn_b2), axis=-1)
    x = x + _layernorm(_L2_attn_ref(_layernorm(x, axis=-1), L2_attn_W_in, L2_attn_conv_w, L2_attn_conv_b, L2_attn_W_dt, L2_attn_b_dt, L2_attn_W_B, L2_attn_W_C, L2_attn_D, L2_attn_W_out), axis=-1)
    x = x + _layernorm(_L2_ffn_ref(_layernorm(x, axis=-1), L2_ffn_Wg, L2_ffn_bg, L2_ffn_W1, L2_ffn_b1, L2_ffn_W2, L2_ffn_b2, L2_ffn_gamma, L2_ffn_beta), axis=-1)
    x = x + _layernorm(_L3_attn_ref(_layernorm(x, axis=-1), L3_attn_q_w, L3_attn_k_w, L3_attn_v_w, L3_attn_Wq, L3_attn_Wk, L3_attn_g_w, L3_attn_g_b, L3_attn_base_decay_logits, L3_attn_out_w, L3_attn_out_b, L3_attn_ln_g, L3_attn_ln_b), axis=-1)
    x = x + _layernorm(_L3_ffn_ref(_layernorm(x, axis=-1), L3_ffn_w_gate, L3_ffn_w_up, L3_ffn_w_down), axis=-1)
    return x

_drawn_inputs = setup_inputs


def setup_inputs(seed=0):
    import zlib

    import numpy as np

    out = dict(_drawn_inputs(seed))
    spreads = {'L0_attn_ln1_g': (1.0, 0.6),
     'L0_attn_ln1_b': (0.0, 0.666),
     'L0_attn_bQ': (0.0, 0.8),
     'L0_attn_bK': (0.0, 2.0),
     'L0_attn_bV': (0.0, 0.385),
     'L0_attn_bO': (0.0, 0.1),
     'L0_attn_bg': (0.0, 0.762),
     'L0_attn_ln2_g': (1.0, 0.6),
     'L0_attn_ln2_b': (0.0, 0.518),
     'L0_attn_b1': (0.0, 0.28),
     'L0_attn_b2': (0.0, 0.1),
     'L0_ffn_q_scale': (1.0, 0.6),
     'L0_ffn_k_scale': (1.0, 0.6),
     'L0_ffn_ln_g': (1.0, 0.6),
     'L0_ffn_ln_b': (0.0, 0.8),
     'L0_ffn_b1': (0.0, 0.457),
     'L0_ffn_b2': (0.0, 0.1),
     'L1_attn_bq': (0.0, 0.1),
     'L1_attn_bk': (0.0, 2.0),
     'L1_attn_bv': (0.0, 0.1),
     'L1_attn_gamma': (1.0, 0.2),
     'L1_attn_beta': (0.0, 0.1),
     'L1_ffn_q_scale': (1.0, 0.6),
     'L1_ffn_k_scale': (1.0, 0.6),
     'L1_ffn_ln_g': (1.0, 0.6),
     'L1_ffn_ln_b': (0.0, 0.8),
     'L1_ffn_b1': (0.0, 0.688),
     'L1_ffn_b2': (0.0, 0.1),
     'L2_attn_conv_b': (0.0, 0.1),
     'L2_attn_D': (1.0, 0.2),
     'L2_ffn_bg': (0.0, 0.417),
     'L2_ffn_b1': (0.0, 0.634),
     'L2_ffn_b2': (0.0, 0.331),
     'L2_ffn_gamma': (1.0, 0.2),
     'L2_ffn_beta': (0.0, 0.283),
     'L3_attn_g_b': (-2.1972246170043945, 0.6),
     'L3_attn_base_decay_logits': (3.891820192337036, 0.6),
     'L3_attn_out_b': (0.0, 2.0),
     'L3_attn_ln_g': (1.0, 0.2),
     'L3_attn_ln_b': (0.0, 0.28)}
    factors = {'L0_attn_WQ': 8.0,
     'L0_attn_WK': 8.0,
     'L0_attn_WV': 5.654,
     'L0_attn_WO': 3.2,
     'L0_attn_Wg': 5.418,
     'L0_attn_A': 8.0,
     'L0_attn_Bw': 3.316,
     'L0_attn_Cw': 3.28,
     'L0_ffn_W1': 3.149,
     'L0_ffn_W2': 3.078,
     'L1_ffn_wqkv': 3.161,
     'L1_ffn_wo': 3.176,
     'L1_ffn_w1': 4.77,
     'L1_ffn_w2': 4.731,
     'L2_attn_W_dt': 64.0,
     'L2_attn_b_dt': 64.0,
     'L2_attn_W_B': 64.0,
     'L2_attn_W_C': 64.0,
     'L2_ffn_Wg': 2.878,
     'L2_ffn_W1': 4.166,
     'L2_ffn_W2': 3.76,
     'L3_attn_q_w': 8.0,
     'L3_attn_k_w': 8.0,
     'L3_attn_v_w': 8.0,
     'L3_attn_Wq': 8.0,
     'L3_attn_Wk': 8.0,
     'L3_attn_g_w': 8.0,
     'L3_attn_out_w': 8.0}
    for name, (base, spread) in spreads.items():
        noise = np.random.default_rng([zlib.crc32(name.encode()), seed]).standard_normal(out[name].shape)
        drawn = base * np.exp(spread * noise) if base else spread * noise
        out[name] = jnp.asarray(drawn.astype(out[name].dtype))
    for name, factor in factors.items():
        out[name] = (out[name] * factor).astype(out[name].dtype)
    return out
```

```python
from contextlib import ExitStack, contextmanager

import numpy as np

import concourse.bass as bass
from concourse import mybir

P = 128
B, T, D = 8, 512, 128
NT = T // P
EPS = 1e-5
NEG = -1e30
F32 = mybir.dt.float32
BF16 = mybir.dt.bfloat16
U32 = mybir.dt.uint32
ALU = mybir.AluOpType
ACT = mybir.ActivationFunctionType
AX = mybir.AxisListType.X


class Results:

    def __init__(self, nc, stage, engine, plan):
        self.sem = nc.alloc_semaphore(f"{stage}_{engine}_done")
        self.key, self.plan = f"{stage}_{engine}", plan
        self.at, self.once, self.each = plan.get(self.key, ({}, 0, 1))
        self.found, self.n, self.n_once = {}, 0, 0

    def __call__(self, *name):
        self.n += 1
        self.found[name] = self.n
        return self.sem, 1

    def end_once(self):
        self.n_once, self.n = self.n, 0

    def close(self):
        self.plan[self.key] = (self.found, self.n_once, self.n)


class Waits:

    def __init__(self, eng, own, turns=None, layer=None, trips=1):
        self.eng, self.own_results, self.turn, self.layer, self.trips = eng, own, turns, layer, trips

    def value(self, r, n, back):
        v = n + r.each * (1 - back)
        if self.turn is not None:
            v = v + r.once + self.turn * r.each
        if self.layer is not None:
            v = v + self.layer * (r.once + self.trips * r.each)
        return v

    def __call__(self, r, *name, back=0):
        return r.sem, self.value(r, r.at.get(name, 1), back)

    def layer_start(self, r):
        return r.sem, r.each + self.layer * (r.once + self.trips * r.each)

    def own(self):
        r = self.own_results
        return r.sem, self.value(r, r.n, 0)


class Stage:

    def __init__(self, nc, name, plan, trips=B, layers=None):
        self.nc, self.name, self.trips, self.layers = nc, name, trips, layers
        self.stack = ExitStack()
        self.PE, self.ACT, self.DVE, self.POOL = (Results(nc, name, e, plan) for e in ("pe", "act", "dve", "pool"))
        self.loaded = nc.alloc_semaphore(f"{name}_weights_loaded")
        self.loads = 0

    def sb(self, name, shape, dt=F32):
        return self.stack.enter_context(self.nc.sbuf_tensor(f"{self.name}_{name}", shape, dt))

    def once(self, eng, own):
        if self.layers is None:
            eng.sem_inc(own.sem, own.each)
        return Waits(eng, own)

    @contextmanager
    def loop(self, eng, own):
        own.end_once()
        with eng.Fori(0, self.trips, 1) as i:
            yield i, Waits(eng, own, i)

    @contextmanager
    def layer_loop(self, eng, own):
        eng.sem_inc(own.sem, own.each)
        with eng.Fori(0, self.layers, 1) as l:
            w = Waits(eng, own, None, l, self.trips)
            yield l, w

    @contextmanager
    def sequence_loop(self, eng, own, l):
        own.end_once()
        with eng.Fori(0, self.trips, 1) as i:
            yield i, Waits(eng, own, i, l, self.trips)

    def load(self, sp, dst, src):
        sp.dma_start(dst, src).then_inc(self.loaded, 16)
        self.loads += 16

    def close(self):
        for r in (self.PE, self.ACT, self.DVE, self.POOL):
            r.close()
        self.stack.close()


class Common:

    def __init__(self, nc, d):
        self.nc, self.d = nc, d
        self.ps = nc.alloc_psum_tensor("ps", [P, 8, 512], F32)
        self.x = nc.alloc_sbuf_tensor("x_all", [P, B * NT, D], F32)
        self.y = nc.alloc_sbuf_tensor("y_all", [P, B * NT, D], F32)
        self.ident = nc.alloc_sbuf_tensor("ident", [P, P], F32)
        self.ident_bf = nc.alloc_sbuf_tensor("ident_bf", [P, P], BF16)
        self.ones = nc.alloc_sbuf_tensor("ones", [P, P], F32)
        self.neghalf = nc.alloc_sbuf_tensor("neghalf", [P, 64], F32)
        self.xb = nc.alloc_sbuf_tensor("xb", [P, NT, D], F32)
        self.yb = nc.alloc_sbuf_tensor("yb", [P, NT, D], F32)
        self.nb = nc.alloc_sbuf_tensor("nb", [P, NT, D], F32)
        self.st = nc.alloc_sbuf_tensor("bn_st", [P, NT, 6], F32)
        self.mv = nc.alloc_sbuf_tensor("bn_mv", [P, NT, 2], F32)
        self.ve = nc.alloc_sbuf_tensor("bn_ve", [P, NT], F32)
        self.rs = nc.alloc_sbuf_tensor("bn_rs", [P, NT], F32)

    def bank(self, b, rows=P):
        return self.ps[0:rows, b, :]


def column(v):
    return v.rearrange("(p o) -> p o", o=1)


def row(v):
    return v.rearrange("(o n) -> o n", o=1)



def dve_norm(nc, C, S, w, src, dst, name):
    V, G = S.DVE, S.POOL
    for t in range(NT):
        nc.vector.bn_stats(C.st[:, t, :], src[:, t, :]).then_inc(*V(name, "stats", t))
    nc.vector.wait_ge(*w.own())
    nc.vector.memset(C.ve[:, :], 0.0).then_inc(*V(name, "clear"))
    for t in range(NT):
        nc.vector.bn_aggr(C.mv[:, t, :], C.st[:, t, :]).then_inc(*V(name, "moments", t))
    nc.vector.wait_ge(*w.own())
    nc.vector.tensor_scalar(C.ve[:, :], C.mv[:, :, 1], EPS, None, ALU.add).then_inc(*V(name, "var"))
    nc.vector.wait_ge(*w(G, name, "rstd"))
    for t in range(NT):
        nc.vector.tensor_scalar(dst[:, t, :], src[:, t, :], C.mv[:, t, 0:1], C.rs[:, t:t + 1],
                                ALU.subtract, ALU.mult).then_inc(*V(name, t))


def pool_norm(nc, C, S, w, name):
    nc.gpsimd.wait_ge(*w(S.DVE, name, "var"))
    nc.gpsimd.tensor_tensor(C.rs[:, :], C.ve[:, :], C.neghalf[:, 0:NT], ALU.pow).then_inc(*S.POOL(name, "rstd"))


def dve_add_norm(nc, C, S, w, i, name):
    dve_norm(nc, C, S, w, C.yb, C.nb, name)
    nc.vector.wait_ge(*w.own())
    nc.vector.tensor_tensor(C.x[:, bass.ds(i * NT, NT), :], C.xb[:, :, :], C.nb[:, :, :],
                            ALU.add).then_inc(*S.DVE(name, "x"))


def pe_turn(nc, C, S, w, src, bank, name):
    for t in range(NT):
        nc.tensor.transpose(C.ps[:, bank, t * P:(t + 1) * P], src[:, t, :], C.ident[:, :]).then_inc(*S.PE(name, t))


def pe_rows(nc, C, w, bank, lhs, weights, bias=None):
    for t in range(NT):
        o = C.ps[:, bank, t * P:(t + 1) * P]
        for c in range(len(lhs)):
            last = nc.tensor.matmul(o, lhs[c][:, t * P:(t + 1) * P], weights[c], start=(c == 0),
                                    stop=(bias is None and c == len(lhs) - 1))
        if bias is not None:
            last = nc.tensor.matmul(o, C.ones[0:1, :], bias, start=False, stop=True)
    return last


def stage_norm_in(nc, C, plan, name="normin"):
    S = Stage(nc, name, plan)
    A, V, G = S.ACT, S.DVE, S.POOL
    with nc.Block() as block:
        @block.scalar
        def _(act):
            S.once(act, A)
            with S.loop(act, A) as (i, w):
                act.wait_ge(*w(V, "norm", NT - 1, back=1))
                nc.scalar.activation(C.xb[:, :, :], C.x[:, bass.ds(i * NT, NT), :], ACT.Copy).then_inc(*A("xb"))

        @block.gpsimd
        def _(pool):
            S.once(pool, G)
            with S.loop(pool, G) as (i, w):
                pool_norm(nc, C, S, w, "norm")

        @block.vector
        def _(dve):
            S.once(dve, V)
            with S.loop(dve, V) as (i, w):
                dve.wait_ge(*w(A, "xb"))
                dve_norm(nc, C, S, w, C.xb, C.nb, "norm")
                dve.wait_ge(*w.own())
                nc.vector.tensor_copy(C.y[:, bass.ds(i * NT, NT), :], C.nb[:, :, :]).then_inc(*V("y"))
    S.close()


def stage_norm_out(nc, C, plan, name="normout"):
    S = Stage(nc, name, plan)
    A, V, G = S.ACT, S.DVE, S.POOL
    with nc.Block() as block:
        @block.scalar
        def _(act):
            S.once(act, A)
            with S.loop(act, A) as (i, w):
                act.wait_ge(*w(V, "norm", "x", back=1))
                nc.scalar.activation(C.xb[:, :, :], C.x[:, bass.ds(i * NT, NT), :], ACT.Copy).then_inc(*A("xb"))
                nc.scalar.activation(C.yb[:, :, :], C.y[:, bass.ds(i * NT, NT), :], ACT.Copy).then_inc(*A("yb"))

        @block.gpsimd
        def _(pool):
            S.once(pool, G)
            with S.loop(pool, G) as (i, w):
                pool_norm(nc, C, S, w, "norm")

        @block.vector
        def _(dve):
            S.once(dve, V)
            with S.loop(dve, V) as (i, w):
                dve.wait_ge(*w(A, "yb"))
                dve_add_norm(nc, C, S, w, i, "norm")
    S.close()


def setup(nc, C, d_x):
    x_loaded = nc.alloc_semaphore("x_loaded")
    filled = nc.alloc_semaphore("constants_filled")
    with nc.Block() as block:
        @block.sync
        def _(sp):
            sp.dma_start(C.x[:, :, :], d_x.rearrange("b (t p) d -> p (b t) d", p=P)).then_inc(x_loaded, 16)
            sp.wait_ge(x_loaded, 16)

        @block.gpsimd
        def _(pool):
            nc.gpsimd.memset(C.ident[:, :], 0.0).then_inc(filled, 1)
            nc.gpsimd.memset(C.ones[:, :], 1.0).then_inc(filled, 1)
            nc.gpsimd.memset(C.neghalf[:, :], -0.5).then_inc(filled, 1)
            pool.wait_ge(filled, 3)
            nc.gpsimd.affine_select(out=C.ident[:, :], in_=C.ident[:, :], compare_op=ALU.not_equal, fill=1.0,
                                    base=0, pattern=[[-1, P]], channel_multiplier=1).then_inc(filled, 1)
            pool.wait_ge(filled, 4)
            nc.gpsimd.tensor_copy(C.ident_bf[:, :], C.ident[:, :]).then_inc(filled, 1)
            pool.wait_ge(filled, 5)



def stage_l0_attn(nc, C, plan):
    H, DH, WIN, N, FF = 16, 8, 128, 64, 4
    SCALE = float(np.float32(1.0) / np.sqrt(np.float32(DH)))
    d = C.d
    S = Stage(nc, "l0attn", plan)
    PE, A, V, G = S.PE, S.ACT, S.DVE, S.POOL
    ps = C.ps
    wq, wk, wv, wo, wg = (S.sb(n, [P, D]) for n in ("wq", "wk", "wv", "wo", "wg"))
    bw, cw = S.sb("bw", [P, N]), S.sb("cw", [N, D])
    w1, w2 = S.sb("w1", [P, FF, P]), S.sb("w2", [P, FF, D])
    cols = S.sb("cols", [P, 16])
    LN1G, LN1B, BQ, BK, LN2G, LN2B, B1, DEC = 0, 1, 2, 3, 4, 5, 6, 10
    rows = S.sb("rows", [1, 4, D])
    BV, BO, BG, B2 = 0, 1, 2, 3
    headmask = S.sb("headmask", [P, 4])
    mask = S.sb("mask", [P, 2, 2, 2 * P])
    mask_bf = S.sb("mask_bf", [P, 2, 2, 2 * P], BF16)
    y0, hT, qm = S.sb("y0", [P, NT, D]), S.sb("hT", [P, T]), S.sb("qm", [P, 4, T])
    kT = S.sb("kT", [P, P + T])
    va = S.sb("va", [P, NT + 1, H, DH + 1])
    gate, sT = S.sb("gate", [P, NT, D]), S.sb("sT", [N, T])
    mx, nm = S.sb("mx", [P, 4, 2]), S.sb("nm", [P, 4, 2])
    pr, pT = S.sb("pr", [P, 3, 2, 2 * P]), S.sb("pT", [P, 2, 4, P])
    rec, ao, aoT = S.sb("rec", [P, H]), S.sb("ao", [P, NT, D]), S.sb("aoT", [P, T])
    ssm, x1, hid = S.sb("ssm", [P, NT, D]), S.sb("x1", [P, NT, D]), S.sb("hid", [P, FF, T])
    K = NT * H // 2
    LN1, LN2, LN3, LN4 = "norm_x", "norm_1", "norm_2", "norm_y"

    with nc.Block() as block:
        @block.sync
        def _(sp):
            for dst, n in ((wq, "WQ"), (wk, "WK"), (wv, "WV"), (wo, "WO"), (wg, "Wg"), (bw, "Bw"), (cw, "Cw")):
                S.load(sp, dst[:, :], d["L0_attn_" + n])
            S.load(sp, w1[:, :, :], d["L0_attn_W1"].rearrange("k (c n) -> k c n", c=FF))
            S.load(sp, w2[:, :, :], d["L0_attn_W2"].rearrange("(c k) n -> k c n", c=FF))
            for c, n in ((LN1G, "ln1_g"), (LN1B, "ln1_b"), (BQ, "bQ"), (BK, "bK"), (LN2G, "ln2_g"), (LN2B, "ln2_b")):
                S.load(sp, cols[:, c:c + 1], column(d["L0_attn_" + n]))
            for c in range(FF):
                S.load(sp, cols[:, B1 + c:B1 + c + 1], column(d["L0_attn_b1"][c * P:(c + 1) * P]))
            S.load(sp, cols[0:N, DEC:DEC + 1], column(d["L0_attn_A"]))
            for c, n in ((BV, "bV"), (BO, "bO"), (BG, "bg"), (B2, "b2")):
                S.load(sp, rows[:, c, :], row(d["L0_attn_" + n]))
            S.load(sp, headmask[:, :], d["const_head_of_four"])
            S.load(sp, mask[:, :, :, :], d["const_l0_mask"])
            sp.wait_ge(S.loaded, S.loads)

        @block.gpsimd
        def _(pool):
            w = S.once(pool, G)
            nc.gpsimd.memset(kT[:, 0:P], 0.0).then_inc(*G("kT_pad"))
            nc.gpsimd.memset(va[:, :, :, :], 0.0).then_inc(*G("va_pad"))
            pool.wait_ge(*w.own())
            nc.gpsimd.memset(va[:, :, :, DH:DH + 1], 1.0).then_inc(*G("va_ones"))
            pool.wait_ge(S.loaded, S.loads)
            nc.gpsimd.tensor_copy(mask_bf[:, :, :, :], mask[:, :, :, :]).then_inc(*G("mask"))
            pool.wait_ge(*w.own())
            with S.loop(pool, G) as (i, w):
                for name in (LN1, LN2, LN3, LN4):
                    pool_norm(nc, C, S, w, name)

        @block.scalar
        def _(act):
            w = S.once(act, A)
            act.wait_ge(S.loaded, S.loads)
            act.wait_ge(*w(G, "va_ones"))
            with S.loop(act, A) as (i, w):
                act.wait_ge(*w(V, LN4, "x", back=1))
                nc.scalar.activation(C.xb[:, :, :], C.x[:, bass.ds(i * NT, NT), :], ACT.Copy).then_inc(*A("xb"))
                act.wait_ge(*w(PE, "hT", NT - 1))
                nc.scalar.activation(hT[:, :], C.bank(0), ACT.Identity, bias=cols[:, LN1B:LN1B + 1],
                                     scale=cols[:, LN1G:LN1G + 1]).then_inc(*A("hT"))
                act.wait_ge(*w(PE, "K"))
                nc.scalar.activation(kT[:, P:], C.bank(2), ACT.Identity,
                                     bias=cols[:, BK:BK + 1]).then_inc(*A("kT"))
                act.wait_ge(*w(PE, "V"))
                nc.scalar.activation(va[:, 1:, :, 0:DH], C.bank(4).rearrange("p (t h e) -> p t h e", t=NT, h=H),
                                     ACT.Copy).then_inc(*A("va"))
                act.wait_ge(*w(PE, "gate"))
                nc.scalar.activation(gate[:, :, :], C.bank(5).rearrange("p (t e) -> p t e", t=NT), ACT.Tanh,
                                     scale=0.5).then_inc(*A("tanh"))
                act.wait_ge(*w(PE, "ssm"))
                nc.scalar.activation(ssm[:, :, :], C.bank(6).rearrange("p (t e) -> p t e", t=NT),
                                     ACT.Copy).then_inc(*A("ssm"))
                for k in range(K):
                    act.wait_ge(*w(V, "negmax", k))
                    if k >= 3:
                        act.wait_ge(*w(PE, "pT", k - 3))
                    for j in range(2):
                        nc.scalar.activation(pr[:, k % 3, j, :], ps[:, k % 3, j * 2 * P:(j + 1) * 2 * P], ACT.Exp,
                                             bias=nm[:, k % 4, j:j + 1], scale=SCALE).then_inc(*A("exp", k, j))
                act.wait_ge(*w(PE, "aoT", NT - 1))
                nc.scalar.activation(aoT[:, :], C.bank(7), ACT.Copy).then_inc(*A("aoT"))
                act.wait_ge(*w(PE, "h2T", NT - 1))
                nc.scalar.activation(hT[:, :], C.bank(1), ACT.Identity, bias=cols[:, LN2B:LN2B + 1],
                                     scale=cols[:, LN2G:LN2G + 1]).then_inc(*A("h2T"))
                for c in range(FF):
                    act.wait_ge(*w(PE, "up", c))
                    nc.scalar.activation(hid[:, c, :], C.bank(2 + c), ACT.Gelu,
                                         bias=cols[:, B1 + c:B1 + c + 1]).then_inc(*A("hid", c))

        @block.vector
        def _(dve):
            w = S.once(dve, V)
            dve.wait_ge(S.loaded, S.loads)
            dve.wait_ge(*w(G, "mask"))
            with S.loop(dve, V) as (i, w):
                dve.wait_ge(*w(A, "xb"))
                dve_norm(nc, C, S, w, C.xb, y0, LN1)
                dve.wait_ge(*w.own())
                dve_norm(nc, C, S, w, y0, C.nb, LN2)
                dve.wait_ge(*w(PE, "Q"))
                for j in range(4):
                    nc.vector.tensor_scalar(qm[:, j, :], C.bank(1), cols[:, BQ:BQ + 1], headmask[:, j:j + 1],
                                            ALU.add, ALU.mult).then_inc(*V("qm", j))
                dve.wait_ge(*w(PE, "u"))
                nc.vector.tensor_tensor_scan(sT[:, :], cols[0:N, DEC:DEC + 1].to_broadcast([N, T]), C.bank(3, N),
                                             0.0, ALU.mult, ALU.add).then_inc(*V("sT"))
                dve.wait_ge(*w(A, "tanh"))
                nc.vector.tensor_scalar(gate[:, :, :], gate[:, :, :], 0.5, 0.5, ALU.mult,
                                        ALU.add).then_inc(*V("gate"))

                def maximum(k):
                    dve.wait_ge(*w(PE, "S", k))
                    nc.vector.tensor_reduce(mx[:, k % 4, :], C.bank(k % 3).rearrange("p (j n) -> p j n", j=2),
                                            AX, ALU.max).then_inc(*V("max", k))
                    dve.wait_ge(*w.own())
                    nc.vector.tensor_scalar(nm[:, k % 4, :], mx[:, k % 4, :], -SCALE, None,
                                            ALU.mult).then_inc(*V("negmax", k))

                def copy_probs(k):
                    dve.wait_ge(*w(PE, "pT", k))
                    if k >= 2:
                        dve.wait_ge(*w(PE, "O", k - 2))
                    nc.vector.tensor_copy(pT[:, k % 2, :, :],
                                          C.bank(3 + k % 2).rearrange("p (j n) -> p j n", j=4)).then_inc(*V("pT", k))

                def normalise(t):
                    dve.wait_ge(*w(PE, "O", (t + 1) * H // 2 - 1))
                    o = ps[:, 5 + t % 2, 0:H * (DH + 1)].rearrange("p (h e) -> p h e", h=H)
                    nc.vector.reciprocal(rec[:, :], o[:, :, DH]).then_inc(*V("rec", t))
                    dve.wait_ge(*w.own())
                    nc.vector.tensor_tensor(ao[:, t, :].rearrange("p (h e) -> p h e", h=H), o[:, :, 0:DH],
                                            rec[:, :].unsqueeze(2).to_broadcast([P, H, DH]),
                                            ALU.mult).then_inc(*V("ao", t))

                for k in range(K + 3):
                    if k < K:
                        maximum(k)
                    if 2 <= k < K + 2:
                        copy_probs(k - 2)
                    if k >= 3 and (k - 3) % (H // 2) == H // 2 - 1:
                        normalise((k - 3) // (H // 2))
                dve.wait_ge(*w(PE, "attn"))
                dve.wait_ge(*w(A, "ssm"))
                attn = C.bank(0).rearrange("p (t e) -> p t e", t=NT)
                nc.vector.tensor_tensor(x1[:, :, :], attn, ssm[:, :, :], ALU.subtract).then_inc(*V("x1", 0))
                dve.wait_ge(*w.own())
                nc.vector.tensor_tensor(x1[:, :, :], x1[:, :, :], gate[:, :, :], ALU.mult).then_inc(*V("x1", 1))
                dve.wait_ge(*w.own())
                nc.vector.tensor_tensor(x1[:, :, :], x1[:, :, :], ssm[:, :, :], ALU.add).then_inc(*V("x1", 2))
                dve.wait_ge(*w.own())
                nc.vector.tensor_tensor(x1[:, :, :], x1[:, :, :], y0[:, :, :], ALU.add).then_inc(*V("x1", 3))
                dve.wait_ge(*w.own())
                dve_norm(nc, C, S, w, x1, C.nb, LN3)
                dve.wait_ge(*w(PE, "down"))
                nc.vector.tensor_tensor(C.yb[:, :, :], x1[:, :, :], C.bank(6).rearrange("p (t e) -> p t e", t=NT),
                                        ALU.add).then_inc(*V("y"))
                dve.wait_ge(*w.own())
                dve_add_norm(nc, C, S, w, i, LN4)

        @block.tensor
        def _(pe):
            w = S.once(pe, PE)
            pe.wait_ge(S.loaded, S.loads)
            pe.wait_ge(*w(G, "mask"))
            with S.loop(pe, PE) as (i, w):
                pe.wait_ge(*w(A, "xb"))
                pe.wait_ge(*w(V, LN2, NT - 1))
                pe_turn(nc, C, S, w, C.nb, 0, "hT")
                pe.wait_ge(*w(A, "hT"))
                pe.wait_ge(*w(V, "y", back=1))
                nc.tensor.matmul(C.bank(1), wq[:, :], hT[:, :], start=True, stop=True).then_inc(*PE("Q"))
                nc.tensor.matmul(C.bank(2), wk[:, :], hT[:, :], start=True, stop=True).then_inc(*PE("K"))
                nc.tensor.matmul(C.bank(3, N), bw[:, :], hT[:, :], start=True, stop=True).then_inc(*PE("u"))
                for bank, wt, b, name in ((4, wv, BV, "V"), (5, wg, BG, "gate")):
                    for t in range(NT):
                        o = ps[:, bank, t * P:(t + 1) * P]
                        nc.tensor.matmul(o, hT[:, t * P:(t + 1) * P], wt[:, :], start=True, stop=False)
                        last = nc.tensor.matmul(o, C.ones[0:1, :], rows[:, b, :], start=False, stop=True)
                    last.then_inc(*PE(name))
                pe.wait_ge(*w(V, "sT"))
                for t in range(NT):
                    last = nc.tensor.matmul(ps[:, 6, t * P:(t + 1) * P], sT[:, t * P:(t + 1) * P], cw[:, :],
                                            start=True, stop=True)
                last.then_inc(*PE("ssm"))
                pe.wait_ge(*w(V, "qm", 3))
                pe.wait_ge(*w(A, "va"))
                pe.wait_ge(*w(A, "ssm"))

                def scores(k):
                    t, h = k // (H // 2), k % (H // 2) * 2
                    if k >= 3:
                        pe.wait_ge(*w(A, "exp", k - 3, 1))
                    b = k % 3
                    nc.tensor.matmul(C.bank(b), C.ident_bf[:, :], mask_bf[:, int(t > 0), :, :], start=True,
                                     stop=False)
                    r = 32 * (h // 4)
                    for j in range(2):
                        last = nc.tensor.matmul(ps[:, b, j * 2 * P:(j + 1) * 2 * P],
                                                qm[r:r + 32, (h + j) % 4, t * P:(t + 1) * P],
                                                kT[r:r + 32, t * P:(t + 2) * P], start=False, stop=(j == 1))
                    last.then_inc(*PE("S", k))

                def turn_probs(k):
                    pe.wait_ge(*w(A, "exp", k, 1))
                    if k >= 2:
                        pe.wait_ge(*w(V, "pT", k - 2))
                    for j in range(2):
                        for s in range(2):
                            n = 2 * j + s
                            last = nc.tensor.transpose(ps[:, 3 + k % 2, n * P:(n + 1) * P],
                                                       pr[:, k % 3, j, s * P:(s + 1) * P], C.ident[:, :])
                    last.then_inc(*PE("pT", k))

                def values(k):
                    t, h = k // (H // 2), k % (H // 2) * 2
                    pe.wait_ge(*w(V, "pT", k))
                    if h == 0 and t >= 2:
                        pe.wait_ge(*w(V, "ao", t - 2))
                    for j in range(2):
                        for s in range(2):
                            c = (h + j) * (DH + 1)
                            last = nc.tensor.matmul(ps[:, 5 + t % 2, c:c + DH + 1], pT[:, k % 2, 2 * j + s, :],
                                                    va[:, t + s, h + j, :], start=(s == 0), stop=(s == 1))
                    last.then_inc(*PE("O", k))

                for k in range(K + 3):
                    if k < K:
                        scores(k)
                    if 2 <= k < K + 2:
                        turn_probs(k - 2)
                    if k >= 3:
                        values(k - 3)
                pe.wait_ge(*w(V, "ao", NT - 1))
                pe_turn(nc, C, S, w, ao, 7, "aoT")
                pe.wait_ge(*w(A, "aoT"))
                for t in range(NT):
                    o = ps[:, 0, t * P:(t + 1) * P]
                    nc.tensor.matmul(o, aoT[:, t * P:(t + 1) * P], wo[:, :], start=True, stop=False)
                    last = nc.tensor.matmul(o, C.ones[0:1, :], rows[:, BO, :], start=False, stop=True)
                last.then_inc(*PE("attn"))
                pe.wait_ge(*w(V, LN3, NT - 1))
                pe_turn(nc, C, S, w, C.nb, 1, "h2T")
                pe.wait_ge(*w(A, "h2T"))
                for c in range(FF):
                    nc.tensor.matmul(C.bank(2 + c), w1[:, c, :], hT[:, :], start=True,
                                     stop=True).then_inc(*PE("up", c))
                for t in range(NT):
                    o = ps[:, 6, t * P:(t + 1) * P]
                    for c in range(FF):
                        pe.wait_ge(*w(A, "hid", c))
                        nc.tensor.matmul(o, hid[:, c, t * P:(t + 1) * P], w2[:, c, :], start=(c == 0), stop=False)
                    last = nc.tensor.matmul(o, C.ones[0:1, :], rows[:, B2, :], start=False, stop=True)
                last.then_inc(*PE("down"))
    S.close()



def local_layers(nc, C, plan, name, block_name, H, DEPTH, WIN, weights):
    E = 64
    INNER, HID = H * E, int(D * 4 * 2 / 3)
    HG = H // 8
    CH = INNER // P
    QT = P - WIN
    QR = 96
    NA = -(-T // QT)
    HC = -(-HID // P)
    hid_rows = [min(P, HID - c * P) for c in range(HC)]
    nq = [min(QT, T - QT * a) for a in range(NA)]
    nk = [WIN + n for n in nq]
    QK_SCALE = 8.0
    d = C.d
    Wqkv, qs, ksc, Wo, lng, lnb, W1, b1, W2, b2 = (d[f"{block_name}_{n}"] for n in weights)
    S = Stage(nc, name, plan, layers=DEPTH)
    PE, A, V, G = S.PE, S.ACT, S.DVE, S.POOL
    ps = C.ps
    wqkv, wo = S.sb("wqkv", [P, 3 * INNER]), S.sb("wo", [P, CH, D])
    w1, w2 = S.sb("w1", [P, 2 * HID]), S.sb("w2", [P, HC, D])
    cols, b2row = S.sb("cols", [P, 2 + 2 * HC]), S.sb("b2row", [1, D])
    scales = S.sb("scales", [P, 2, E])
    base = S.sb("tables", [P, 4, NT, E])
    tab = S.sb("tables_scaled", [P, 4, NT, E])
    mask_f, mask = S.sb("mask_f", [P, 2, 4, P]), S.sb("mask", [P, 2, 4, P], BF16)
    shift = S.sb("shift", [P, 2, P])
    hT = S.sb("hT", [P, WIN + T])
    work = S.sb("work", [P, 4, 8 * P])
    sq, r2 = work[:, 0:2, 0:INNER], work[:, 2:4, 0:INNER]
    pr = work[:, :, :].rearrange("p k (h n) -> p k h n", h=8)
    ge, hid = (work[:, k:k + 2, :].rearrange("p k n -> p (k n)")[:, 0:HC * T].rearrange("p (c n) -> p c n", c=HC)
               for k in (0, 2))
    rq = S.sb("rq", [P, 2, INNER])
    n2, rn = S.sb("n2", [P, 2, H]), S.sb("rn", [P, 2, H])
    qT = S.sb("qT", [P, CH, T])
    kT = S.sb("kT", [P, CH, 2, WIN + T])
    va = S.sb("va", [P, NA, INNER])
    mx, sm, rec = (S.sb(n, [P, 4, 8]) for n in ("mx", "sm", "rec"))
    pT, aoT = S.sb("pT", [P, 2, 8, QR]), S.sb("aoT", [P, CH, T])
    ys, hnT = S.sb("ys", [P, NT, D]), S.sb("hnT", [P, T])
    U = 2 * NT
    NU = NA * HG
    LN = "norm"
    halves = INNER // 512
    pads = nc.alloc_semaphore(f"{name}_pads_filled")
    LOADS = 16 * (5 + 2 + 2 + 2 * HC + 1)

    with nc.Block() as block:
        @block.sync
        def _(sp):
            for dst, n in ((base, "tables"), (mask_f, "mask")):
                sp.dma_start(dst[:, :, :, :], d[f"const_{name}_{n}"]).then_inc(S.loaded, 16)
            sp.dma_start(shift[:, :, :], d["const_shift"]).then_inc(S.loaded, 16)
            sp.wait_ge(S.loaded, 48)

        @block.gpsimd
        def _(pool):
            w = Waits(pool, G)
            pool.wait_ge(S.loaded, 48)
            nc.gpsimd.memset(hT[:, 0:WIN + 1], 0.0).then_inc(pads, 1)
            nc.gpsimd.memset(va[:, :, :], 0.0).then_inc(pads, 1)
            nc.gpsimd.memset(work[:, :, :], 0.0).then_inc(pads, 1)
            nc.gpsimd.memset(qT[:, :, :], 0.0).then_inc(pads, 1)
            nc.gpsimd.memset(kT[:, :, :, :], 0.0).then_inc(pads, 1)
            nc.gpsimd.tensor_copy(mask[:, :, :, :], mask_f[:, :, :, :]).then_inc(pads, 1)
            with S.layer_loop(pool, G) as (l, w):
                pool.wait_ge(S.loaded, 48 + LOADS * (l + 1))
                pool.wait_ge(*w.layer_start(V))
                for x in range(2):
                    sc = scales[:, x, :].unsqueeze(1).to_broadcast([P, NT, E])
                    nc.gpsimd.tensor_tensor(tab[:, 2 * x], base[:, 2 * x], sc, ALU.mult).then_inc(*G("tab", x, 0))
                    for a, b in ((0, E // 2), (E // 2, 0)):
                        nc.gpsimd.tensor_tensor(tab[:, 2 * x + 1, :, a:a + E // 2], base[:, 2 * x + 1, :, a:a + E // 2],
                                                sc[:, :, b:b + E // 2], ALU.mult).then_inc(*G("tab", x, 1, a))
                with S.sequence_loop(pool, G, l) as (i, w):
                    for u in range(U):
                        x = u % 2
                        pool.wait_ge(*w(V, "n2", u))
                        nc.gpsimd.tensor_tensor(rn[:, x, :], n2[:, x, :], C.neghalf[:, 0:H],
                                                ALU.pow).then_inc(*G("rn", u))
                        pool.wait_ge(*w.own())
                        pool.wait_ge(*w(V, "rot", u))
                        v = rq[:, x, :].rearrange("p (h e) -> p h e", h=H)
                        nc.gpsimd.tensor_tensor(v, v, rn[:, x, :].unsqueeze(2).to_broadcast([P, H, E]),
                                                ALU.mult).then_inc(*G("unit", u))
                    for n in range(NU):
                        pool.wait_ge(*w(V, "rec", n))
                        nc.gpsimd.tensor_tensor(pr[0:QR, n % 4], pr[0:QR, n % 4],
                                                rec[0:QR, n % 4, :].unsqueeze(2).to_broadcast([QR, 8, P]),
                                                ALU.mult).then_inc(*G("probs", n))
                    pool_norm(nc, C, S, w, LN)

        @block.scalar
        def _(act):
            act.wait_ge(pads, 6)
            with S.layer_loop(act, A) as (l, w):
                act.wait_ge(*w.layer_start(A))
                for r in (PE, V, G):
                    act.wait_ge(*w.layer_start(r))

                def load(dst, src):
                    act.dma_start(dst, src).then_inc(S.loaded, 16)

                def of_layer(x):
                    return x[bass.ds(l, 1)]

                load(wqkv[:, :], of_layer(Wqkv).rearrange("o k n -> (o k) n"))
                load(wo[:, :, :], of_layer(Wo).rearrange("o (c k) n -> k (o c) n", k=P))
                load(w1[:, :], of_layer(W1).rearrange("o k n -> (o k) n"))
                full = HID // P
                load(w2[:, 0:full, :], W2[bass.ds(l, 1), 0:full * P].rearrange("o (c k) n -> k (o c) n", k=P))
                load(w2[0:hid_rows[-1], full, :], W2[bass.ds(l, 1), full * P:].rearrange("o k n -> (o k) n"))
                load(scales[:, 0, :], of_layer(qs).to_broadcast([P, E]))
                load(scales[:, 1, :], of_layer(ksc).to_broadcast([P, E]))
                load(cols[:, 0:1], of_layer(lng).rearrange("o p -> p o"))
                load(cols[:, 1:2], of_layer(lnb).rearrange("o p -> p o"))
                for g in range(2):
                    for c in range(HC):
                        a, m = g * HID + c * P, hid_rows[c]
                        load(cols[0:m, 2 + g * HC + c:3 + g * HC + c],
                             b1[bass.ds(l, 1), a:a + m].rearrange("o p -> p o"))
                load(b2row[:, :], of_layer(b2))
                act.wait_ge(S.loaded, 48 + LOADS * (l + 1))
                with S.sequence_loop(act, A, l) as (i, w):
                    act.wait_ge(*w(V, "y_mlp", back=1))
                    nc.scalar.activation(C.yb[:, :, :], C.y[:, bass.ds(i * NT, NT), :], ACT.Copy).then_inc(*A("yb"))
                    act.wait_ge(*w(PE, "yT", NT - 1))
                    act.wait_ge(*w(PE, "V", NA - 1, back=1))
                    nc.scalar.activation(hT[0:64, WIN:], C.bank(0, 64), ACT.Copy).then_inc(*A("hT", 0))
                    nc.scalar.activation(hT[64:128, WIN + 1:], ps[64:128, 0, 0:T - 1], ACT.Copy).then_inc(*A("hT", 1))

                    def square(u):
                        act.wait_ge(*w(PE, "qk", u))
                        if u >= 2:
                            act.wait_ge(*w(V, "n2sum", u - 2))
                        for hf in range(halves):
                            nc.scalar.activation(sq[:, u % 2, hf * 512:(hf + 1) * 512],
                                                 C.bank(2 * (u % 2) + hf), ACT.Square).then_inc(*A("sq", u, hf))

                    def keep_turned(u):
                        t, x = u // 2, u % 2
                        act.wait_ge(*w(PE, "qkT", u))
                        src = ps[:, 4:4 + halves, :].rearrange("p b (c n) -> p (b c) n", n=P)
                        if x == 0:
                            nc.scalar.activation(qT[:, :, t * P:(t + 1) * P], src, ACT.Copy).then_inc(*A("qkT", u))
                        else:
                            for b in range(2):
                                r = 64 * b
                                nc.scalar.activation(kT[r:r + 64, :, b, WIN + t * P:WIN + (t + 1) * P],
                                                     src[r:r + 64], ACT.Copy).then_inc(
                                                         *A("qkT" if b else "kT_even", u))

                    def keep_values(a):
                        act.wait_ge(*w(PE, "V", a))
                        nc.scalar.activation(va[0:nk[a], a, :],
                                             ps[0:nk[a], 6:6 + halves, :].rearrange("p b n -> p (b n)"),
                                             ACT.Copy).then_inc(*A("va", a))

                    for u in range(U + 2):
                        if u < U:
                            square(u)
                        if u >= 2:
                            keep_turned(u - 2)
                        if u < NA:
                            keep_values(u)

                    def exponent(n):
                        act.wait_ge(*w(V, "sub", n))
                        nc.scalar.activation(pr[0:QR, n % 4], pr[0:QR, n % 4], ACT.Exp,
                                             scale=QK_SCALE).then_inc(*A("exp", n))

                    def keep_probs(n):
                        act.wait_ge(*w(PE, "pT", n))
                        if n >= 2:
                            act.wait_ge(*w(PE, "O", n - 2))
                        nc.scalar.activation(pT[:, n % 2],
                                             ps[:, 4:6, :].rearrange("p b (h n) -> p (b h) n", n=P)[:, :, 0:QR],
                                             ACT.Copy).then_inc(*A("pT", n))

                    def keep_out(n):
                        a, g = n // HG, n % HG
                        act.wait_ge(*w(PE, "O", n))
                        nc.scalar.activation(aoT[:, 4 * g:4 * g + 4, QT * a:QT * a + nq[a]],
                                             ps[:, 6 + n % 2, 0:4 * QR].rearrange("p (c n) -> p c n", c=4)[:, :, 0:nq[a]],
                                             ACT.Copy).then_inc(*A("aoT", n))

                    for n in range(NU + 4):
                        if n < NU:
                            exponent(n)
                        if 3 <= n < NU + 3:
                            keep_probs(n - 3)
                        if n >= 4:
                            keep_out(n - 4)
                    act.wait_ge(*w(PE, "shifted"))
                    act.wait_ge(*w(V, "y_attn"))
                    nc.scalar.activation(ys[:, :, 0:64], C.yb[:, :, 0:64], ACT.Copy).then_inc(*A("ys", 0))
                    nc.scalar.activation(ys[:, :, 64:], ps[:, 1, 0:NT * 64].rearrange("p (t e) -> p t e", t=NT),
                                         ACT.Copy).then_inc(*A("ys", 1))
                    act.wait_ge(*w(PE, "hnT", NT - 1))
                    nc.scalar.activation(hnT[:, :], C.bank(2), ACT.Identity, bias=cols[:, 1:2],
                                         scale=cols[:, 0:1]).then_inc(*A("hnT"))
                    for c in range(HC):
                        m = hid_rows[c]
                        act.wait_ge(*w(PE, "gate", c))
                        nc.scalar.activation(ge[0:m, c, :], C.bank(3 + c, m), ACT.Gelu,
                                             bias=cols[0:m, 2 + HC + c:3 + HC + c]).then_inc(*A("gelu", c))

        @block.vector
        def _(dve):
            dve.wait_ge(pads, 6)
            with S.layer_loop(dve, V) as (l, w):
                dve.wait_ge(S.loaded, 48 + LOADS * (l + 1))
                dve.wait_ge(*w(G, "tab", 1, 1, E // 2))
                nc.vector.memset(rec[:, :, :], 0.0).then_inc(*V("layer"))
                with S.sequence_loop(dve, V, l) as (i, w):
                    def norms_and_rotary(u):
                        t, x = u // 2, u % 2
                        banks = ps[:, 2 * x:2 * x + halves, :].rearrange("p b (h e) -> p (b h) e", e=E)
                        dve.wait_ge(*w(A, "sq", u, halves - 1))
                        if u >= 2:
                            dve.wait_ge(*w(G, "rn", u - 2))
                        nc.vector.tensor_reduce(n2[:, x, :], sq[:, x, :].rearrange("p (h e) -> p h e", h=H), AX,
                                                ALU.add).then_inc(*V("n2sum", u))
                        dve.wait_ge(*w.own())
                        nc.vector.tensor_scalar(n2[:, x, :], n2[:, x, :], 1e-24, None, ALU.max).then_inc(*V("n2", u))
                        if u >= 2:
                            dve.wait_ge(*w(PE, "qkT", u - 2))
                        cs, sn = tab[:, 2 * x, t, :], tab[:, 2 * x + 1, t, :]
                        dst = rq[:, x, :].rearrange("p (h e) -> p h e", h=H)
                        nc.vector.tensor_tensor(dst, banks, cs.unsqueeze(1).to_broadcast([P, H, E]),
                                                ALU.mult).then_inc(*V("cos", u))
                        dst = r2[:, x, :].rearrange("p (h e) -> p h e", h=H)
                        for a, b in ((0, E // 2), (E // 2, 0)):
                            last = nc.vector.tensor_tensor(
                                dst[:, :, a:a + E // 2], banks[:, :, b:b + E // 2],
                                sn[:, a:a + E // 2].unsqueeze(1).to_broadcast([P, H, E // 2]), ALU.mult)
                            last.then_inc(*V("sin" if a else "sin_low", u))
                        dve.wait_ge(*w.own())
                        nc.vector.tensor_tensor(rq[:, x, :], rq[:, x, :], r2[:, x, :], ALU.add).then_inc(*V("rot", u))

                    for u in range(U):
                        norms_and_rotary(u)

                    def subtract_max(n):
                        s = ps[0:QR, 2 * (n % 2):2 * (n % 2) + 2, :].rearrange("p b (h n) -> p (b h) n", n=P)
                        dve.wait_ge(*w(PE, "S", n))
                        nc.vector.tensor_reduce(mx[0:QR, n % 4, :], s, AX, ALU.max).then_inc(*V("max", n))
                        dve.wait_ge(*w.own())
                        if n >= 4:
                            dve.wait_ge(*w(PE, "pT", n - 4))
                        nc.vector.tensor_tensor(pr[0:QR, n % 4], s,
                                                mx[0:QR, n % 4, :].unsqueeze(2).to_broadcast([QR, 8, P]),
                                                ALU.subtract).then_inc(*V("sub", n))

                    def sums(n):
                        dve.wait_ge(*w(A, "exp", n))
                        nc.vector.tensor_reduce(sm[0:QR, n % 4, :], pr[0:QR, n % 4], AX, ALU.add).then_inc(*V("sum", n))
                        dve.wait_ge(*w.own())
                        nc.vector.reciprocal(rec[0:QR, n % 4, :], sm[0:QR, n % 4, :]).then_inc(*V("rec", n))

                    for n in range(NU + 1):
                        if n < NU:
                            subtract_max(n)
                        if n >= 1:
                            sums(n - 1)
                    dve.wait_ge(*w(PE, "attn"))
                    nc.vector.tensor_tensor(C.yb[:, :, :], C.yb[:, :, :], C.bank(0).rearrange("p (t e) -> p t e", t=NT),
                                            ALU.add).then_inc(*V("y_attn"))
                    dve.wait_ge(*w(A, "ys", 1))
                    dve_norm(nc, C, S, w, ys, C.nb, LN)
                    for c in range(HC):
                        m = hid_rows[c]
                        dve.wait_ge(*w(A, "gelu", c))
                        dve.wait_ge(*w(PE, "up", c))
                        nc.vector.scalar_tensor_tensor(out=hid[0:m, c, :], in0=C.bank([0, 1, 6][c], m),
                                                       scalar=cols[0:m, 2 + c:3 + c], in1=ge[0:m, c, :],
                                                       op0=ALU.add, op1=ALU.mult).then_inc(*V("hid", c))
                    dve.wait_ge(*w(PE, "down"))
                    nc.vector.tensor_tensor(C.y[:, bass.ds(i * NT, NT), :], C.yb[:, :, :],
                                            C.bank(7).rearrange("p (t e) -> p t e", t=NT),
                                            ALU.add).then_inc(*V("y_mlp"))

        @block.tensor
        def _(pe):
            pe.wait_ge(pads, 6)
            with S.layer_loop(pe, PE) as (l, w):
                with S.sequence_loop(pe, PE, l) as (i, w):
                    pe.wait_ge(S.loaded, 48 + LOADS * (l + 1))
                    pe.wait_ge(*w(A, "yb"))
                    pe_turn(nc, C, S, w, C.yb, 0, "yT")
                    pe.wait_ge(*w(A, "hT", 1))
                    pe.wait_ge(*w(V, "y_mlp", back=1))

                    def project(u):
                        t, x = u // 2, u % 2
                        if u >= 2:
                            pe.wait_ge(*w(V, "sin", u - 2))
                        for hf in range(halves):
                            last = nc.tensor.matmul(C.bank(2 * x + hf), hT[:, WIN + t * P:WIN + (t + 1) * P],
                                                    wqkv[:, x * INNER + hf * 512:x * INNER + (hf + 1) * 512],
                                                    start=True, stop=True)
                        last.then_inc(*PE("qk", u))

                    def turn_unit(u):
                        pe.wait_ge(*w(G, "unit", u))
                        if u >= 1:
                            pe.wait_ge(*w(A, "qkT", u - 1))
                        for c in range(CH):
                            last = nc.tensor.transpose(ps[:, 4 + c // 4, c % 4 * P:(c % 4 + 1) * P],
                                                       rq[:, u % 2, c * P:(c + 1) * P], C.ident[:, :])
                        last.then_inc(*PE("qkT", u))

                    def project_values(a):
                        if a >= 1:
                            pe.wait_ge(*w(A, "va", a - 1))
                        for hf in range(halves):
                            last = nc.tensor.matmul(ps[0:nk[a], 6 + hf, :], hT[:, QT * a:QT * a + nk[a]],
                                                    wqkv[:, 2 * INNER + hf * 512:2 * INNER + (hf + 1) * 512],
                                                    start=True, stop=True)
                        last.then_inc(*PE("V", a))

                    for u in range(U + 2):
                        if u < U:
                            project(u)
                        if u < NA:
                            project_values(u)
                        if u >= 2:
                            turn_unit(u - 2)
                    for a in range(U + 2, NA):
                        project_values(a)
                    pe.wait_ge(*w(A, "va", NA - 1))
                    pe.wait_ge(*w(V, "sin", U - 1))

                    def scores(n):
                        a, g = n // HG, n % HG
                        if n >= 2:
                            pe.wait_ge(*w(V, "sub", n - 2))
                        pe.wait_ge(*w(A, "qkT", U - 1))
                        for b in range(2):
                            bank = 2 * (n % 2) + b
                            nc.tensor.matmul(C.bank(bank), C.ident_bf[:, :], mask[:, int(a > 0), :, :],
                                             start=True, stop=True)
                        for c in range(4):
                            bank, o = 2 * (n % 2) + c // 2, c % 2 * 2 * P
                            out = ps[0:nq[a], bank, o:o + 2 * P].rearrange("p (b n) -> p b n", b=2)
                            last = nc.tensor.matmul(out[:, :, 0:nk[a]], qT[:, 4 * g + c, QT * a:QT * a + nq[a]],
                                                    kT[:, 4 * g + c, :, QT * a:QT * a + nk[a]],
                                                    start=False, stop=True, skip_group_check=True)
                        last.then_inc(*PE("S", n))

                    def turn_probs(n):
                        pe.wait_ge(*w(G, "probs", n))
                        if n >= 1:
                            pe.wait_ge(*w(A, "pT", n - 1))
                        for h in range(8):
                            last = nc.tensor.transpose(ps[:, 4 + h // 4, h % 4 * P:(h % 4 + 1) * P],
                                                       pr[:, n % 4, h, :], C.ident[:, :])
                        last.then_inc(*PE("pT", n))

                    def weigh_values(n):
                        a, g = n // HG, n % HG
                        pe.wait_ge(*w(A, "pT", n))
                        if n >= 2:
                            pe.wait_ge(*w(A, "aoT", n - 2))
                        for h in range(8):
                            r, c, v = h % 2 * 64, h // 2 * QR, (8 * g + h) * E
                            last = nc.tensor.matmul(ps[r:r + 64, 6 + n % 2, c:c + QR], va[:, a, v:v + E],
                                                    pT[:, n % 2, h, :], start=True, stop=True)
                        last.then_inc(*PE("O", n))

                    for n in range(NU + 4):
                        if n < NU:
                            scores(n)
                        if 3 <= n < NU + 3:
                            turn_probs(n - 3)
                        if n >= 4:
                            weigh_values(n - 4)
                    pe.wait_ge(*w(A, "aoT", NU - 1))
                    pe.wait_ge(*w(V, "sub", NU - 1))
                    last = pe_rows(nc, C, w, 0, [aoT[:, c, :] for c in range(CH)], [wo[:, c, :] for c in range(CH)])
                    last.then_inc(*PE("attn"))
                    pe.wait_ge(*w(V, "y_attn"))
                    nc.tensor.matmul(ps[:, 1, 0:NT * 64], shift[:, 0, :], C.yb[:, :, 64:], start=True, stop=False)
                    nc.tensor.matmul(ps[:, 1, 64:NT * 64], shift[:, 1, :], C.yb[:, 0:NT - 1, 64:], start=False,
                                     stop=True).then_inc(*PE("shifted"))
                    pe.wait_ge(*w(V, LN, NT - 1))
                    pe_turn(nc, C, S, w, C.nb, 2, "hnT")
                    pe.wait_ge(*w(A, "hnT"))
                    for c in range(HC):
                        m = hid_rows[c]
                        nc.tensor.matmul(C.bank(3 + c, m), w1[:, HID + c * P:HID + c * P + m], hnT[:, :], start=True,
                                         stop=True).then_inc(*PE("gate", c))
                        nc.tensor.matmul(C.bank([0, 1, 6][c], m), w1[:, c * P:c * P + m], hnT[:, :], start=True,
                                         stop=True).then_inc(*PE("up", c))
                    pe.wait_ge(*w(V, "hid", HC - 1))
                    last = pe_rows(nc, C, w, 7, [hid[0:hid_rows[c], c, :] for c in range(HC)],
                                   [w2[0:hid_rows[c], c, :] for c in range(HC)], b2row[:, :])
                    last.then_inc(*PE("down"))
    S.close()


def stage_l0_ffn(nc, C, plan):
    local_layers(nc, C, plan, "l0ffn", "L0_ffn", 16, 6, 32,
                 ("Wqkv", "q_scale", "k_scale", "Wo", "ln_g", "ln_b", "W1", "b1", "W2", "b2"))


def stage_l1_ffn(nc, C, plan):
    local_layers(nc, C, plan, "l1ffn", "L1_ffn", 8, 2, 64,
                 ("wqkv", "q_scale", "k_scale", "wo", "ln_g", "ln_b", "w1", "b1", "w2", "b2"))


def stage_norm_in_0(nc, C, plan):
    stage_norm_in(nc, C, plan, "normin0")


def stage_norm_out_0(nc, C, plan):
    stage_norm_out(nc, C, plan, "normout0")


def stage_norm_in_1(nc, C, plan):
    stage_norm_in(nc, C, plan, "normin1")


def stage_norm_out_1(nc, C, plan):
    stage_norm_out(nc, C, plan, "normout1")



def stage_l1_attn(nc, C, plan):
    H, DK, GR = 8, 16, 8
    DV = D // GR
    SCALE = 0.25
    d = C.d
    S = Stage(nc, "l1attn", plan)
    PE, A, V, G = S.PE, S.ACT, S.DVE, S.POOL
    ps = C.ps
    wq, wk, wv = S.sb("wq", [P, D]), S.sb("wk", [P, D]), S.sb("wv", [P, H * D])
    wvs, bv, bvs = S.sb("wvs", [P, D]), S.sb("bv", [1, H * D]), S.sb("bvs", [1, D])
    cols, headmask = S.sb("cols", [P, 4]), S.sb("headmask", [P, 2])
    y0, hT, qm, kT = S.sb("y0", [P, NT, D]), S.sb("hT", [P, T]), S.sb("qm", [P, 2, T]), S.sb("kT", [P, T])
    va = S.sb("va", [P, NT, H, DV + 1])
    mx, nm = S.sb("mx", [P, 4]), S.sb("nm", [P, 4])
    pr, pT = S.sb("pr", [P, 3, T]), S.sb("pT", [P, 2, NT, P])
    rec, ao = S.sb("rec", [P, H]), S.sb("ao", [P, NT, H, DV])
    mixed = nc.dram_tensor("l1_mixed", (B, H, T, DV), F32).ap()
    stored = nc.alloc_semaphore("l1attn_ao_stored")
    y_back = nc.alloc_semaphore("l1attn_y_loaded")
    K = NT * H
    ST = 16 * NT

    with nc.Block() as block:
        @block.sync
        def _(sp):
            for dst, n in ((wq, "Wq"), (wk, "Wk"), (wv, "Wv")):
                S.load(sp, dst[:, :], d["L1_attn_" + n])
            for c, n in enumerate(("gamma", "beta", "bq", "bk")):
                S.load(sp, cols[:, c:c + 1], column(d["L1_attn_" + n]))
            S.load(sp, bv[:, :], row(d["L1_attn_bv"]))
            S.load(sp, headmask[:, :], d["const_head_of_two"])
            sp.wait_ge(S.loaded, S.loads)
            sp.sem_inc(stored, ST)
            with sp.Fori(0, B, 1) as i:
                w = Waits(sp, V, i)
                for t in range(NT):
                    sp.wait_ge(*w(V, "ao", t))
                    sp.dma_start(mixed[bass.ds(i, 1), :, t * P:(t + 1) * P, :].rearrange("o h p j -> p (o h) j"),
                                 ao[:, t, :, :]).then_inc(stored, 16)
            sp.wait_ge(stored, ST * (B + 1))
            sp.dma_start(C.y[:, :, :], mixed.rearrange("b h (r a) j -> (b h r) (a j)", a=P // DV).rearrange(
                "(n p) e -> p n e", p=P)).then_inc(y_back, 16)
            sp.wait_ge(y_back, 16)

        @block.gpsimd
        def _(pool):
            w = S.once(pool, G)
            nc.gpsimd.memset(va[:, :, :, DV:DV + 1], 1.0).then_inc(*G("va_ones"))
            with S.loop(pool, G) as (i, w):
                for name in ("norm_x", "norm_1"):
                    pool_norm(nc, C, S, w, name)

        @block.scalar
        def _(act):
            w = S.once(act, A)
            act.wait_ge(S.loaded, S.loads)
            with S.loop(act, A) as (i, w):
                act.wait_ge(*w(V, "norm_x", NT - 1, back=1))
                nc.scalar.activation(C.xb[:, :, :], C.x[:, bass.ds(i * NT, NT), :], ACT.Copy).then_inc(*A("xb"))
                act.wait_ge(*w(PE, "hT", NT - 1))
                nc.scalar.activation(hT[:, :], C.bank(7), ACT.Identity, bias=cols[:, 1:2],
                                     scale=cols[:, 0:1]).then_inc(*A("hT"))
                act.wait_ge(*w(PE, "K"))
                nc.scalar.activation(kT[:, :], C.bank(1), ACT.Identity, bias=cols[:, 3:4]).then_inc(*A("kT"))
                act.wait_ge(*w(PE, "V"))
                nc.scalar.activation(va[:, :, :, 0:DV], C.bank(2).rearrange("p (t h e) -> p t h e", t=NT, h=H),
                                     ACT.Copy).then_inc(*A("va"))

                def exponent(k):
                    act.wait_ge(*w(V, "negmax", k))
                    if k >= 3:
                        act.wait_ge(*w(PE, "pT", k - 3))
                    nc.scalar.activation(pr[:, k % 3, :], C.bank(k % 3), ACT.Exp, bias=nm[:, k % 4:k % 4 + 1],
                                         scale=SCALE).then_inc(*A("exp", k))

                def copy_probs(k):
                    act.wait_ge(*w(PE, "pT", k))
                    if k >= 2:
                        act.wait_ge(*w(PE, "O", k - 2))
                    nc.scalar.activation(pT[:, k % 2, :, :], C.bank(3 + k % 2).rearrange("p (j n) -> p j n", j=NT),
                                         ACT.Copy).then_inc(*A("pT", k))

                for k in range(K + 2):
                    if k < K:
                        exponent(k)
                    if k >= 2:
                        copy_probs(k - 2)

        @block.vector
        def _(dve):
            w = S.once(dve, V)
            dve.wait_ge(S.loaded, S.loads)
            nc.vector.tensor_reduce(wvs[:, :], wv[:, :].rearrange("p (n g) -> p n g", g=GR), AX,
                                    ALU.add).then_inc(*V("wvs"))
            nc.vector.tensor_reduce(bvs[:, :], bv[:, :].rearrange("p (n g) -> p n g", g=GR), AX,
                                    ALU.add).then_inc(*V("bvs"))
            with S.loop(dve, V) as (i, w):
                dve.wait_ge(*w(A, "xb"))
                dve_norm(nc, C, S, w, C.xb, y0, "norm_x")
                dve.wait_ge(*w.own())
                dve_norm(nc, C, S, w, y0, C.nb, "norm_1")
                dve.wait_ge(*w(PE, "Q"))
                for j in range(2):
                    nc.vector.tensor_scalar(qm[:, j, :], C.bank(0), cols[:, 2:3], headmask[:, j:j + 1],
                                            ALU.add, ALU.mult).then_inc(*V("qm", j))

                def maximum(k):
                    dve.wait_ge(*w(PE, "S", k))
                    nc.vector.tensor_reduce(mx[:, k % 4:k % 4 + 1], C.bank(k % 3), AX, ALU.max).then_inc(*V("max", k))
                    dve.wait_ge(*w.own())
                    nc.vector.tensor_scalar(nm[:, k % 4:k % 4 + 1], mx[:, k % 4:k % 4 + 1], -SCALE, None,
                                            ALU.mult).then_inc(*V("negmax", k))

                def normalise(t):
                    dve.wait_ge(*w(PE, "O", (t + 1) * H - 1))
                    o = ps[:, 5 + t % 2, 0:H * (DV + 1)].rearrange("p (h e) -> p h e", h=H)
                    nc.vector.reciprocal(rec[:, :], o[:, :, DV]).then_inc(*V("rec", t))
                    dve.wait_ge(*w.own())
                    if t == 0:
                        dve.wait_ge(stored, ST * (i + 1))
                    nc.vector.tensor_tensor(ao[:, t, :, :], o[:, :, 0:DV], rec[:, :].unsqueeze(2).to_broadcast(
                        [P, H, DV]), ALU.mult).then_inc(*V("ao", t))

                for k in range(K + 3):
                    if k < K:
                        maximum(k)
                    if k >= 3 and (k - 3) % H == H - 1:
                        normalise((k - 3) // H)

        @block.tensor
        def _(pe):
            w = S.once(pe, PE)
            pe.wait_ge(S.loaded, S.loads)
            pe.wait_ge(*w(G, "va_ones"))
            pe.wait_ge(*w(V, "bvs"))
            with S.loop(pe, PE) as (i, w):
                pe.wait_ge(*w(V, "norm_1", NT - 1))
                pe_turn(nc, C, S, w, C.nb, 7, "hT")
                pe.wait_ge(*w(A, "hT"))
                pe.wait_ge(*w(V, "ao", NT - 1, back=1))
                nc.tensor.matmul(C.bank(0), wq[:, :], hT[:, :], start=True, stop=True).then_inc(*PE("Q"))
                nc.tensor.matmul(C.bank(1), wk[:, :], hT[:, :], start=True, stop=True).then_inc(*PE("K"))
                pe_rows(nc, C, w, 2, [hT], [wvs[:, :]], bvs[:, :]).then_inc(*PE("V"))
                pe.wait_ge(*w(V, "qm", 1))
                pe.wait_ge(*w(A, "va"))

                def scores(k):
                    t, h = k // H, k % H
                    if k >= 3:
                        pe.wait_ge(*w(A, "exp", k - 3))
                    r = 32 * (h // 2)
                    nc.tensor.matmul(C.bank(k % 3), qm[r:r + 32, h % 2, t * P:(t + 1) * P], kT[r:r + 32, :],
                                     start=True, stop=True).then_inc(*PE("S", k))

                def turn_probs(k):
                    pe.wait_ge(*w(A, "exp", k))
                    if k >= 2:
                        pe.wait_ge(*w(A, "pT", k - 2))
                    for s in range(NT):
                        last = nc.tensor.transpose(ps[:, 3 + k % 2, s * P:(s + 1) * P],
                                                   pr[:, k % 3, s * P:(s + 1) * P], C.ident[:, :])
                    last.then_inc(*PE("pT", k))

                def values(k):
                    t, h = k // H, k % H
                    pe.wait_ge(*w(A, "pT", k))
                    if h == 0 and t >= 2:
                        pe.wait_ge(*w(V, "ao", t - 2))
                    c = h * (DV + 1)
                    for s in range(NT):
                        last = nc.tensor.matmul(ps[:, 5 + t % 2, c:c + DV + 1], pT[:, k % 2, s, :], va[:, s, h, :],
                                                start=(s == 0), stop=(s == NT - 1))
                    last.then_inc(*PE("O", k))

                for k in range(K + 3):
                    if k < K:
                        scores(k)
                    if 2 <= k < K + 2:
                        turn_probs(k - 2)
                    if k >= 3:
                        values(k - 3)
    S.close()


def stage_l1_attn_out(nc, C, plan):
    stage_norm_out(nc, C, plan, "l1attnout")



def stage_l2_attn(nc, C, plan):
    CH, N, KC, LV = 2, 64, 4, 7
    I = CH * P
    PREV, DIAG, END, TOTAL = 7, 8, 9, 10
    d = C.d
    S = Stage(nc, "l2attn", plan)
    PE, A, V, G = S.PE, S.ACT, S.DVE, S.POOL
    ps = C.ps
    w_in, w_out = S.sb("w_in", [P, 2 * I]), S.sb("w_out", [P, CH, D])
    w_dt, w_b, w_c = S.sb("w_dt", [P, CH, I]), S.sb("w_b", [P, CH, N]), S.sb("w_c", [P, CH, N])
    conv_w, cols, b_dt = S.sb("conv_w", [P, CH, KC]), S.sb("cols", [P, 2, CH]), S.sb("b_dt", [1, I])
    sums = S.sb("sums", [P, LV + 2, P])
    pairs = S.sb("pairs", [P, LV + 1, P])
    y0T, xi, zs = S.sb("y0T", [P, T]), S.sb("xi", [P, CH, KC - 1 + T]), S.sb("zs", [P, CH, T])
    cv, xcT = S.sb("cv", [P, CH, T]), S.sb("xcT", [P, CH, T])
    bT, cT, bk = S.sb("bT", [N, T]), S.sb("cT", [N, T]), S.sb("bk", [P, NT, N])
    ab, dt, dtx = S.sb("ab", [P, NT, I]), S.sb("dt", [P, NT, I]), S.sb("dtx", [P, NT, I])
    dec, gm = S.sb("dec", [P, 11, I]), S.sb("gm", [P, LV + 1, P])
    rr, re = S.sb("rr", [P, LV, I]), S.sb("re", [P, I])
    tmp, yt, state, gT = S.sb("tmp", [P, 9, I]), S.sb("yt", [P, I]), S.sb("state", [N, I]), S.sb("gT", [P, CH, T])

    with nc.Block() as block:
        @block.sync
        def _(sp):
            S.load(sp, w_in[:, :], d["L2_attn_W_in"])
            for dst, n in ((w_out, "W_out"), (w_dt, "W_dt"), (w_b, "W_B"), (w_c, "W_C")):
                S.load(sp, dst[:, :, :], d["L2_attn_" + n].rearrange("(c k) n -> k c n", c=CH))
            S.load(sp, conv_w[:, :, :], d["L2_attn_conv_w"].rearrange("(c k) o n -> k c (o n)", c=CH))
            for c in range(CH):
                S.load(sp, cols[:, 0, c:c + 1], column(d["L2_attn_conv_b"][c * P:(c + 1) * P]))
                S.load(sp, cols[:, 1, c:c + 1], column(d["L2_attn_D"][c * P:(c + 1) * P]))
            S.load(sp, b_dt[:, :], row(d["L2_attn_b_dt"]))
            S.load(sp, sums[:, :, :], d["const_l2_sums"])
            S.load(sp, pairs[:, :, :], d["const_l2_pairs"])
            sp.wait_ge(S.loaded, S.loads)

        @block.gpsimd
        def _(pool):
            w = S.once(pool, G)
            nc.gpsimd.memset(xi[:, :, 0:KC - 1], 0.0).then_inc(*G("xi_pad"))
            nc.gpsimd.memset(dec[:, DIAG, :], 1.0).then_inc(*G("diag_ones"))
            with S.loop(pool, G) as (i, w):
                for name in ("norm_x", "norm_y"):
                    pool_norm(nc, C, S, w, name)

        @block.scalar
        def _(act):
            w = S.once(act, A)
            act.wait_ge(S.loaded, S.loads)
            act.wait_ge(*w(G, "diag_ones"))
            with S.loop(act, A) as (i, w):
                act.wait_ge(*w(V, "norm_y", "x", back=1))
                nc.scalar.activation(C.xb[:, :, :], C.x[:, bass.ds(i * NT, NT), :], ACT.Copy).then_inc(*A("xb"))
                act.wait_ge(*w(PE, "y0T", NT - 1))
                nc.scalar.activation(y0T[:, :], C.bank(0), ACT.Copy).then_inc(*A("y0T"))
                for c in range(CH):
                    act.wait_ge(*w(PE, "in", c))
                    nc.scalar.activation(xi[:, c, KC - 1:], C.bank(1 + c), ACT.Copy).then_inc(*A("xi", c))
                for c in range(CH):
                    act.wait_ge(*w(PE, "in", CH + c))
                    nc.scalar.activation(zs[:, c, :], C.bank(3 + c), ACT.Silu).then_inc(*A("zs", c))
                for c in range(CH):
                    act.wait_ge(*w(V, "conv", c))
                    nc.scalar.activation(xcT[:, c, :], cv[:, c, :], ACT.Silu,
                                         bias=cols[:, 0, c:c + 1]).then_inc(*A("xcT", c))
                act.wait_ge(*w(PE, "B"))
                nc.scalar.activation(bT[:, :], C.bank(5, N), ACT.Copy).then_inc(*A("bT"))
                act.wait_ge(*w(PE, "C"))
                nc.scalar.activation(cT[:, :], C.bank(6, N), ACT.Copy).then_inc(*A("cT"))
                act.wait_ge(*w(PE, "Bk"))
                nc.scalar.activation(bk[:, :, :], ps[:, 7, 0:NT * N].rearrange("p (t n) -> p t n", t=NT),
                                     ACT.Copy).then_inc(*A("bk"))
                for b in range(2):
                    act.wait_ge(*w(PE, "dt", b))
                    nc.scalar.activation(ab[:, 2 * b:2 * b + 2, :], C.bank(1 + b).rearrange("p (t n) -> p t n", t=2),
                                         ACT.Abs).then_inc(*A("abs", b))
                act.wait_ge(*w.own())
                nc.scalar.activation(ab[:, :, :], ab[:, :, :], ACT.Exp, scale=-1.0).then_inc(*A("exp"))
                act.wait_ge(*w.own())
                nc.scalar.activation(ab[:, :, :], ab[:, :, :], ACT.Ln, bias=C.ones[:, 0:1]).then_inc(*A("ln"))
                for t in range(NT):
                    act.wait_ge(*w(PE, "decay", t))
                    if t >= 1:
                        act.wait_ge(*w(V, "tmp", t - 1))
                        act.wait_ge(*w(V, "state", t - 1))
                        act.wait_ge(*w(V, "re", t - 1))
                    for b in range(4):
                        nc.scalar.activation(dec[:, 2 * b:2 * b + 2, :], C.bank(b).rearrange("p (j n) -> p j n", j=2),
                                             ACT.Exp, scale=-1.0).then_inc(*A("dec", t, b))
                    nc.scalar.activation(dec[:, END, :], ps[:, 4, 0:I], ACT.Exp, scale=-1.0).then_inc(*A("dec", t, 4))
                    nc.scalar.activation(dec[0:N, TOTAL, :], ps[0:N, 4, I:2 * I], ACT.Exp,
                                         scale=-1.0).then_inc(*A("dec", t, 5))
                act.wait_ge(*w(PE, "out"))
                act.wait_ge(*w(V, "norm_y", NT - 1, back=1))
                nc.scalar.activation(C.yb[:, :, :], C.bank(5).rearrange("p (t e) -> p t e", t=NT),
                                     ACT.Copy).then_inc(*A("y"))

        @block.vector
        def _(dve):
            w = S.once(dve, V)
            dve.wait_ge(S.loaded, S.loads)
            with S.loop(dve, V) as (i, w):
                dve.wait_ge(*w(A, "xb"))
                dve_norm(nc, C, S, w, C.xb, C.nb, "norm_x")
                for c in range(CH):
                    dve.wait_ge(*w(A, "xi", c))
                    nc.vector.tensor_scalar(cv[:, c, :], xi[:, c, 0:T], conv_w[:, c, 0:1], None,
                                            ALU.mult).then_inc(*V("tap", c, 0))
                    for k in range(1, KC):
                        dve.wait_ge(*w.own())
                        last = nc.vector.scalar_tensor_tensor(out=cv[:, c, :], in0=xi[:, c, k:k + T],
                                                              scalar=conv_w[:, c, k:k + 1], in1=cv[:, c, :],
                                                              op0=ALU.mult, op1=ALU.add)
                        last.then_inc(*(V("conv", c) if k == KC - 1 else V("tap", c, k)))
                dve.wait_ge(*w(A, "ln"))
                for b in range(2):
                    nc.vector.scalar_tensor_tensor(out=dt[:, 2 * b:2 * b + 2, :],
                                                   in0=C.bank(1 + b).rearrange("p (t n) -> p t n", t=2), scalar=0.0,
                                                   in1=ab[:, 2 * b:2 * b + 2, :], op0=ALU.max,
                                                   op1=ALU.add).then_inc(*V("dt", b))
                dve.wait_ge(*w.own())
                for b in range(2):
                    dve.wait_ge(*w(PE, "xc", b))
                    nc.vector.tensor_tensor(dtx[:, 2 * b:2 * b + 2, :], dt[:, 2 * b:2 * b + 2, :],
                                            C.bank(3 + b).rearrange("p (t n) -> p t n", t=2),
                                            ALU.mult).then_inc(*V("dtx", b))
                dve.wait_ge(*w(PE, "prev", NT - 1, back=1))
                nc.vector.memset(state[:, :], 0.0).then_inc(*V("state_zero"))
                for t in range(NT):
                    dve.wait_ge(*w(PE, "G", t))
                    if t >= 1:
                        dve.wait_ge(*w(PE, "Y", t - 1))
                    nc.vector.tensor_tensor(gm[:, :, :], ps[:, 5, 0:P].unsqueeze(1).to_broadcast([P, LV + 1, P]),
                                            pairs[:, :, :], ALU.mult).then_inc(*V("gm", t))
                    dve.wait_ge(*w(A, "dec", t, 5))
                    dve.wait_ge(*w.own())
                    nc.vector.tensor_tensor(rr[:, :, :], dec[:, 0:LV, :], dtx[:, t, :].unsqueeze(1).to_broadcast(
                        [P, LV, I]), ALU.mult).then_inc(*V("rr", t))
                    nc.vector.tensor_tensor(re[:, :], dec[:, END, :], dtx[:, t, :], ALU.mult).then_inc(*V("re", t))
                    dve.wait_ge(*w(PE, "Y", t))
                    for b in range(5):
                        n = min(2, 9 - 2 * b)
                        last = nc.vector.tensor_tensor(tmp[:, 2 * b:2 * b + n, :], dec[:, 2 * b:2 * b + n, :],
                                                       ps[:, b, 0:n * I].rearrange("p (j n) -> p j n", j=n), ALU.mult)
                        last.then_inc(*(V("tmp", t) if b == 4 else V("tmp_part", t, b)))
                    nc.vector.tensor_tensor(state[:, :], state[:, :], dec[0:N, TOTAL, :],
                                            ALU.mult).then_inc(*V("state_decayed", t))
                    dve.wait_ge(*w.own())
                    if t >= 1:
                        dve.wait_ge(*w(PE, "yT", t - 1))
                    nc.vector.tensor_reduce(yt[:, :], tmp[:, :, :].rearrange("p l n -> p n l"), AX,
                                            ALU.add).then_inc(*V("yt", t))
                    dve.wait_ge(*w(PE, "U", t))
                    nc.vector.tensor_tensor(state[:, :], state[:, :], ps[0:N, 6, 0:I],
                                            ALU.add).then_inc(*V("state", t))
                    dve.wait_ge(*w(PE, "yT", t))
                    for c in range(CH):
                        nc.vector.scalar_tensor_tensor(out=gT[:, c, t * P:(t + 1) * P], in0=xcT[:, c, t * P:(t + 1) * P],
                                                       scalar=cols[:, 1, c:c + 1], in1=ps[:, 7, c * P:(c + 1) * P],
                                                       op0=ALU.mult, op1=ALU.add).then_inc(*V("gT", t, c))
                dve.wait_ge(*w.own())
                nc.vector.tensor_tensor(gT[:, :, :], gT[:, :, :], zs[:, :, :], ALU.mult).then_inc(*V("g"))
                dve.wait_ge(*w(A, "y"))
                dve_add_norm(nc, C, S, w, i, "norm_y")

        @block.tensor
        def _(pe):
            w = S.once(pe, PE)
            pe.wait_ge(S.loaded, S.loads)
            with S.loop(pe, PE) as (i, w):
                pe.wait_ge(*w(V, "norm_x", NT - 1))
                pe_turn(nc, C, S, w, C.nb, 0, "y0T")
                pe.wait_ge(*w(A, "y0T"))
                for c in range(2 * CH):
                    nc.tensor.matmul(C.bank(1 + c), w_in[:, c * P:(c + 1) * P], y0T[:, :], start=True,
                                     stop=True).then_inc(*PE("in", c))
                pe.wait_ge(*w(A, "xcT", 1))
                pe.wait_ge(*w(A, "zs", 1))
                for bank, wt, name in ((5, w_b, "B"), (6, w_c, "C")):
                    pe.wait_ge(*w(A, "y", back=1))
                    for c in range(CH):
                        last = nc.tensor.matmul(C.bank(bank, N), wt[:, c, :], xcT[:, c, :], start=(c == 0),
                                                stop=(c == CH - 1))
                    last.then_inc(*PE(name))
                for t in range(NT):
                    for c in range(CH):
                        last = nc.tensor.matmul(ps[:, 7, t * N:(t + 1) * N], xcT[:, c, t * P:(t + 1) * P],
                                                w_b[:, c, :], start=(c == 0), stop=(c == CH - 1))
                last.then_inc(*PE("Bk"))
                for b in range(2):
                    for j in range(2):
                        o, t = ps[:, 1 + b, j * I:(j + 1) * I], 2 * b + j
                        for c in range(CH):
                            nc.tensor.matmul(o, xcT[:, c, t * P:(t + 1) * P], w_dt[:, c, :], start=(c == 0), stop=False)
                        last = nc.tensor.matmul(o, C.ones[0:1, :], b_dt[:, :], start=False, stop=True)
                    last.then_inc(*PE("dt", b))
                for b in range(2):
                    for j in range(2):
                        t = 2 * b + j
                        for c in range(CH):
                            last = nc.tensor.transpose(ps[:, 3 + b, j * I + c * P:j * I + (c + 1) * P],
                                                       xcT[:, c, t * P:(t + 1) * P], C.ident[:, :])
                    last.then_inc(*PE("xc", b))
                pe.wait_ge(*w(V, "dtx", 1))
                pe.wait_ge(*w(A, "bk"))
                for t in range(NT):
                    if t >= 1:
                        pe.wait_ge(*w(V, "tmp", t - 1))
                    for l in range(LV + 2):
                        nc.tensor.matmul(ps[:, l // 2, l % 2 * I:(l % 2 + 1) * I], sums[:, l, :], dt[:, t, :],
                                         start=True, stop=True)
                    nc.tensor.matmul(ps[0:N, 4, I:2 * I], C.ones[:, 0:N], dt[:, t, :], start=True,
                                     stop=True).then_inc(*PE("decay", t))
                    if t >= 1:
                        pe.wait_ge(*w(V, "gm", t - 1))
                    nc.tensor.matmul(ps[:, 5, 0:P], bT[:, t * P:(t + 1) * P], cT[:, t * P:(t + 1) * P],
                                     start=True, stop=True).then_inc(*PE("G", t))
                    pe.wait_ge(*w(V, "re", t))
                    pe.wait_ge(*w(A, "dec", t, 5))
                    for l in range(LV):
                        nc.tensor.matmul(ps[:, l // 2, l % 2 * I:(l % 2 + 1) * I], gm[:, l, :], rr[:, l, :],
                                         start=True, stop=True)
                    pe.wait_ge(*w(V, "state" if t else "state_zero", *([t - 1] if t else [])))
                    nc.tensor.matmul(ps[:, 3, I:2 * I], cT[:, t * P:(t + 1) * P], state[:, :], start=True,
                                     stop=True).then_inc(*PE("prev", t))
                    nc.tensor.matmul(ps[:, 4, 0:I], gm[:, LV, :], dtx[:, t, :], start=True,
                                     stop=True).then_inc(*PE("Y", t))
                    nc.tensor.matmul(ps[0:N, 6, 0:I], bk[:, t, :], re[:, :], start=True, stop=True).then_inc(*PE("U", t))
                    pe.wait_ge(*w(V, "yt", t))
                    if t >= 1:
                        pe.wait_ge(*w(V, "gT", t - 1, 1))
                    for c in range(CH):
                        last = nc.tensor.transpose(ps[:, 7, c * P:(c + 1) * P], yt[:, c * P:(c + 1) * P], C.ident[:, :])
                    last.then_inc(*PE("yT", t))
                pe.wait_ge(*w(V, "g"))
                pe_rows(nc, C, w, 5, [gT[:, c, :] for c in range(CH)],
                        [w_out[:, c, :] for c in range(CH)]).then_inc(*PE("out"))
    S.close()



def stage_l2_ffn(nc, C, plan):
    EX, F, CH, TOP = 8, 2 * D, 2, 2
    d = C.d
    S = Stage(nc, "l2ffn", plan)
    PE, A, V, G = S.PE, S.ACT, S.DVE, S.POOL
    ps = C.ps
    wg, bg = S.sb("wg", [P, EX]), S.sb("bg", [1, EX])
    w1, b1 = S.sb("w1", [P, EX, F]), S.sb("b1", [P, EX, CH])
    w2, b2 = S.sb("w2", [P, EX, CH, D]), S.sb("b2", [EX, D])
    gains, before = S.sb("gains", [P, 2, D]), S.sb("before", [P, EX, EX])
    y0, hT = S.sb("y0", [P, NT, D]), S.sb("hT", [P, T])
    lg, top, ex, s = S.sb("lg", [P, NT, EX]), S.sb("top", [P, NT]), S.sb("ex", [P, NT, EX]), S.sb("s", [P, NT])
    gt, eq = S.sb("gt", [P, NT, EX, EX]), S.sb("eq", [P, NT, EX, EX])
    rank, coef, coefT = S.sb("rank", [P, NT, EX]), S.sb("coef", [P, NT, EX]), S.sb("coefT", [EX, T])
    hid, acc = S.sb("hid", [P, 2, CH, T]), S.sb("acc", [P, NT, D])

    with nc.Block() as block:
        @block.sync
        def _(sp):
            S.load(sp, wg[:, :], d["L2_ffn_Wg"])
            S.load(sp, bg[:, :], row(d["L2_ffn_bg"]))
            S.load(sp, w1[:, :, :], d["L2_ffn_W1"].rearrange("e k n -> k e n"))
            S.load(sp, b1[:, :, :], d["L2_ffn_b1_turned"])
            S.load(sp, w2[:, :, :, :], d["L2_ffn_W2"].rearrange("e (c k) n -> k e c n", c=CH))
            S.load(sp, b2[:, :], d["L2_ffn_b2"])
            S.load(sp, gains[:, 0, :], row(d["L2_ffn_gamma"]).to_broadcast([P, D]))
            S.load(sp, gains[:, 1, :], row(d["L2_ffn_beta"]).to_broadcast([P, D]))
            S.load(sp, before[:, :, :], d["const_before"])
            sp.wait_ge(S.loaded, S.loads)

        @block.gpsimd
        def _(pool):
            S.once(pool, G)
            with S.loop(pool, G) as (i, w):
                for name in ("norm_x", "norm_1", "norm_y"):
                    pool_norm(nc, C, S, w, name)

        @block.scalar
        def _(act):
            S.once(act, A)
            act.wait_ge(S.loaded, S.loads)
            with S.loop(act, A) as (i, w):
                act.wait_ge(*w(V, "norm_y", "x", back=1))
                nc.scalar.activation(C.xb[:, :, :], C.x[:, bass.ds(i * NT, NT), :], ACT.Copy).then_inc(*A("xb"))
                act.wait_ge(*w(PE, "hT", NT - 1))
                nc.scalar.activation(hT[:, :], C.bank(0), ACT.Copy).then_inc(*A("hT"))
                act.wait_ge(*w(PE, "logits"))
                nc.scalar.activation(lg[:, :, :], ps[:, 1, 0:NT * EX].rearrange("p (t e) -> p t e", t=NT),
                                     ACT.Copy).then_inc(*A("logits"))
                act.wait_ge(*w(V, "centred"))
                nc.scalar.activation(ex[:, :, :], ex[:, :, :], ACT.Exp).then_inc(*A("exp"))
                for e in range(EX):
                    act.wait_ge(*w(PE, "up", e, 0))
                    if e >= 2:
                        act.wait_ge(*w(PE, "down", e - 2))
                    nc.scalar.activation(hid[:, e % 2, 0, :], C.bank(2 + e % 2 * 2), ACT.Relu,
                                         bias=b1[:, e, 0:1]).then_inc(*A("hid", e))
                    if e == 1:
                        act.wait_ge(*w(PE, "coefT"))
                        nc.scalar.activation(coefT[:, :], C.bank(0, EX), ACT.Copy).then_inc(*A("coefT"))

        @block.vector
        def _(dve):
            S.once(dve, V)
            dve.wait_ge(S.loaded, S.loads)
            with S.loop(dve, V) as (i, w):
                dve.wait_ge(*w(A, "xb"))
                dve_norm(nc, C, S, w, C.xb, y0, "norm_x")
                dve.wait_ge(*w(A, "logits"))
                nc.vector.tensor_reduce(top[:, :], lg[:, :, :], AX, ALU.max).then_inc(*V("top"))
                dve.wait_ge(*w.own())
                nc.vector.tensor_tensor(ex[:, :, :], lg[:, :, :], top[:, :].unsqueeze(2).to_broadcast([P, NT, EX]),
                                        ALU.subtract).then_inc(*V("centred"))
                for t in range(NT):
                    mine = lg[:, t, :].unsqueeze(2).to_broadcast([P, EX, EX])
                    other = lg[:, t, :].unsqueeze(1).to_broadcast([P, EX, EX])
                    nc.vector.tensor_tensor(gt[:, t], other, mine, ALU.is_gt).then_inc(*V("gt", t))
                    nc.vector.tensor_tensor(eq[:, t], other, mine, ALU.is_equal).then_inc(*V("eq", t))
                dve.wait_ge(*w.own())
                nc.vector.tensor_tensor(eq[:, :, :, :], eq[:, :, :, :], before[:, :, :].unsqueeze(1).to_broadcast(
                    [P, NT, EX, EX]), ALU.mult).then_inc(*V("eq_before"))
                dve.wait_ge(*w.own())
                nc.vector.tensor_tensor(gt[:, :, :, :], gt[:, :, :, :], eq[:, :, :, :], ALU.add).then_inc(*V("ahead"))
                dve.wait_ge(*w.own())
                nc.vector.tensor_reduce(rank[:, :, :], gt[:, :, :, :], AX, ALU.add).then_inc(*V("rank"))
                dve.wait_ge(*w.own())
                dve.wait_ge(*w(A, "exp"))
                nc.vector.scalar_tensor_tensor(out=coef[:, :, :], in0=rank[:, :, :], scalar=float(TOP),
                                               in1=ex[:, :, :], op0=ALU.is_lt, op1=ALU.mult).then_inc(*V("chosen"))
                dve.wait_ge(*w.own())
                nc.vector.tensor_reduce(s[:, :], coef[:, :, :], AX, ALU.add).then_inc(*V("sum"))
                dve.wait_ge(*w.own())
                nc.vector.reciprocal(s[:, :], s[:, :]).then_inc(*V("rec"))
                dve.wait_ge(*w.own())
                nc.vector.tensor_tensor(coef[:, :, :], coef[:, :, :], s[:, :].unsqueeze(2).to_broadcast([P, NT, EX]),
                                        ALU.mult).then_inc(*V("coef"))

                def hidden(e):
                    dve.wait_ge(*w(PE, "up", e, 1))
                    if e >= 2:
                        dve.wait_ge(*w(PE, "down", e - 2))
                    nc.vector.tensor_scalar(hid[:, e % 2, 1, :], C.bank(3 + e % 2 * 2), b1[:, e, 1:2], 0.0, ALU.add,
                                            ALU.max).then_inc(*V("hid", e))

                def weigh(e):
                    dve.wait_ge(*w(PE, "down", e))
                    dve.wait_ge(*w.own())
                    for t in range(NT):
                        nc.vector.scalar_tensor_tensor(out=acc[:, t, :], in0=ps[:, 6 + e % 2, t * P:(t + 1) * P],
                                                       scalar=coef[:, t, e:e + 1], in1=acc[:, t, :], op0=ALU.mult,
                                                       op1=ALU.add).then_inc(*V("acc", e, t))

                hidden(0)
                hidden(1)
                dve.wait_ge(*w(PE, "bias"))
                nc.vector.tensor_tensor(acc[:, :, :], y0[:, :, :], C.bank(1).rearrange("p (t e) -> p t e", t=NT),
                                        ALU.add).then_inc(*V("acc"))
                for e in range(EX):
                    if e >= 2:
                        hidden(e)
                    weigh(e)
                dve.wait_ge(*w.own())
                dve_norm(nc, C, S, w, acc, C.nb, "norm_1")
                dve.wait_ge(*w.own())
                nc.vector.tensor_tensor(C.nb[:, :, :], C.nb[:, :, :], gains[:, 0, :].unsqueeze(1).to_broadcast(
                    [P, NT, D]), ALU.mult).then_inc(*V("gain"))
                dve.wait_ge(*w.own())
                nc.vector.tensor_tensor(C.yb[:, :, :], C.nb[:, :, :], gains[:, 1, :].unsqueeze(1).to_broadcast(
                    [P, NT, D]), ALU.add).then_inc(*V("y"))
                dve.wait_ge(*w.own())
                dve_add_norm(nc, C, S, w, i, "norm_y")

        @block.tensor
        def _(pe):
            S.once(pe, PE)
            pe.wait_ge(S.loaded, S.loads)
            with S.loop(pe, PE) as (i, w):
                pe.wait_ge(*w(V, "norm_x", NT - 1))
                pe_turn(nc, C, S, w, y0, 0, "hT")
                pe.wait_ge(*w(A, "hT"))
                for t in range(NT):
                    o = ps[:, 1, t * EX:(t + 1) * EX]
                    nc.tensor.matmul(o, hT[:, t * P:(t + 1) * P], wg[:, :], start=True, stop=False)
                    last = nc.tensor.matmul(o, C.ones[0:1, :], bg[:, :], start=False, stop=True)
                last.then_inc(*PE("logits"))

                def up(e):
                    if e >= 2:
                        pe.wait_ge(*w(A, "hid", e - 2))
                        pe.wait_ge(*w(V, "hid", e - 2))
                    for c in range(CH):
                        nc.tensor.matmul(C.bank(2 + e % 2 * 2 + c), w1[:, e, c * P:(c + 1) * P], hT[:, :], start=True,
                                         stop=True).then_inc(*PE("up", e, c))

                def down(e):
                    pe.wait_ge(*w(A, "hid", e))
                    pe.wait_ge(*w(V, "hid", e))
                    if e >= 2:
                        pe.wait_ge(*w(V, "acc", e - 2, NT - 1))
                    pe_rows(nc, C, w, 6 + e % 2, [hid[:, e % 2, c, :] for c in range(CH)],
                            [w2[:, e, c, :] for c in range(CH)]).then_inc(*PE("down", e))

                up(0)
                up(1)
                pe.wait_ge(*w(V, "coef"))
                for t in range(NT):
                    last = nc.tensor.transpose(ps[0:EX, 0, t * P:(t + 1) * P], coef[:, t, :], C.ident[:, :])
                last.then_inc(*PE("coefT"))
                pe.wait_ge(*w(A, "coefT"))
                for t in range(NT):
                    last = nc.tensor.matmul(ps[:, 1, t * P:(t + 1) * P], coefT[:, t * P:(t + 1) * P], b2[:, :],
                                            start=True, stop=True)
                last.then_inc(*PE("bias"))
                for e in range(EX):
                    down(e)
                    if e + 2 < EX:
                        up(e + 2)
    S.close()



def stage_l3_attn(nc, C, plan):
    H, R, E = 16, 16, 8
    HALF_SCALE = float(np.float32(0.5) / np.sqrt(np.float32(E)))
    d = C.d
    S = Stage(nc, "l3attn", plan)
    PE, A, V, G = S.PE, S.ACT, S.DVE, S.POOL
    ps = C.ps
    wqk, wv = S.sb("wqk", [P, 4, D]), S.sb("wv", [P, D])
    wr, wrm = S.sb("wr", [P, 2, R]), S.sb("wrm", [P, 2, 4, R])
    wgt, gb, dec = S.sb("wgt", [P, H * R]), S.sb("gb", [P, H]), S.sb("dec", [P, H])
    wrep = S.sb("wrep", [P, 2, H, P])
    wo, ob = S.sb("wo", [P, H, D]), S.sb("ob", [1, D])
    gains, headmask, rope = S.sb("gains", [P, 2, D]), S.sb("headmask", [P, 4]), S.sb("rope", [P, 2, T])
    rrep = S.sb("rrep", [P, 2, 4, P])
    y0, hT = S.sb("y0", [P, NT, D]), S.sb("hT", [P, T])
    rot, tm = S.sb("rot", [P, 2, T]), S.sb("tm", [P, 2, T])
    th, u, st = S.sb("th", [P, 2, T]), S.sb("u", [P, 2, T]), S.sb("st", [P, 2, T])
    yv, hres = S.sb("yv", [P, 2, T]), S.sb("hres", [P, NT, D])

    with nc.Block() as block:
        @block.sync
        def _(sp):
            S.load(sp, wqk[:, :, :], d["L3_attn_qk_turned"])
            S.load(sp, wv[:, :], d["L3_attn_v_turned"])
            S.load(sp, wr[:, :, :], d["L3_attn_ranks"])
            S.load(sp, wgt[:, :], d["L3_attn_g_turned"])
            S.load(sp, gb[:, :], d["L3_attn_g_b_spread"])
            S.load(sp, dec[:, :], d["L3_attn_decay_spread"])
            for r in range(R):
                S.load(sp, wo[r * E:(r + 1) * E, :, :], d["L3_attn_out_turned"].rearrange("(h e) n -> e h n", h=H))
            S.load(sp, ob[:, :], row(d["L3_attn_out_b"]))
            S.load(sp, gains[:, 0, :], row(d["L3_attn_ln_g"]).to_broadcast([P, D]))
            S.load(sp, gains[:, 1, :], row(d["L3_attn_ln_b"]).to_broadcast([P, D]))
            S.load(sp, headmask[:, :], d["const_head_of_four"])
            S.load(sp, rope[:, :, :], d["const_l3_rope"])
            sp.wait_ge(S.loaded, S.loads)

        @block.gpsimd
        def _(pool):
            S.once(pool, G)
            with S.loop(pool, G) as (i, w):
                for name in ("norm_x", "norm_1", "norm_y"):
                    pool_norm(nc, C, S, w, name)

        @block.scalar
        def _(act):
            w = S.once(act, A)
            act.wait_ge(S.loaded, S.loads)
            nc.scalar.activation(dec[:, :], dec[:, :], ACT.Tanh, scale=0.5).then_inc(*A("dec"))
            nc.scalar.activation(gb[:, :], gb[:, :], ACT.Copy, scale=0.5).then_inc(*A("half_gb"))
            act.wait_ge(*w.own())
            with S.loop(act, A) as (i, w):
                act.wait_ge(*w(V, "norm_y", "x", back=1))
                nc.scalar.activation(C.xb[:, :, :], C.x[:, bass.ds(i * NT, NT), :], ACT.Copy).then_inc(*A("xb"))
                act.wait_ge(*w(PE, "hT", NT - 1))
                nc.scalar.activation(hT[:, :], C.bank(7), ACT.Copy).then_inc(*A("hT"))
                for h in range(H):
                    act.wait_ge(*w(PE, "g", h))
                    if h >= 2:
                        act.wait_ge(*w(V, "gk", h - 2))
                    nc.scalar.activation(th[:, h % 2, :], C.bank(2), ACT.Tanh, bias=gb[:, h:h + 1],
                                         scale=0.5).then_inc(*A("th", h))

        @block.vector
        def _(dve):
            w = S.once(dve, V)
            dve.wait_ge(S.loaded, S.loads)
            dve.wait_ge(*w(A, "dec"))
            nc.vector.tensor_scalar(dec[:, :], dec[:, :], 0.5, 0.5, ALU.mult, ALU.add).then_inc(*V("dec"))
            for x in range(2):
                for j in range(4):
                    nc.vector.tensor_scalar(wrm[:, x, j, :], wr[:, x, :], headmask[:, j:j + 1], None,
                                            ALU.mult).then_inc(*V("wrm", x, j))
            dve.wait_ge(*w.own())
            for x in range(2):
                for j in range(4):
                    nc.vector.tensor_copy(rrep[:, x, j, :].rearrange("p (r e) -> p r e", r=R),
                                          wrm[:, x, j, :].unsqueeze(2).to_broadcast([P, R, E])).then_inc(
                                              *V("rrep", x, j))
            for h in range(H):
                nc.vector.tensor_copy(wrep[:, 0, h, :].rearrange("p (r e) -> p r e", r=R),
                                      wgt[:, h * R:(h + 1) * R].unsqueeze(2).to_broadcast([P, R, E])).then_inc(
                                          *V("wrep", 0, h))
                nc.vector.tensor_copy(wrep[:, 1, h, :].rearrange("p (r e) -> p r e", r=R),
                                      wv[:, h * E:(h + 1) * E].unsqueeze(1).to_broadcast([P, R, E])).then_inc(
                                          *V("wrep", 1, h))
            with S.loop(dve, V) as (i, w):
                dve.wait_ge(*w(A, "xb"))
                dve_norm(nc, C, S, w, C.xb, y0, "norm_x")
                for x in range(2):
                    dve.wait_ge(*w(PE, "qk", x))
                    dve.wait_ge(*w.own())
                    nc.vector.tensor_tensor(tm[:, 0, :], C.bank(2 * x), rope[:, 0, :], ALU.mult).then_inc(*V("cos", x))
                    nc.vector.tensor_tensor(tm[:, 1, :], C.bank(2 * x + 1), rope[:, 1, :],
                                            ALU.mult).then_inc(*V("sin", x))
                    dve.wait_ge(*w.own())
                    nc.vector.tensor_tensor(rot[:, x, :], tm[:, 0, :], tm[:, 1, :], ALU.add).then_inc(*V("rot", x))
                for h in range(H):
                    b = h % 2
                    dve.wait_ge(*w(A, "th", h))
                    dve.wait_ge(*w(PE, "k", h))
                    nc.vector.scalar_tensor_tensor(out=u[:, b, :], in0=th[:, b, :], scalar=1.0, in1=C.bank(b),
                                                   op0=ALU.add, op1=ALU.mult).then_inc(*V("gk", h))
                    dve.wait_ge(*w.own())
                    dve.wait_ge(*w(PE, "v", h))
                    nc.vector.scalar_tensor_tensor(out=u[:, b, :], in0=u[:, b, :], scalar=HALF_SCALE,
                                                   in1=C.bank(3 + b), op0=ALU.mult, op1=ALU.mult).then_inc(
                                                       *V("gkv", h))
                    dve.wait_ge(*w.own())
                    nc.vector.tensor_tensor_scan(st[:, b, :], dec[:, h:h + 1].to_broadcast([P, T]), u[:, b, :], 0.0,
                                                 ALU.mult, ALU.add).then_inc(*V("memory", h))
                    dve.wait_ge(*w.own())
                    dve.wait_ge(*w(PE, "q", h))
                    if h >= 2:
                        dve.wait_ge(*w(PE, "y", h - 2))
                    nc.vector.tensor_tensor(yv[:, b, :], st[:, b, :], C.bank(5 + b), ALU.mult).then_inc(*V("yv", h))
                dve.wait_ge(*w(PE, "out"))
                nc.vector.tensor_tensor(hres[:, :, :], y0[:, :, :], C.bank(7).rearrange("p (t e) -> p t e", t=NT),
                                        ALU.add).then_inc(*V("hres"))
                dve.wait_ge(*w.own())
                dve_norm(nc, C, S, w, hres, C.nb, "norm_1")
                dve.wait_ge(*w.own())
                nc.vector.tensor_tensor(C.nb[:, :, :], C.nb[:, :, :], gains[:, 0, :].unsqueeze(1).to_broadcast(
                    [P, NT, D]), ALU.mult).then_inc(*V("gain"))
                dve.wait_ge(*w.own())
                nc.vector.tensor_tensor(C.yb[:, :, :], C.nb[:, :, :], gains[:, 1, :].unsqueeze(1).to_broadcast(
                    [P, NT, D]), ALU.add).then_inc(*V("y"))
                dve.wait_ge(*w.own())
                dve_add_norm(nc, C, S, w, i, "norm_y")

        @block.tensor
        def _(pe):
            w = S.once(pe, PE)
            pe.wait_ge(S.loaded, S.loads)
            pe.wait_ge(*w(V, "wrep", 1, H - 1))
            with S.loop(pe, PE) as (i, w):
                pe.wait_ge(*w(V, "norm_x", NT - 1))
                pe.wait_ge(*w(V, "hres", back=1))
                pe_turn(nc, C, S, w, y0, 7, "hT")
                pe.wait_ge(*w(A, "hT"))
                for x in range(2):
                    for j in range(2):
                        last = nc.tensor.matmul(C.bank(2 * x + j), wqk[:, 2 * x + j, :], hT[:, :], start=True,
                                                stop=True)
                    last.then_inc(*PE("qk", x))

                def head(h):
                    b, r = h % 2, 32 * (h // 4)
                    if h >= 1:
                        pe.wait_ge(*w(A, "th", h - 1))
                    if h == 0:
                        pe.wait_ge(*w(V, "rot", 1))
                    nc.tensor.matmul(C.bank(2), wrep[:, 0, h, :], hT[:, :], start=True, stop=True).then_inc(*PE("g", h))
                    if h >= 2:
                        pe.wait_ge(*w(V, "gk", h - 2))
                    nc.tensor.matmul(C.bank(b), rrep[r:r + 32, 1, h % 4, :], rot[r:r + 32, 1, :], start=True,
                                     stop=True).then_inc(*PE("k", h))
                    if h >= 2:
                        pe.wait_ge(*w(V, "gkv", h - 2))
                    nc.tensor.matmul(C.bank(3 + b), wrep[:, 1, h, :], hT[:, :], start=True, stop=True).then_inc(
                        *PE("v", h))
                    if h >= 2:
                        pe.wait_ge(*w(V, "yv", h - 2))
                    nc.tensor.matmul(C.bank(5 + b), rrep[r:r + 32, 0, h % 4, :], rot[r:r + 32, 0, :], start=True,
                                     stop=True).then_inc(*PE("q", h))

                def add_out(h):
                    pe.wait_ge(*w(V, "yv", h))
                    for t in range(NT):
                        last = nc.tensor.matmul(ps[:, 7, t * P:(t + 1) * P], yv[:, h % 2, t * P:(t + 1) * P],
                                                wo[:, h, :], start=(h == 0 and t == 0), stop=False,
                                                skip_group_check=True)
                    last.then_inc(*PE("y", h))

                for h in range(H + 1):
                    if h < H:
                        head(h)
                    if h >= 1:
                        add_out(h - 1)
                for t in range(NT):
                    last = nc.tensor.matmul(ps[:, 7, t * P:(t + 1) * P], C.ones[0:1, :], ob[:, :], start=False,
                                            stop=True, skip_group_check=True)
                last.then_inc(*PE("out"))
    S.close()



def stage_l3_ffn(nc, C, plan):
    I, BL = 352, 16
    CH = -(-I // P)
    rows_of = [min(P, I - c * P) for c in range(CH)]
    d = C.d
    S = Stage(nc, "l3ffn", plan)
    PE, A, V, G = S.PE, S.ACT, S.DVE, S.POOL
    ps = C.ps
    wgu, wd = S.sb("wgu", [P, 2, CH, D]), S.sb("wd", [P, I])
    wguT, wdT = S.sb("wguT", [P, 2, I]), S.sb("wdT", [P, CH, D])
    y0, xqT, sg = S.sb("y0", [P, NT, D]), S.sb("xqT", [P, T]), S.sb("sg", [P, 2, I])
    h, hqT = S.sb("h", [P, NT, I]), S.sb("hqT", [P, CH, T])
    WIDE = NT * I
    NB = WIDE // BL
    ab, sign, u = S.sb("ab", [P, WIDE]), S.sb("sign", [P, WIDE]), S.sb("u", [P, WIDE])
    am, rs = S.sb("am", [P, NB]), S.sb("rs", [P, NB])

    def act_quantise(w, src, n, name, first=False):
        if not first:
            nc.scalar.wait_ge(*w(V, "free", back=0 if name != "qx" else 1))
        nc.scalar.activation(ab[:, 0:n], src, ACT.Abs).then_inc(*A(name, "abs"))
        nc.scalar.activation(sign[:, 0:n], src, ACT.Sign).then_inc(*A(name, "sign"))

    def dve_quantise(w, dst, n, name):
        nb = n // BL
        blocks = lambda x: x[:, 0:n].rearrange("p (b k) -> p b k", k=BL)
        each = lambda x: x[:, 0:nb].unsqueeze(2).to_broadcast([P, nb, BL])
        nc.vector.wait_ge(*w(A, name, "abs"))
        nc.vector.tensor_reduce(am[:, 0:nb], blocks(ab), AX, ALU.max).then_inc(*V(name, "max"))
        nc.vector.wait_ge(*w.own())
        nc.vector.tensor_scalar(am[:, 0:nb], am[:, 0:nb], 1.0 / 6.0, 1e-12, ALU.mult, ALU.max).then_inc(
            *V(name, "scale"))
        nc.vector.wait_ge(*w.own())
        nc.vector.reciprocal(rs[:, 0:nb], am[:, 0:nb]).then_inc(*V(name, "rec"))
        nc.vector.wait_ge(*w.own())
        nc.vector.tensor_tensor(blocks(ab), blocks(ab), each(rs), ALU.mult).then_inc(*V(name, "norm"))
        nc.vector.wait_ge(*w.own())
        nc.vector.tensor_scalar(u[:, 0:n], ab[:, 0:n], 5.0, 2.0, ALU.is_gt, ALU.mult).then_inc(*V(name, 5.0))
        for mid in (3.5, 2.5):
            nc.vector.wait_ge(*w.own())
            nc.vector.scalar_tensor_tensor(out=u[:, 0:n], in0=ab[:, 0:n], scalar=mid, in1=u[:, 0:n], op0=ALU.is_gt,
                                           op1=ALU.add).then_inc(*V(name, mid))
        nc.vector.wait_ge(*w.own())
        nc.vector.tensor_scalar(u[:, 0:n], u[:, 0:n], 2.0, None, ALU.mult).then_inc(*V(name, "double"))
        for mid in (1.75, 1.25, 0.75, 0.25):
            nc.vector.wait_ge(*w.own())
            nc.vector.scalar_tensor_tensor(out=u[:, 0:n], in0=ab[:, 0:n], scalar=mid, in1=u[:, 0:n], op0=ALU.is_gt,
                                           op1=ALU.add).then_inc(*V(name, mid))
        nc.vector.wait_ge(*w(A, name, "sign"))
        nc.vector.wait_ge(*w.own())
        nc.vector.scalar_tensor_tensor(out=u[:, 0:n], in0=u[:, 0:n], scalar=0.5, in1=sign[:, 0:n], op0=ALU.mult,
                                       op1=ALU.mult).then_inc(*V(name, "signed"))
        nc.vector.wait_ge(*w.own())
        nc.vector.tensor_tensor(dst.rearrange("p (b k) -> p b k", k=BL), blocks(u), each(am),
                                ALU.mult).then_inc(*V(name))

    with nc.Block() as block:
        @block.sync
        def _(sp):
            w = Waits(sp, None)
            sp.wait_ge(*w(G, "wgu_pad"))
            for x, n in enumerate(("w_gate", "w_up")):
                for c in range(CH):
                    m = rows_of[c]
                    S.load(sp, wgu[0:m, x, c, :], d["L3_ffn_" + n][c * P:c * P + m, :])
            S.load(sp, wd[:, :], d["L3_ffn_w_down"])
            sp.wait_ge(S.loaded, S.loads)

        @block.gpsimd
        def _(pool):
            w = S.once(pool, G)
            nc.gpsimd.memset(wgu[64:P, :, CH - 1, :], 0.0).then_inc(*G("wgu_pad"))
            with S.loop(pool, G) as (i, w):
                for name in ("norm_x", "norm_y"):
                    pool_norm(nc, C, S, w, name)

        @block.scalar
        def _(act):
            w = S.once(act, A)
            act.wait_ge(S.loaded, S.loads)
            act_quantise(w, wgu[:, :, :, :].rearrange("p x c n -> p (x c n)"), 2 * CH * D, "qgu", first=True)
            act.wait_ge(*w(V, "qgu"))
            act_quantise(w, wd[:, :], I, "qd", first=True)
            for x in range(2):
                act.wait_ge(*w(PE, "wT", x))
                nc.scalar.activation(wguT[:, x, :], ps[:, x, 0:I], ACT.Copy).then_inc(*A("wT", x))
            act.wait_ge(*w(PE, "wT", 2))
            for c in range(CH):
                m = rows_of[c]
                nc.scalar.activation(wdT[0:m, c, :], ps[0:m, 2, c * P:(c + 1) * P], ACT.Copy).then_inc(*A("wT", 2, c))
            with S.loop(act, A) as (i, w):
                act.wait_ge(*w(V, "norm_y", "x", back=1))
                nc.scalar.activation(C.xb[:, :, :], C.x[:, bass.ds(i * NT, NT), :], ACT.Copy).then_inc(*A("xb"))
                act.wait_ge(*w(V, "norm_x", NT - 1))
                act_quantise(w, y0[:, :, :].rearrange("p t e -> p (t e)"), T, "qx", first=True)
                act.wait_ge(*w(PE, "xqT", NT - 1))
                nc.scalar.activation(xqT[:, :], C.bank(0), ACT.Copy).then_inc(*A("xqT"))
                for t in range(NT):
                    act.wait_ge(*w(PE, "gate", t))
                    if t >= 2:
                        act.wait_ge(*w(V, "h", t - 2))
                    nc.scalar.activation(sg[:, t % 2, :], ps[:, 1 + t % 2, 0:I], ACT.Silu).then_inc(*A("silu", t))
                act.wait_ge(*w(V, "h", NT - 1))
                act_quantise(w, h[:, :, :].rearrange("p t e -> p (t e)"), WIDE, "qh", first=True)
                for c in range(CH):
                    m = rows_of[c]
                    act.wait_ge(*w(PE, "hqT", c))
                    nc.scalar.activation(hqT[0:m, c, :], C.bank(5 + c, m), ACT.Copy).then_inc(*A("hqT", c))
                act.wait_ge(*w(PE, "out"))
                nc.scalar.activation(C.yb[:, :, :], C.bank(0).rearrange("p (t e) -> p t e", t=NT),
                                     ACT.Copy).then_inc(*A("y"))

        @block.vector
        def _(dve):
            w = S.once(dve, V)
            dve.wait_ge(S.loaded, S.loads)
            dve_quantise(w, wgu[:, :, :, :].rearrange("p x c n -> p (x c n)"), 2 * CH * D, "qgu")
            dve_quantise(w, wd[:, :], I, "qd")
            with S.loop(dve, V) as (i, w):
                dve.wait_ge(*w(A, "xb"))
                dve_norm(nc, C, S, w, C.xb, y0, "norm_x")
                dve_quantise(w, y0[:, :, :].rearrange("p t e -> p (t e)"), T, "qx")
                for t in range(NT):
                    dve.wait_ge(*w(A, "silu", t))
                    dve.wait_ge(*w(PE, "up", t))
                    nc.vector.tensor_tensor(h[:, t, :], sg[:, t % 2, :], ps[:, 3 + t % 2, 0:I],
                                            ALU.mult).then_inc(*V("h", t))
                dve_quantise(w, h[:, :, :].rearrange("p t e -> p (t e)"), WIDE, "qh")
                dve.wait_ge(*w(A, "y"))
                dve_add_norm(nc, C, S, w, i, "norm_y")

        @block.tensor
        def _(pe):
            w = S.once(pe, PE)
            pe.wait_ge(*w(V, "qd"))
            for x in range(2):
                for c in range(CH):
                    m = rows_of[c]
                    last = nc.tensor.transpose(ps[:, x, c * P:c * P + m], wgu[0:m, x, c, :], C.ident[0:m, 0:m])
                last.then_inc(*PE("wT", x))
            for c in range(CH):
                m = rows_of[c]
                last = nc.tensor.transpose(ps[0:m, 2, c * P:(c + 1) * P], wd[:, c * P:c * P + m], C.ident[:, :])
            last.then_inc(*PE("wT", 2))
            pe.wait_ge(*w(A, "wT", 2, CH - 1))
            with S.loop(pe, PE) as (i, w):
                pe.wait_ge(*w(V, "qx"))
                pe.wait_ge(*w(A, "y", back=1))
                pe_turn(nc, C, S, w, y0, 0, "xqT")
                pe.wait_ge(*w(A, "xqT"))
                for t in range(NT):
                    for x, name in enumerate(("gate", "up")):
                        if t >= 2:
                            pe.wait_ge(*w(V, "h", t - 2))
                        nc.tensor.matmul(ps[:, 1 + 2 * x + t % 2, 0:I], xqT[:, t * P:(t + 1) * P], wguT[:, x, :],
                                         start=True, stop=True).then_inc(*PE(name, t))
                pe.wait_ge(*w(V, "qh"))
                for c in range(CH):
                    m = rows_of[c]
                    for t in range(NT):
                        last = nc.tensor.transpose(ps[0:m, 5 + c, t * P:(t + 1) * P], h[:, t, c * P:c * P + m],
                                                   C.ident[:, :])
                    last.then_inc(*PE("hqT", c))
                pe.wait_ge(*w(A, "hqT", CH - 1))
                pe_rows(nc, C, w, 0, [hqT[0:rows_of[c], c, :] for c in range(CH)],
                        [wdT[0:rows_of[c], c, :] for c in range(CH)]).then_inc(*PE("out"))
    S.close()



def position_tables():
    import numpy as np

    p = np.arange(P)
    c = {"const_head_of_four": (p[:, None] // 8 % 4 == np.arange(4)[None, :]).astype(np.float32)}
    j = np.arange(2 * P)
    seen = (j[None, :] > p[:, None]) & (j[None, :] <= p[:, None] + P)
    both = np.stack([seen & (j >= P)[None, :], seen], 1)
    c["const_l0_mask"] = np.ascontiguousarray(
        np.repeat(np.where(both, 0.0, NEG).astype(np.float32)[:, :, None, :], 2, 2))
    for name, win in (("l0ffn", 32), ("l1ffn", 64)):
        j, r = np.arange(P)[None, :], p[:, None]
        seen = (j >= r) & (j <= r + win)
        both = np.where(np.stack([seen & (j >= win), seen], 1), 0.0, NEG).astype(np.float32)
        c[f"const_{name}_mask"] = np.ascontiguousarray(np.repeat(both[:, :, None, :], 4, 2))
        c[f"const_{name}_tables"] = rotary(win)
    shift = np.zeros((P, 2, P), np.float32)
    shift[p[:-1], 0, p[1:]] = 1.0
    shift[P - 1, 1, 0] = 1.0
    c["const_shift"] = shift
    c["const_head_of_two"] = (p[:, None] // 16 % 2 == np.arange(2)[None, :]).astype(np.float32)
    sums, pairs = np.zeros((P, 9, P), np.float32), np.zeros((P, 8, P), np.float32)
    r, x = p[:, None], p[None, :]
    for l in range(7):
        mid = (x >> (l + 1) << (l + 1)) + (1 << l)
        sums[:, l, :] = np.where(x < mid, (r > x) & (r < mid), (r >= mid) & (r <= x))
        pairs[:, l, :] = (r >> (l + 1) == x >> (l + 1)) & (r < mid) & (x >= mid)
    sums[:, 7, :], sums[:, 8, :] = r <= x, r > x
    pairs[:, 7, :] = r == x
    c["const_l2_sums"], c["const_l2_pairs"] = sums, pairs
    e = np.arange(8)
    c["const_before"] = np.ascontiguousarray(np.tile((e[None, :] < e[:, None]).astype(np.float32), (P, 1, 1)))
    f = np.float32
    inv_freq = f(1.0) / np.power(f(10000.0), np.arange(4, dtype=f) / f(4), dtype=f)
    freqs = (np.arange(T, dtype=f)[None, :] * inv_freq[p % 8 // 2][:, None]).astype(f).astype(np.float64)
    sign = np.where(p % 2 == 0, -1.0, 1.0)[:, None]
    c["const_l3_rope"] = np.stack([np.cos(freqs), sign * np.sin(freqs)], 1).astype(f)
    return c


def rotary(win, head=64):
    import numpy as np

    f = np.float32
    half = np.arange(0, head, 2, dtype=f)
    inv_freq = f(1.0) / np.power(f(10000.0), half / f(head), dtype=f)
    t = np.arange(T, dtype=f)
    freqs = (t[:, None] * inv_freq[None, :]).astype(f)
    base = ((half + f(0.4 * head)) / f(1.4 * head)).astype(f)
    power = (t - f(T // 2)) / f(win // 2)
    scale = np.power(base[None, :].astype(np.float64), power[:, None].astype(np.float64)).astype(f)
    cos, sin = np.cos(freqs.astype(np.float64)), np.sin(freqs.astype(np.float64))
    parts = []
    for s in (scale.astype(np.float64), 1.0 / scale.astype(np.float64)):
        parts += [np.concatenate([cos * s, cos * s], 1), np.concatenate([-sin * s, sin * s], 1)]
    x = np.stack(parts, 0).astype(f).reshape(4, NT, P, head)
    return np.ascontiguousarray(x.transpose(2, 0, 1, 3))


def lay_out(inputs):
    import numpy as np

    a = {n: np.ascontiguousarray(x) for n, x in inputs.items()}
    q, k, v, g, o = (a.pop("L3_attn_" + n) for n in ("q_w", "k_w", "v_w", "g_w", "out_w"))
    partner = np.arange(D) ^ 1
    a["L3_attn_qk_turned"] = np.ascontiguousarray(np.stack([q, q[partner], k, k[partner]]).transpose(2, 0, 1))
    a["L3_attn_v_turned"] = np.ascontiguousarray(v.transpose())
    a["L3_attn_g_turned"] = np.ascontiguousarray(g.transpose())
    a["L3_attn_out_turned"] = np.ascontiguousarray(o.transpose())
    ranks = np.stack([a.pop("L3_attn_Wq"), a.pop("L3_attn_Wk")])
    a["L3_attn_ranks"] = np.ascontiguousarray(ranks.transpose(1, 3, 0, 2).reshape(D, 2, 16))
    for name, x in (("g_b_spread", a.pop("L3_attn_g_b").reshape(16, 16)),
                    ("decay_spread", a.pop("L3_attn_base_decay_logits"))):
        a["L3_attn_" + name] = np.ascontiguousarray(np.repeat(x.transpose(), 8, 0))
    b1 = a.pop("L2_ffn_b1")
    a["L2_ffn_b1_turned"] = np.ascontiguousarray(b1.reshape(8, 2, P).transpose(2, 0, 1))
    a.update(position_tables())
    return a


def build(nc, d, out, plan, stages):
    C = Common(nc, d)
    setup(nc, C, d["L0_attn_x"])
    for stage in stages:
        stage(nc, C, plan)
    stored = nc.alloc_semaphore("out_stored")
    with nc.Block() as block:
        @block.sync
        def _(sp):
            sp.dma_start(out.rearrange("b (t p) d -> p (b t) d", p=P), C.x[:, :, :]).then_inc(stored, 16)
            sp.wait_ge(stored, 16)


STAGES = [stage_l0_attn, stage_norm_in_0, stage_l0_ffn, stage_norm_out_0, stage_l1_attn, stage_l1_attn_out, stage_norm_in_1,
          stage_l1_ffn, stage_norm_out_1, stage_l2_attn, stage_l2_ffn, stage_l3_attn, stage_l3_ffn]


def program(bacc, shapes, stages=None):
    plan = {}
    for _ in range(2):
        nc = bacc.Bacc("TRN2", target_bir_lowering=False, num_devices=1)
        d = {n: nc.dram_tensor(f"in_{n}_dram", s, F32, kind="ExternalInput").ap() for n, s in shapes.items()}
        out = nc.dram_tensor("out_0_dram", (B, T, D), F32, kind="ExternalOutput").ap()
        build(nc, d, out, plan, STAGES if stages is None else stages)
    return nc



def kernel(**inputs):
    import concourse.bacc as _bacc
    from concourse.bass_utils import run_bass_kernel_spmd as _run

    arrays = lay_out(inputs)
    nc = program(_bacc, {n: a.shape for n, a in arrays.items()})
    r = _run(nc, [{f"in_{n}_dram": a for n, a in arrays.items()}], core_ids=[0])
    return r.results[0]["out_0_dram"]
```

```python
from contextlib import ExitStack, contextmanager

import numpy as np

import concourse.bass as bass
from concourse import mybir

P = 128
B, T, D = 8, 512, 128
NT = T // P
EPS = 1e-5
NEG = -1e30
F32 = mybir.dt.float32
BF16 = mybir.dt.bfloat16
U32 = mybir.dt.uint32
ALU = mybir.AluOpType
ACT = mybir.ActivationFunctionType
AX = mybir.AxisListType.X


class Results:

    def __init__(self, nc, stage, engine, plan):
        self.sem = nc.alloc_semaphore(f"{stage}_{engine}_done")
        self.key, self.plan = f"{stage}_{engine}", plan
        self.at, self.once, self.each = plan.get(self.key, ({}, 0, 1))
        self.found, self.n, self.n_once = {}, 0, 0

    def __call__(self, *name):
        self.n += 1
        self.found[name] = self.n
        return self.sem, 1

    def end_once(self):
        self.n_once, self.n = self.n, 0

    def close(self):
        self.plan[self.key] = (self.found, self.n_once, self.n)


class Waits:

    def __init__(self, eng, own, turns=None, layer=None, trips=1):
        self.eng, self.own_results, self.turn, self.layer, self.trips = eng, own, turns, layer, trips

    def value(self, r, n, back):
        v = n + r.each * (1 - back)
        if self.turn is not None:
            v = v + r.once + self.turn * r.each
        if self.layer is not None:
            v = v + self.layer * (r.once + self.trips * r.each)
        return v

    def __call__(self, r, *name, back=0):
        return r.sem, self.value(r, r.at.get(name, 1), back)

    def layer_start(self, r):
        return r.sem, r.each + self.layer * (r.once + self.trips * r.each)

    def own(self):
        r = self.own_results
        return r.sem, self.value(r, r.n, 0)


class Stage:

    def __init__(self, nc, name, plan, trips=B, layers=None):
        self.nc, self.name, self.trips, self.layers = nc, name, trips, layers
        self.stack = ExitStack()
        self.PE, self.ACT, self.DVE, self.POOL = (Results(nc, name, e, plan) for e in ("pe", "act", "dve", "pool"))
        self.loaded = nc.alloc_semaphore(f"{name}_weights_loaded")
        self.loads = 0

    def sb(self, name, shape, dt=F32):
        return self.stack.enter_context(self.nc.sbuf_tensor(f"{self.name}_{name}", shape, dt))

    def once(self, eng, own):
        if self.layers is None:
            eng.sem_inc(own.sem, own.each)
        return Waits(eng, own)

    @contextmanager
    def loop(self, eng, own):
        own.end_once()
        with eng.Fori(0, self.trips, 1) as i:
            yield i, Waits(eng, own, i)

    @contextmanager
    def layer_loop(self, eng, own):
        eng.sem_inc(own.sem, own.each)
        with eng.Fori(0, self.layers, 1) as l:
            w = Waits(eng, own, None, l, self.trips)
            yield l, w

    @contextmanager
    def sequence_loop(self, eng, own, l):
        own.end_once()
        with eng.Fori(0, self.trips, 1) as i:
            yield i, Waits(eng, own, i, l, self.trips)

    def load(self, sp, dst, src):
        sp.dma_start(dst, src).then_inc(self.loaded, 16)
        self.loads += 16

    def close(self):
        for r in (self.PE, self.ACT, self.DVE, self.POOL):
            r.close()
        self.stack.close()


class Common:

    def __init__(self, nc, d):
        self.nc, self.d = nc, d
        self.ps = nc.alloc_psum_tensor("ps", [P, 8, 512], F32)
        self.x = nc.alloc_sbuf_tensor("x_all", [P, B * NT, D], F32)
        self.y = nc.alloc_sbuf_tensor("y_all", [P, B * NT + NT, D], F32)
        self.ident = nc.alloc_sbuf_tensor("ident", [P, P], F32)
        self.ident_bf = nc.alloc_sbuf_tensor("ident_bf", [P, P], BF16)
        self.ones = nc.alloc_sbuf_tensor("ones", [P, P], F32)
        self.neghalf = nc.alloc_sbuf_tensor("neghalf", [P, 64], F32)
        self.xb = nc.alloc_sbuf_tensor("xb", [P, NT, D], F32)
        self.yb = nc.alloc_sbuf_tensor("yb", [P, NT, D], F32)
        self.nb = nc.alloc_sbuf_tensor("nb", [P, NT, D], F32)
        self.st = nc.alloc_sbuf_tensor("bn_st", [P, NT, 6], F32)
        self.mv = nc.alloc_sbuf_tensor("bn_mv", [P, NT, 2], F32)
        self.ve = nc.alloc_sbuf_tensor("bn_ve", [P, NT], F32)
        self.rs = nc.alloc_sbuf_tensor("bn_rs", [P, NT], F32)

    def bank(self, b, rows=P):
        return self.ps[0:rows, b, :]


def column(v):
    return v.rearrange("(p o) -> p o", o=1)


def row(v):
    return v.rearrange("(o n) -> o n", o=1)



def dve_norm(nc, C, S, w, src, dst, name):
    V, G = S.DVE, S.POOL
    for t in range(NT):
        nc.vector.bn_stats(C.st[:, t, :], src[:, t, :]).then_inc(*V(name, "stats", t))
    nc.vector.wait_ge(*w.own())
    nc.vector.memset(C.ve[:, :], 0.0).then_inc(*V(name, "clear"))
    for t in range(NT):
        nc.vector.bn_aggr(C.mv[:, t, :], C.st[:, t, :]).then_inc(*V(name, "moments", t))
    nc.vector.wait_ge(*w.own())
    nc.vector.tensor_scalar(C.ve[:, :], C.mv[:, :, 1], EPS, None, ALU.add).then_inc(*V(name, "var"))
    nc.vector.wait_ge(*w(G, name, "rstd"))
    for t in range(NT):
        nc.vector.tensor_scalar(dst[:, t, :], src[:, t, :], C.mv[:, t, 0:1], C.rs[:, t:t + 1],
                                ALU.subtract, ALU.mult).then_inc(*V(name, t))


def pool_norm(nc, C, S, w, name):
    nc.gpsimd.wait_ge(*w(S.DVE, name, "var"))
    nc.gpsimd.tensor_tensor(C.rs[:, :], C.ve[:, :], C.neghalf[:, 0:NT], ALU.pow).then_inc(*S.POOL(name, "rstd"))


def pe_turn(nc, C, S, w, src, bank, name):
    for t in range(NT):
        nc.tensor.transpose(C.ps[:, bank, t * P:(t + 1) * P], src[:, t, :], C.ident[:, :]).then_inc(*S.PE(name, t))


def pe_rows(nc, C, w, bank, lhs, weights, bias=None):
    for t in range(NT):
        o = C.ps[:, bank, t * P:(t + 1) * P]
        for c in range(len(lhs)):
            last = nc.tensor.matmul(o, lhs[c][:, t * P:(t + 1) * P], weights[c], start=(c == 0),
                                    stop=(bias is None and c == len(lhs) - 1))
        if bias is not None:
            last = nc.tensor.matmul(o, C.ident[:, :], bias, start=False, stop=True)
    return last


def stage_norms(nc, C, plan, name, add=True, then=True):
    TURNS = 2
    N = B * NT // TURNS
    S = Stage(nc, name, plan, trips=TURNS)
    A, V, G = S.ACT, S.DVE, S.POOL
    st, mv, nb = S.sb("stats", [P, N, 6]), S.sb("moments", [P, N, 2]), S.sb("normed", [P, N, D])
    ve, rs, nm = (S.sb(n, [P, N]) for n in ("variance", "rstd", "shift"))
    passes = [n for n, on in (("out", add), ("in", then)) if on]

    def tiles(x, i, t=0, n=N):
        return x[:, bass.ds(i * N + t, n), :]

    def tile(x, i, t):
        return tiles(x, i, t, 1).rearrange("p o d -> p (o d)")

    with nc.Block() as block:
        @block.gpsimd
        def _(pool):
            S.once(pool, G)
            with S.loop(pool, G) as (i, w):
                for k in passes:
                    pool.wait_ge(*w(V, k, "var"))
                    nc.gpsimd.tensor_tensor(rs[:, :], ve[:, :], C.neghalf[:, 0:N], ALU.pow).then_inc(*G(k, "rstd"))

        @block.scalar
        def _(act):
            S.once(act, A)
            with S.loop(act, A) as (i, w):
                for k in passes:
                    act.wait_ge(*w(V, k, "shift"))
                    for t in range(1, N, 2):
                        dst = nb[:, t, :] if k == "out" else tile(C.y, i, t)
                        nc.scalar.activation(dst, tile(C.y if k == "out" else C.x, i, t), ACT.Identity,
                                             bias=nm[:, t:t + 1], scale=rs[:, t:t + 1]).then_inc(*A(k, t))

        @block.vector
        def _(dve):
            S.once(dve, V)
            with S.loop(dve, V) as (i, w):
                for k in passes:
                    src = C.y if k == "out" else C.x
                    dve.wait_ge(*w(A, passes[-1], N - 1, back=1) if k == passes[0] else w(A, passes[0], N - 1))
                    dve.wait_ge(*w.own())
                    nc.vector.memset(ve[:, :], 0.0).then_inc(*V(k, "clear"))
                    for t in range(N):
                        nc.vector.bn_stats(st[:, t, :], tile(src, i, t)).then_inc(*V(k, "stats", t))
                    dve.wait_ge(*w.own())
                    nc.vector.memset(nm[:, :], 0.0).then_inc(*V(k, "clear_shift"))
                    for t in range(N):
                        nc.vector.bn_aggr(mv[:, t, :], st[:, t, :]).then_inc(*V(k, "moments", t))
                    dve.wait_ge(*w.own())
                    nc.vector.tensor_scalar(ve[:, :], mv[:, :, 1], EPS, None, ALU.add).then_inc(*V(k, "var"))
                    dve.wait_ge(*w(G, k, "rstd"))
                    nc.vector.scalar_tensor_tensor(out=nm[:, :], in0=mv[:, :, 0], scalar=-1.0, in1=rs[:, :],
                                                   op0=ALU.mult, op1=ALU.mult).then_inc(*V(k, "shift"))
                    for t in range(0, N, 2):
                        dst = nb[:, t, :] if k == "out" else tile(C.y, i, t)
                        nc.vector.tensor_scalar(dst, tile(src, i, t), mv[:, t, 0:1], rs[:, t:t + 1],
                                                ALU.subtract, ALU.mult).then_inc(*V(k, t))
                    if k == "out":
                        dve.wait_ge(*w(A, k, N - 1))
                        dve.wait_ge(*w.own())
                        nc.vector.tensor_tensor(tiles(C.x, i), tiles(C.x, i), nb[:, :, :],
                                                ALU.add).then_inc(*V("x"))
    S.close()


def setup(nc, C, d_x):
    x_loaded = nc.alloc_semaphore("x_loaded")
    filled = nc.alloc_semaphore("constants_filled")
    with nc.Block() as block:
        @block.sync
        def _(sp):
            sp.dma_start(C.x[:, :, :], d_x.rearrange("b (t p) d -> p (b t) d", p=P)).then_inc(x_loaded, 16)
            sp.wait_ge(x_loaded, 16)

        @block.gpsimd
        def _(pool):
            nc.gpsimd.memset(C.ident[:, :], 0.0).then_inc(filled, 1)
            nc.gpsimd.memset(C.ones[:, :], 1.0).then_inc(filled, 1)
            nc.gpsimd.memset(C.neghalf[:, :], -0.5).then_inc(filled, 1)
            nc.gpsimd.memset(C.y[:, B * NT:, :], 0.0).then_inc(filled, 1)
            pool.wait_ge(filled, 4)
            nc.gpsimd.affine_select(out=C.ident[:, :], in_=C.ident[:, :], compare_op=ALU.not_equal, fill=1.0,
                                    base=0, pattern=[[-1, P]], channel_multiplier=1).then_inc(filled, 1)
            pool.wait_ge(filled, 5)
            nc.gpsimd.tensor_copy(C.ident_bf[:, :], C.ident[:, :]).then_inc(filled, 1)
            pool.wait_ge(filled, 6)



def stage_l0_attn(nc, C, plan):
    H, DH, WIN, N, FF = 16, 8, 128, 64, 4
    SCALE = float(np.float32(1.0) / np.sqrt(np.float32(DH)))
    d = C.d
    S = Stage(nc, "l0attn", plan)
    PE, A, V, G = S.PE, S.ACT, S.DVE, S.POOL
    ps = C.ps
    wq, wk, wv, wo, wg = (S.sb(n, [P, D]) for n in ("wq", "wk", "wv", "wo", "wg"))
    bw, cw = S.sb("bw", [P, N]), S.sb("cw", [P, D])
    w1, w2 = S.sb("w1", [P, FF, P]), S.sb("w2", [P, FF, D])
    cols = S.sb("cols", [P, 16])
    LN1G, LN1B, BQ, BK, LN2G, LN2B, B1, DEC = 0, 1, 2, 3, 4, 5, 6, 10
    rows = S.sb("rows", [P, 4, D])
    BV, BO, BG, B2 = 0, 1, 2, 3
    headmask = S.sb("headmask", [P, H])
    mask = S.sb("mask", [P, 2, 2, 2 * P])
    mask_bf = S.sb("mask_bf", [P, 2, 2, 2 * P], BF16)
    hT, qm = S.sb("hT", [P, T]), S.sb("qm", [P, H, T])
    kT = S.sb("kT", [P, P + T])
    qT = S.sb("qT", [P, T])
    va = S.sb("va", [P, NT + 1, 4, P + 32])
    gate, sT = S.sb("gate", [P, NT, D]), S.sb("sT", [P, T])
    mx, nm, sm, rec = (S.sb(n, [P, 4, 2]) for n in ("mx", "nm", "sm", "rec"))
    pr, pT = S.sb("pr", [P, 4, 2, 2 * P]), S.sb("pT", [P, 2, 4, P])
    aoT = S.sb("aoT", [P, T])
    ssm, x1, hid = S.sb("ssm", [P, NT, D]), S.sb("x1", [P, NT, D]), S.sb("hid", [P, FF, T])
    K = NT * H // 2
    cw_zero = nc.alloc_semaphore("l0attn_cw_zero")
    LN1, LN2 = "norm_1", "norm_2"

    with nc.Block() as block:
        @block.sync
        def _(sp):
            for dst, n in ((wq, "WQ"), (wk, "WK"), (wv, "WV"), (wo, "WO"), (wg, "Wg"), (bw, "Bw")):
                S.load(sp, dst[:, :], d["L0_attn_" + n])
            sp.wait_ge(cw_zero, 1)
            S.load(sp, cw[0:N, :], d["L0_attn_Cw"])
            S.load(sp, w1[:, :, :], d["L0_attn_W1"].rearrange("k (c n) -> k c n", c=FF))
            S.load(sp, w2[:, :, :], d["L0_attn_W2"].rearrange("(c k) n -> k c n", c=FF))
            for c, n in ((LN1G, "ln1_g"), (LN1B, "ln1_b"), (BQ, "bQ"), (BK, "bK"), (LN2G, "ln2_g"), (LN2B, "ln2_b")):
                S.load(sp, cols[:, c:c + 1], column(d["L0_attn_" + n]))
            for c in range(FF):
                S.load(sp, cols[:, B1 + c:B1 + c + 1], column(d["L0_attn_b1"][c * P:(c + 1) * P]))
            S.load(sp, cols[0:N, DEC:DEC + 1], column(d["L0_attn_A"]))
            for c, n in ((BV, "bV"), (BO, "bO"), (BG, "bg"), (B2, "b2")):
                S.load(sp, rows[:, c, :], row(d["L0_attn_" + n]).to_broadcast([P, D]))
            S.load(sp, headmask[:, :], d["const_head_of_16"])
            S.load(sp, mask[:, :, :, :], d["const_l0_mask"])
            sp.wait_ge(S.loaded, S.loads)

        @block.gpsimd
        def _(pool):
            w = S.once(pool, G)
            nc.gpsimd.memset(cw[:, :], 0.0).then_inc(cw_zero, 1)
            nc.gpsimd.memset(kT[:, 0:P], 0.0).then_inc(*G("kT_pad"))
            nc.gpsimd.memset(sT[:, :], 0.0).then_inc(*G("sT_pad"))
            nc.gpsimd.memset(va[:, :, :, :], 0.0).then_inc(*G("va_pad"))
            pool.wait_ge(S.loaded, S.loads)
            nc.gpsimd.tensor_copy(mask_bf[:, :, :, :], mask[:, :, :, :]).then_inc(*G("mask"))
            pool.wait_ge(*w.own())
            with S.loop(pool, G) as (i, w):
                pool_norm(nc, C, S, w, LN1)
                for k in range(K):
                    pool.wait_ge(*w(V, "rec", k))
                    nc.gpsimd.tensor_tensor(pr[:, k % 4], pr[:, k % 4], rec[:, k % 4, :].unsqueeze(2).to_broadcast(
                        [P, 2, 2 * P]), ALU.mult).then_inc(*G("probs", k))
                pool_norm(nc, C, S, w, LN2)

        @block.scalar
        def _(act):
            w = S.once(act, A)
            act.wait_ge(S.loaded, S.loads)
            act.wait_ge(*w(G, "va_pad"))
            with S.loop(act, A) as (i, w):
                act.wait_ge(*w(V, "y", back=1))
                nc.scalar.activation(C.xb[:, :, :], C.y[:, bass.ds(i * NT, NT), :], ACT.Copy).then_inc(*A("xb"))
                act.wait_ge(*w(PE, "hT", NT - 1))
                nc.scalar.activation(hT[:, :], C.bank(0), ACT.Identity, bias=cols[:, LN1B:LN1B + 1],
                                     scale=cols[:, LN1G:LN1G + 1]).then_inc(*A("hT"))
                act.wait_ge(*w(PE, "K"))
                nc.scalar.activation(kT[:, P:], C.bank(2), ACT.Identity,
                                     bias=cols[:, BK:BK + 1]).then_inc(*A("kT"))
                act.wait_ge(*w(PE, "V"))
                for j in range(4):
                    nc.scalar.activation(va[:, 1:, :, 40 * j:40 * j + DH],
                                         C.bank(4).rearrange("p (t g e) -> p t g e", t=NT, g=4)[:, :, :, 8 * j:8 * j + 8],
                                         ACT.Copy).then_inc(*A("va", j))
                act.wait_ge(*w(V, "qT"))
                for h in range(H // 2, H):
                    nc.scalar.activation(qm[:, h, :], qT[:, :], ACT.Copy,
                                         scale=headmask[:, h:h + 1]).then_inc(*A("qm", h))
                act.wait_ge(*w(PE, "gate"))
                nc.scalar.activation(gate[:, :, :], C.bank(5).rearrange("p (t e) -> p t e", t=NT), ACT.Tanh,
                                     scale=0.5).then_inc(*A("tanh"))
                for k in range(K):
                    act.wait_ge(*w(V, "negmax", k))
                    if k >= 4:
                        act.wait_ge(*w(PE, "pT", k - 4))
                    for j in range(2):
                        nc.scalar.activation(pr[:, k % 4, j, :], ps[:, k % 3, j * 2 * P:(j + 1) * 2 * P], ACT.Exp,
                                             bias=nm[:, k % 4, j:j + 1], scale=SCALE,
                                             accum_out=sm[:, k % 4, j:j + 1]).then_inc(*A("exp", k, j))
                act.wait_ge(*w(PE, "ssm"))
                nc.scalar.activation(ssm[:, :, :], C.bank(6).rearrange("p (t e) -> p t e", t=NT),
                                     ACT.Copy).then_inc(*A("ssm"))
                act.wait_ge(*w(PE, "O", K - 1))
                nc.scalar.activation(aoT[:, :], C.bank(7), ACT.Copy).then_inc(*A("aoT"))
                act.wait_ge(*w(PE, "h2T", NT - 1))
                nc.scalar.activation(hT[:, :], C.bank(1), ACT.Identity, bias=cols[:, LN2B:LN2B + 1],
                                     scale=cols[:, LN2G:LN2G + 1]).then_inc(*A("h2T"))
                for c in range(FF):
                    act.wait_ge(*w(PE, "up", c))
                    nc.scalar.activation(hid[:, c, :], C.bank(2 + c), ACT.Gelu,
                                         bias=cols[:, B1 + c:B1 + c + 1]).then_inc(*A("hid", c))

        @block.vector
        def _(dve):
            w = S.once(dve, V)
            dve.wait_ge(S.loaded, S.loads)
            dve.wait_ge(*w(G, "mask"))
            with S.loop(dve, V) as (i, w):
                dve.wait_ge(*w(A, "xb"))
                dve_norm(nc, C, S, w, C.xb, C.nb, LN1)
                dve.wait_ge(*w(PE, "Q"))
                nc.vector.tensor_scalar(qT[:, :], C.bank(1), cols[:, BQ:BQ + 1], None, ALU.add).then_inc(*V("qT"))
                dve.wait_ge(*w.own())
                for h in range(H // 2):
                    nc.vector.tensor_scalar(qm[:, h, :], qT[:, :], headmask[:, h:h + 1], None,
                                            ALU.mult).then_inc(*V("qm", h))
                dve.wait_ge(*w(PE, "u"))
                nc.vector.tensor_tensor_scan(sT[0:N, :], cols[0:N, DEC:DEC + 1].to_broadcast([N, T]), C.bank(3, N),
                                             0.0, ALU.mult, ALU.add).then_inc(*V("sT"))
                dve.wait_ge(*w(A, "tanh"))
                nc.vector.tensor_scalar(gate[:, :, :], gate[:, :, :], 0.5, 0.5, ALU.mult,
                                        ALU.add).then_inc(*V("gate"))

                def maximum(k):
                    dve.wait_ge(*w(PE, "S", k))
                    nc.vector.tensor_reduce(mx[:, k % 4, :], C.bank(k % 3).rearrange("p (j n) -> p j n", j=2),
                                            AX, ALU.max).then_inc(*V("max", k))
                    dve.wait_ge(*w.own())
                    nc.vector.tensor_scalar(nm[:, k % 4, :], mx[:, k % 4, :], -SCALE, None,
                                            ALU.mult).then_inc(*V("negmax", k))

                def copy_probs(k):
                    dve.wait_ge(*w(PE, "pT", k))
                    if k >= 2:
                        dve.wait_ge(*w(PE, "O", k - 2))
                    nc.vector.tensor_copy(pT[:, k % 2, :, :],
                                          C.bank(3 + k % 2).rearrange("p (j n) -> p j n", j=4)).then_inc(*V("pT", k))

                def reciprocals(k):
                    dve.wait_ge(*w(A, "exp", k, 1))
                    nc.vector.reciprocal(rec[:, k % 4, :], sm[:, k % 4, :]).then_inc(*V("rec", k))

                for k in range(K + 3):
                    if k < K:
                        maximum(k)
                    if 1 <= k <= K:
                        reciprocals(k - 1)
                    if k >= 3:
                        copy_probs(k - 3)
                dve.wait_ge(*w(PE, "attn"))
                dve.wait_ge(*w(A, "ssm"))
                attn = C.bank(0).rearrange("p (t e) -> p t e", t=NT)
                nc.vector.tensor_tensor(x1[:, :, :], attn, ssm[:, :, :], ALU.subtract).then_inc(*V("x1", 0))
                dve.wait_ge(*w.own())
                nc.vector.tensor_tensor(x1[:, :, :], x1[:, :, :], gate[:, :, :], ALU.mult).then_inc(*V("x1", 1))
                dve.wait_ge(*w.own())
                nc.vector.tensor_tensor(x1[:, :, :], x1[:, :, :], ssm[:, :, :], ALU.add).then_inc(*V("x1", 2))
                dve.wait_ge(*w.own())
                nc.vector.tensor_tensor(x1[:, :, :], x1[:, :, :], C.xb[:, :, :], ALU.add).then_inc(*V("x1", 3))
                dve.wait_ge(*w.own())
                dve_norm(nc, C, S, w, x1, C.nb, LN2)
                dve.wait_ge(*w(PE, "down"))
                nc.vector.tensor_tensor(C.y[:, bass.ds(i * NT, NT), :], x1[:, :, :], C.bank(6).rearrange("p (t e) -> p t e", t=NT),
                                        ALU.add).then_inc(*V("y"))

        @block.tensor
        def _(pe):
            w = S.once(pe, PE)
            pe.wait_ge(S.loaded, S.loads)
            pe.wait_ge(*w(G, "mask"))
            with S.loop(pe, PE) as (i, w):
                pe.wait_ge(*w(A, "xb"))
                pe.wait_ge(*w(V, LN1, NT - 1))
                pe_turn(nc, C, S, w, C.nb, 0, "hT")
                pe.wait_ge(*w(A, "hT"))
                pe.wait_ge(*w(V, "y", back=1))
                nc.tensor.matmul(C.bank(1), wq[:, :], hT[:, :], start=True, stop=True).then_inc(*PE("Q"))
                nc.tensor.matmul(C.bank(2), wk[:, :], hT[:, :], start=True, stop=True).then_inc(*PE("K"))
                nc.tensor.matmul(C.bank(3, N), bw[:, :], hT[:, :], start=True, stop=True).then_inc(*PE("u"))
                for bank, wt, b, name in ((4, wv, BV, "V"), (5, wg, BG, "gate")):
                    for t in range(NT):
                        o = ps[:, bank, t * P:(t + 1) * P]
                        nc.tensor.matmul(o, hT[:, t * P:(t + 1) * P], wt[:, :], start=True, stop=False)
                        last = nc.tensor.matmul(o, C.ident[:, :], rows[:, b, :], start=False, stop=True)
                    last.then_inc(*PE(name))
                pe.wait_ge(*w(A, "va", 3))

                def scores(k):
                    t, h = k // (H // 2), k % (H // 2)
                    if t == 0:
                        pe.wait_ge(*w(V, "qm", h))
                        pe.wait_ge(*w(A, "qm", h + H // 2))
                    if k >= 3:
                        pe.wait_ge(*w(A, "exp", k - 3, 1))
                    b = k % 3
                    nc.tensor.matmul(C.bank(b), C.ident_bf[:, :], mask_bf[:, int(t > 0), :, :], start=True,
                                     stop=False)
                    for j in range(2):
                        last = nc.tensor.matmul(ps[:, b, j * 2 * P:(j + 1) * 2 * P],
                                                qm[:, h + j * H // 2, t * P:(t + 1) * P],
                                                kT[:, t * P:(t + 2) * P], start=False, stop=(j == 1))
                    last.then_inc(*PE("S", k))

                def turn_probs(k):
                    pe.wait_ge(*w(G, "probs", k))
                    if k >= 2:
                        pe.wait_ge(*w(V, "pT", k - 2))
                    for j in range(2):
                        for s in range(2):
                            n = 2 * j + s
                            last = nc.tensor.transpose(ps[:, 3 + k % 2, n * P:(n + 1) * P],
                                                       pr[:, k % 4, j, s * P:(s + 1) * P], C.ident[:, :])
                    last.then_inc(*PE("pT", k))

                def values(k):
                    t, h = k // (H // 2), k % (H // 2)
                    pe.wait_ge(*w(V, "pT", k))
                    for s in range(2):
                        for j in range(2):
                            g, c = h // 4 + 2 * j, h % 4
                            last = nc.tensor.matmul(ps[32 * g:32 * g + 32, 7, t * P:(t + 1) * P],
                                                    va[:, t + s, g, 32 * c:32 * c + 32], pT[:, k % 2, 2 * j + s, :],
                                                    start=(c == 0 and s == 0), stop=(c == 3 and s == 1))
                    last.then_inc(*PE("O", k))

                for k in range(K + 4):
                    if k < K:
                        scores(k)
                    if 3 <= k < K + 3:
                        turn_probs(k - 3)
                    if k >= 4:
                        values(k - 4)
                pe.wait_ge(*w(V, "sT"))
                for t in range(NT):
                    last = nc.tensor.matmul(ps[:, 6, t * P:(t + 1) * P], sT[:, t * P:(t + 1) * P], cw[:, :],
                                            start=True, stop=True)
                last.then_inc(*PE("ssm"))
                pe.wait_ge(*w(A, "aoT"))
                for t in range(NT):
                    o = ps[:, 0, t * P:(t + 1) * P]
                    nc.tensor.matmul(o, aoT[:, t * P:(t + 1) * P], wo[:, :], start=True, stop=False)
                    last = nc.tensor.matmul(o, C.ident[:, :], rows[:, BO, :], start=False, stop=True)
                last.then_inc(*PE("attn"))
                pe.wait_ge(*w(V, LN2, NT - 1))
                pe_turn(nc, C, S, w, C.nb, 1, "h2T")
                pe.wait_ge(*w(A, "h2T"))
                for c in range(FF):
                    nc.tensor.matmul(C.bank(2 + c), w1[:, c, :], hT[:, :], start=True,
                                     stop=True).then_inc(*PE("up", c))
                for t in range(NT):
                    o = ps[:, 6, t * P:(t + 1) * P]
                    for c in range(FF):
                        pe.wait_ge(*w(A, "hid", c))
                        nc.tensor.matmul(o, hid[:, c, t * P:(t + 1) * P], w2[:, c, :], start=(c == 0), stop=False)
                    last = nc.tensor.matmul(o, C.ident[:, :], rows[:, B2, :], start=False, stop=True)
                last.then_inc(*PE("down"))
    S.close()



def local_layers(nc, C, plan, name, block_name, H, DEPTH, WIN, weights):
    E = 64
    INNER, HID = H * E, int(D * 4 * 2 / 3)
    HG = H // 8
    CH = INNER // P
    QT = P - WIN
    QR = 96
    NA = -(-T // QT)
    HC = -(-HID // P)
    hid_rows = [min(P, HID - c * P) for c in range(HC)]
    nq = [min(QT, T - QT * a) for a in range(NA)]
    nk = [WIN + n for n in nq]
    QK_SCALE = 8.0
    d = C.d
    Wqkv, qs, ksc, Wo, lng, lnb, W1, b1, W2, b2 = (d[f"{block_name}_{n}"] for n in weights)
    S = Stage(nc, name, plan, layers=DEPTH)
    PE, A, V, G = S.PE, S.ACT, S.DVE, S.POOL
    ps = C.ps
    wqkv, wo = S.sb("wqkv", [P, 3 * INNER]), S.sb("wo", [P, CH, D])
    w1, w2 = S.sb("w1", [P, 2 * HID]), S.sb("w2", [P, HC, D])
    cols, b2row = S.sb("cols", [P, 2 + 2 * HC]), S.sb("b2row", [P, D])
    scales = S.sb("scales", [P, 2, E])
    base = S.sb("tables", [P, 4, NT, E])
    tab = S.sb("tables_scaled", [P, 4, NT, E])
    mask_f, mask = S.sb("mask_f", [P, 2, 4, P]), S.sb("mask", [P, 2, 4, P], BF16)
    shift = S.sb("shift", [P, 2, P])
    hT = S.sb("hT", [P, WIN + T])
    work = S.sb("work", [P, 4, 8 * P])
    sq, r2 = work[:, 0:2, 0:INNER], work[:, 2, 0:INNER]
    pr = work[:, :, :].rearrange("p k (h n) -> p k h n", h=8)
    rq01 = S.sb("rq01", [P, 2, INNER])
    rq = (rq01[:, 0], rq01[:, 1], work[:, 3, 0:INNER])
    n2, rn = S.sb("n2", [P, 2, H]), S.sb("rn", [P, 2, H])
    qT = S.sb("qT", [P, max(CH, 2 * HC), T])
    ge, hid = qT[:, 0:HC, :], qT[:, HC:2 * HC, :]
    kT = S.sb("kT", [P, CH, 2, WIN + T])
    va = S.sb("va", [P, NA, INNER])
    mx, sm, rec = (S.sb(n, [P, 4, 8]) for n in ("mx", "sm", "rec"))
    pT, aoT = S.sb("pT", [P, 2, 8, QR]), S.sb("aoT", [P, CH, T])
    ys, hnT = S.sb("ys", [P, NT, D]), S.sb("hnT", [P, T])
    U = 2 * NT
    NU = NA * HG
    AHEAD, VALUES_AHEAD = 3, 2
    LN = "norm"
    gate_bank, up_bank = (5, 7, 5), (6, 4, 6)

    def before(u):
        return int(u < AHEAD)

    def age(u):
        return before(u - 2) - before(u)
    halves = INNER // 512
    pads = nc.alloc_semaphore(f"{name}_pads_filled")
    LOADS = 16 * (5 + 2 + 2 + 2 * HC + 1)

    with nc.Block() as block:
        @block.sync
        def _(sp):
            for dst, n in ((base, "tables"), (mask_f, "mask")):
                sp.dma_start(dst[:, :, :, :], d[f"const_{name}_{n}"]).then_inc(S.loaded, 16)
            sp.dma_start(shift[:, :, :], d["const_shift"]).then_inc(S.loaded, 16)
            sp.wait_ge(S.loaded, 48)

        @block.gpsimd
        def _(pool):
            w = Waits(pool, G)
            pool.wait_ge(S.loaded, 48)
            nc.gpsimd.memset(hT[:, 0:WIN + 1], 0.0).then_inc(pads, 1)
            nc.gpsimd.memset(va[:, :, :], 0.0).then_inc(pads, 1)
            nc.gpsimd.memset(work[:, :, :], 0.0).then_inc(pads, 1)
            nc.gpsimd.memset(qT[:, :, :], 0.0).then_inc(pads, 1)
            nc.gpsimd.memset(kT[:, :, :, :], 0.0).then_inc(pads, 1)
            nc.gpsimd.tensor_copy(mask[:, :, :, :], mask_f[:, :, :, :]).then_inc(pads, 1)
            with S.layer_loop(pool, G) as (l, w):
                pool.wait_ge(S.loaded, 48 + LOADS * (l + 1))
                pool.wait_ge(*w.layer_start(V))
                for x in range(2):
                    sc = scales[:, x, :].unsqueeze(1).to_broadcast([P, NT, E])
                    nc.gpsimd.tensor_tensor(tab[:, 2 * x], base[:, 2 * x], sc, ALU.mult).then_inc(*G("tab", x, 0))
                    for a, b in ((0, E // 2), (E // 2, 0)):
                        nc.gpsimd.tensor_tensor(tab[:, 2 * x + 1, :, a:a + E // 2], base[:, 2 * x + 1, :, a:a + E // 2],
                                                sc[:, :, b:b + E // 2], ALU.mult).then_inc(*G("tab", x, 1, a))
                def norm_factor(w, u, *mark):
                    pool.wait_ge(*w(V, *mark, "n2", u))
                    nc.gpsimd.tensor_tensor(rn[:, u % 2, :], n2[:, u % 2, :], C.neghalf[:, 0:H],
                                            ALU.pow).then_inc(*G(*mark, "rn", u))

                def unit_vectors(w, u, *mark):
                    v = rq[u % 3].rearrange("p (h e) -> p h e", h=H)
                    pool.wait_ge(*w.own())
                    pool.wait_ge(*w(V, *mark, "rot", u))
                    nc.gpsimd.tensor_tensor(v, v, rn[:, u % 2, :].unsqueeze(2).to_broadcast([P, H, E]),
                                            ALU.mult).then_inc(*G(*mark, "unit", u))

                for u in range(AHEAD):
                    norm_factor(w, u, "first")
                    unit_vectors(w, u, "first")
                with S.sequence_loop(pool, G, l) as (i, w):
                    for u in range(AHEAD, U):
                        norm_factor(w, u)
                        unit_vectors(w, u)
                    for n in range(NU):
                        pool.wait_ge(*w(V, "rec", n))
                        nc.gpsimd.tensor_tensor(pr[0:QR, n % 4], pr[0:QR, n % 4],
                                                rec[0:QR, n % 4, :].unsqueeze(2).to_broadcast([QR, 8, P]),
                                                ALU.mult).then_inc(*G("probs", n))
                    norm_factor(w, 0)
                    unit_vectors(w, 0)
                    pool_norm(nc, C, S, w, LN)
                    for u in range(1, AHEAD):
                        norm_factor(w, u)
                        unit_vectors(w, u)

        @block.scalar
        def _(act):
            act.wait_ge(pads, 6)
            with S.layer_loop(act, A) as (l, w):
                act.wait_ge(*w.layer_start(A))
                for r in (PE, V, G):
                    act.wait_ge(*w.layer_start(r))

                def load(dst, src):
                    act.dma_start(dst, src).then_inc(S.loaded, 16)

                def of_layer(x):
                    return x[bass.ds(l, 1)]

                load(wqkv[:, :], of_layer(Wqkv).rearrange("o k n -> (o k) n"))
                load(wo[:, :, :], of_layer(Wo).rearrange("o (c k) n -> k (o c) n", k=P))
                load(w1[:, :], of_layer(W1).rearrange("o k n -> (o k) n"))
                full = HID // P
                load(w2[:, 0:full, :], W2[bass.ds(l, 1), 0:full * P].rearrange("o (c k) n -> k (o c) n", k=P))
                load(w2[0:hid_rows[-1], full, :], W2[bass.ds(l, 1), full * P:].rearrange("o k n -> (o k) n"))
                load(scales[:, 0, :], of_layer(qs).to_broadcast([P, E]))
                load(scales[:, 1, :], of_layer(ksc).to_broadcast([P, E]))
                load(cols[:, 0:1], of_layer(lng).rearrange("o p -> p o"))
                load(cols[:, 1:2], of_layer(lnb).rearrange("o p -> p o"))
                for g in range(2):
                    for c in range(HC):
                        a, m = g * HID + c * P, hid_rows[c]
                        load(cols[0:m, 2 + g * HC + c:3 + g * HC + c],
                             b1[bass.ds(l, 1), a:a + m].rearrange("o p -> p o"))
                load(b2row[:, :], of_layer(b2).to_broadcast([P, D]))
                act.wait_ge(S.loaded, 48 + LOADS * (l + 1))
                def copy_shifted(w, *mark):
                    act.wait_ge(*w(PE, *mark, "yT", NT - 1))
                    nc.scalar.activation(hT[0:64, WIN:], C.bank(0, 64), ACT.Copy).then_inc(*A(*mark, "hT", 0))
                    nc.scalar.activation(hT[64:128, WIN + 1:], ps[64:128, 0, 0:T - 1],
                                         ACT.Copy).then_inc(*A(*mark, "hT", 1))

                def square(w, u, *mark):
                    act.wait_ge(*w(PE, *mark, "qk", u))
                    if u >= 2:
                        act.wait_ge(*w(V, *mark, "n2sum", u - 2, back=age(u)))
                    for hf in range(halves):
                        nc.scalar.activation(sq[:, u % 2, hf * 512:(hf + 1) * 512],
                                             C.bank(2 * (u % 2) + hf), ACT.Square).then_inc(*A(*mark, "sq", u, hf))

                def keep_values(w, a, *mark):
                    act.wait_ge(*w(PE, *mark, "V", a))
                    nc.scalar.activation(va[0:nk[a], a, :],
                                         ps[0:nk[a], 6:6 + halves, :].rearrange("p b n -> p (b n)"),
                                         ACT.Copy).then_inc(*A(*mark, "va", a))

                nc.scalar.activation(C.xb[:, :, :], C.y[:, 0:NT, :], ACT.Copy).then_inc(*A("first", "xb"))
                copy_shifted(w, "first")
                for u in range(AHEAD):
                    square(w, u, "first")
                for a in range(VALUES_AHEAD):
                    keep_values(w, a, "first")
                act.wait_ge(*w(V, "first", "n2sum", AHEAD - 1))
                with S.sequence_loop(act, A, l) as (i, w):
                    def keep_turned(u):
                        t, x = u // 2, u % 2
                        act.wait_ge(*w(PE, "qkT", u))
                        src = ps[:, 4:4 + halves, :].rearrange("p b (c n) -> p (b c) n", n=P)
                        if x == 0:
                            nc.scalar.activation(qT[:, 0:CH, t * P:(t + 1) * P], src,
                                                 ACT.Copy).then_inc(*A("qkT", u))
                        else:
                            for b in range(2):
                                r = 64 * b
                                nc.scalar.activation(kT[r:r + 64, :, b, WIN + t * P:WIN + (t + 1) * P],
                                                     src[r:r + 64], ACT.Copy).then_inc(
                                                         *A("qkT" if b else "kT_even", u))

                    for u in range(U):
                        keep_turned(u)
                        if AHEAD + u < U:
                            square(w, AHEAD + u)
                        if VALUES_AHEAD + u < NA:
                            keep_values(w, VALUES_AHEAD + u)
                    act.wait_ge(*w(PE, "yT", NT - 1, back=1))
                    nc.scalar.activation(C.xb[:, :, :], C.y[:, bass.ds(i * NT + NT, NT), :],
                                         ACT.Copy).then_inc(*A("xb"))

                    def exponent(n):
                        act.wait_ge(*w(V, "sub", n))
                        nc.scalar.activation(pr[0:QR, n % 4], pr[0:QR, n % 4], ACT.Exp,
                                             scale=QK_SCALE).then_inc(*A("exp", n))

                    def keep_probs(n):
                        act.wait_ge(*w(PE, "pT", n))
                        if n >= 2:
                            act.wait_ge(*w(PE, "O", n - 2))
                        nc.scalar.activation(pT[:, n % 2],
                                             ps[:, 4:6, :].rearrange("p b (h n) -> p (b h) n", n=P)[:, :, 0:QR],
                                             ACT.Copy).then_inc(*A("pT", n))

                    def keep_out(n):
                        a, g = n // HG, n % HG
                        act.wait_ge(*w(PE, "O", n))
                        nc.scalar.activation(aoT[:, 4 * g:4 * g + 4, QT * a:QT * a + nq[a]],
                                             ps[:, 6 + n % 2, 0:4 * QR].rearrange("p (c n) -> p c n", c=4)[:, :, 0:nq[a]],
                                             ACT.Copy).then_inc(*A("aoT", n))

                    for n in range(NU + 4):
                        if n < NU:
                            exponent(n)
                        if 3 <= n < NU + 3:
                            keep_probs(n - 3)
                        if n >= 4:
                            keep_out(n - 4)
                        if n == NU:
                            copy_shifted(w)
                        if n == NU + 1:
                            square(w, 0)
                    act.wait_ge(*w(PE, "shifted"))
                    act.wait_ge(*w(V, "y_attn"))
                    nc.scalar.activation(ys[:, :, 0:64], C.yb[:, :, 0:64], ACT.Copy).then_inc(*A("ys", 0))
                    nc.scalar.activation(ys[:, :, 64:], ps[:, 5, 0:NT * 64].rearrange("p (t e) -> p t e", t=NT),
                                         ACT.Copy).then_inc(*A("ys", 1))
                    square(w, 1)
                    for a in range(VALUES_AHEAD):
                        keep_values(w, a)
                    act.wait_ge(*w(PE, "hnT", NT - 1))
                    nc.scalar.activation(hnT[:, :], C.bank(4), ACT.Identity, bias=cols[:, 1:2],
                                         scale=cols[:, 0:1]).then_inc(*A("hnT"))
                    for c in range(HC):
                        m = hid_rows[c]
                        act.wait_ge(*w(PE, "gate", c))
                        nc.scalar.activation(ge[0:m, c, :], C.bank(gate_bank[c], m), ACT.Gelu,
                                             bias=cols[0:m, 2 + HC + c:3 + HC + c]).then_inc(*A("gelu", c))
                    for u in range(2, AHEAD):
                        square(w, u)

        @block.vector
        def _(dve):
            dve.wait_ge(pads, 6)
            with S.layer_loop(dve, V) as (l, w):
                dve.wait_ge(S.loaded, 48 + LOADS * (l + 1))
                dve.wait_ge(*w(G, "tab", 1, 1, E // 2))
                def norms_and_rotary(w, u, *mark):
                    t, x = u // 2, u % 2
                    banks = ps[:, 2 * x:2 * x + halves, :].rearrange("p b (h e) -> p (b h) e", e=E)
                    dve.wait_ge(*w(A, *mark, "sq", u, halves - 1))
                    if u >= 2:
                        dve.wait_ge(*w(G, *mark, "rn", u - 2, back=age(u)))
                    nc.vector.tensor_reduce(n2[:, x, :], sq[:, x, :].rearrange("p (h e) -> p h e", h=H), AX,
                                            ALU.add).then_inc(*V(*mark, "n2sum", u))
                    dve.wait_ge(*w.own())
                    nc.vector.tensor_scalar(n2[:, x, :], n2[:, x, :], 1e-24, None,
                                            ALU.max).then_inc(*V(*mark, "n2", u))
                    if u >= 3:
                        dve.wait_ge(*w(PE, "qkT", u - 3))
                    cs, sn = tab[:, 2 * x, t, :], tab[:, 2 * x + 1, t, :]
                    dst = rq[u % 3].rearrange("p (h e) -> p h e", h=H)
                    nc.vector.tensor_tensor(dst, banks, cs.unsqueeze(1).to_broadcast([P, H, E]),
                                            ALU.mult).then_inc(*V(*mark, "cos", u))
                    dst = r2.rearrange("p (h e) -> p h e", h=H)
                    for a, b in ((0, E // 2), (E // 2, 0)):
                        last = nc.vector.tensor_tensor(
                            dst[:, :, a:a + E // 2], banks[:, :, b:b + E // 2],
                            sn[:, a:a + E // 2].unsqueeze(1).to_broadcast([P, H, E // 2]), ALU.mult)
                        last.then_inc(*V(*mark, "sin" if a else "sin_low", u))
                    dve.wait_ge(*w.own())
                    nc.vector.tensor_tensor(rq[u % 3], rq[u % 3], r2,
                                            ALU.add).then_inc(*V(*mark, "rot", u))

                for u in range(AHEAD):
                    norms_and_rotary(w, u, "first")
                dve.wait_ge(*w(G, "first", "unit", AHEAD - 1))
                nc.vector.memset(rec[:, :, :], 0.0).then_inc(*V("first", "rec"))
                with S.sequence_loop(dve, V, l) as (i, w):
                    for u in range(AHEAD, U):
                        norms_and_rotary(w, u)

                    def subtract_max(n):
                        s = ps[0:QR, 2 * (n % 2):2 * (n % 2) + 2, :].rearrange("p b (h n) -> p (b h) n", n=P)
                        dve.wait_ge(*w(PE, "S", n))
                        nc.vector.tensor_reduce(mx[0:QR, n % 4, :], s, AX, ALU.max).then_inc(*V("max", n))
                        dve.wait_ge(*w.own())
                        if n == 3:
                            dve.wait_ge(*w(PE, "qkT", U - 1))
                        if n >= 4:
                            dve.wait_ge(*w(PE, "pT", n - 4))
                        nc.vector.tensor_tensor(pr[0:QR, n % 4], s,
                                                mx[0:QR, n % 4, :].unsqueeze(2).to_broadcast([QR, 8, P]),
                                                ALU.subtract).then_inc(*V("sub", n))

                    def sums(n):
                        dve.wait_ge(*w(A, "exp", n))
                        nc.vector.tensor_reduce(sm[0:QR, n % 4, :], pr[0:QR, n % 4], AX, ALU.add).then_inc(*V("sum", n))
                        dve.wait_ge(*w.own())
                        nc.vector.reciprocal(rec[0:QR, n % 4, :], sm[0:QR, n % 4, :]).then_inc(*V("rec", n))

                    for n in range(NU + 1):
                        if n < NU:
                            subtract_max(n)
                        if n >= 1:
                            sums(n - 1)
                    norms_and_rotary(w, 0)
                    dve.wait_ge(*w(PE, "attn", NT - 1))
                    nc.vector.tensor_tensor(C.yb[:, :, :], C.y[:, bass.ds(i * NT, NT), :],
                                            C.bank(3).rearrange("p (t e) -> p t e", t=NT),
                                            ALU.add).then_inc(*V("y_attn"))
                    dve.wait_ge(*w(A, "ys", 1))
                    dve_norm(nc, C, S, w, ys, C.nb, LN)
                    norms_and_rotary(w, 1)
                    for c in range(HC):
                        m = hid_rows[c]
                        dve.wait_ge(*w(A, "gelu", c))
                        dve.wait_ge(*w(PE, "up", c))
                        nc.vector.scalar_tensor_tensor(out=hid[0:m, c, :], in0=C.bank(up_bank[c], m),
                                                       scalar=cols[0:m, 2 + c:3 + c], in1=ge[0:m, c, :],
                                                       op0=ALU.add, op1=ALU.mult).then_inc(*V("hid", c))
                    for u in range(2, AHEAD):
                        norms_and_rotary(w, u)
                    dve.wait_ge(*w(PE, "down"))
                    nc.vector.tensor_tensor(C.y[:, bass.ds(i * NT, NT), :], C.yb[:, :, :],
                                            C.bank(7).rearrange("p (t e) -> p t e", t=NT),
                                            ALU.add).then_inc(*V("y_mlp"))

        @block.tensor
        def _(pe):
            pe.wait_ge(pads, 6)
            with S.layer_loop(pe, PE) as (l, w):
                def turn_next(w, *mark):
                    pe.wait_ge(*w(A, *mark, "xb"))
                    for t in range(NT):
                        nc.tensor.transpose(ps[:, 0, t * P:(t + 1) * P], C.xb[:, t, :],
                                            C.ident[:, :]).then_inc(*PE(*mark, "yT", t))

                def project(w, u, *mark):
                    t, x = u // 2, u % 2
                    if u >= 2:
                        pe.wait_ge(*w(V, *mark, "sin", u - 2, back=age(u)))
                    for hf in range(halves):
                        last = nc.tensor.matmul(C.bank(2 * x + hf), hT[:, WIN + t * P:WIN + (t + 1) * P],
                                                wqkv[:, x * INNER + hf * 512:x * INNER + (hf + 1) * 512],
                                                start=True, stop=True)
                    last.then_inc(*PE(*mark, "qk", u))

                def project_values(w, a, *mark):
                    if a >= 1:
                        pe.wait_ge(*w(A, *mark, "va", a - 1, back=int(a == VALUES_AHEAD)))
                    for hf in range(halves):
                        last = nc.tensor.matmul(ps[0:nk[a], 6 + hf, :], hT[:, QT * a:QT * a + nk[a]],
                                                wqkv[:, 2 * INNER + hf * 512:2 * INNER + (hf + 1) * 512],
                                                start=True, stop=True)
                    last.then_inc(*PE(*mark, "V", a))

                pe.wait_ge(S.loaded, 48 + LOADS * (l + 1))
                turn_next(w, "first")
                pe.wait_ge(*w(A, "first", "hT", 1))
                for u in range(AHEAD):
                    project(w, u, "first")
                for a in range(VALUES_AHEAD):
                    project_values(w, a, "first")
                pe.wait_ge(*w(A, "first", "va", VALUES_AHEAD - 1))
                pe.wait_ge(*w(G, "first", "unit", AHEAD - 1))
                nc.tensor.transpose(ps[:, 0, 0:P], C.ident[:, :], C.ident[:, :]).then_inc(*PE("first", "end"))
                with S.sequence_loop(pe, PE, l) as (i, w):
                    def turn_unit(u):
                        pe.wait_ge(*w(G, "unit", u, back=before(u)))
                        if u >= 1:
                            pe.wait_ge(*w(A, "qkT", u - 1))
                        for c in range(CH):
                            last = nc.tensor.transpose(ps[:, 4 + c // 4, c % 4 * P:(c % 4 + 1) * P],
                                                       rq[u % 3][:, c * P:(c + 1) * P], C.ident[:, :])
                        last.then_inc(*PE("qkT", u))

                    def scores(n):
                        a, g = n // HG, n % HG
                        if n >= 2:
                            pe.wait_ge(*w(V, "sub", n - 2))
                        else:
                            pe.wait_ge(*w(V, "sin", U - 2 + n))
                        pe.wait_ge(*w(A, "qkT", 2 * ((QT * a + nq[a] - 1) // P) + 1))
                        for b in range(2):
                            bank = 2 * (n % 2) + b
                            nc.tensor.matmul(C.bank(bank), C.ident_bf[:, :], mask[:, int(a > 0), :, :],
                                             start=True, stop=True)
                        for c in range(4):
                            bank, o = 2 * (n % 2) + c // 2, c % 2 * 2 * P
                            out = ps[0:nq[a], bank, o:o + 2 * P].rearrange("p (b n) -> p b n", b=2)
                            last = nc.tensor.matmul(out[:, :, 0:nk[a]], qT[:, 4 * g + c, QT * a:QT * a + nq[a]],
                                                    kT[:, 4 * g + c, :, QT * a:QT * a + nk[a]],
                                                    start=False, stop=True, skip_group_check=True)
                        last.then_inc(*PE("S", n))

                    def turn_probs(n):
                        pe.wait_ge(*w(G, "probs", n))
                        if n >= 1:
                            pe.wait_ge(*w(A, "pT", n - 1))
                        for h in range(8):
                            last = nc.tensor.transpose(ps[:, 4 + h // 4, h % 4 * P:(h % 4 + 1) * P],
                                                       pr[:, n % 4, h, :], C.ident[:, :])
                        last.then_inc(*PE("pT", n))

                    def weigh_values(n):
                        a, g = n // HG, n % HG
                        pe.wait_ge(*w(A, "pT", n))
                        if n >= 2:
                            pe.wait_ge(*w(A, "aoT", n - 2))
                        for h in range(8):
                            r, c, v = h % 2 * 64, h // 2 * QR, (8 * g + h) * E
                            last = nc.tensor.matmul(ps[r:r + 64, 6 + n % 2, c:c + QR], va[:, a, v:v + E],
                                                    pT[:, n % 2, h, :], start=True, stop=True)
                        last.then_inc(*PE("O", n))

                    def mix_heads(t):
                        pe.wait_ge(*w(A, "aoT", HG * min(NA, (P * (t + 1) - 1) // QT + 1) - 1))
                        for c in range(CH):
                            last = nc.tensor.matmul(ps[:, 3, t * P:(t + 1) * P], aoT[:, c, t * P:(t + 1) * P],
                                                    wo[:, c, :], start=(c == 0), stop=(c == CH - 1))
                        last.then_inc(*PE("attn", t))

                    for u in range(U):
                        if u == U - 1:
                            scores(0)
                            scores(1)
                        turn_unit(u)
                        if AHEAD + u < U:
                            project(w, AHEAD + u)
                        if u == 0:
                            pe.wait_ge(*w(V, "y_mlp", back=1))
                        if VALUES_AHEAD + u < NA:
                            project_values(w, VALUES_AHEAD + u)
                    for n in range(NU + 4):
                        if 2 <= n < NU:
                            scores(n)
                        if 3 <= n < NU + 3:
                            turn_probs(n - 3)
                        if n >= 4:
                            weigh_values(n - 4)
                        if n == NU:
                            pe.wait_ge(*w(V, "sub", NU - 2))
                            turn_next(w)
                        if n == NU + 1:
                            pe.wait_ge(*w(A, "hT", 1))
                            project(w, 0)
                            pe.wait_ge(*w(V, "sub", NU - 1))
                        if n > NU:
                            mix_heads(n - NU - 1)
                    mix_heads(NT - 1)
                    pe.wait_ge(*w(V, "y_attn"))
                    nc.tensor.matmul(ps[:, 5, 0:NT * 64], shift[:, 0, :], C.yb[:, :, 64:], start=True, stop=False)
                    nc.tensor.matmul(ps[:, 5, 64:NT * 64], shift[:, 1, :], C.yb[:, 0:NT - 1, 64:], start=False,
                                     stop=True).then_inc(*PE("shifted"))
                    project(w, 1)
                    for a in range(VALUES_AHEAD):
                        project_values(w, a)
                    pe.wait_ge(*w(V, LN, NT - 1))
                    pe_turn(nc, C, S, w, C.nb, 4, "hnT")
                    pe.wait_ge(*w(A, "va", VALUES_AHEAD - 1))
                    pe.wait_ge(*w(A, "hnT"))
                    for c in range(HC):
                        m = hid_rows[c]
                        if c == 2:
                            pe.wait_ge(*w(V, "hid", 0))
                        nc.tensor.matmul(C.bank(gate_bank[c], m), w1[:, HID + c * P:HID + c * P + m], hnT[:, :], start=True,
                                         stop=True).then_inc(*PE("gate", c))
                        nc.tensor.matmul(C.bank(up_bank[c], m), w1[:, c * P:c * P + m], hnT[:, :], start=True,
                                         stop=True).then_inc(*PE("up", c))
                    for u in range(2, AHEAD):
                        project(w, u)
                    pe.wait_ge(*w(V, "hid", HC - 1))
                    last = pe_rows(nc, C, w, 7, [hid[0:hid_rows[c], c, :] for c in range(HC)],
                                   [w2[0:hid_rows[c], c, :] for c in range(HC)], b2row[:, :])
                    last.then_inc(*PE("down"))
    S.close()


def stage_l0_ffn(nc, C, plan):
    local_layers(nc, C, plan, "l0ffn", "L0_ffn", 16, 6, 32,
                 ("Wqkv", "q_scale", "k_scale", "Wo", "ln_g", "ln_b", "W1", "b1", "W2", "b2"))


def stage_l1_ffn(nc, C, plan):
    local_layers(nc, C, plan, "l1ffn", "L1_ffn", 8, 2, 64,
                 ("wqkv", "q_scale", "k_scale", "wo", "ln_g", "ln_b", "w1", "b1", "w2", "b2"))



def stage_l1_attn(nc, C, plan):
    H, DK, GR = 8, 16, 8
    DV = D // GR
    SCALE = 0.25
    d = C.d
    S = Stage(nc, "l1attn", plan)
    PE, A, V, G = S.PE, S.ACT, S.DVE, S.POOL
    ps = C.ps
    wq, wk, wv = S.sb("wq", [P, D]), S.sb("wk", [P, D]), S.sb("wv", [P, H * D])
    wvs, bv, bvs = S.sb("wvs", [P, D]), S.sb("bv", [P, H * D]), S.sb("bvs", [P, D])
    cols, headmask = S.sb("cols", [P, 4]), S.sb("headmask", [P, H])
    hT, qT, qm, kT = (S.sb("hT", [P, T]), S.sb("qT", [P, T]), S.sb("qm", [P, H, T]),
                          S.sb("kT", [P, T]))
    va = S.sb("va", [P, NT, 4, 2, 32])
    mx, nm, sm, rec = (S.sb(n, [P, 4]) for n in ("mx", "nm", "sm", "rec"))
    pr, pT = S.sb("pr", [P, 4, T]), S.sb("pT", [P, 4, NT, P])
    aoT, ao = S.sb("aoT", [P, T]), S.sb("ao", [P, NT, H, DV])
    mixed = nc.dram_tensor("l1_mixed", (B, H, T, DV), F32).ap()
    stored = nc.alloc_semaphore("l1attn_ao_stored")
    y_back = nc.alloc_semaphore("l1attn_y_loaded")
    K = NT * H
    head_of = [k % 2 * (H // 2) + k // 2 % (H // 2) for k in range(K)]
    ST = 16 * NT

    with nc.Block() as block:
        @block.sync
        def _(sp):
            for dst, n in ((wq, "Wq"), (wk, "Wk"), (wv, "Wv")):
                S.load(sp, dst[:, :], d["L1_attn_" + n])
            for c, n in enumerate(("gamma", "beta", "bq", "bk")):
                S.load(sp, cols[:, c:c + 1], column(d["L1_attn_" + n]))
            S.load(sp, bv[:, :], row(d["L1_attn_bv"]).to_broadcast([P, H * D]))
            S.load(sp, headmask[:, :], d["const_head_of_8"])
            sp.wait_ge(S.loaded, S.loads)
            sp.sem_inc(stored, ST)
            with sp.Fori(0, B, 1) as i:
                w = Waits(sp, A, i)
                sp.wait_ge(*w(A, "ao"))
                for t in range(NT):
                    sp.dma_start(mixed[bass.ds(i, 1), :, t * P:(t + 1) * P, :].rearrange("o h p j -> p (o h) j"),
                                 ao[:, t, :, :]).then_inc(stored, 16)
            sp.wait_ge(stored, ST * (B + 1))
            sp.dma_start(C.y[:, 0:B * NT, :], mixed.rearrange("b h (r a) j -> (b h r) (a j)", a=P // DV).rearrange(
                "(n p) e -> p n e", p=P)).then_inc(y_back, 16)
            sp.wait_ge(y_back, 16)

        @block.gpsimd
        def _(pool):
            w = S.once(pool, G)
            nc.gpsimd.memset(va[:, :, :, :, :], 0.0).then_inc(*G("va_pad"))
            with S.loop(pool, G) as (i, w):
                pool_norm(nc, C, S, w, "norm_1")
                for k in range(K):
                    pool.wait_ge(*w(V, "rec", k))
                    nc.gpsimd.tensor_tensor(pr[:, k % 4, :], pr[:, k % 4, :], rec[:, k % 4:k % 4 + 1].to_broadcast([P, T]),
                                            ALU.mult).then_inc(*G("probs", k))

        @block.scalar
        def _(act):
            w = S.once(act, A)
            act.wait_ge(S.loaded, S.loads)
            act.wait_ge(*w(G, "va_pad"))
            with S.loop(act, A) as (i, w):
                act.wait_ge(*w(V, "norm_1", NT - 1, back=1))
                nc.scalar.activation(C.xb[:, :, :], C.y[:, bass.ds(i * NT, NT), :], ACT.Copy).then_inc(*A("xb"))
                act.wait_ge(*w(PE, "hT", NT - 1))
                nc.scalar.activation(hT[:, :], C.bank(7), ACT.Identity, bias=cols[:, 1:2],
                                     scale=cols[:, 0:1]).then_inc(*A("hT"))
                act.wait_ge(*w(PE, "K"))
                nc.scalar.activation(kT[:, :], C.bank(1), ACT.Identity, bias=cols[:, 3:4]).then_inc(*A("kT"))
                act.wait_ge(*w(PE, "V"))
                for j in range(2):
                    nc.scalar.activation(va[:, :, :, j, DV * j:DV * j + DV],
                                         C.bank(2).rearrange("p (t g e) -> p t g e", t=NT, g=4)[
                                             :, :, :, DV * j:DV * j + DV], ACT.Copy).then_inc(*A("va", j))
                act.wait_ge(*w(V, "qT"))
                for h in range(H // 2, H):
                    nc.scalar.activation(qm[:, h, :], qT[:, :], ACT.Copy,
                                         scale=headmask[:, h:h + 1]).then_inc(*A("qm", h))

                def exponent(k):
                    act.wait_ge(*w(V, "negmax", k))
                    if k >= 4:
                        act.wait_ge(*w(PE, "pT", k - 4))
                    nc.scalar.activation(pr[:, k % 4, :], C.bank(k % 3), ACT.Exp, bias=nm[:, k % 4:k % 4 + 1],
                                         scale=SCALE, accum_out=sm[:, k % 4:k % 4 + 1]).then_inc(*A("exp", k))

                def copy_probs(k):
                    act.wait_ge(*w(PE, "pT", k))
                    if k >= 4:
                        act.wait_ge(*w(PE, "O", (k - 4) // 2))
                    nc.scalar.activation(pT[:, k % 4, :, :], C.bank(3 + k % 2).rearrange("p (j n) -> p j n", j=NT),
                                         ACT.Copy).then_inc(*A("pT", k))

                for k in range(K + 3):
                    if k < K:
                        exponent(k)
                    if k >= 3:
                        copy_probs(k - 3)
                act.wait_ge(*w(PE, "O", K // 2 - 1))
                nc.scalar.activation(aoT[:, :], C.bank(5), ACT.Copy).then_inc(*A("aoT"))
                act.wait_ge(*w(PE, "ao"))
                act.wait_ge(stored, ST * (i + 1))
                nc.scalar.activation(ao[:, :, :, :], C.bank(6).rearrange("p (t h e) -> p t h e", t=NT, h=H),
                                     ACT.Copy).then_inc(*A("ao"))

        @block.vector
        def _(dve):
            w = S.once(dve, V)
            dve.wait_ge(S.loaded, S.loads)
            nc.vector.tensor_reduce(wvs[:, :], wv[:, :].rearrange("p (n g) -> p n g", g=GR), AX,
                                    ALU.add).then_inc(*V("wvs"))
            nc.vector.tensor_reduce(bvs[:, :], bv[:, :].rearrange("p (n g) -> p n g", g=GR), AX,
                                    ALU.add).then_inc(*V("bvs"))
            with S.loop(dve, V) as (i, w):
                dve.wait_ge(*w(A, "xb"))
                dve_norm(nc, C, S, w, C.xb, C.nb, "norm_1")
                dve.wait_ge(*w(PE, "Q"))
                nc.vector.tensor_scalar(qT[:, :], C.bank(0), cols[:, 2:3], None, ALU.add).then_inc(*V("qT"))
                dve.wait_ge(*w.own())
                for h in range(H // 2):
                    nc.vector.tensor_scalar(qm[:, h, :], qT[:, :], headmask[:, h:h + 1], None,
                                            ALU.mult).then_inc(*V("qm", h))

                def maximum(k):
                    dve.wait_ge(*w(PE, "S", k))
                    nc.vector.tensor_reduce(mx[:, k % 4:k % 4 + 1], C.bank(k % 3), AX, ALU.max).then_inc(*V("max", k))
                    dve.wait_ge(*w.own())
                    nc.vector.tensor_scalar(nm[:, k % 4:k % 4 + 1], mx[:, k % 4:k % 4 + 1], -SCALE, None,
                                            ALU.mult).then_inc(*V("negmax", k))

                def reciprocal(k):
                    dve.wait_ge(*w(A, "exp", k))
                    nc.vector.reciprocal(rec[:, k % 4:k % 4 + 1], sm[:, k % 4:k % 4 + 1]).then_inc(*V("rec", k))

                for k in range(K + 1):
                    if k < K:
                        maximum(k)
                    if k >= 1:
                        reciprocal(k - 1)

        @block.tensor
        def _(pe):
            w = S.once(pe, PE)
            pe.wait_ge(S.loaded, S.loads)
            pe.wait_ge(*w(V, "bvs"))
            with S.loop(pe, PE) as (i, w):
                pe.wait_ge(*w(V, "norm_1", NT - 1))
                pe_turn(nc, C, S, w, C.nb, 7, "hT")
                pe.wait_ge(*w(A, "hT"))
                pe.wait_ge(*w(A, "ao", back=1))
                nc.tensor.matmul(C.bank(0), wq[:, :], hT[:, :], start=True, stop=True).then_inc(*PE("Q"))
                nc.tensor.matmul(C.bank(1), wk[:, :], hT[:, :], start=True, stop=True).then_inc(*PE("K"))
                pe_rows(nc, C, w, 2, [hT], [wvs[:, :]], bvs[:, :]).then_inc(*PE("V"))
                pe.wait_ge(*w(A, "va", 1))

                def scores(k):
                    t, h = k // H, head_of[k]
                    if t == 0:
                        pe.wait_ge(*w(V if h < H // 2 else A, "qm", h))
                    if k >= 3:
                        pe.wait_ge(*w(A, "exp", k - 3))
                    nc.tensor.matmul(C.bank(k % 3), qm[:, h, t * P:(t + 1) * P], kT[:, :],
                                     start=True, stop=True).then_inc(*PE("S", k))

                def turn_probs(k):
                    pe.wait_ge(*w(G, "probs", k))
                    if k >= 2:
                        pe.wait_ge(*w(A, "pT", k - 2))
                    for s in range(NT):
                        last = nc.tensor.transpose(ps[:, 3 + k % 2, s * P:(s + 1) * P],
                                                   pr[:, k % 4, s * P:(s + 1) * P], C.ident[:, :])
                    last.then_inc(*PE("pT", k))

                def values(m):
                    t = 2 * m // H
                    pe.wait_ge(*w(A, "pT", 2 * m + 1))
                    for s in range(NT):
                        for k in (2 * m, 2 * m + 1):
                            g, j = head_of[k] // 2, head_of[k] % 2
                            last = nc.tensor.matmul(ps[32 * g:32 * g + 32, 5, t * P:(t + 1) * P], va[:, s, g, j, :],
                                                    pT[:, k % 4, s, :], start=(j == 0 and s == 0),
                                                    stop=(j == 1 and s == NT - 1))
                    last.then_inc(*PE("O", m))

                for k in range(K + 5):
                    if k < K:
                        scores(k)
                    if 3 <= k < K + 3:
                        turn_probs(k - 3)
                    if k >= 5 and k % 2 == 1 and (k - 5) // 2 < K // 2:
                        values((k - 5) // 2)
                pe.wait_ge(*w(A, "aoT"))
                for t in range(NT):
                    last = nc.tensor.transpose(ps[:, 6, t * P:(t + 1) * P], aoT[:, t * P:(t + 1) * P], C.ident[:, :])
                last.then_inc(*PE("ao"))
    S.close()



def stage_l2_attn(nc, C, plan):
    CH, N, KC, LV = 2, 64, 4, 7
    I = CH * P
    PREV, DIAG, END, TOTAL = 7, 8, 9, 10
    d = C.d
    S = Stage(nc, "l2attn", plan)
    PE, A, V, G = S.PE, S.ACT, S.DVE, S.POOL
    ps = C.ps
    w_in, w_out = S.sb("w_in", [P, 2 * I]), S.sb("w_out", [P, CH, D])
    w_dt, w_b, w_c = S.sb("w_dt", [P, CH, I]), S.sb("w_b", [P, CH, N]), S.sb("w_c", [P, CH, N])
    conv_w, cols, b_dt = S.sb("conv_w", [P, CH, KC]), S.sb("cols", [P, 2, CH]), S.sb("b_dt", [P, I])
    sums = S.sb("sums", [P, LV + 2, P])
    pairs = S.sb("pairs", [P, LV + 1, P])
    y0T, xi, zs = S.sb("y0T", [P, T]), S.sb("xi", [P, CH, KC - 1 + T]), S.sb("zs", [P, CH, T])
    cv, xcT = S.sb("cv", [P, CH, T]), S.sb("xcT", [P, CH, T])
    bT, cT, bk = S.sb("bT", [P, T]), S.sb("cT", [P, T]), S.sb("bk", [P, NT, N])
    ab, dt, dtx = S.sb("ab", [P, NT, I]), S.sb("dt", [P, NT, I]), S.sb("dtx", [P, NT, I])
    gs = S.sb("gs", [P, NT, P])
    dec, gm = S.sb("dec", [P, 3, 11, I]), S.sb("gm", [P, 2, LV + 1, P])
    rr, re = S.sb("rr", [P, 2, LV, I]), S.sb("re", [P, 2, I])
    tmp, yt, state, gT = S.sb("tmp", [P, 9, I]), S.sb("yt", [P, I]), S.sb("state", [P, I]), S.sb("gT", [P, CH, T])

    with nc.Block() as block:
        @block.sync
        def _(sp):
            S.load(sp, w_in[:, :], d["L2_attn_W_in"])
            for dst, n in ((w_out, "W_out"), (w_dt, "W_dt"), (w_b, "W_B"), (w_c, "W_C")):
                S.load(sp, dst[:, :, :], d["L2_attn_" + n].rearrange("(c k) n -> k c n", c=CH))
            S.load(sp, conv_w[:, :, :], d["L2_attn_conv_w"].rearrange("(c k) o n -> k c (o n)", c=CH))
            for c in range(CH):
                S.load(sp, cols[:, 0, c:c + 1], column(d["L2_attn_conv_b"][c * P:(c + 1) * P]))
                S.load(sp, cols[:, 1, c:c + 1], column(d["L2_attn_D"][c * P:(c + 1) * P]))
            S.load(sp, b_dt[:, :], row(d["L2_attn_b_dt"]).to_broadcast([P, I]))
            S.load(sp, sums[:, :, :], d["const_l2_sums"])
            S.load(sp, pairs[:, :, :], d["const_l2_pairs"])
            sp.wait_ge(S.loaded, S.loads)

        @block.gpsimd
        def _(pool):
            w = S.once(pool, G)
            nc.gpsimd.memset(xi[:, :, 0:KC - 1], 0.0).then_inc(*G("xi_pad"))
            nc.gpsimd.memset(bT[:, :], 0.0).then_inc(*G("bT_pad"))
            nc.gpsimd.memset(cT[:, :], 0.0).then_inc(*G("cT_pad"))
            nc.gpsimd.memset(state[:, :], 0.0).then_inc(*G("state_pad"))
            nc.gpsimd.memset(dec[:, :, DIAG, :], 1.0).then_inc(*G("diag_ones"))
            pool.wait_ge(S.loaded, S.loads)
            with S.loop(pool, G) as (i, w):
                for t in range(NT):
                    pool.wait_ge(*w(A, "gs"))
                    if t >= 2:
                        pool.wait_ge(*w(PE, "Y", t - 2))
                    nc.gpsimd.tensor_tensor(gm[:, t % 2], gs[:, t, :].unsqueeze(1).to_broadcast([P, LV + 1, P]),
                                            pairs[:, :, :], ALU.mult).then_inc(*G("gm", t))

        @block.scalar
        def _(act):
            w = S.once(act, A)
            act.wait_ge(S.loaded, S.loads)
            act.wait_ge(*w(G, "diag_ones"))
            with S.loop(act, A) as (i, w):
                act.wait_ge(*w(PE, "y0T", NT - 1, back=1))
                nc.scalar.activation(C.xb[:, :, :], C.y[:, bass.ds(i * NT, NT), :], ACT.Copy).then_inc(*A("xb"))
                act.wait_ge(*w(PE, "y0T", NT - 1))
                nc.scalar.activation(y0T[:, :], C.bank(0), ACT.Copy).then_inc(*A("y0T"))
                for c in range(CH):
                    act.wait_ge(*w(PE, "in", c))
                    nc.scalar.activation(xi[:, c, KC - 1:], C.bank(1 + c), ACT.Copy).then_inc(*A("xi", c))
                for c in range(CH):
                    act.wait_ge(*w(PE, "in", CH + c))
                    nc.scalar.activation(zs[:, c, :], C.bank(3 + c), ACT.Silu).then_inc(*A("zs", c))
                for c in range(CH):
                    act.wait_ge(*w(V, "conv", c))
                    nc.scalar.activation(xcT[:, c, :], cv[:, c, :], ACT.Silu,
                                         bias=cols[:, 0, c:c + 1]).then_inc(*A("xcT", c))
                act.wait_ge(*w(PE, "B"))
                nc.scalar.activation(bT[0:N, :], C.bank(5, N), ACT.Copy).then_inc(*A("bT"))
                act.wait_ge(*w(PE, "C"))
                nc.scalar.activation(cT[0:N, :], C.bank(6, N), ACT.Copy).then_inc(*A("cT"))
                act.wait_ge(*w(PE, "Bk"))
                nc.scalar.activation(bk[:, :, :], ps[:, 7, 0:NT * N].rearrange("p (t n) -> p t n", t=NT),
                                     ACT.Copy).then_inc(*A("bk"))
                for b in range(2):
                    act.wait_ge(*w(PE, "dt", b))
                    nc.scalar.activation(ab[:, 2 * b:2 * b + 2, :], C.bank(1 + b).rearrange("p (t n) -> p t n", t=2),
                                         ACT.Abs).then_inc(*A("abs", b))
                act.wait_ge(*w.own())
                nc.scalar.activation(ab[:, :, :], ab[:, :, :], ACT.Exp, scale=-1.0).then_inc(*A("exp"))
                act.wait_ge(*w.own())
                nc.scalar.activation(ab[:, :, :], ab[:, :, :], ACT.Ln, bias=C.ones[:, 0:1]).then_inc(*A("ln"))
                act.wait_ge(*w(PE, "G"))
                nc.scalar.activation(gs[:, :, :], C.bank(0).rearrange("p (t n) -> p t n", t=NT),
                                     ACT.Copy).then_inc(*A("gs"))
                for t in range(NT):
                    if t >= 3:
                        act.wait_ge(*w(V, "tmp", t - 3))
                        act.wait_ge(*w(V, "state_decayed", t - 3))
                    for b in range(5):
                        act.wait_ge(*w(PE, "decay", t, b))
                        slots = dec[:, t % 3, 2 * b:2 * b + 2, :] if b < 4 else dec[:, t % 3, END:TOTAL + 1, :]
                        nc.scalar.activation(slots, C.bank(5 + b % 2).rearrange("p (j n) -> p j n", j=2),
                                             ACT.Exp, scale=-1.0).then_inc(*A("dec", t, b))

        @block.vector
        def _(dve):
            w = S.once(dve, V)
            dve.wait_ge(S.loaded, S.loads)
            with S.loop(dve, V) as (i, w):
                for c in range(CH):
                    dve.wait_ge(*w(A, "xi", c))
                    nc.vector.tensor_scalar(cv[:, c, :], xi[:, c, 0:T], conv_w[:, c, 0:1], None,
                                            ALU.mult).then_inc(*V("tap", c, 0))
                    for k in range(1, KC):
                        dve.wait_ge(*w.own())
                        last = nc.vector.scalar_tensor_tensor(out=cv[:, c, :], in0=xi[:, c, k:k + T],
                                                              scalar=conv_w[:, c, k:k + 1], in1=cv[:, c, :],
                                                              op0=ALU.mult, op1=ALU.add)
                        last.then_inc(*(V("conv", c) if k == KC - 1 else V("tap", c, k)))
                dve.wait_ge(*w(A, "ln"))
                for b in range(2):
                    nc.vector.scalar_tensor_tensor(out=dt[:, 2 * b:2 * b + 2, :],
                                                   in0=C.bank(1 + b).rearrange("p (t n) -> p t n", t=2), scalar=0.0,
                                                   in1=ab[:, 2 * b:2 * b + 2, :], op0=ALU.max,
                                                   op1=ALU.add).then_inc(*V("dt", b))
                dve.wait_ge(*w.own())
                for b in range(2):
                    dve.wait_ge(*w(PE, "xc", b))
                    nc.vector.tensor_tensor(dtx[:, 2 * b:2 * b + 2, :], dt[:, 2 * b:2 * b + 2, :],
                                            C.bank(3 + b).rearrange("p (t n) -> p t n", t=2),
                                            ALU.mult).then_inc(*V("dtx", b))
                dve.wait_ge(*w(PE, "prev", NT - 1, back=1))
                nc.vector.memset(state[0:N, :], 0.0).then_inc(*V("state_zero"))

                def sources(t):
                    dve.wait_ge(*w(A, "dec", t, 4))
                    if t >= 2:
                        dve.wait_ge(*w(PE, "Y", t - 2))
                    nc.vector.tensor_tensor(rr[:, t % 2], dec[:, t % 3, 0:LV, :], dtx[:, t, :].unsqueeze(1).to_broadcast(
                        [P, LV, I]), ALU.mult).then_inc(*V("rr", t))
                    nc.vector.tensor_tensor(re[:, t % 2, :], dec[:, t % 3, END, :], dtx[:, t, :],
                                            ALU.mult).then_inc(*V("re", t))

                def gather(t):
                    dve.wait_ge(*w(PE, "Y", t))
                    for b in range(5):
                        n = min(2, 9 - 2 * b)
                        last = nc.vector.tensor_tensor(tmp[:, 2 * b:2 * b + n, :], dec[:, t % 3, 2 * b:2 * b + n, :],
                                                       ps[:, b, 0:n * I].rearrange("p (j n) -> p j n", j=n), ALU.mult)
                        last.then_inc(*(V("tmp", t) if b == 4 else V("tmp_part", t, b)))
                    nc.vector.tensor_tensor(state[0:N, :], state[0:N, :], dec[0:N, t % 3, TOTAL, :],
                                            ALU.mult).then_inc(*V("state_decayed", t))
                    dve.wait_ge(*w.own())
                    dve.wait_ge(*w(PE, "Y", t))
                    nc.vector.tensor_tensor(state[0:N, :], state[0:N, :], ps[0:N, 4, I:2 * I],
                                            ALU.add).then_inc(*V("state", t))
                    if t >= 1:
                        dve.wait_ge(*w(PE, "yT", t - 1))
                    nc.vector.tensor_reduce(yt[:, :], tmp[:, :, :].rearrange("p l n -> p n l"), AX,
                                            ALU.add).then_inc(*V("yt", t))

                def skip(t):
                    dve.wait_ge(*w(PE, "yT", t))
                    for c in range(CH):
                        nc.vector.scalar_tensor_tensor(out=gT[:, c, t * P:(t + 1) * P], in0=xcT[:, c, t * P:(t + 1) * P],
                                                       scalar=cols[:, 1, c:c + 1], in1=ps[:, 7, c * P:(c + 1) * P],
                                                       op0=ALU.mult, op1=ALU.add).then_inc(*V("gT", t, c))

                sources(0)
                for t in range(NT):
                    if t + 1 < NT:
                        sources(t + 1)
                    gather(t)
                    if t >= 1:
                        skip(t - 1)
                skip(NT - 1)
                dve.wait_ge(*w.own())
                nc.vector.tensor_tensor(gT[:, :, :], gT[:, :, :], zs[:, :, :], ALU.mult).then_inc(*V("g"))
                dve.wait_ge(*w(PE, "out"))
                nc.vector.tensor_copy(C.y[:, bass.ds(i * NT, NT), :],
                                      C.bank(5).rearrange("p (t e) -> p t e", t=NT)).then_inc(*V("y"))

        @block.tensor
        def _(pe):
            w = S.once(pe, PE)
            pe.wait_ge(S.loaded, S.loads)
            with S.loop(pe, PE) as (i, w):
                pe.wait_ge(*w(A, "xb"))
                pe.wait_ge(*w(V, "g", back=1))
                pe_turn(nc, C, S, w, C.xb, 0, "y0T")
                pe.wait_ge(*w(A, "y0T"))
                for c in range(2 * CH):
                    nc.tensor.matmul(C.bank(1 + c), w_in[:, c * P:(c + 1) * P], y0T[:, :], start=True,
                                     stop=True).then_inc(*PE("in", c))
                pe.wait_ge(*w(A, "xcT", 1))
                pe.wait_ge(*w(A, "zs", 1))
                for bank, wt, name in ((5, w_b, "B"), (6, w_c, "C")):
                    pe.wait_ge(*w(V, "y", back=1))
                    for c in range(CH):
                        last = nc.tensor.matmul(C.bank(bank, N), wt[:, c, :], xcT[:, c, :], start=(c == 0),
                                                stop=(c == CH - 1))
                    last.then_inc(*PE(name))
                for t in range(NT):
                    for c in range(CH):
                        last = nc.tensor.matmul(ps[:, 7, t * N:(t + 1) * N], xcT[:, c, t * P:(t + 1) * P],
                                                w_b[:, c, :], start=(c == 0), stop=(c == CH - 1))
                last.then_inc(*PE("Bk"))
                for b in range(2):
                    for j in range(2):
                        o, t = ps[:, 1 + b, j * I:(j + 1) * I], 2 * b + j
                        for c in range(CH):
                            nc.tensor.matmul(o, xcT[:, c, t * P:(t + 1) * P], w_dt[:, c, :], start=(c == 0), stop=False)
                        last = nc.tensor.matmul(o, C.ident[:, :], b_dt[:, :], start=False, stop=True)
                    last.then_inc(*PE("dt", b))
                for b in range(2):
                    for j in range(2):
                        t = 2 * b + j
                        for c in range(CH):
                            last = nc.tensor.transpose(ps[:, 3 + b, j * I + c * P:j * I + (c + 1) * P],
                                                       xcT[:, c, t * P:(t + 1) * P], C.ident[:, :])
                    last.then_inc(*PE("xc", b))
                pe.wait_ge(*w(A, "bk"))
                pe.wait_ge(*w(A, "bT"))
                for t in range(NT):
                    last = nc.tensor.matmul(ps[:, 0, t * P:(t + 1) * P], bT[:, t * P:(t + 1) * P],
                                            cT[:, t * P:(t + 1) * P], start=True, stop=True)
                last.then_inc(*PE("G"))
                pe.wait_ge(*w(V, "dtx", 1))
                pe.wait_ge(*w(A, "gs"))

                def decays(t):
                    for b in range(5):
                        if b >= 2:
                            pe.wait_ge(*w(A, "dec", t, b - 2))
                        elif t >= 1:
                            pe.wait_ge(*w(A, "dec", t - 1, 4 - b))
                        for j in range(2):
                            l = 2 * b + j
                            tokens = C.ones[:, :] if l == LV + 2 else sums[:, l, :]
                            last = nc.tensor.matmul(ps[:, 5 + b % 2, j * I:(j + 1) * I], tokens, dt[:, t, :],
                                                    start=True, stop=True)
                        last.then_inc(*PE("decay", t, b))

                decays(0)
                decays(1)
                for t in range(NT):
                    if t >= 1:
                        pe.wait_ge(*w(V, "tmp", t - 1))
                    pe.wait_ge(*w(V, "re", t))
                    pe.wait_ge(*w(G, "gm", t))
                    for l in range(LV):
                        nc.tensor.matmul(ps[:, l // 2, l % 2 * I:(l % 2 + 1) * I], gm[:, t % 2, l, :], rr[:, t % 2, l, :],
                                         start=True, stop=True)
                    pe.wait_ge(*w(V, "state" if t else "state_zero", *([t - 1] if t else [])))
                    nc.tensor.matmul(ps[:, 3, I:2 * I], cT[:, t * P:(t + 1) * P], state[:, :], start=True,
                                     stop=True).then_inc(*PE("prev", t))
                    nc.tensor.matmul(ps[:, 4, 0:I], gm[:, t % 2, LV, :], dtx[:, t, :], start=True,
                                     stop=True).then_inc(*PE("Y_diagonal", t))
                    nc.tensor.matmul(ps[0:N, 4, I:2 * I], bk[:, t, :], re[:, t % 2, :], start=True,
                                     stop=True).then_inc(*PE("Y", t))
                    if t + 2 < NT:
                        decays(t + 2)
                    pe.wait_ge(*w(V, "yt", t))
                    if t >= 1:
                        pe.wait_ge(*w(V, "gT", t - 1, 1))
                    for c in range(CH):
                        last = nc.tensor.transpose(ps[:, 7, c * P:(c + 1) * P], yt[:, c * P:(c + 1) * P], C.ident[:, :])
                    last.then_inc(*PE("yT", t))
                pe.wait_ge(*w(V, "g"))
                pe_rows(nc, C, w, 5, [gT[:, c, :] for c in range(CH)],
                        [w_out[:, c, :] for c in range(CH)]).then_inc(*PE("out"))
    S.close()



def stage_l2_ffn(nc, C, plan):
    EX, F, CH, TOP = 8, 2 * D, 2, 2
    d = C.d
    S = Stage(nc, "l2ffn", plan)
    PE, A, V, G = S.PE, S.ACT, S.DVE, S.POOL
    ps = C.ps
    wg, bg = S.sb("wg", [P, EX]), S.sb("bg", [P, EX])
    w1, b1 = S.sb("w1", [P, EX, F]), S.sb("b1", [P, EX, CH])
    w2, b2 = S.sb("w2", [P, EX, CH, D]), S.sb("b2", [EX, D])
    gains, before = S.sb("gains", [P, 2, D]), S.sb("before", [P, EX, EX])
    hT = S.sb("hT", [P, T])
    lg, top, ex, s = S.sb("lg", [P, NT, EX]), S.sb("top", [P, NT]), S.sb("ex", [P, NT, EX]), S.sb("s", [P, NT])
    gt, eq = S.sb("gt", [P, NT, EX, EX]), S.sb("eq", [P, NT, EX, EX])
    rank, coef, coefT = S.sb("rank", [P, NT, EX]), S.sb("coef", [P, NT, EX]), S.sb("coefT", [EX, T])
    hid, acc = S.sb("hid", [P, 2, CH, T]), S.sb("acc", [P, NT, D])

    with nc.Block() as block:
        @block.sync
        def _(sp):
            S.load(sp, wg[:, :], d["L2_ffn_Wg"])
            S.load(sp, bg[:, :], row(d["L2_ffn_bg"]).to_broadcast([P, EX]))
            S.load(sp, w1[:, :, :], d["L2_ffn_W1"].rearrange("e k n -> k e n"))
            S.load(sp, b1[:, :, :], d["L2_ffn_b1_turned"])
            S.load(sp, w2[:, :, :, :], d["L2_ffn_W2"].rearrange("e (c k) n -> k e c n", c=CH))
            S.load(sp, b2[:, :], d["L2_ffn_b2"])
            S.load(sp, gains[:, 0, :], row(d["L2_ffn_gamma"]).to_broadcast([P, D]))
            S.load(sp, gains[:, 1, :], row(d["L2_ffn_beta"]).to_broadcast([P, D]))
            S.load(sp, before[:, :, :], d["const_before"])
            sp.wait_ge(S.loaded, S.loads)

        @block.gpsimd
        def _(pool):
            S.once(pool, G)
            with S.loop(pool, G) as (i, w):
                pool_norm(nc, C, S, w, "norm_1")

        @block.scalar
        def _(act):
            S.once(act, A)
            act.wait_ge(S.loaded, S.loads)
            with S.loop(act, A) as (i, w):
                act.wait_ge(*w(V, "y", back=1))
                nc.scalar.activation(C.xb[:, :, :], C.y[:, bass.ds(i * NT, NT), :], ACT.Copy).then_inc(*A("xb"))
                act.wait_ge(*w(PE, "hT", NT - 1))
                nc.scalar.activation(hT[:, :], C.bank(0), ACT.Copy).then_inc(*A("hT"))
                act.wait_ge(*w(PE, "logits"))
                nc.scalar.activation(lg[:, :, :], ps[:, 1, 0:NT * EX].rearrange("p (t e) -> p t e", t=NT),
                                     ACT.Copy).then_inc(*A("logits"))
                act.wait_ge(*w(V, "centred"))
                nc.scalar.activation(ex[:, :, :], ex[:, :, :], ACT.Exp).then_inc(*A("exp"))
                for e in range(EX):
                    act.wait_ge(*w(PE, "up", e, 0))
                    if e >= 2:
                        act.wait_ge(*w(PE, "down", e - 2))
                    nc.scalar.activation(hid[:, e % 2, 0, :], C.bank(2 + e % 2 * 2), ACT.Relu,
                                         bias=b1[:, e, 0:1]).then_inc(*A("hid", e))
                    if e == 1:
                        act.wait_ge(*w(PE, "coefT"))
                        nc.scalar.activation(coefT[:, :], C.bank(0, EX), ACT.Copy).then_inc(*A("coefT"))

        @block.vector
        def _(dve):
            S.once(dve, V)
            dve.wait_ge(S.loaded, S.loads)
            with S.loop(dve, V) as (i, w):
                dve.wait_ge(*w(A, "xb"))
                dve.wait_ge(*w(A, "logits"))
                nc.vector.tensor_reduce(top[:, :], lg[:, :, :], AX, ALU.max).then_inc(*V("top"))
                dve.wait_ge(*w.own())
                nc.vector.tensor_tensor(ex[:, :, :], lg[:, :, :], top[:, :].unsqueeze(2).to_broadcast([P, NT, EX]),
                                        ALU.subtract).then_inc(*V("centred"))
                for t in range(NT):
                    mine = lg[:, t, :].unsqueeze(2).to_broadcast([P, EX, EX])
                    other = lg[:, t, :].unsqueeze(1).to_broadcast([P, EX, EX])
                    nc.vector.tensor_tensor(gt[:, t], other, mine, ALU.is_gt).then_inc(*V("gt", t))
                    nc.vector.tensor_tensor(eq[:, t], other, mine, ALU.is_equal).then_inc(*V("eq", t))
                dve.wait_ge(*w.own())
                nc.vector.tensor_tensor(eq[:, :, :, :], eq[:, :, :, :], before[:, :, :].unsqueeze(1).to_broadcast(
                    [P, NT, EX, EX]), ALU.mult).then_inc(*V("eq_before"))
                dve.wait_ge(*w.own())
                nc.vector.tensor_tensor(gt[:, :, :, :], gt[:, :, :, :], eq[:, :, :, :], ALU.add).then_inc(*V("ahead"))
                dve.wait_ge(*w.own())
                nc.vector.tensor_reduce(rank[:, :, :], gt[:, :, :, :], AX, ALU.add).then_inc(*V("rank"))
                dve.wait_ge(*w.own())
                dve.wait_ge(*w(A, "exp"))
                nc.vector.scalar_tensor_tensor(out=coef[:, :, :], in0=rank[:, :, :], scalar=float(TOP),
                                               in1=ex[:, :, :], op0=ALU.is_lt, op1=ALU.mult).then_inc(*V("chosen"))
                dve.wait_ge(*w.own())
                nc.vector.tensor_reduce(s[:, :], coef[:, :, :], AX, ALU.add).then_inc(*V("sum"))
                dve.wait_ge(*w.own())
                nc.vector.reciprocal(s[:, :], s[:, :]).then_inc(*V("rec"))
                dve.wait_ge(*w.own())
                nc.vector.tensor_tensor(coef[:, :, :], coef[:, :, :], s[:, :].unsqueeze(2).to_broadcast([P, NT, EX]),
                                        ALU.mult).then_inc(*V("coef"))

                def hidden(e):
                    dve.wait_ge(*w(PE, "up", e, 1))
                    if e >= 2:
                        dve.wait_ge(*w(PE, "down", e - 2))
                    nc.vector.tensor_scalar(hid[:, e % 2, 1, :], C.bank(3 + e % 2 * 2), b1[:, e, 1:2], 0.0, ALU.add,
                                            ALU.max).then_inc(*V("hid", e))

                def weigh(e):
                    dve.wait_ge(*w(PE, "down", e))
                    dve.wait_ge(*w.own())
                    for t in range(NT):
                        nc.vector.scalar_tensor_tensor(out=acc[:, t, :], in0=ps[:, 6 + e % 2, t * P:(t + 1) * P],
                                                       scalar=coef[:, t, e:e + 1], in1=acc[:, t, :], op0=ALU.mult,
                                                       op1=ALU.add).then_inc(*V("acc", e, t))

                hidden(0)
                hidden(1)
                dve.wait_ge(*w(PE, "bias"))
                nc.vector.tensor_tensor(acc[:, :, :], C.xb[:, :, :], C.bank(1).rearrange("p (t e) -> p t e", t=NT),
                                        ALU.add).then_inc(*V("acc"))
                for e in range(EX):
                    if e >= 2:
                        hidden(e)
                    weigh(e)
                dve.wait_ge(*w.own())
                dve_norm(nc, C, S, w, acc, C.nb, "norm_1")
                dve.wait_ge(*w.own())
                nc.vector.tensor_tensor(C.nb[:, :, :], C.nb[:, :, :], gains[:, 0, :].unsqueeze(1).to_broadcast(
                    [P, NT, D]), ALU.mult).then_inc(*V("gain"))
                dve.wait_ge(*w.own())
                nc.vector.tensor_tensor(C.y[:, bass.ds(i * NT, NT), :], C.nb[:, :, :], gains[:, 1, :].unsqueeze(1).to_broadcast(
                    [P, NT, D]), ALU.add).then_inc(*V("y"))

        @block.tensor
        def _(pe):
            S.once(pe, PE)
            pe.wait_ge(S.loaded, S.loads)
            with S.loop(pe, PE) as (i, w):
                pe.wait_ge(*w(A, "xb"))
                pe_turn(nc, C, S, w, C.xb, 0, "hT")
                pe.wait_ge(*w(A, "hT"))
                for t in range(NT):
                    o = ps[:, 1, t * EX:(t + 1) * EX]
                    nc.tensor.matmul(o, hT[:, t * P:(t + 1) * P], wg[:, :], start=True, stop=False)
                    last = nc.tensor.matmul(o, C.ident[:, :], bg[:, :], start=False, stop=True)
                last.then_inc(*PE("logits"))

                def up(e):
                    if e >= 2:
                        pe.wait_ge(*w(A, "hid", e - 2))
                        pe.wait_ge(*w(V, "hid", e - 2))
                    for c in range(CH):
                        nc.tensor.matmul(C.bank(2 + e % 2 * 2 + c), w1[:, e, c * P:(c + 1) * P], hT[:, :], start=True,
                                         stop=True).then_inc(*PE("up", e, c))

                def down(e):
                    pe.wait_ge(*w(A, "hid", e))
                    pe.wait_ge(*w(V, "hid", e))
                    if e >= 2:
                        pe.wait_ge(*w(V, "acc", e - 2, NT - 1))
                    pe_rows(nc, C, w, 6 + e % 2, [hid[:, e % 2, c, :] for c in range(CH)],
                            [w2[:, e, c, :] for c in range(CH)]).then_inc(*PE("down", e))

                up(0)
                up(1)
                pe.wait_ge(*w(V, "coef"))
                for t in range(NT):
                    last = nc.tensor.transpose(ps[0:EX, 0, t * P:(t + 1) * P], coef[:, t, :], C.ident[:, :])
                last.then_inc(*PE("coefT"))
                pe.wait_ge(*w(A, "coefT"))
                for t in range(NT):
                    last = nc.tensor.matmul(ps[:, 1, t * P:(t + 1) * P], coefT[:, t * P:(t + 1) * P], b2[:, :],
                                            start=True, stop=True)
                last.then_inc(*PE("bias"))
                for e in range(EX):
                    down(e)
                    if e + 2 < EX:
                        up(e + 2)
    S.close()



def stage_l3_attn(nc, C, plan):
    H, R, E = 16, 16, 8
    HALF_SCALE = float(np.float32(0.5) / np.sqrt(np.float32(E)))
    d = C.d
    S = Stage(nc, "l3attn", plan)
    PE, A, V, G = S.PE, S.ACT, S.DVE, S.POOL
    ps = C.ps
    wqk, wv = S.sb("wqk", [P, 4, D]), S.sb("wv", [P, D])
    wr, wrm = S.sb("wr", [P, 2, R]), S.sb("wrm", [P, 2, H, R])
    wgt, gb, dec = S.sb("wgt", [P, H * R]), S.sb("gb", [P, H]), S.sb("dec", [P, H])
    wrep = S.sb("wrep", [P, 2, H, P])
    wo, ob = S.sb("wo", [P, H, D]), S.sb("ob", [P, D])
    gains, headmask, rope = S.sb("gains", [P, 2, D]), S.sb("headmask", [P, H]), S.sb("rope", [P, 2, T])
    rrep = S.sb("rrep", [P, 2, H, P])
    hT = S.sb("hT", [P, T])
    rot, tm = S.sb("rot", [P, 2, T]), S.sb("tm", [P, 2, T])
    th, u, st = S.sb("th", [P, 2, T]), S.sb("u", [P, 2, T]), S.sb("st", [P, 2, T])
    yv, hres = S.sb("yv", [P, 2, T]), S.sb("hres", [P, NT, D])

    with nc.Block() as block:
        @block.sync
        def _(sp):
            S.load(sp, wqk[:, :, :], d["L3_attn_qk_turned"])
            S.load(sp, wv[:, :], d["L3_attn_v_turned"])
            S.load(sp, wr[:, :, :], d["L3_attn_ranks"])
            S.load(sp, wgt[:, :], d["L3_attn_g_turned"])
            S.load(sp, gb[:, :], d["L3_attn_g_b_spread"])
            S.load(sp, dec[:, :], d["L3_attn_decay_spread"])
            for r in range(R):
                S.load(sp, wo[r * E:(r + 1) * E, :, :], d["L3_attn_out_turned"].rearrange("(h e) n -> e h n", h=H))
            S.load(sp, ob[:, :], row(d["L3_attn_out_b"]).to_broadcast([P, D]))
            S.load(sp, gains[:, 0, :], row(d["L3_attn_ln_g"]).to_broadcast([P, D]))
            S.load(sp, gains[:, 1, :], row(d["L3_attn_ln_b"]).to_broadcast([P, D]))
            S.load(sp, headmask[:, :], d["const_head_of_16"])
            S.load(sp, rope[:, :, :], d["const_l3_rope"])
            sp.wait_ge(S.loaded, S.loads)

        @block.gpsimd
        def _(pool):
            S.once(pool, G)
            with S.loop(pool, G) as (i, w):
                pool_norm(nc, C, S, w, "norm_1")

        @block.scalar
        def _(act):
            w = S.once(act, A)
            act.wait_ge(S.loaded, S.loads)
            nc.scalar.activation(dec[:, :], dec[:, :], ACT.Tanh, scale=0.5).then_inc(*A("dec"))
            nc.scalar.activation(gb[:, :], gb[:, :], ACT.Copy, scale=0.5).then_inc(*A("half_gb"))
            act.wait_ge(*w.own())
            with S.loop(act, A) as (i, w):
                act.wait_ge(*w(V, "y", back=1))
                nc.scalar.activation(C.xb[:, :, :], C.y[:, bass.ds(i * NT, NT), :], ACT.Copy).then_inc(*A("xb"))
                act.wait_ge(*w(PE, "hT", NT - 1))
                nc.scalar.activation(hT[:, :], C.bank(7), ACT.Copy).then_inc(*A("hT"))
                for h in range(H):
                    act.wait_ge(*w(PE, "g", h))
                    if h >= 2:
                        act.wait_ge(*w(V, "gk", h - 2))
                    nc.scalar.activation(th[:, h % 2, :], C.bank(2), ACT.Tanh, bias=gb[:, h:h + 1],
                                         scale=0.5).then_inc(*A("th", h))

        @block.vector
        def _(dve):
            w = S.once(dve, V)
            dve.wait_ge(S.loaded, S.loads)
            dve.wait_ge(*w(A, "dec"))
            nc.vector.tensor_scalar(dec[:, :], dec[:, :], 0.5, 0.5, ALU.mult, ALU.add).then_inc(*V("dec"))
            for x in range(2):
                for j in range(H):
                    nc.vector.tensor_scalar(wrm[:, x, j, :], wr[:, x, :], headmask[:, j:j + 1], None,
                                            ALU.mult).then_inc(*V("wrm", x, j))
            dve.wait_ge(*w.own())
            for x in range(2):
                for j in range(H):
                    nc.vector.tensor_copy(rrep[:, x, j, :].rearrange("p (r e) -> p r e", r=R),
                                          wrm[:, x, j, :].unsqueeze(2).to_broadcast([P, R, E])).then_inc(
                                              *V("rrep", x, j))
            for h in range(H):
                nc.vector.tensor_copy(wrep[:, 0, h, :].rearrange("p (r e) -> p r e", r=R),
                                      wgt[:, h * R:(h + 1) * R].unsqueeze(2).to_broadcast([P, R, E])).then_inc(
                                          *V("wrep", 0, h))
                nc.vector.tensor_copy(wrep[:, 1, h, :].rearrange("p (r e) -> p r e", r=R),
                                      wv[:, h * E:(h + 1) * E].unsqueeze(1).to_broadcast([P, R, E])).then_inc(
                                          *V("wrep", 1, h))
            with S.loop(dve, V) as (i, w):
                dve.wait_ge(*w(A, "xb"))
                for x in range(2):
                    dve.wait_ge(*w(PE, "qk", x))
                    dve.wait_ge(*w.own())
                    nc.vector.tensor_tensor(tm[:, 0, :], C.bank(2 * x), rope[:, 0, :], ALU.mult).then_inc(*V("cos", x))
                    nc.vector.tensor_tensor(tm[:, 1, :], C.bank(2 * x + 1), rope[:, 1, :],
                                            ALU.mult).then_inc(*V("sin", x))
                    dve.wait_ge(*w.own())
                    nc.vector.tensor_tensor(rot[:, x, :], tm[:, 0, :], tm[:, 1, :], ALU.add).then_inc(*V("rot", x))
                for h in range(H):
                    b = h % 2
                    dve.wait_ge(*w(A, "th", h))
                    dve.wait_ge(*w(PE, "k", h))
                    nc.vector.scalar_tensor_tensor(out=u[:, b, :], in0=th[:, b, :], scalar=1.0, in1=C.bank(b),
                                                   op0=ALU.add, op1=ALU.mult).then_inc(*V("gk", h))
                    dve.wait_ge(*w.own())
                    dve.wait_ge(*w(PE, "v", h))
                    nc.vector.scalar_tensor_tensor(out=u[:, b, :], in0=u[:, b, :], scalar=HALF_SCALE,
                                                   in1=C.bank(3 + b), op0=ALU.mult, op1=ALU.mult).then_inc(
                                                       *V("gkv", h))
                    dve.wait_ge(*w.own())
                    nc.vector.tensor_tensor_scan(st[:, b, :], dec[:, h:h + 1].to_broadcast([P, T]), u[:, b, :], 0.0,
                                                 ALU.mult, ALU.add).then_inc(*V("memory", h))
                    dve.wait_ge(*w.own())
                    dve.wait_ge(*w(PE, "q", h))
                    if h >= 2:
                        dve.wait_ge(*w(PE, "y", h - 2))
                    nc.vector.tensor_tensor(yv[:, b, :], st[:, b, :], C.bank(5 + b), ALU.mult).then_inc(*V("yv", h))
                dve.wait_ge(*w(PE, "out"))
                nc.vector.tensor_tensor(hres[:, :, :], C.xb[:, :, :], C.bank(7).rearrange("p (t e) -> p t e", t=NT),
                                        ALU.add).then_inc(*V("hres"))
                dve.wait_ge(*w.own())
                dve_norm(nc, C, S, w, hres, C.nb, "norm_1")
                dve.wait_ge(*w.own())
                nc.vector.tensor_tensor(C.nb[:, :, :], C.nb[:, :, :], gains[:, 0, :].unsqueeze(1).to_broadcast(
                    [P, NT, D]), ALU.mult).then_inc(*V("gain"))
                dve.wait_ge(*w.own())
                nc.vector.tensor_tensor(C.y[:, bass.ds(i * NT, NT), :], C.nb[:, :, :], gains[:, 1, :].unsqueeze(1).to_broadcast(
                    [P, NT, D]), ALU.add).then_inc(*V("y"))

        @block.tensor
        def _(pe):
            w = S.once(pe, PE)
            pe.wait_ge(S.loaded, S.loads)
            pe.wait_ge(*w(V, "wrep", 1, H - 1))
            with S.loop(pe, PE) as (i, w):
                pe.wait_ge(*w(A, "xb"))
                pe.wait_ge(*w(V, "hres", back=1))
                pe_turn(nc, C, S, w, C.xb, 7, "hT")
                pe.wait_ge(*w(A, "hT"))
                for x in range(2):
                    for j in range(2):
                        last = nc.tensor.matmul(C.bank(2 * x + j), wqk[:, 2 * x + j, :], hT[:, :], start=True,
                                                stop=True)
                    last.then_inc(*PE("qk", x))

                def head(h):
                    b = h % 2
                    if h >= 1:
                        pe.wait_ge(*w(A, "th", h - 1))
                    if h == 0:
                        pe.wait_ge(*w(V, "rot", 1))
                    nc.tensor.matmul(C.bank(2), wrep[:, 0, h, :], hT[:, :], start=True, stop=True).then_inc(*PE("g", h))
                    if h >= 2:
                        pe.wait_ge(*w(V, "gk", h - 2))
                    nc.tensor.matmul(C.bank(b), rrep[:, 1, h, :], rot[:, 1, :], start=True,
                                     stop=True).then_inc(*PE("k", h))
                    if h >= 2:
                        pe.wait_ge(*w(V, "gkv", h - 2))
                    nc.tensor.matmul(C.bank(3 + b), wrep[:, 1, h, :], hT[:, :], start=True, stop=True).then_inc(
                        *PE("v", h))
                    if h >= 2:
                        pe.wait_ge(*w(V, "yv", h - 2))
                    nc.tensor.matmul(C.bank(5 + b), rrep[:, 0, h, :], rot[:, 0, :], start=True,
                                     stop=True).then_inc(*PE("q", h))

                def add_out(h):
                    pe.wait_ge(*w(V, "yv", h))
                    for t in range(NT):
                        last = nc.tensor.matmul(ps[:, 7, t * P:(t + 1) * P], yv[:, h % 2, t * P:(t + 1) * P],
                                                wo[:, h, :], start=(h == 0 and t == 0), stop=False,
                                                skip_group_check=True)
                    last.then_inc(*PE("y", h))

                for h in range(H + 1):
                    if h < H:
                        head(h)
                    if h >= 1:
                        add_out(h - 1)
                for t in range(NT):
                    last = nc.tensor.matmul(ps[:, 7, t * P:(t + 1) * P], C.ident[:, :], ob[:, :], start=False,
                                            stop=True, skip_group_check=True)
                last.then_inc(*PE("out"))
    S.close()



def stage_l3_ffn(nc, C, plan):
    I, BL = 352, 16
    CH = -(-I // P)
    rows_of = [min(P, I - c * P) for c in range(CH)]
    d = C.d
    S = Stage(nc, "l3ffn", plan)
    PE, A, V, G = S.PE, S.ACT, S.DVE, S.POOL
    ps = C.ps
    wgu, wd = S.sb("wgu", [P, 2, CH, D]), S.sb("wd", [P, I])
    wguT, wdT = S.sb("wguT", [P, 2, I]), S.sb("wdT", [P, CH, D])
    xqT, sg = S.sb("xqT", [P, T]), S.sb("sg", [P, 2, I])
    h, hqT = S.sb("h", [P, NT, I]), S.sb("hqT", [P, CH, T])
    WIDE = NT * I
    NB = WIDE // BL
    ab, sign, u = S.sb("ab", [P, WIDE]), S.sb("sign", [P, WIDE]), S.sb("u", [P, WIDE])
    am, rs = S.sb("am", [P, NB]), S.sb("rs", [P, NB])

    def act_quantise(w, src, n, name, first=False):
        if not first:
            nc.scalar.wait_ge(*w(V, "free", back=0 if name != "qx" else 1))
        nc.scalar.activation(ab[:, 0:n], src, ACT.Abs).then_inc(*A(name, "abs"))
        nc.scalar.activation(sign[:, 0:n], src, ACT.Sign).then_inc(*A(name, "sign"))

    def dve_quantise(w, dst, n, name):
        nb = n // BL
        blocks = lambda x: x[:, 0:n].rearrange("p (b k) -> p b k", k=BL)
        each = lambda x: x[:, 0:nb].unsqueeze(2).to_broadcast([P, nb, BL])
        nc.vector.wait_ge(*w(A, name, "abs"))
        nc.vector.tensor_reduce(am[:, 0:nb], blocks(ab), AX, ALU.max).then_inc(*V(name, "max"))
        nc.vector.wait_ge(*w.own())
        nc.vector.tensor_scalar(am[:, 0:nb], am[:, 0:nb], 1.0 / 6.0, 1e-12, ALU.mult, ALU.max).then_inc(
            *V(name, "scale"))
        nc.vector.wait_ge(*w.own())
        nc.vector.reciprocal(rs[:, 0:nb], am[:, 0:nb]).then_inc(*V(name, "rec"))
        nc.vector.wait_ge(*w.own())
        nc.vector.tensor_tensor(blocks(ab), blocks(ab), each(rs), ALU.mult).then_inc(*V(name, "norm"))
        nc.vector.wait_ge(*w.own())
        nc.vector.tensor_scalar(u[:, 0:n], ab[:, 0:n], 5.0, 2.0, ALU.is_gt, ALU.mult).then_inc(*V(name, 5.0))
        for mid in (3.5, 2.5):
            nc.vector.wait_ge(*w.own())
            nc.vector.scalar_tensor_tensor(out=u[:, 0:n], in0=ab[:, 0:n], scalar=mid, in1=u[:, 0:n], op0=ALU.is_gt,
                                           op1=ALU.add).then_inc(*V(name, mid))
        nc.vector.wait_ge(*w.own())
        nc.vector.tensor_scalar(u[:, 0:n], u[:, 0:n], 2.0, None, ALU.mult).then_inc(*V(name, "double"))
        for mid in (1.75, 1.25, 0.75, 0.25):
            nc.vector.wait_ge(*w.own())
            nc.vector.scalar_tensor_tensor(out=u[:, 0:n], in0=ab[:, 0:n], scalar=mid, in1=u[:, 0:n], op0=ALU.is_gt,
                                           op1=ALU.add).then_inc(*V(name, mid))
        nc.vector.wait_ge(*w(A, name, "sign"))
        nc.vector.wait_ge(*w.own())
        nc.vector.scalar_tensor_tensor(out=u[:, 0:n], in0=u[:, 0:n], scalar=0.5, in1=sign[:, 0:n], op0=ALU.mult,
                                       op1=ALU.mult).then_inc(*V(name, "signed"))
        nc.vector.wait_ge(*w.own())
        nc.vector.tensor_tensor(dst.rearrange("p (b k) -> p b k", k=BL), blocks(u), each(am),
                                ALU.mult).then_inc(*V(name))

    with nc.Block() as block:
        @block.sync
        def _(sp):
            w = Waits(sp, None)
            sp.wait_ge(*w(G, "wgu_pad"))
            for x, n in enumerate(("w_gate", "w_up")):
                for c in range(CH):
                    m = rows_of[c]
                    S.load(sp, wgu[0:m, x, c, :], d["L3_ffn_" + n][c * P:c * P + m, :])
            S.load(sp, wd[:, :], d["L3_ffn_w_down"])
            sp.wait_ge(S.loaded, S.loads)

        @block.gpsimd
        def _(pool):
            w = S.once(pool, G)
            nc.gpsimd.memset(wgu[64:P, :, CH - 1, :], 0.0).then_inc(*G("wgu_pad"))

        @block.scalar
        def _(act):
            w = S.once(act, A)
            act.wait_ge(S.loaded, S.loads)
            act_quantise(w, wgu[:, :, :, :].rearrange("p x c n -> p (x c n)"), 2 * CH * D, "qgu", first=True)
            act.wait_ge(*w(V, "qgu"))
            act_quantise(w, wd[:, :], I, "qd", first=True)
            for x in range(2):
                act.wait_ge(*w(PE, "wT", x))
                nc.scalar.activation(wguT[:, x, :], ps[:, x, 0:I], ACT.Copy).then_inc(*A("wT", x))
            act.wait_ge(*w(PE, "wT", 2))
            for c in range(CH):
                m = rows_of[c]
                nc.scalar.activation(wdT[0:m, c, :], ps[0:m, 2, c * P:(c + 1) * P], ACT.Copy).then_inc(*A("wT", 2, c))
            with S.loop(act, A) as (i, w):
                act.wait_ge(*w(PE, "xqT", NT - 1, back=1))
                nc.scalar.activation(C.xb[:, :, :], C.y[:, bass.ds(i * NT, NT), :], ACT.Copy).then_inc(*A("xb"))
                act.wait_ge(*w.own())
                act_quantise(w, C.xb[:, :, :].rearrange("p t e -> p (t e)"), T, "qx", first=True)
                act.wait_ge(*w(PE, "xqT", NT - 1))
                nc.scalar.activation(xqT[:, :], C.bank(0), ACT.Copy).then_inc(*A("xqT"))
                for t in range(NT):
                    act.wait_ge(*w(PE, "gate", t))
                    if t >= 2:
                        act.wait_ge(*w(V, "h", t - 2))
                    nc.scalar.activation(sg[:, t % 2, :], ps[:, 1 + t % 2, 0:I], ACT.Silu).then_inc(*A("silu", t))
                act.wait_ge(*w(V, "h", NT - 1))
                act_quantise(w, h[:, :, :].rearrange("p t e -> p (t e)"), WIDE, "qh", first=True)
                for c in range(CH):
                    m = rows_of[c]
                    act.wait_ge(*w(PE, "hqT", c))
                    nc.scalar.activation(hqT[0:m, c, :], C.bank(5 + c, m), ACT.Copy).then_inc(*A("hqT", c))

        @block.vector
        def _(dve):
            w = S.once(dve, V)
            dve.wait_ge(S.loaded, S.loads)
            dve_quantise(w, wgu[:, :, :, :].rearrange("p x c n -> p (x c n)"), 2 * CH * D, "qgu")
            dve_quantise(w, wd[:, :], I, "qd")
            with S.loop(dve, V) as (i, w):
                dve.wait_ge(*w(A, "xb"))
                dve_quantise(w, C.xb[:, :, :].rearrange("p t e -> p (t e)"), T, "qx")
                for t in range(NT):
                    dve.wait_ge(*w(A, "silu", t))
                    dve.wait_ge(*w(PE, "up", t))
                    nc.vector.tensor_tensor(h[:, t, :], sg[:, t % 2, :], ps[:, 3 + t % 2, 0:I],
                                            ALU.mult).then_inc(*V("h", t))
                dve_quantise(w, h[:, :, :].rearrange("p t e -> p (t e)"), WIDE, "qh")
                dve.wait_ge(*w(PE, "out"))
                nc.vector.tensor_copy(C.y[:, bass.ds(i * NT, NT), :],
                                      C.bank(0).rearrange("p (t e) -> p t e", t=NT)).then_inc(*V("y"))

        @block.tensor
        def _(pe):
            w = S.once(pe, PE)
            pe.wait_ge(*w(V, "qd"))
            for x in range(2):
                for c in range(CH):
                    m = rows_of[c]
                    last = nc.tensor.transpose(ps[:, x, c * P:c * P + m], wgu[0:m, x, c, :], C.ident[0:m, 0:m])
                last.then_inc(*PE("wT", x))
            for c in range(CH):
                m = rows_of[c]
                last = nc.tensor.transpose(ps[0:m, 2, c * P:(c + 1) * P], wd[:, c * P:c * P + m], C.ident[:, :])
            last.then_inc(*PE("wT", 2))
            pe.wait_ge(*w(A, "wT", 2, CH - 1))
            with S.loop(pe, PE) as (i, w):
                pe.wait_ge(*w(V, "qx"))
                pe.wait_ge(*w(V, "y", back=1))
                pe_turn(nc, C, S, w, C.xb, 0, "xqT")
                pe.wait_ge(*w(A, "xqT"))
                for t in range(NT):
                    for x, name in enumerate(("gate", "up")):
                        if t >= 2:
                            pe.wait_ge(*w(V, "h", t - 2))
                        nc.tensor.matmul(ps[:, 1 + 2 * x + t % 2, 0:I], xqT[:, t * P:(t + 1) * P], wguT[:, x, :],
                                         start=True, stop=True).then_inc(*PE(name, t))
                pe.wait_ge(*w(V, "qh"))
                for c in range(CH):
                    m = rows_of[c]
                    for t in range(NT):
                        last = nc.tensor.transpose(ps[0:m, 5 + c, t * P:(t + 1) * P], h[:, t, c * P:c * P + m],
                                                   C.ident[:, :])
                    last.then_inc(*PE("hqT", c))
                pe.wait_ge(*w(A, "hqT", CH - 1))
                pe_rows(nc, C, w, 0, [hqT[0:rows_of[c], c, :] for c in range(CH)],
                        [wdT[0:rows_of[c], c, :] for c in range(CH)]).then_inc(*PE("out"))
    S.close()



def position_tables():
    import numpy as np

    p = np.arange(P)
    c = {f"const_head_of_{h}": (p[:, None] // (P // h) == np.arange(h)[None, :]).astype(np.float32) for h in (8, 16)}
    j = np.arange(2 * P)
    seen = (j[None, :] > p[:, None]) & (j[None, :] <= p[:, None] + P)
    both = np.stack([seen & (j >= P)[None, :], seen], 1)
    c["const_l0_mask"] = np.ascontiguousarray(
        np.repeat(np.where(both, 0.0, NEG).astype(np.float32)[:, :, None, :], 2, 2))
    for name, win in (("l0ffn", 32), ("l1ffn", 64)):
        j, r = np.arange(P)[None, :], p[:, None]
        seen = (j >= r) & (j <= r + win)
        both = np.where(np.stack([seen & (j >= win), seen], 1), 0.0, NEG).astype(np.float32)
        c[f"const_{name}_mask"] = np.ascontiguousarray(np.repeat(both[:, :, None, :], 4, 2))
        c[f"const_{name}_tables"] = rotary(win)
    shift = np.zeros((P, 2, P), np.float32)
    shift[p[:-1], 0, p[1:]] = 1.0
    shift[P - 1, 1, 0] = 1.0
    c["const_shift"] = shift
    sums, pairs = np.zeros((P, 9, P), np.float32), np.zeros((P, 8, P), np.float32)
    r, x = p[:, None], p[None, :]
    for l in range(7):
        mid = (x >> (l + 1) << (l + 1)) + (1 << l)
        sums[:, l, :] = np.where(x < mid, (r > x) & (r < mid), (r >= mid) & (r <= x))
        pairs[:, l, :] = (r >> (l + 1) == x >> (l + 1)) & (r < mid) & (x >= mid)
    sums[:, 7, :], sums[:, 8, :] = r <= x, r > x
    pairs[:, 7, :] = r == x
    c["const_l2_sums"], c["const_l2_pairs"] = sums, pairs
    e = np.arange(8)
    c["const_before"] = np.ascontiguousarray(np.tile((e[None, :] < e[:, None]).astype(np.float32), (P, 1, 1)))
    f = np.float32
    inv_freq = f(1.0) / np.power(f(10000.0), np.arange(4, dtype=f) / f(4), dtype=f)
    freqs = (np.arange(T, dtype=f)[None, :] * inv_freq[p % 8 // 2][:, None]).astype(f).astype(np.float64)
    sign = np.where(p % 2 == 0, -1.0, 1.0)[:, None]
    c["const_l3_rope"] = np.stack([np.cos(freqs), sign * np.sin(freqs)], 1).astype(f)
    return c


def rotary(win, head=64):
    import numpy as np

    f = np.float32
    half = np.arange(0, head, 2, dtype=f)
    inv_freq = f(1.0) / np.power(f(10000.0), half / f(head), dtype=f)
    t = np.arange(T, dtype=f)
    freqs = (t[:, None] * inv_freq[None, :]).astype(f)
    base = ((half + f(0.4 * head)) / f(1.4 * head)).astype(f)
    power = (t - f(T // 2)) / f(win // 2)
    scale = np.power(base[None, :].astype(np.float64), power[:, None].astype(np.float64)).astype(f)
    cos, sin = np.cos(freqs.astype(np.float64)), np.sin(freqs.astype(np.float64))
    parts = []
    for s in (scale.astype(np.float64), 1.0 / scale.astype(np.float64)):
        parts += [np.concatenate([cos * s, cos * s], 1), np.concatenate([-sin * s, sin * s], 1)]
    x = np.stack(parts, 0).astype(f).reshape(4, NT, P, head)
    return np.ascontiguousarray(x.transpose(2, 0, 1, 3))


def lay_out(inputs):
    import numpy as np

    a = {n: np.ascontiguousarray(x) for n, x in inputs.items()}
    q, k, v, g, o = (a.pop("L3_attn_" + n) for n in ("q_w", "k_w", "v_w", "g_w", "out_w"))
    partner = np.arange(D) ^ 1
    a["L3_attn_qk_turned"] = np.ascontiguousarray(np.stack([q, q[partner], k, k[partner]]).transpose(2, 0, 1))
    a["L3_attn_v_turned"] = np.ascontiguousarray(v.transpose())
    a["L3_attn_g_turned"] = np.ascontiguousarray(g.transpose())
    a["L3_attn_out_turned"] = np.ascontiguousarray(o.transpose())
    ranks = np.stack([a.pop("L3_attn_Wq"), a.pop("L3_attn_Wk")])
    a["L3_attn_ranks"] = np.ascontiguousarray(ranks.transpose(1, 3, 0, 2).reshape(D, 2, 16))
    for name, x in (("g_b_spread", a.pop("L3_attn_g_b").reshape(16, 16)),
                    ("decay_spread", a.pop("L3_attn_base_decay_logits"))):
        a["L3_attn_" + name] = np.ascontiguousarray(np.repeat(x.transpose(), 8, 0))
    b1 = a.pop("L2_ffn_b1")
    a["L2_ffn_b1_turned"] = np.ascontiguousarray(b1.reshape(8, 2, P).transpose(2, 0, 1))
    a.update(position_tables())
    return a


BLOCKS = [stage_l0_attn, stage_l0_ffn, stage_l1_attn, stage_l1_ffn, stage_l2_attn, stage_l2_ffn, stage_l3_attn,
          stage_l3_ffn]


def build(nc, d, out, plan, blocks):
    C = Common(nc, d)
    setup(nc, C, d["L0_attn_x"])
    stage_norms(nc, C, plan, "norms_first", add=False)
    for n, block in enumerate(blocks):
        block(nc, C, plan)
        stage_norms(nc, C, plan, f"norms_{n}", then=n + 1 < len(blocks))
    stored = nc.alloc_semaphore("out_stored")
    with nc.Block() as block:
        @block.sync
        def _(sp):
            sp.dma_start(out.rearrange("b (t p) d -> p (b t) d", p=P), C.x[:, :, :]).then_inc(stored, 16)
            sp.wait_ge(stored, 16)


def program(bacc, shapes, blocks=None):
    plan = {}
    for _ in range(2):
        nc = bacc.Bacc("TRN2", target_bir_lowering=False, num_devices=1)
        d = {n: nc.dram_tensor(f"in_{n}_dram", s, F32, kind="ExternalInput").ap() for n, s in shapes.items()}
        out = nc.dram_tensor("out_0_dram", (B, T, D), F32, kind="ExternalOutput").ap()
        build(nc, d, out, plan, BLOCKS if blocks is None else blocks)
    return nc



def kernel(**inputs):
    import concourse.bacc as _bacc
    from concourse.bass_utils import run_bass_kernel_spmd as _run

    arrays = lay_out(inputs)
    nc = program(_bacc, {n: a.shape for n, a in arrays.items()})
    r = _run(nc, [{f"in_{n}_dram": a for n, a in arrays.items()}], core_ids=[0])
    return r.results[0]["out_0_dram"]
```

```python
from contextlib import ExitStack, contextmanager

import numpy as np

import concourse.bass as bass
from concourse import mybir

P = 128
B, T, D = 8, 512, 128
NT = T // P
EPS = 1e-5
NEG = -1e30
F32 = mybir.dt.float32
BF16 = mybir.dt.bfloat16
U32 = mybir.dt.uint32
ALU = mybir.AluOpType
ACT = mybir.ActivationFunctionType
AX = mybir.AxisListType.X


class Results:

    def __init__(self, nc, stage, engine, plan):
        self.sem = nc.alloc_semaphore(f"{stage}_{engine}_done")
        self.key, self.plan = f"{stage}_{engine}", plan
        self.at, self.once, self.each = plan.get(self.key, ({}, 0, 1))
        self.found, self.n, self.n_once = {}, 0, 0

    def __call__(self, *name):
        self.n += 1
        self.found[name] = self.n
        return self.sem, 1

    def end_once(self):
        self.n_once, self.n = self.n, 0

    def close(self):
        self.plan[self.key] = (self.found, self.n_once, self.n)


class Waits:

    def __init__(self, eng, own, turns=None, layer=None, trips=1):
        self.eng, self.own_results, self.turn, self.layer, self.trips = eng, own, turns, layer, trips

    def value(self, r, n, back):
        v = n + r.each * (1 - back)
        if self.turn is not None:
            v = v + r.once + self.turn * r.each
        if self.layer is not None:
            v = v + self.layer * (self.trips * r.each)
        return v

    def __call__(self, r, *name, back=0):
        return r.sem, self.value(r, r.at.get(name, 1), back)

    def own(self):
        r = self.own_results
        return r.sem, self.value(r, r.n, 0)


class Stage:

    def __init__(self, nc, name, plan, trips=B, layers=None):
        self.nc, self.name, self.trips, self.layers = nc, name, trips, layers
        self.stack = ExitStack()
        self.PE, self.ACT, self.DVE, self.POOL = (Results(nc, name, e, plan) for e in ("pe", "act", "dve", "pool"))
        self.loaded = nc.alloc_semaphore(f"{name}_weights_loaded")
        self.loads = 0

    def sb(self, name, shape, dt=F32):
        return self.stack.enter_context(self.nc.sbuf_tensor(f"{self.name}_{name}", shape, dt))

    def once(self, eng, own):
        eng.sem_inc(own.sem, own.each)
        return Waits(eng, own)

    @contextmanager
    def loop(self, eng, own):
        own.end_once()
        with eng.Fori(0, self.trips, 1) as i:
            yield i, Waits(eng, own, i)

    def run(self, eng, own, turn):
        own.end_once()
        with eng.Fori(0, self.trips - 1, 1) as i:
            turn(Waits(eng, own, i), i)
        each, own.n = own.n, 0
        turn(Waits(eng, own, self.trips - 1), self.trips - 1, last=True)
        assert own.n == each

    def run_layers(self, eng, own, turn):
        own.end_once()
        with eng.Fori(0, self.layers, 1) as l:
            with eng.Fori(0, self.trips - 1, 1) as i:
                turn(Waits(eng, own, i, l, self.trips), l, i)
            each, own.n = own.n, 0
            turn(Waits(eng, own, self.trips - 1, l, self.trips), l, self.trips - 1, last=True)
            assert own.n == each

    def load(self, sp, dst, src):
        sp.dma_start(dst, src).then_inc(self.loaded, 16)
        self.loads += 16

    def close(self):
        for r in (self.PE, self.ACT, self.DVE, self.POOL):
            r.close()
        self.stack.close()


class Common:

    def __init__(self, nc, d):
        self.nc, self.d = nc, d
        self.ps = nc.alloc_psum_tensor("ps", [P, 8, 512], F32)
        self.x = nc.alloc_sbuf_tensor("x_all", [P, B * NT, D], F32)
        self.y = nc.alloc_sbuf_tensor("y_all", [P, B * NT, D], F32)
        self.ident = nc.alloc_sbuf_tensor("ident", [P, P], F32)
        self.ident_bf = nc.alloc_sbuf_tensor("ident_bf", [P, P], BF16)
        self.ones = nc.alloc_sbuf_tensor("ones", [P, P], F32)
        self.neghalf = nc.alloc_sbuf_tensor("neghalf", [P, 64], F32)
        self.xb = nc.alloc_sbuf_tensor("xb", [P, NT, D], F32)
        self.yb = nc.alloc_sbuf_tensor("yb", [P, NT, D], F32)
        self.nb = nc.alloc_sbuf_tensor("nb", [P, NT, D], F32)
        self.st = nc.alloc_sbuf_tensor("bn_st", [P, NT, 6], F32)
        self.mv = nc.alloc_sbuf_tensor("bn_mv", [P, NT, 2], F32)
        self.ve = nc.alloc_sbuf_tensor("bn_ve", [P, NT], F32)
        self.rs = nc.alloc_sbuf_tensor("bn_rs", [P, NT], F32)

    def bank(self, b, rows=P):
        return self.ps[0:rows, b, :]


def column(v):
    return v.rearrange("(p o) -> p o", o=1)


def row(v):
    return v.rearrange("(o n) -> o n", o=1)



def following(x, i, last):
    return x[:, 0:NT, :] if last else x[:, bass.ds(i * NT + NT, NT), :]


def dve_norm(nc, C, S, w, src, dst, name):
    V, G = S.DVE, S.POOL
    for t in range(NT):
        nc.vector.bn_stats(C.st[:, t, :], src[:, t, :]).then_inc(*V(name, "stats", t))
    nc.vector.wait_ge(*w.own())
    nc.vector.memset(C.ve[:, :], 0.0).then_inc(*V(name, "clear"))
    for t in range(NT):
        nc.vector.bn_aggr(C.mv[:, t, :], C.st[:, t, :]).then_inc(*V(name, "moments", t))
    nc.vector.wait_ge(*w.own())
    nc.vector.tensor_scalar(C.ve[:, :], C.mv[:, :, 1], EPS, None, ALU.add).then_inc(*V(name, "var"))
    nc.vector.wait_ge(*w(G, name, "rstd"))
    for t in range(NT):
        nc.vector.tensor_scalar(dst[:, t, :], src[:, t, :], C.mv[:, t, 0:1], C.rs[:, t:t + 1],
                                ALU.subtract, ALU.mult).then_inc(*V(name, t))


def pool_norm(nc, C, S, w, name):
    nc.gpsimd.wait_ge(*w(S.DVE, name, "var"))
    nc.gpsimd.tensor_tensor(C.rs[:, :], C.ve[:, :], C.neghalf[:, 0:NT], ALU.pow).then_inc(*S.POOL(name, "rstd"))


def pe_turn(nc, C, S, w, src, bank, name):
    for t in range(NT):
        nc.tensor.transpose(C.ps[:, bank, t * P:(t + 1) * P], src[:, t, :], C.ident[:, :]).then_inc(*S.PE(name, t))


def pe_rows(nc, C, w, bank, lhs, weights, bias=None):
    for t in range(NT):
        o = C.ps[:, bank, t * P:(t + 1) * P]
        for c in range(len(lhs)):
            last = nc.tensor.matmul(o, lhs[c][:, t * P:(t + 1) * P], weights[c], start=(c == 0),
                                    stop=(bias is None and c == len(lhs) - 1))
        if bias is not None:
            last = nc.tensor.matmul(o, C.ident[:, :], bias, start=False, stop=True)
    return last


def stage_norms(nc, C, plan, name, add=True, then=True):
    TURNS = 2
    N = B * NT // TURNS
    S = Stage(nc, name, plan, trips=TURNS)
    A, V, G = S.ACT, S.DVE, S.POOL
    st, mv, nb = S.sb("stats", [P, N, 6]), S.sb("moments", [P, N, 2]), S.sb("normed", [P, N, D])
    ve, rs, nm = (S.sb(n, [P, N]) for n in ("variance", "rstd", "shift"))
    passes = [n for n, on in (("out", add), ("in", then)) if on]

    def tiles(x, i, t=0, n=N):
        return x[:, bass.ds(i * N + t, n), :]

    def tile(x, i, t):
        return tiles(x, i, t, 1).rearrange("p o d -> p (o d)")

    with nc.Block() as block:
        @block.gpsimd
        def _(pool):
            S.once(pool, G)
            with S.loop(pool, G) as (i, w):
                for k in passes:
                    pool.wait_ge(*w(V, k, "var"))
                    nc.gpsimd.tensor_tensor(rs[:, :], ve[:, :], C.neghalf[:, 0:N], ALU.pow).then_inc(*G(k, "rstd"))

        @block.scalar
        def _(act):
            S.once(act, A)
            with S.loop(act, A) as (i, w):
                for k in passes:
                    act.wait_ge(*w(V, k, "shift"))
                    for t in range(1, N, 2):
                        dst = nb[:, t, :] if k == "out" else tile(C.y, i, t)
                        nc.scalar.activation(dst, tile(C.y if k == "out" else C.x, i, t), ACT.Identity,
                                             bias=nm[:, t:t + 1], scale=rs[:, t:t + 1]).then_inc(*A(k, t))

        @block.vector
        def _(dve):
            S.once(dve, V)
            with S.loop(dve, V) as (i, w):
                for k in passes:
                    src = C.y if k == "out" else C.x
                    dve.wait_ge(*w(A, passes[-1], N - 1, back=1) if k == passes[0] else w(A, passes[0], N - 1))
                    dve.wait_ge(*w.own())
                    nc.vector.memset(ve[:, :], 0.0).then_inc(*V(k, "clear"))
                    for t in range(N):
                        nc.vector.bn_stats(st[:, t, :], tile(src, i, t)).then_inc(*V(k, "stats", t))
                    dve.wait_ge(*w.own())
                    nc.vector.memset(nm[:, :], 0.0).then_inc(*V(k, "clear_shift"))
                    for t in range(N):
                        nc.vector.bn_aggr(mv[:, t, :], st[:, t, :]).then_inc(*V(k, "moments", t))
                    dve.wait_ge(*w.own())
                    nc.vector.tensor_scalar(ve[:, :], mv[:, :, 1], EPS, None, ALU.add).then_inc(*V(k, "var"))
                    dve.wait_ge(*w(G, k, "rstd"))
                    nc.vector.scalar_tensor_tensor(out=nm[:, :], in0=mv[:, :, 0], scalar=-1.0, in1=rs[:, :],
                                                   op0=ALU.mult, op1=ALU.mult).then_inc(*V(k, "shift"))
                    for t in range(0, N, 2):
                        dst = nb[:, t, :] if k == "out" else tile(C.y, i, t)
                        nc.vector.tensor_scalar(dst, tile(src, i, t), mv[:, t, 0:1], rs[:, t:t + 1],
                                                ALU.subtract, ALU.mult).then_inc(*V(k, t))
                    if k == "out":
                        dve.wait_ge(*w(A, k, N - 1))
                        dve.wait_ge(*w.own())
                        nc.vector.tensor_tensor(tiles(C.x, i), tiles(C.x, i), nb[:, :, :],
                                                ALU.add).then_inc(*V("x"))
    S.close()


def setup(nc, C, d_x):
    x_loaded = nc.alloc_semaphore("x_loaded")
    filled = nc.alloc_semaphore("constants_filled")
    with nc.Block() as block:
        @block.sync
        def _(sp):
            sp.dma_start(C.x[:, :, :], d_x.rearrange("b (t p) d -> p (b t) d", p=P)).then_inc(x_loaded, 16)
            sp.wait_ge(x_loaded, 16)

        @block.gpsimd
        def _(pool):
            nc.gpsimd.memset(C.ident[:, :], 0.0).then_inc(filled, 1)
            nc.gpsimd.memset(C.ones[:, :], 1.0).then_inc(filled, 1)
            nc.gpsimd.memset(C.neghalf[:, :], -0.5).then_inc(filled, 1)
            pool.wait_ge(filled, 3)
            nc.gpsimd.affine_select(out=C.ident[:, :], in_=C.ident[:, :], compare_op=ALU.not_equal, fill=1.0,
                                    base=0, pattern=[[-1, P]], channel_multiplier=1).then_inc(filled, 1)
            pool.wait_ge(filled, 4)
            nc.gpsimd.tensor_copy(C.ident_bf[:, :], C.ident[:, :]).then_inc(filled, 1)
            pool.wait_ge(filled, 5)



def stage_l0_attn(nc, C, plan):
    H, DH, WIN, N, FF = 16, 8, 128, 64, 4
    SCALE = float(np.float32(1.0) / np.sqrt(np.float32(DH)))
    d = C.d
    S = Stage(nc, "l0attn", plan)
    PE, A, V, G = S.PE, S.ACT, S.DVE, S.POOL
    ps = C.ps
    wq, wk, wv, wo, wg = (S.sb(n, [P, D]) for n in ("wq", "wk", "wv", "wo", "wg"))
    bw, cw = S.sb("bw", [P, N]), S.sb("cw", [P, D])
    w1, w2 = S.sb("w1", [P, FF, P]), S.sb("w2", [P, FF, D])
    cols = S.sb("cols", [P, 16])
    LN1G, LN1B, BQ, BK, LN2G, LN2B, B1, DEC = 0, 1, 2, 3, 4, 5, 6, 10
    rows = S.sb("rows", [P, 4, D])
    BV, BO, BG, B2 = 0, 1, 2, 3
    headmask = S.sb("headmask", [P, H])
    mask = S.sb("mask", [P, 2, 2, 2 * P])
    mask_bf = S.sb("mask_bf", [P, 2, 2, 2 * P], BF16)
    hT, h2T, qm = S.sb("hT", [P, T]), S.sb("h2T", [P, T]), S.sb("qm", [P, H, T])
    kT = S.sb("kT", [P, P + T])
    qT = S.sb("qT", [P, T])
    va = S.sb("va", [P, NT + 1, 4, P + 32])
    gate, sT = S.sb("gate", [P, NT, D]), S.sb("sT", [P, T])
    mx, nm, sm, rec = (S.sb(n, [P, 4, 2]) for n in ("mx", "nm", "sm", "rec"))
    pr, pT = S.sb("pr", [P, 4, 2, 2 * P]), S.sb("pT", [P, 2, 4, P])
    aoT = S.sb("aoT", [P, T])
    ssm, x1, hid = S.sb("ssm", [P, NT, D]), S.sb("x1", [P, NT, D]), S.sb("hid", [P, FF, T])
    K = NT * H // 2
    cw_zero = nc.alloc_semaphore("l0attn_cw_zero")
    LN1, LN2 = "norm_1", "norm_2"
    UP_BANKS = (3, 4, 5, 7)
    NORM, TURN, Q_STEP, U_STEP, K_STEP, V_STEP = 5, 8, 10, 12, 14, 16

    with nc.Block() as block:
        @block.sync
        def _(sp):
            for dst, n in ((wq, "WQ"), (wk, "WK"), (wv, "WV"), (wo, "WO"), (wg, "Wg"), (bw, "Bw")):
                S.load(sp, dst[:, :], d["L0_attn_" + n])
            sp.wait_ge(cw_zero, 1)
            S.load(sp, cw[0:N, :], d["L0_attn_Cw"])
            S.load(sp, w1[:, :, :], d["L0_attn_W1"].rearrange("k (c n) -> k c n", c=FF))
            S.load(sp, w2[:, :, :], d["L0_attn_W2"].rearrange("(c k) n -> k c n", c=FF))
            for c, n in ((LN1G, "ln1_g"), (LN1B, "ln1_b"), (BQ, "bQ"), (BK, "bK"), (LN2G, "ln2_g"), (LN2B, "ln2_b")):
                S.load(sp, cols[:, c:c + 1], column(d["L0_attn_" + n]))
            for c in range(FF):
                S.load(sp, cols[:, B1 + c:B1 + c + 1], column(d["L0_attn_b1"][c * P:(c + 1) * P]))
            S.load(sp, cols[0:N, DEC:DEC + 1], column(d["L0_attn_A"]))
            for c, n in ((BV, "bV"), (BO, "bO"), (BG, "bg"), (B2, "b2")):
                S.load(sp, rows[:, c, :], row(d["L0_attn_" + n]).to_broadcast([P, D]))
            S.load(sp, headmask[:, :], d["const_head_of_16"])
            S.load(sp, mask[:, :, :, :], d["const_l0_mask"])
            sp.wait_ge(S.loaded, S.loads)

        @block.gpsimd
        def _(pool):
            w = S.once(pool, G)
            nc.gpsimd.memset(cw[:, :], 0.0).then_inc(cw_zero, 1)
            nc.gpsimd.memset(kT[:, 0:P], 0.0).then_inc(*G("kT_pad"))
            nc.gpsimd.memset(sT[:, :], 0.0).then_inc(*G("sT_pad"))
            nc.gpsimd.memset(va[:, :, :, :], 0.0).then_inc(*G("va_pad"))
            pool.wait_ge(S.loaded, S.loads)
            nc.gpsimd.tensor_copy(mask_bf[:, :, :, :], mask[:, :, :, :]).then_inc(*G("mask"))
            pool.wait_ge(*w.own())
            pool_norm(nc, C, S, w, (LN1, "first"))

            def turn(w, i, last=False):
                for k in range(K):
                    pool.wait_ge(*w(V, "rec", k))
                    nc.gpsimd.tensor_tensor(pr[:, k % 4], pr[:, k % 4], rec[:, k % 4, :].unsqueeze(2).to_broadcast(
                        [P, 2, 2 * P]), ALU.mult).then_inc(*G("probs", k))
                    if k == NORM - 1:
                        pool_norm(nc, C, S, w, LN1)
                pool_norm(nc, C, S, w, LN2)

            S.run(pool, G, turn)

        @block.scalar
        def _(act):
            w = S.once(act, A)
            act.wait_ge(S.loaded, S.loads)
            act.wait_ge(*w(G, "va_pad"))

            def keep_turned(w, *mark):
                act.wait_ge(*w(PE, *mark, "hT", NT - 1))
                nc.scalar.activation(hT[:, :], C.bank(5), ACT.Identity, bias=cols[:, LN1B:LN1B + 1],
                                     scale=cols[:, LN1G:LN1G + 1]).then_inc(*A(*mark, "hT"))

            def keep_qkv(w, *mark):
                act.wait_ge(*w(PE, *mark, "K"))
                nc.scalar.activation(kT[:, P:], C.bank(6), ACT.Identity,
                                     bias=cols[:, BK:BK + 1]).then_inc(*A(*mark, "kT"))
                act.wait_ge(*w(PE, *mark, "V"))
                for j in range(4):
                    nc.scalar.activation(va[:, 1:, :, 40 * j:40 * j + DH],
                                         C.bank(5).rearrange("p (t g e) -> p t g e", t=NT, g=4)[:, :, :, 8 * j:8 * j + 8],
                                         ACT.Copy).then_inc(*A(*mark, "va", j))
                act.wait_ge(*w(V, *mark, "qT"))
                for h in range(H // 2, H):
                    nc.scalar.activation(qm[:, h, :], qT[:, :], ACT.Copy,
                                         scale=headmask[:, h:h + 1]).then_inc(*A(*mark, "qm", h))

            def keep_gate(w, *mark):
                act.wait_ge(*w(PE, *mark, "gate"))
                nc.scalar.activation(gate[:, :, :], C.bank(2).rearrange("p (t e) -> p t e", t=NT), ACT.Tanh,
                                     scale=0.5).then_inc(*A(*mark, "tanh"))

            nc.scalar.activation(C.xb[:, :, :], C.y[:, 0:NT, :], ACT.Copy).then_inc(*A("first", "xb"))
            for step in (keep_turned, keep_qkv, keep_gate):
                step(w, "first")

            def turn(w, i, last=False):
                act.wait_ge(*w(V, LN1, NT - 1, back=1))
                nc.scalar.activation(C.xb[:, :, :], following(C.y, i, last), ACT.Copy).then_inc(*A("xb"))
                for k in range(K):
                    act.wait_ge(*w(V, "negmax", k))
                    if k >= 4:
                        act.wait_ge(*w(PE, "pT", k - 4))
                    for j in range(2):
                        nc.scalar.activation(pr[:, k % 4, j, :], ps[:, k % 3, j * 2 * P:(j + 1) * 2 * P], ACT.Exp,
                                             bias=nm[:, k % 4, j:j + 1], scale=SCALE,
                                             accum_out=sm[:, k % 4, j:j + 1]).then_inc(*A("exp", k, j))
                    if k == 4:
                        act.wait_ge(*w(PE, "ssm"))
                        nc.scalar.activation(ssm[:, :, :], C.bank(6).rearrange("p (t e) -> p t e", t=NT),
                                             ACT.Copy).then_inc(*A("ssm"))
                    if k == TURN:
                        keep_turned(w)
                act.wait_ge(*w(PE, "O", K - 1))
                nc.scalar.activation(aoT[:, :], C.bank(7), ACT.Copy).then_inc(*A("aoT"))
                keep_qkv(w)
                act.wait_ge(*w(V, "x1", 1))
                keep_gate(w)
                act.wait_ge(*w(PE, "h2T", NT - 1))
                nc.scalar.activation(h2T[:, :], C.bank(1), ACT.Identity, bias=cols[:, LN2B:LN2B + 1],
                                     scale=cols[:, LN2G:LN2G + 1]).then_inc(*A("h2T"))
                for c in range(FF):
                    act.wait_ge(*w(PE, "up", c))
                    nc.scalar.activation(hid[:, c, :], C.bank(UP_BANKS[c]), ACT.Gelu,
                                         bias=cols[:, B1 + c:B1 + c + 1]).then_inc(*A("hid", c))

            S.run(act, A, turn)

        @block.vector
        def _(dve):
            w = S.once(dve, V)
            dve.wait_ge(S.loaded, S.loads)
            dve.wait_ge(*w(G, "mask"))

            def keep_q(w, *mark):
                dve.wait_ge(*w(PE, *mark, "Q"))
                nc.vector.tensor_scalar(qT[:, :], C.bank(6), cols[:, BQ:BQ + 1], None, ALU.add).then_inc(
                    *V(*mark, "qT"))

            def scan(w, *mark):
                dve.wait_ge(*w(PE, *mark, "u"))
                nc.vector.tensor_tensor_scan(sT[0:N, :], cols[0:N, DEC:DEC + 1].to_broadcast([N, T]), C.bank(5, N),
                                             0.0, ALU.mult, ALU.add).then_inc(*V(*mark, "sT"))

            def mask_heads(w, *mark):
                dve.wait_ge(*w.own())
                for h in range(H // 2):
                    nc.vector.tensor_scalar(qm[:, h, :], qT[:, :], headmask[:, h:h + 1], None,
                                            ALU.mult).then_inc(*V(*mark, "qm", h))

            dve.wait_ge(*w(A, "first", "xb"))
            dve_norm(nc, C, S, w, C.xb, C.nb, (LN1, "first"))
            for step in (keep_q, scan, mask_heads):
                step(w, "first")
            dve.wait_ge(*w(A, "first", "tanh"))
            nc.vector.memset(x1[:, :, :], 0.0).then_inc(*V("first", "end"))

            def turn(w, i, last=False):
                dve.wait_ge(*w(A, "tanh", back=1))
                nc.vector.tensor_scalar(gate[:, :, :], gate[:, :, :], 0.5, 0.5, ALU.mult,
                                        ALU.add).then_inc(*V("gate"))

                def maximum(k):
                    dve.wait_ge(*w(PE, "S", k))
                    nc.vector.tensor_reduce(mx[:, k % 4, :], C.bank(k % 3).rearrange("p (j n) -> p j n", j=2),
                                            AX, ALU.max).then_inc(*V("max", k))
                    dve.wait_ge(*w.own())
                    nc.vector.tensor_scalar(nm[:, k % 4, :], mx[:, k % 4, :], -SCALE, None,
                                            ALU.mult).then_inc(*V("negmax", k))

                def copy_probs(k):
                    dve.wait_ge(*w(PE, "pT", k))
                    if k >= 2:
                        dve.wait_ge(*w(PE, "O", k - 2))
                    nc.vector.tensor_copy(pT[:, k % 2, :, :],
                                          C.bank(3 + k % 2).rearrange("p (j n) -> p j n", j=4)).then_inc(*V("pT", k))

                def reciprocals(k):
                    dve.wait_ge(*w(A, "exp", k, 1))
                    nc.vector.reciprocal(rec[:, k % 4, :], sm[:, k % 4, :]).then_inc(*V("rec", k))

                for k in range(K + 3):
                    if k < K:
                        maximum(k)
                    if 1 <= k <= K:
                        reciprocals(k - 1)
                    if k >= 3:
                        copy_probs(k - 3)
                    if k == NORM:
                        dve.wait_ge(*w(A, "xb"))
                        dve_norm(nc, C, S, w, C.xb, C.nb, LN1)
                    if k == Q_STEP:
                        keep_q(w)
                    if k == U_STEP:
                        scan(w)
                dve.wait_ge(*w(PE, "S", K - 1))
                mask_heads(w)
                dve.wait_ge(*w(PE, "attn"))
                dve.wait_ge(*w(A, "ssm"))
                attn = C.bank(0).rearrange("p (t e) -> p t e", t=NT)
                nc.vector.tensor_tensor(x1[:, :, :], attn, ssm[:, :, :], ALU.subtract).then_inc(*V("x1", 0))
                dve.wait_ge(*w.own())
                nc.vector.tensor_tensor(x1[:, :, :], x1[:, :, :], gate[:, :, :], ALU.mult).then_inc(*V("x1", 1))
                dve.wait_ge(*w.own())
                nc.vector.tensor_tensor(x1[:, :, :], x1[:, :, :], ssm[:, :, :], ALU.add).then_inc(*V("x1", 2))
                dve.wait_ge(*w.own())
                nc.vector.tensor_tensor(x1[:, :, :], x1[:, :, :], C.y[:, bass.ds(i * NT, NT), :], ALU.add).then_inc(*V("x1", 3))
                dve.wait_ge(*w.own())
                dve_norm(nc, C, S, w, x1, C.nb, LN2)
                dve.wait_ge(*w(PE, "down"))
                nc.vector.tensor_tensor(C.y[:, bass.ds(i * NT, NT), :], x1[:, :, :], C.bank(6).rearrange("p (t e) -> p t e", t=NT),
                                        ALU.add).then_inc(*V("y"))

            S.run(dve, V, turn)

        @block.tensor
        def _(pe):
            w = S.once(pe, PE)
            pe.wait_ge(S.loaded, S.loads)
            pe.wait_ge(*w(G, "mask"))

            def turn_x(w, *mark):
                pe.wait_ge(*w(V, *((LN1, *mark), NT - 1) if mark else (LN1, NT - 1)))
                for t in range(NT):
                    nc.tensor.transpose(ps[:, 5, t * P:(t + 1) * P], C.nb[:, t, :],
                                        C.ident[:, :]).then_inc(*PE(*mark, "hT", t))

            def project_q(w, *mark):
                pe.wait_ge(*w(A, *mark, "hT"))
                nc.tensor.matmul(C.bank(6), wq[:, :], hT[:, :], start=True, stop=True).then_inc(*PE(*mark, "Q"))

            def project_u(w, *mark):
                nc.tensor.matmul(C.bank(5, N), bw[:, :], hT[:, :], start=True, stop=True).then_inc(*PE(*mark, "u"))

            def project_k(w, *mark):
                pe.wait_ge(*w(V, *mark, "qT"))
                nc.tensor.matmul(C.bank(6), wk[:, :], hT[:, :], start=True, stop=True).then_inc(*PE(*mark, "K"))

            def project_rows(w, bank, wt, b, *name):
                for t in range(NT):
                    o = ps[:, bank, t * P:(t + 1) * P]
                    nc.tensor.matmul(o, hT[:, t * P:(t + 1) * P], wt[:, :], start=True, stop=False)
                    product = nc.tensor.matmul(o, C.ident[:, :], rows[:, b, :], start=False, stop=True)
                product.then_inc(*PE(*name))

            def project_v(w, *mark):
                pe.wait_ge(*w(V, *mark, "sT"))
                project_rows(w, 5, wv, BV, *mark, "V")

            for step in (turn_x, project_q, project_u, project_k, project_v):
                step(w, "first")
            project_rows(w, 2, wg, BG, "first", "gate")
            pe.wait_ge(*w(A, "first", "tanh"))
            pe.wait_ge(*w(V, "first", "qm", H // 2 - 1))
            nc.tensor.transpose(ps[:, 0, 0:P], C.ident[:, :], C.ident[:, :]).then_inc(*PE("first", "end"))

            def turn(w, i, last=False):
                pe.wait_ge(*w(A, "tanh", back=1))

                def scores(k):
                    t, h = k // (H // 2), k % (H // 2)
                    if t == 0:
                        pe.wait_ge(*w(V, "qm", h, back=1))
                        pe.wait_ge(*w(A, "qm", h + H // 2, back=1))
                    if k >= 3:
                        pe.wait_ge(*w(A, "exp", k - 3, 1))
                    b = k % 3
                    nc.tensor.matmul(C.bank(b), C.ident_bf[:, :], mask_bf[:, int(t > 0), :, :], start=True,
                                     stop=False)
                    for j in range(2):
                        product = nc.tensor.matmul(ps[:, b, j * 2 * P:(j + 1) * 2 * P],
                                                qm[:, h + j * H // 2, t * P:(t + 1) * P],
                                                kT[:, t * P:(t + 2) * P], start=False, stop=(j == 1))
                    product.then_inc(*PE("S", k))

                def turn_probs(k):
                    pe.wait_ge(*w(G, "probs", k))
                    if k >= 2:
                        pe.wait_ge(*w(V, "pT", k - 2))
                    for j in range(2):
                        for s in range(2):
                            n = 2 * j + s
                            product = nc.tensor.transpose(ps[:, 3 + k % 2, n * P:(n + 1) * P],
                                                       pr[:, k % 4, j, s * P:(s + 1) * P], C.ident[:, :])
                    product.then_inc(*PE("pT", k))

                def values(k):
                    t, h = k // (H // 2), k % (H // 2)
                    pe.wait_ge(*w(V, "pT", k))
                    for s in range(2):
                        for j in range(2):
                            g, c = h // 4 + 2 * j, h % 4
                            product = nc.tensor.matmul(ps[32 * g:32 * g + 32, 7, t * P:(t + 1) * P],
                                                    va[:, t + s, g, 32 * c:32 * c + 32], pT[:, k % 2, 2 * j + s, :],
                                                    start=(c == 0 and s == 0), stop=(c == 3 and s == 1))
                    product.then_inc(*PE("O", k))

                for k in range(K + 4):
                    if k < K:
                        scores(k)
                    if 3 <= k < K + 3:
                        turn_probs(k - 3)
                    if k >= 4:
                        values(k - 4)
                    if k == 2:
                        pe.wait_ge(*w(V, "y", back=1))
                        for t in range(NT):
                            product = nc.tensor.matmul(ps[:, 6, t * P:(t + 1) * P], sT[:, t * P:(t + 1) * P],
                                                       cw[:, :], start=True, stop=True)
                        product.then_inc(*PE("ssm"))
                    if k == TURN:
                        turn_x(w)
                    if k == Q_STEP:
                        project_q(w)
                    if k == U_STEP:
                        project_u(w)
                    if k == K_STEP:
                        project_k(w)
                    if k == V_STEP:
                        project_v(w)
                project_rows(w, 2, wg, BG, "gate")
                pe.wait_ge(*w(A, "aoT"))
                for t in range(NT):
                    o = ps[:, 0, t * P:(t + 1) * P]
                    nc.tensor.matmul(o, aoT[:, t * P:(t + 1) * P], wo[:, :], start=True, stop=False)
                    product = nc.tensor.matmul(o, C.ident[:, :], rows[:, BO, :], start=False, stop=True)
                product.then_inc(*PE("attn"))
                pe.wait_ge(*w(V, LN2, NT - 1))
                pe_turn(nc, C, S, w, C.nb, 1, "h2T")
                pe.wait_ge(*w(A, "h2T"))
                for c in range(FF):
                    nc.tensor.matmul(C.bank(UP_BANKS[c]), w1[:, c, :], h2T[:, :], start=True,
                                     stop=True).then_inc(*PE("up", c))
                for t in range(NT):
                    o = ps[:, 6, t * P:(t + 1) * P]
                    for c in range(FF):
                        pe.wait_ge(*w(A, "hid", c))
                        nc.tensor.matmul(o, hid[:, c, t * P:(t + 1) * P], w2[:, c, :], start=(c == 0), stop=False)
                    product = nc.tensor.matmul(o, C.ident[:, :], rows[:, B2, :], start=False, stop=True)
                product.then_inc(*PE("down"))

            S.run(pe, PE, turn)
    S.close()



def local_layers(nc, C, plan, name, block_name, H, DEPTH, WIN, weights):
    E = 64
    INNER, HID = H * E, int(D * 4 * 2 / 3)
    HG = H // 8
    CH = INNER // P
    QT = P - WIN
    QR = 96
    NA = -(-T // QT)
    HC = -(-HID // P)
    hid_rows = [min(P, HID - c * P) for c in range(HC)]
    nq = [min(QT, T - QT * a) for a in range(NA)]
    nk = [WIN + n for n in nq]
    QK_SCALE = 8.0
    d = C.d
    Wqkv, qs, ksc, Wo, lng, lnb, W1, b1, W2, b2 = (d[f"{block_name}_{n}"] for n in weights)
    S = Stage(nc, name, plan, layers=DEPTH)
    PE, A, V, G = S.PE, S.ACT, S.DVE, S.POOL
    ps = C.ps
    wqkv, wo = S.sb("wqkv", [P, 3 * INNER]), S.sb("wo", [P, CH, D])
    w1, w2 = S.sb("w1", [P, 2 * HID]), S.sb("w2", [P, HC, D])
    cols, b2row = S.sb("cols", [P, 2 + 2 * HC]), S.sb("b2row", [P, D])
    scales = S.sb("scales", [P, 2, E])
    base = S.sb("tables", [P, 4, NT, E])
    tab = S.sb("tables_scaled", [P, 4, NT, E])
    mask_f, mask = S.sb("mask_f", [P, 2, 4, P]), S.sb("mask", [P, 2, 4, P], BF16)
    shift = S.sb("shift", [P, 2, P])
    hT = S.sb("hT", [P, WIN + T])
    work = S.sb("work", [P, 4, 8 * P])
    sq, r2 = work[:, 0:2, 0:INNER], work[:, 2, 0:INNER]
    pr = work[:, :, :].rearrange("p k (h n) -> p k h n", h=8)
    rq01 = S.sb("rq01", [P, 2, INNER])
    rq = (rq01[:, 0], rq01[:, 1], work[:, 3, 0:INNER])
    n2, rn = S.sb("n2", [P, 2, H]), S.sb("rn", [P, 2, H])
    qT = S.sb("qT", [P, max(CH, 2 * HC), T])
    ge, hid = qT[:, 0:HC, :], qT[:, HC:2 * HC, :]
    kT = S.sb("kT", [P, CH, 2, WIN + T])
    va = S.sb("va", [P, NA, INNER])
    mx, sm, rec = (S.sb(n, [P, 4, 8]) for n in ("mx", "sm", "rec"))
    pT, aoT = S.sb("pT", [P, 2, 8, QR]), S.sb("aoT", [P, CH, T])
    ys, hnT = S.sb("ys", [P, NT, D]), S.sb("hnT", [P, T])
    U = 2 * NT
    NU = NA * HG
    AHEAD, VALUES_AHEAD = 3, 2
    LN = "norm"
    gate_bank, up_bank = (5, 7, 5), (6, 4, 6)

    def before(u):
        return int(u < AHEAD)

    def age(u):
        return before(u - 2) - before(u)
    halves = INNER // 512
    pads = nc.alloc_semaphore(f"{name}_pads_filled")
    first_loaded, rest_loaded, tables_ready = (nc.alloc_semaphore(f"{name}_{n}") for n in (
        "wqkv_and_scales_loaded", "other_weights_loaded", "tables_ready"))
    FIRST, REST, TABLES = 16 * 3, 16 * (4 + 2 + 2 * HC + 1), 6

    with nc.Block() as block:
        @block.sync
        def _(sp):
            for dst, n in ((base, "tables"), (mask_f, "mask")):
                sp.dma_start(dst[:, :, :, :], d[f"const_{name}_{n}"]).then_inc(S.loaded, 16)
            sp.dma_start(shift[:, :, :], d["const_shift"]).then_inc(S.loaded, 16)
            sp.wait_ge(S.loaded, 48)

        @block.gpsimd
        def _(pool):
            w = S.once(pool, G)
            pool.wait_ge(S.loaded, 48)
            nc.gpsimd.memset(hT[:, 0:WIN + 1], 0.0).then_inc(pads, 1)
            nc.gpsimd.memset(va[:, :, :], 0.0).then_inc(pads, 1)
            nc.gpsimd.memset(work[:, :, :], 0.0).then_inc(pads, 1)
            nc.gpsimd.memset(qT[:, :, :], 0.0).then_inc(pads, 1)
            nc.gpsimd.memset(kT[:, :, :, :], 0.0).then_inc(pads, 1)
            nc.gpsimd.tensor_copy(mask[:, :, :, :], mask_f[:, :, :, :]).then_inc(pads, 1)
            def scale_tables(layer):
                pool.wait_ge(first_loaded, FIRST * (layer + 1))
                for x in range(2):
                    sc = scales[:, x, :].unsqueeze(1).to_broadcast([P, NT, E])
                    nc.gpsimd.tensor_tensor(tab[:, 2 * x], base[:, 2 * x], sc, ALU.mult).then_inc(tables_ready, 1)
                    for a, b in ((0, E // 2), (E // 2, 0)):
                        nc.gpsimd.tensor_tensor(tab[:, 2 * x + 1, :, a:a + E // 2], base[:, 2 * x + 1, :, a:a + E // 2],
                                                sc[:, :, b:b + E // 2], ALU.mult).then_inc(tables_ready, 1)

            def norm_factor(w, u, *mark):
                pool.wait_ge(*w(V, *mark, "n2", u))
                nc.gpsimd.tensor_tensor(rn[:, u % 2, :], n2[:, u % 2, :], C.neghalf[:, 0:H],
                                        ALU.pow).then_inc(*G(*mark, "rn", u))

            def unit_vectors(w, u, *mark):
                v = rq[u % 3].rearrange("p (h e) -> p h e", h=H)
                pool.wait_ge(*w.own())
                pool.wait_ge(*w(V, *mark, "rot", u))
                nc.gpsimd.tensor_tensor(v, v, rn[:, u % 2, :].unsqueeze(2).to_broadcast([P, H, E]),
                                        ALU.mult).then_inc(*G(*mark, "unit", u))

            scale_tables(0)
            for u in range(AHEAD):
                norm_factor(w, u, "first")
                unit_vectors(w, u, "first")
            def turn(w, l, i, last=False):
                for u in range(AHEAD, U):
                    norm_factor(w, u)
                    unit_vectors(w, u)
                for n in range(NU):
                    pool.wait_ge(*w(V, "rec", n))
                    nc.gpsimd.tensor_tensor(pr[0:QR, n % 4], pr[0:QR, n % 4],
                                            rec[0:QR, n % 4, :].unsqueeze(2).to_broadcast([QR, 8, P]),
                                            ALU.mult).then_inc(*G("probs", n))
                    if last and n == NU - 3:
                        scale_tables(l + 1)
                norm_factor(w, 0)
                unit_vectors(w, 0)
                pool_norm(nc, C, S, w, LN)
                for u in range(1, AHEAD):
                    norm_factor(w, u)
                    unit_vectors(w, u)

            S.run_layers(pool, G, turn)

        @block.scalar
        def _(act):
            act.wait_ge(pads, 6)
            def load_first(layer):
                for dst, src in ((wqkv[:, :], Wqkv[bass.ds(layer, 1)].rearrange("o k n -> (o k) n")),
                                 (scales[:, 0, :], qs[bass.ds(layer, 1)].to_broadcast([P, E])),
                                 (scales[:, 1, :], ksc[bass.ds(layer, 1)].to_broadcast([P, E]))):
                    act.dma_start(dst, src).then_inc(first_loaded, 16)

            def load_rest(layer):
                def load(dst, src):
                    act.dma_start(dst, src).then_inc(rest_loaded, 16)

                def of_layer(x):
                    return x[bass.ds(layer, 1)]

                full = HID // P
                load(wo[:, :, :], of_layer(Wo).rearrange("o (c k) n -> k (o c) n", k=P))
                load(w1[:, :], of_layer(W1).rearrange("o k n -> (o k) n"))
                load(w2[:, 0:full, :], W2[bass.ds(layer, 1), 0:full * P].rearrange("o (c k) n -> k (o c) n", k=P))
                load(w2[0:hid_rows[-1], full, :], W2[bass.ds(layer, 1), full * P:].rearrange("o k n -> (o k) n"))
                load(cols[:, 0:1], of_layer(lng).rearrange("o p -> p o"))
                load(cols[:, 1:2], of_layer(lnb).rearrange("o p -> p o"))
                for g in range(2):
                    for c in range(HC):
                        a, m = g * HID + c * P, hid_rows[c]
                        load(cols[0:m, 2 + g * HC + c:3 + g * HC + c],
                             b1[bass.ds(layer, 1), a:a + m].rearrange("o p -> p o"))
                load(b2row[:, :], of_layer(b2).to_broadcast([P, D]))

            def copy_shifted(w, *mark):
                act.wait_ge(*w(PE, *mark, "yT", NT - 1))
                nc.scalar.activation(hT[0:64, WIN:], C.bank(0, 64), ACT.Copy).then_inc(*A(*mark, "hT", 0))
                nc.scalar.activation(hT[64:128, WIN + 1:], ps[64:128, 0, 0:T - 1],
                                     ACT.Copy).then_inc(*A(*mark, "hT", 1))

            def square(w, u, *mark):
                act.wait_ge(*w(PE, *mark, "qk", u))
                if u >= 2:
                    act.wait_ge(*w(V, *mark, "n2sum", u - 2, back=age(u)))
                for hf in range(halves):
                    nc.scalar.activation(sq[:, u % 2, hf * 512:(hf + 1) * 512],
                                         C.bank(2 * (u % 2) + hf), ACT.Square).then_inc(*A(*mark, "sq", u, hf))

            def keep_values(w, a, *mark):
                act.wait_ge(*w(PE, *mark, "V", a))
                nc.scalar.activation(va[0:nk[a], a, :],
                                     ps[0:nk[a], 6:6 + halves, :].rearrange("p b n -> p (b n)"),
                                     ACT.Copy).then_inc(*A(*mark, "va", a))

            w = S.once(act, A)
            load_first(0)
            load_rest(0)
            nc.scalar.activation(C.xb[:, :, :], C.y[:, 0:NT, :], ACT.Copy).then_inc(*A("first", "xb"))
            copy_shifted(w, "first")
            for u in range(AHEAD):
                square(w, u, "first")
            for a in range(VALUES_AHEAD):
                keep_values(w, a, "first")
            act.wait_ge(*w(V, "first", "n2sum", AHEAD - 1))
            def turn(w, l, i, last=False):
                def keep_turned(u):
                    t, x = u // 2, u % 2
                    act.wait_ge(*w(PE, "qkT", u))
                    src = ps[:, 4:4 + halves, :].rearrange("p b (c n) -> p (b c) n", n=P)
                    if x == 0:
                        nc.scalar.activation(qT[:, 0:CH, t * P:(t + 1) * P], src,
                                             ACT.Copy).then_inc(*A("qkT", u))
                    else:
                        for b in range(2):
                            r = 64 * b
                            nc.scalar.activation(kT[r:r + 64, :, b, WIN + t * P:WIN + (t + 1) * P],
                                                 src[r:r + 64], ACT.Copy).then_inc(
                                                     *A("qkT" if b else "kT_even", u))

                for u in range(U):
                    if AHEAD + u < U:
                        square(w, AHEAD + u)
                    keep_turned(u)
                    if VALUES_AHEAD + u < NA:
                        keep_values(w, VALUES_AHEAD + u)
                if last:
                    load_first(l + 1)
                act.wait_ge(*w(PE, "yT", NT - 1, back=1))
                nc.scalar.activation(C.xb[:, :, :], following(C.y, i, last), ACT.Copy).then_inc(*A("xb"))

                def exponent(n):
                    act.wait_ge(*w(V, "sub", n))
                    nc.scalar.activation(pr[0:QR, n % 4], pr[0:QR, n % 4], ACT.Exp,
                                         scale=QK_SCALE).then_inc(*A("exp", n))

                def keep_probs(n):
                    act.wait_ge(*w(PE, "pT", n))
                    if n >= 2:
                        act.wait_ge(*w(PE, "O", n - 2))
                    nc.scalar.activation(pT[:, n % 2],
                                         ps[:, 4:6, :].rearrange("p b (h n) -> p (b h) n", n=P)[:, :, 0:QR],
                                         ACT.Copy).then_inc(*A("pT", n))

                def keep_out(n):
                    a, g = n // HG, n % HG
                    act.wait_ge(*w(PE, "O", n))
                    nc.scalar.activation(aoT[:, 4 * g:4 * g + 4, QT * a:QT * a + nq[a]],
                                         ps[:, 6 + n % 2, 0:4 * QR].rearrange("p (c n) -> p c n", c=4)[:, :, 0:nq[a]],
                                         ACT.Copy).then_inc(*A("aoT", n))

                for n in range(NU + 4):
                    if n < NU:
                        exponent(n)
                    if 3 <= n < NU + 3:
                        keep_probs(n - 3)
                    if n >= 4:
                        keep_out(n - 4)
                    if n == NU:
                        copy_shifted(w)
                    if n == NU + 1:
                        square(w, 0)
                act.wait_ge(*w(PE, "shifted"))
                act.wait_ge(*w(V, "y_attn"))
                nc.scalar.activation(ys[:, :, 0:64], C.yb[:, :, 0:64], ACT.Copy).then_inc(*A("ys", 0))
                nc.scalar.activation(ys[:, :, 64:], ps[:, 5, 0:NT * 64].rearrange("p (t e) -> p t e", t=NT),
                                     ACT.Copy).then_inc(*A("ys", 1))
                square(w, 1)
                for a in range(VALUES_AHEAD):
                    keep_values(w, a)
                act.wait_ge(*w(PE, "hnT", NT - 1))
                nc.scalar.activation(hnT[:, :], C.bank(4), ACT.Identity, bias=cols[:, 1:2],
                                     scale=cols[:, 0:1]).then_inc(*A("hnT"))
                for c in range(HC):
                    m = hid_rows[c]
                    act.wait_ge(*w(PE, "gate", c))
                    nc.scalar.activation(ge[0:m, c, :], C.bank(gate_bank[c], m), ACT.Gelu,
                                         bias=cols[0:m, 2 + HC + c:3 + HC + c]).then_inc(*A("gelu", c))
                for u in range(2, AHEAD):
                    square(w, u)
                if last:
                    act.wait_ge(*w.own())
                    act.wait_ge(*w(PE, "down"))
                    load_rest(l + 1)

            S.run_layers(act, A, turn)
            act.wait_ge(rest_loaded, REST * (DEPTH + 1))

        @block.vector
        def _(dve):
            dve.wait_ge(pads, 6)
            w = S.once(dve, V)

            def norms_and_rotary(w, u, *mark):
                t, x = u // 2, u % 2
                banks = ps[:, 2 * x:2 * x + halves, :].rearrange("p b (h e) -> p (b h) e", e=E)
                dve.wait_ge(*w(A, *mark, "sq", u, halves - 1))
                if u >= 2:
                    dve.wait_ge(*w(G, *mark, "rn", u - 2, back=age(u)))
                nc.vector.tensor_reduce(n2[:, x, :], sq[:, x, :].rearrange("p (h e) -> p h e", h=H), AX,
                                        ALU.add).then_inc(*V(*mark, "n2sum", u))
                dve.wait_ge(*w.own())
                nc.vector.tensor_scalar(n2[:, x, :], n2[:, x, :], 1e-24, None,
                                        ALU.max).then_inc(*V(*mark, "n2", u))
                if u >= 3:
                    dve.wait_ge(*w(PE, "qkT", u - 3))
                cs, sn = tab[:, 2 * x, t, :], tab[:, 2 * x + 1, t, :]
                dst = rq[u % 3].rearrange("p (h e) -> p h e", h=H)
                nc.vector.tensor_tensor(dst, banks, cs.unsqueeze(1).to_broadcast([P, H, E]),
                                        ALU.mult).then_inc(*V(*mark, "cos", u))
                dst = r2.rearrange("p (h e) -> p h e", h=H)
                for a, b in ((0, E // 2), (E // 2, 0)):
                    last = nc.vector.tensor_tensor(
                        dst[:, :, a:a + E // 2], banks[:, :, b:b + E // 2],
                        sn[:, a:a + E // 2].unsqueeze(1).to_broadcast([P, H, E // 2]), ALU.mult)
                    last.then_inc(*V(*mark, "sin" if a else "sin_low", u))
                dve.wait_ge(*w.own())
                nc.vector.tensor_tensor(rq[u % 3], rq[u % 3], r2,
                                        ALU.add).then_inc(*V(*mark, "rot", u))

            dve.wait_ge(tables_ready, TABLES)
            for u in range(AHEAD):
                norms_and_rotary(w, u, "first")
            dve.wait_ge(*w(G, "first", "unit", AHEAD - 1))
            nc.vector.memset(rec[:, :, :], 0.0).then_inc(*V("first", "rec"))
            def turn(w, l, i, last=False):
                for u in range(AHEAD, U):
                    norms_and_rotary(w, u)

                def subtract_max(n):
                    s = ps[0:QR, 2 * (n % 2):2 * (n % 2) + 2, :].rearrange("p b (h n) -> p (b h) n", n=P)
                    dve.wait_ge(*w(PE, "S", n))
                    nc.vector.tensor_reduce(mx[0:QR, n % 4, :], s, AX, ALU.max).then_inc(*V("max", n))
                    dve.wait_ge(*w.own())
                    if n == 3:
                        dve.wait_ge(*w(PE, "qkT", U - 1))
                    if n >= 4:
                        dve.wait_ge(*w(PE, "pT", n - 4))
                    nc.vector.tensor_tensor(pr[0:QR, n % 4], s,
                                            mx[0:QR, n % 4, :].unsqueeze(2).to_broadcast([QR, 8, P]),
                                            ALU.subtract).then_inc(*V("sub", n))

                def sums(n):
                    dve.wait_ge(*w(A, "exp", n))
                    nc.vector.tensor_reduce(sm[0:QR, n % 4, :], pr[0:QR, n % 4], AX, ALU.add).then_inc(*V("sum", n))
                    dve.wait_ge(*w.own())
                    nc.vector.reciprocal(rec[0:QR, n % 4, :], sm[0:QR, n % 4, :]).then_inc(*V("rec", n))

                for n in range(NU + 1):
                    if n < NU:
                        subtract_max(n)
                    if n >= 1:
                        sums(n - 1)
                if last:
                    dve.wait_ge(tables_ready, TABLES * (l + 2))
                norms_and_rotary(w, 0)
                dve.wait_ge(*w(PE, "attn", NT - 1))
                nc.vector.tensor_tensor(C.yb[:, :, :], C.y[:, bass.ds(i * NT, NT), :],
                                        C.bank(3).rearrange("p (t e) -> p t e", t=NT),
                                        ALU.add).then_inc(*V("y_attn"))
                dve.wait_ge(*w(A, "ys", 1))
                dve_norm(nc, C, S, w, ys, C.nb, LN)
                norms_and_rotary(w, 1)
                for c in range(HC):
                    m = hid_rows[c]
                    dve.wait_ge(*w(A, "gelu", c))
                    dve.wait_ge(*w(PE, "up", c))
                    nc.vector.scalar_tensor_tensor(out=hid[0:m, c, :], in0=C.bank(up_bank[c], m),
                                                   scalar=cols[0:m, 2 + c:3 + c], in1=ge[0:m, c, :],
                                                   op0=ALU.add, op1=ALU.mult).then_inc(*V("hid", c))
                for u in range(2, AHEAD):
                    norms_and_rotary(w, u)
                dve.wait_ge(*w(PE, "down"))
                nc.vector.tensor_tensor(C.y[:, bass.ds(i * NT, NT), :], C.yb[:, :, :],
                                        C.bank(7).rearrange("p (t e) -> p t e", t=NT),
                                        ALU.add).then_inc(*V("y_mlp"))

            S.run_layers(dve, V, turn)

        @block.tensor
        def _(pe):
            pe.wait_ge(pads, 6)
            def turn_next(w, *mark):
                pe.wait_ge(*w(A, *mark, "xb"))
                for t in range(NT):
                    nc.tensor.transpose(ps[:, 0, t * P:(t + 1) * P], C.xb[:, t, :],
                                        C.ident[:, :]).then_inc(*PE(*mark, "yT", t))

            def project(w, u, *mark):
                t, x = u // 2, u % 2
                if u >= 2:
                    pe.wait_ge(*w(V, *mark, "sin", u - 2, back=age(u)))
                for hf in range(halves):
                    product = nc.tensor.matmul(C.bank(2 * x + hf), hT[:, WIN + t * P:WIN + (t + 1) * P],
                                            wqkv[:, x * INNER + hf * 512:x * INNER + (hf + 1) * 512],
                                            start=True, stop=True)
                product.then_inc(*PE(*mark, "qk", u))

            def project_values(w, a, *mark):
                if a >= 1:
                    pe.wait_ge(*w(A, *mark, "va", a - 1, back=int(a == VALUES_AHEAD)))
                for hf in range(halves):
                    product = nc.tensor.matmul(ps[0:nk[a], 6 + hf, :], hT[:, QT * a:QT * a + nk[a]],
                                            wqkv[:, 2 * INNER + hf * 512:2 * INNER + (hf + 1) * 512],
                                            start=True, stop=True)
                product.then_inc(*PE(*mark, "V", a))

            w = S.once(pe, PE)
            pe.wait_ge(S.loaded, 48)
            pe.wait_ge(first_loaded, FIRST)
            turn_next(w, "first")
            pe.wait_ge(*w(A, "first", "hT", 1))
            for u in range(AHEAD):
                project(w, u, "first")
            for a in range(VALUES_AHEAD):
                project_values(w, a, "first")
            pe.wait_ge(*w(A, "first", "va", VALUES_AHEAD - 1))
            pe.wait_ge(*w(G, "first", "unit", AHEAD - 1))
            nc.tensor.transpose(ps[:, 0, 0:P], C.ident[:, :], C.ident[:, :]).then_inc(*PE("first", "end"))
            def turn(w, l, i, last=False):
                def turn_unit(u):
                    pe.wait_ge(*w(G, "unit", u, back=before(u)))
                    if u >= 1:
                        pe.wait_ge(*w(A, "qkT", u - 1))
                    for c in range(CH):
                        product = nc.tensor.transpose(ps[:, 4 + c // 4, c % 4 * P:(c % 4 + 1) * P],
                                                   rq[u % 3][:, c * P:(c + 1) * P], C.ident[:, :])
                    product.then_inc(*PE("qkT", u))

                def scores(n):
                    a, g = n // HG, n % HG
                    if n >= 2:
                        pe.wait_ge(*w(V, "sub", n - 2))
                    else:
                        pe.wait_ge(*w(V, "sin", U - 2 + n))
                    pe.wait_ge(*w(A, "qkT", 2 * ((QT * a + nq[a] - 1) // P) + 1))
                    for b in range(2):
                        bank = 2 * (n % 2) + b
                        nc.tensor.matmul(C.bank(bank), C.ident_bf[:, :], mask[:, int(a > 0), :, :],
                                         start=True, stop=True)
                    for c in range(4):
                        bank, o = 2 * (n % 2) + c // 2, c % 2 * 2 * P
                        out = ps[0:nq[a], bank, o:o + 2 * P].rearrange("p (b n) -> p b n", b=2)
                        product = nc.tensor.matmul(out[:, :, 0:nk[a]], qT[:, 4 * g + c, QT * a:QT * a + nq[a]],
                                                kT[:, 4 * g + c, :, QT * a:QT * a + nk[a]],
                                                start=False, stop=True, skip_group_check=True)
                    product.then_inc(*PE("S", n))

                def turn_probs(n):
                    pe.wait_ge(*w(G, "probs", n))
                    if n >= 1:
                        pe.wait_ge(*w(A, "pT", n - 1))
                    for h in range(8):
                        product = nc.tensor.transpose(ps[:, 4 + h // 4, h % 4 * P:(h % 4 + 1) * P],
                                                   pr[:, n % 4, h, :], C.ident[:, :])
                    product.then_inc(*PE("pT", n))

                def weigh_values(n):
                    a, g = n // HG, n % HG
                    pe.wait_ge(*w(A, "pT", n))
                    if n >= 2:
                        pe.wait_ge(*w(A, "aoT", n - 2))
                    for h in range(8):
                        r, c, v = h % 2 * 64, h // 2 * QR, (8 * g + h) * E
                        product = nc.tensor.matmul(ps[r:r + 64, 6 + n % 2, c:c + QR], va[:, a, v:v + E],
                                                pT[:, n % 2, h, :], start=True, stop=True)
                    product.then_inc(*PE("O", n))

                def mix_heads(t):
                    pe.wait_ge(*w(A, "aoT", HG * min(NA, (P * (t + 1) - 1) // QT + 1) - 1))
                    for c in range(CH):
                        product = nc.tensor.matmul(ps[:, 3, t * P:(t + 1) * P], aoT[:, c, t * P:(t + 1) * P],
                                                wo[:, c, :], start=(c == 0), stop=(c == CH - 1))
                    product.then_inc(*PE("attn", t))

                for u in range(U):
                    if u == U - 1:
                        scores(0)
                        scores(1)
                    if AHEAD + u < U:
                        project(w, AHEAD + u)
                    turn_unit(u)
                    if u == 0:
                        pe.wait_ge(*w(V, "y_mlp", back=1))
                    if VALUES_AHEAD + u < NA:
                        project_values(w, VALUES_AHEAD + u)
                for n in range(NU + 4):
                    if 2 <= n < NU:
                        scores(n)
                    if 3 <= n < NU + 3:
                        turn_probs(n - 3)
                    if n >= 4:
                        weigh_values(n - 4)
                    if n == NU:
                        pe.wait_ge(*w(V, "sub", NU - 2))
                        turn_next(w)
                    if n == NU + 1:
                        pe.wait_ge(*w(A, "hT", 1))
                        if last:
                            pe.wait_ge(first_loaded, FIRST * (l + 2))
                        project(w, 0)
                        pe.wait_ge(*w(V, "sub", NU - 1))
                    if n == NU + 1:
                        pe.wait_ge(rest_loaded, REST * (l + 1))
                    if n > NU:
                        mix_heads(n - NU - 1)
                mix_heads(NT - 1)
                pe.wait_ge(*w(V, "y_attn"))
                nc.tensor.matmul(ps[:, 5, 0:NT * 64], shift[:, 0, :], C.yb[:, :, 64:], start=True, stop=False)
                nc.tensor.matmul(ps[:, 5, 64:NT * 64], shift[:, 1, :], C.yb[:, 0:NT - 1, 64:], start=False,
                                 stop=True).then_inc(*PE("shifted"))
                project(w, 1)
                for a in range(VALUES_AHEAD):
                    project_values(w, a)
                pe.wait_ge(*w(V, LN, NT - 1))
                pe_turn(nc, C, S, w, C.nb, 4, "hnT")
                pe.wait_ge(*w(A, "va", VALUES_AHEAD - 1))
                pe.wait_ge(*w(A, "hnT"))
                for c in range(HC):
                    m = hid_rows[c]
                    if c == 2:
                        pe.wait_ge(*w(V, "hid", 0))
                    nc.tensor.matmul(C.bank(gate_bank[c], m), w1[:, HID + c * P:HID + c * P + m], hnT[:, :], start=True,
                                     stop=True).then_inc(*PE("gate", c))
                    nc.tensor.matmul(C.bank(up_bank[c], m), w1[:, c * P:c * P + m], hnT[:, :], start=True,
                                     stop=True).then_inc(*PE("up", c))
                for u in range(2, AHEAD):
                    project(w, u)
                pe.wait_ge(*w(V, "hid", HC - 1))
                product = pe_rows(nc, C, w, 7, [hid[0:hid_rows[c], c, :] for c in range(HC)],
                               [w2[0:hid_rows[c], c, :] for c in range(HC)], b2row[:, :])
                product.then_inc(*PE("down"))

            S.run_layers(pe, PE, turn)
    S.close()


def stage_l0_ffn(nc, C, plan):
    local_layers(nc, C, plan, "l0ffn", "L0_ffn", 16, 6, 32,
                 ("Wqkv", "q_scale", "k_scale", "Wo", "ln_g", "ln_b", "W1", "b1", "W2", "b2"))


def stage_l1_ffn(nc, C, plan):
    local_layers(nc, C, plan, "l1ffn", "L1_ffn", 8, 2, 64,
                 ("wqkv", "q_scale", "k_scale", "wo", "ln_g", "ln_b", "w1", "b1", "w2", "b2"))



def stage_l1_attn(nc, C, plan):
    H, DK, GR = 8, 16, 8
    DV = D // GR
    SCALE = 0.25
    d = C.d
    S = Stage(nc, "l1attn", plan)
    PE, A, V, G = S.PE, S.ACT, S.DVE, S.POOL
    ps = C.ps
    wq, wk, wv = S.sb("wq", [P, D]), S.sb("wk", [P, D]), S.sb("wv", [P, H * D])
    wvs, bv, bvs = S.sb("wvs", [P, D]), S.sb("bv", [P, H * D]), S.sb("bvs", [P, D])
    cols, headmask = S.sb("cols", [P, 4]), S.sb("headmask", [P, H])
    hT, qT, qm, kT = (S.sb("hT", [P, T]), S.sb("qT", [P, T]), S.sb("qm", [P, H, T]),
                          S.sb("kT", [P, T]))
    va = S.sb("va", [P, NT, 4, 2, 32])
    mx, nm, sm, rec = (S.sb(n, [P, 4]) for n in ("mx", "nm", "sm", "rec"))
    pr, pT = S.sb("pr", [P, 4, T]), S.sb("pT", [P, 4, NT, P])
    aoT, ao = S.sb("aoT", [P, T]), S.sb("ao", [P, NT, H, DV])
    mixed = nc.dram_tensor("l1_mixed", (B, H, T, DV), F32).ap()
    stored = nc.alloc_semaphore("l1attn_ao_stored")
    y_back = nc.alloc_semaphore("l1attn_y_loaded")
    K = NT * H
    NORM, TURN, Q_STEP, K_STEP, V_STEP = 5, 8, 10, 12, 14
    head_of = [k % 2 * (H // 2) + k // 2 % (H // 2) for k in range(K)]
    ST = 16 * NT

    with nc.Block() as block:
        @block.sync
        def _(sp):
            for dst, n in ((wq, "Wq"), (wk, "Wk"), (wv, "Wv")):
                S.load(sp, dst[:, :], d["L1_attn_" + n])
            for c, n in enumerate(("gamma", "beta", "bq", "bk")):
                S.load(sp, cols[:, c:c + 1], column(d["L1_attn_" + n]))
            S.load(sp, bv[:, :], row(d["L1_attn_bv"]).to_broadcast([P, H * D]))
            S.load(sp, headmask[:, :], d["const_head_of_8"])
            sp.wait_ge(S.loaded, S.loads)
            sp.sem_inc(stored, ST)
            with sp.Fori(0, B, 1) as i:
                w = Waits(sp, A, i)
                sp.wait_ge(*w(A, "ao"))
                for t in range(NT):
                    sp.dma_start(mixed[bass.ds(i, 1), :, t * P:(t + 1) * P, :].rearrange("o h p j -> p (o h) j"),
                                 ao[:, t, :, :]).then_inc(stored, 16)
            sp.wait_ge(stored, ST * (B + 1))
            sp.dma_start(C.y[:, 0:B * NT, :], mixed.rearrange("b h (r a) j -> (b h r) (a j)", a=P // DV).rearrange(
                "(n p) e -> p n e", p=P)).then_inc(y_back, 16)
            sp.wait_ge(y_back, 16)

        @block.gpsimd
        def _(pool):
            w = S.once(pool, G)
            nc.gpsimd.memset(va[:, :, :, :, :], 0.0).then_inc(*G("va_pad"))
            pool_norm(nc, C, S, w, ("norm_1", "first"))

            def turn(w, i, last=False):
                for k in range(K):
                    pool.wait_ge(*w(V, "rec", k))
                    nc.gpsimd.tensor_tensor(pr[:, k % 4, :], pr[:, k % 4, :], rec[:, k % 4:k % 4 + 1].to_broadcast([P, T]),
                                            ALU.mult).then_inc(*G("probs", k))
                    if k == NORM - 1:
                        pool_norm(nc, C, S, w, "norm_1")

            S.run(pool, G, turn)

        @block.scalar
        def _(act):
            w = S.once(act, A)
            act.wait_ge(S.loaded, S.loads)
            act.wait_ge(*w(G, "va_pad"))

            def keep_turned(w, *mark):
                act.wait_ge(*w(PE, *mark, "hT", NT - 1))
                nc.scalar.activation(hT[:, :], C.bank(7), ACT.Identity, bias=cols[:, 1:2],
                                     scale=cols[:, 0:1]).then_inc(*A(*mark, "hT"))

            def keep_qkv(w, *mark):
                act.wait_ge(*w(PE, *mark, "K"))
                nc.scalar.activation(kT[:, :], C.bank(7), ACT.Identity, bias=cols[:, 3:4]).then_inc(*A(*mark, "kT"))
                act.wait_ge(*w(PE, *mark, "V"))
                for j in range(2):
                    nc.scalar.activation(va[:, :, :, j, DV * j:DV * j + DV],
                                         C.bank(6).rearrange("p (t g e) -> p t g e", t=NT, g=4)[
                                             :, :, :, DV * j:DV * j + DV], ACT.Copy).then_inc(*A(*mark, "va", j))

            nc.scalar.activation(C.xb[:, :, :], C.y[:, 0:NT, :], ACT.Copy).then_inc(*A("first", "xb"))
            keep_turned(w, "first")
            keep_qkv(w, "first")

            def turn(w, i, last=False):
                act.wait_ge(*w(V, "norm_1", NT - 1, back=1))
                nc.scalar.activation(C.xb[:, :, :], following(C.y, i, last), ACT.Copy).then_inc(*A("xb"))

                def exponent(k):
                    act.wait_ge(*w(V, "negmax", k))
                    if k >= 4:
                        act.wait_ge(*w(PE, "pT", k - 4))
                    nc.scalar.activation(pr[:, k % 4, :], C.bank(k % 3), ACT.Exp, bias=nm[:, k % 4:k % 4 + 1],
                                         scale=SCALE, accum_out=sm[:, k % 4:k % 4 + 1]).then_inc(*A("exp", k))

                def copy_probs(k):
                    act.wait_ge(*w(PE, "pT", k))
                    if k >= 4:
                        act.wait_ge(*w(PE, "O", (k - 4) // 2))
                    nc.scalar.activation(pT[:, k % 4, :, :], C.bank(3 + k % 2).rearrange("p (j n) -> p j n", j=NT),
                                         ACT.Copy).then_inc(*A("pT", k))

                for k in range(K + 3):
                    if k < K:
                        exponent(k)
                    if k >= 3:
                        copy_probs(k - 3)
                    if k == TURN:
                        keep_turned(w)
                act.wait_ge(*w(PE, "O", K // 2 - 1))
                nc.scalar.activation(aoT[:, :], C.bank(5), ACT.Copy).then_inc(*A("aoT"))
                keep_qkv(w)
                act.wait_ge(*w(PE, "ao"))
                act.wait_ge(stored, ST * (i + 1))
                nc.scalar.activation(ao[:, :, :, :], C.bank(3).rearrange("p (t h e) -> p t h e", t=NT, h=H),
                                     ACT.Copy).then_inc(*A("ao"))

            S.run(act, A, turn)

        @block.vector
        def _(dve):
            w = S.once(dve, V)
            dve.wait_ge(S.loaded, S.loads)
            nc.vector.tensor_reduce(wvs[:, :], wv[:, :].rearrange("p (n g) -> p n g", g=GR), AX,
                                    ALU.add).then_inc(*V("wvs"))
            nc.vector.tensor_reduce(bvs[:, :], bv[:, :].rearrange("p (n g) -> p n g", g=GR), AX,
                                    ALU.add).then_inc(*V("bvs"))

            def keep_q(w, *mark):
                dve.wait_ge(*w(PE, *mark, "Q"))
                nc.vector.tensor_scalar(qT[:, :], C.bank(6), cols[:, 2:3], None, ALU.add).then_inc(*V(*mark, "qT"))

            def mask_heads(w, *mark):
                dve.wait_ge(*w.own())
                for h in head_of[0:H]:
                    nc.vector.tensor_scalar(qm[:, h, :], qT[:, :], headmask[:, h:h + 1], None,
                                            ALU.mult).then_inc(*V(*mark, "qm", h))

            dve.wait_ge(*w(A, "first", "xb"))
            dve_norm(nc, C, S, w, C.xb, C.nb, ("norm_1", "first"))
            keep_q(w, "first")
            mask_heads(w, "first")

            def turn(w, i, last=False):
                def maximum(k):
                    dve.wait_ge(*w(PE, "S", k))
                    nc.vector.tensor_reduce(mx[:, k % 4:k % 4 + 1], C.bank(k % 3), AX, ALU.max).then_inc(*V("max", k))
                    dve.wait_ge(*w.own())
                    nc.vector.tensor_scalar(nm[:, k % 4:k % 4 + 1], mx[:, k % 4:k % 4 + 1], -SCALE, None,
                                            ALU.mult).then_inc(*V("negmax", k))

                def reciprocal(k):
                    dve.wait_ge(*w(A, "exp", k))
                    nc.vector.reciprocal(rec[:, k % 4:k % 4 + 1], sm[:, k % 4:k % 4 + 1]).then_inc(*V("rec", k))

                for k in range(K + 1):
                    if k < K:
                        maximum(k)
                    if k >= 1:
                        reciprocal(k - 1)
                    if k == NORM:
                        dve.wait_ge(*w(A, "xb"))
                        dve_norm(nc, C, S, w, C.xb, C.nb, "norm_1")
                    if k == Q_STEP:
                        keep_q(w)
                dve.wait_ge(*w(PE, "S", K - 1))
                mask_heads(w)

            S.run(dve, V, turn)

        @block.tensor
        def _(pe):
            w = S.once(pe, PE)
            pe.wait_ge(S.loaded, S.loads)
            pe.wait_ge(*w(V, "bvs"))

            def turn_x(w, *mark):
                pe.wait_ge(*w(V, *((("norm_1", *mark), NT - 1) if mark else ("norm_1", NT - 1))))
                for t in range(NT):
                    nc.tensor.transpose(ps[:, 7, t * P:(t + 1) * P], C.nb[:, t, :],
                                        C.ident[:, :]).then_inc(*PE(*mark, "hT", t))

            def project_q(w, *mark):
                pe.wait_ge(*w(A, *mark, "hT"))
                nc.tensor.matmul(C.bank(6), wq[:, :], hT[:, :], start=True, stop=True).then_inc(*PE(*mark, "Q"))

            def project_k(w, *mark):
                nc.tensor.matmul(C.bank(7), wk[:, :], hT[:, :], start=True, stop=True).then_inc(*PE(*mark, "K"))

            def project_v(w, *mark):
                pe.wait_ge(*w(V, *mark, "qT"))
                pe_rows(nc, C, w, 6, [hT], [wvs[:, :]], bvs[:, :]).then_inc(*PE(*mark, "V"))

            for step in (turn_x, project_q, project_k, project_v):
                step(w, "first")
            pe.wait_ge(*w(A, "first", "va", 1))
            pe.wait_ge(*w(V, "first", "qm", H - 1))
            nc.tensor.transpose(ps[:, 0, 0:P], C.ident[:, :], C.ident[:, :]).then_inc(*PE("first", "end"))

            def turn(w, i, last=False):
                pe.wait_ge(*w(A, "ao", back=1))

                def scores(k):
                    t, h = k // H, head_of[k]
                    if t == 0:
                        pe.wait_ge(*w(V, "qm", h, back=1))
                    if k >= 3:
                        pe.wait_ge(*w(A, "exp", k - 3))
                    nc.tensor.matmul(C.bank(k % 3), qm[:, h, t * P:(t + 1) * P], kT[:, :],
                                     start=True, stop=True).then_inc(*PE("S", k))

                def turn_probs(k):
                    pe.wait_ge(*w(G, "probs", k))
                    if k >= 2:
                        pe.wait_ge(*w(A, "pT", k - 2))
                    for s in range(NT):
                        product = nc.tensor.transpose(ps[:, 3 + k % 2, s * P:(s + 1) * P],
                                                   pr[:, k % 4, s * P:(s + 1) * P], C.ident[:, :])
                    product.then_inc(*PE("pT", k))

                def values(m):
                    t = 2 * m // H
                    pe.wait_ge(*w(A, "pT", 2 * m + 1))
                    for s in range(NT):
                        for k in (2 * m, 2 * m + 1):
                            g, j = head_of[k] // 2, head_of[k] % 2
                            product = nc.tensor.matmul(ps[32 * g:32 * g + 32, 5, t * P:(t + 1) * P], va[:, s, g, j, :],
                                                    pT[:, k % 4, s, :], start=(j == 0 and s == 0),
                                                    stop=(j == 1 and s == NT - 1))
                    product.then_inc(*PE("O", m))

                for k in range(K + 5):
                    if k < K:
                        scores(k)
                    if 3 <= k < K + 3:
                        turn_probs(k - 3)
                    if k >= 5 and k % 2 == 1 and (k - 5) // 2 < K // 2:
                        values((k - 5) // 2)
                    if k == TURN:
                        turn_x(w)
                    if k == Q_STEP:
                        project_q(w)
                    if k == K_STEP:
                        project_k(w)
                    if k == V_STEP:
                        project_v(w)
                pe.wait_ge(*w(A, "aoT"))
                for t in range(NT):
                    product = nc.tensor.transpose(ps[:, 3, t * P:(t + 1) * P], aoT[:, t * P:(t + 1) * P], C.ident[:, :])
                product.then_inc(*PE("ao"))

            S.run(pe, PE, turn)
    S.close()



def stage_l2_attn(nc, C, plan):
    CH, N, KC, LV = 2, 64, 4, 7
    I = CH * P
    PREV, DIAG, END, TOTAL = 7, 8, 9, 10
    d = C.d
    S = Stage(nc, "l2attn", plan)
    PE, A, V, G = S.PE, S.ACT, S.DVE, S.POOL
    ps = C.ps
    w_in, w_out = S.sb("w_in", [P, 2 * I]), S.sb("w_out", [P, CH, D])
    w_dt, w_b, w_c = S.sb("w_dt", [P, CH, I]), S.sb("w_b", [P, CH, N]), S.sb("w_c", [P, CH, N])
    conv_w, cols, b_dt = S.sb("conv_w", [P, CH, KC]), S.sb("cols", [P, 2, CH]), S.sb("b_dt", [P, I])
    sums = S.sb("sums", [P, LV + 2, P])
    pairs = S.sb("pairs", [P, LV + 1, P])
    y0T, xi, zs = S.sb("y0T", [P, T]), S.sb("xi", [P, CH, KC - 1 + T]), S.sb("zs", [P, CH, T])
    cv, xcT = S.sb("cv", [P, CH, T]), S.sb("xcT", [P, CH, T])
    bT, cT, bk = S.sb("bT", [P, T]), S.sb("cT", [P, T]), S.sb("bk", [P, NT, N])
    ab, dt, dtx = S.sb("ab", [P, NT, I]), S.sb("dt", [P, NT, I]), S.sb("dtx", [P, NT, I])
    gs = S.sb("gs", [P, NT, P])
    dec, gm = S.sb("dec", [P, 3, 11, I]), S.sb("gm", [P, 2, LV + 1, P])
    rr, re = S.sb("rr", [P, 2, LV, I]), S.sb("re", [P, 2, I])
    tmp, yt, state, gT = S.sb("tmp", [P, 9, I]), S.sb("yt", [P, I]), S.sb("state", [P, I]), S.sb("gT", [P, CH, T])

    with nc.Block() as block:
        @block.sync
        def _(sp):
            S.load(sp, w_in[:, :], d["L2_attn_W_in"])
            for dst, n in ((w_out, "W_out"), (w_dt, "W_dt"), (w_b, "W_B"), (w_c, "W_C")):
                S.load(sp, dst[:, :, :], d["L2_attn_" + n].rearrange("(c k) n -> k c n", c=CH))
            S.load(sp, conv_w[:, :, :], d["L2_attn_conv_w"].rearrange("(c k) o n -> k c (o n)", c=CH))
            for c in range(CH):
                S.load(sp, cols[:, 0, c:c + 1], column(d["L2_attn_conv_b"][c * P:(c + 1) * P]))
                S.load(sp, cols[:, 1, c:c + 1], column(d["L2_attn_D"][c * P:(c + 1) * P]))
            S.load(sp, b_dt[:, :], row(d["L2_attn_b_dt"]).to_broadcast([P, I]))
            S.load(sp, sums[:, :, :], d["const_l2_sums"])
            S.load(sp, pairs[:, :, :], d["const_l2_pairs"])
            sp.wait_ge(S.loaded, S.loads)

        @block.gpsimd
        def _(pool):
            w = S.once(pool, G)
            nc.gpsimd.memset(xi[:, :, 0:KC - 1], 0.0).then_inc(*G("xi_pad"))
            nc.gpsimd.memset(bT[:, :], 0.0).then_inc(*G("bT_pad"))
            nc.gpsimd.memset(cT[:, :], 0.0).then_inc(*G("cT_pad"))
            nc.gpsimd.memset(state[:, :], 0.0).then_inc(*G("state_pad"))
            nc.gpsimd.memset(dec[:, :, DIAG, :], 1.0).then_inc(*G("diag_ones"))
            pool.wait_ge(S.loaded, S.loads)
            with S.loop(pool, G) as (i, w):
                for t in range(NT):
                    pool.wait_ge(*w(A, "gs"))
                    if t >= 2:
                        pool.wait_ge(*w(PE, "Y", t - 2, 4))
                    nc.gpsimd.tensor_tensor(gm[:, t % 2], gs[:, t, :].unsqueeze(1).to_broadcast([P, LV + 1, P]),
                                            pairs[:, :, :], ALU.mult).then_inc(*G("gm", t))

        @block.scalar
        def _(act):
            w = S.once(act, A)
            act.wait_ge(S.loaded, S.loads)
            act.wait_ge(*w(G, "diag_ones"))
            with S.loop(act, A) as (i, w):
                act.wait_ge(*w(PE, "y0T", NT - 1, back=1))
                nc.scalar.activation(C.xb[:, :, :], C.y[:, bass.ds(i * NT, NT), :], ACT.Copy).then_inc(*A("xb"))
                act.wait_ge(*w(PE, "y0T", NT - 1))
                nc.scalar.activation(y0T[:, :], C.bank(0), ACT.Copy).then_inc(*A("y0T"))
                for c in range(CH):
                    act.wait_ge(*w(PE, "in", c))
                    nc.scalar.activation(xi[:, c, KC - 1:], C.bank(1 + c), ACT.Copy).then_inc(*A("xi", c))
                for c in range(CH):
                    act.wait_ge(*w(PE, "in", CH + c))
                    nc.scalar.activation(zs[:, c, :], C.bank(3 + c), ACT.Silu).then_inc(*A("zs", c))
                for c in range(CH):
                    act.wait_ge(*w(V, "conv", c))
                    nc.scalar.activation(xcT[:, c, :], cv[:, c, :], ACT.Silu,
                                         bias=cols[:, 0, c:c + 1]).then_inc(*A("xcT", c))
                act.wait_ge(*w(PE, "B"))
                nc.scalar.activation(bT[0:N, :], C.bank(5, N), ACT.Copy).then_inc(*A("bT"))
                act.wait_ge(*w(PE, "C"))
                nc.scalar.activation(cT[0:N, :], C.bank(6, N), ACT.Copy).then_inc(*A("cT"))
                act.wait_ge(*w(PE, "Bk"))
                nc.scalar.activation(bk[:, :, :], ps[:, 7, 0:NT * N].rearrange("p (t n) -> p t n", t=NT),
                                     ACT.Copy).then_inc(*A("bk"))
                for b in range(2):
                    act.wait_ge(*w(PE, "dt", b))
                    nc.scalar.activation(ab[:, 2 * b:2 * b + 2, :], C.bank(1 + b).rearrange("p (t n) -> p t n", t=2),
                                         ACT.Abs).then_inc(*A("abs", b))
                act.wait_ge(*w.own())
                nc.scalar.activation(ab[:, :, :], ab[:, :, :], ACT.Exp, scale=-1.0).then_inc(*A("exp"))
                act.wait_ge(*w.own())
                nc.scalar.activation(ab[:, :, :], ab[:, :, :], ACT.Ln, bias=C.ones[:, 0:1]).then_inc(*A("ln"))
                act.wait_ge(*w(PE, "G"))
                nc.scalar.activation(gs[:, :, :], C.bank(0).rearrange("p (t n) -> p t n", t=NT),
                                     ACT.Copy).then_inc(*A("gs"))
                for t in range(NT):
                    if t >= 3:
                        act.wait_ge(*w(V, "tmp", t - 3, 4))
                        act.wait_ge(*w(V, "state_decayed", t - 3))
                    for b in range(5):
                        act.wait_ge(*w(PE, "decay", t, b))
                        slots = dec[:, t % 3, 2 * b:2 * b + 2, :] if b < 4 else dec[:, t % 3, END:TOTAL + 1, :]
                        nc.scalar.activation(slots, C.bank(5 + b % 2).rearrange("p (j n) -> p j n", j=2),
                                             ACT.Exp, scale=-1.0).then_inc(*A("dec", t, b))

        @block.vector
        def _(dve):
            w = S.once(dve, V)
            dve.wait_ge(S.loaded, S.loads)
            with S.loop(dve, V) as (i, w):
                for c in range(CH):
                    dve.wait_ge(*w(A, "xi", c))
                    nc.vector.tensor_scalar(cv[:, c, :], xi[:, c, 0:T], conv_w[:, c, 0:1], None,
                                            ALU.mult).then_inc(*V("tap", c, 0))
                    for k in range(1, KC):
                        dve.wait_ge(*w.own())
                        last = nc.vector.scalar_tensor_tensor(out=cv[:, c, :], in0=xi[:, c, k:k + T],
                                                              scalar=conv_w[:, c, k:k + 1], in1=cv[:, c, :],
                                                              op0=ALU.mult, op1=ALU.add)
                        last.then_inc(*(V("conv", c) if k == KC - 1 else V("tap", c, k)))
                dve.wait_ge(*w(A, "ln"))
                for b in range(2):
                    nc.vector.scalar_tensor_tensor(out=dt[:, 2 * b:2 * b + 2, :],
                                                   in0=C.bank(1 + b).rearrange("p (t n) -> p t n", t=2), scalar=0.0,
                                                   in1=ab[:, 2 * b:2 * b + 2, :], op0=ALU.max,
                                                   op1=ALU.add).then_inc(*V("dt", b))
                dve.wait_ge(*w.own())
                for b in range(2):
                    dve.wait_ge(*w(PE, "xc", b))
                    nc.vector.tensor_tensor(dtx[:, 2 * b:2 * b + 2, :], dt[:, 2 * b:2 * b + 2, :],
                                            C.bank(3 + b).rearrange("p (t n) -> p t n", t=2),
                                            ALU.mult).then_inc(*V("dtx", b))
                dve.wait_ge(*w(PE, "Y", NT - 1, 3, back=1))
                nc.vector.memset(state[0:N, :], 0.0).then_inc(*V("state_zero"))

                def sources(t):
                    dve.wait_ge(*w(A, "dec", t, 4))
                    if t >= 2:
                        dve.wait_ge(*w(PE, "Y", t - 2, 4))
                    nc.vector.tensor_tensor(rr[:, t % 2], dec[:, t % 3, 0:LV, :], dtx[:, t, :].unsqueeze(1).to_broadcast(
                        [P, LV, I]), ALU.mult).then_inc(*V("rr", t))
                    nc.vector.tensor_tensor(re[:, t % 2, :], dec[:, t % 3, END, :], dtx[:, t, :],
                                            ALU.mult).then_inc(*V("re", t))

                def gather(t):
                    for b in range(5):
                        dve.wait_ge(*w(PE, "Y", t, b))
                        n = min(2, 9 - 2 * b)
                        last = nc.vector.tensor_tensor(tmp[:, 2 * b:2 * b + n, :], dec[:, t % 3, 2 * b:2 * b + n, :],
                                                       ps[:, b, 0:n * I].rearrange("p (j n) -> p j n", j=n), ALU.mult)
                        last.then_inc(*V("tmp", t, b))
                    nc.vector.tensor_tensor(state[0:N, :], state[0:N, :], dec[0:N, t % 3, TOTAL, :],
                                            ALU.mult).then_inc(*V("state_decayed", t))
                    dve.wait_ge(*w.own())
                    nc.vector.tensor_tensor(state[0:N, :], state[0:N, :], ps[0:N, 4, I:2 * I],
                                            ALU.add).then_inc(*V("state", t))
                    if t >= 1:
                        dve.wait_ge(*w(PE, "yT", t - 1))
                    nc.vector.tensor_reduce(yt[:, :], tmp[:, :, :].rearrange("p l n -> p n l"), AX,
                                            ALU.add).then_inc(*V("yt", t))

                def skip(t):
                    dve.wait_ge(*w(PE, "yT", t))
                    for c in range(CH):
                        nc.vector.scalar_tensor_tensor(out=gT[:, c, t * P:(t + 1) * P], in0=xcT[:, c, t * P:(t + 1) * P],
                                                       scalar=cols[:, 1, c:c + 1], in1=ps[:, 7, c * P:(c + 1) * P],
                                                       op0=ALU.mult, op1=ALU.add).then_inc(*V("gT", t, c))

                sources(0)
                for t in range(NT):
                    if t + 1 < NT:
                        sources(t + 1)
                    gather(t)
                    if t >= 1:
                        skip(t - 1)
                skip(NT - 1)
                dve.wait_ge(*w.own())
                nc.vector.tensor_tensor(gT[:, :, :], gT[:, :, :], zs[:, :, :], ALU.mult).then_inc(*V("g"))
                dve.wait_ge(*w(PE, "out"))
                nc.vector.tensor_copy(C.y[:, bass.ds(i * NT, NT), :],
                                      C.bank(5).rearrange("p (t e) -> p t e", t=NT)).then_inc(*V("y"))

        @block.tensor
        def _(pe):
            w = S.once(pe, PE)
            pe.wait_ge(S.loaded, S.loads)
            with S.loop(pe, PE) as (i, w):
                pe.wait_ge(*w(A, "xb"))
                pe.wait_ge(*w(V, "g", back=1))
                pe_turn(nc, C, S, w, C.xb, 0, "y0T")
                pe.wait_ge(*w(A, "y0T"))
                for c in range(2 * CH):
                    nc.tensor.matmul(C.bank(1 + c), w_in[:, c * P:(c + 1) * P], y0T[:, :], start=True,
                                     stop=True).then_inc(*PE("in", c))
                pe.wait_ge(*w(A, "xcT", 1))
                pe.wait_ge(*w(A, "zs", 1))
                for bank, wt, name in ((5, w_b, "B"), (6, w_c, "C")):
                    pe.wait_ge(*w(V, "y", back=1))
                    for c in range(CH):
                        last = nc.tensor.matmul(C.bank(bank, N), wt[:, c, :], xcT[:, c, :], start=(c == 0),
                                                stop=(c == CH - 1))
                    last.then_inc(*PE(name))
                for t in range(NT):
                    for c in range(CH):
                        last = nc.tensor.matmul(ps[:, 7, t * N:(t + 1) * N], xcT[:, c, t * P:(t + 1) * P],
                                                w_b[:, c, :], start=(c == 0), stop=(c == CH - 1))
                last.then_inc(*PE("Bk"))
                for b in range(2):
                    for j in range(2):
                        o, t = ps[:, 1 + b, j * I:(j + 1) * I], 2 * b + j
                        for c in range(CH):
                            nc.tensor.matmul(o, xcT[:, c, t * P:(t + 1) * P], w_dt[:, c, :], start=(c == 0), stop=False)
                        last = nc.tensor.matmul(o, C.ident[:, :], b_dt[:, :], start=False, stop=True)
                    last.then_inc(*PE("dt", b))
                for b in range(2):
                    for j in range(2):
                        t = 2 * b + j
                        for c in range(CH):
                            last = nc.tensor.transpose(ps[:, 3 + b, j * I + c * P:j * I + (c + 1) * P],
                                                       xcT[:, c, t * P:(t + 1) * P], C.ident[:, :])
                    last.then_inc(*PE("xc", b))
                pe.wait_ge(*w(A, "bk"))
                pe.wait_ge(*w(A, "bT"))
                for t in range(NT):
                    last = nc.tensor.matmul(ps[:, 0, t * P:(t + 1) * P], bT[:, t * P:(t + 1) * P],
                                            cT[:, t * P:(t + 1) * P], start=True, stop=True)
                last.then_inc(*PE("G"))
                pe.wait_ge(*w(V, "dtx", 1))
                pe.wait_ge(*w(A, "gs"))

                def decays(t):
                    for b in range(5):
                        if b >= 2:
                            pe.wait_ge(*w(A, "dec", t, b - 2))
                        elif t >= 1:
                            pe.wait_ge(*w(A, "dec", t - 1, 4 - b))
                        for j in range(2):
                            l = 2 * b + j
                            tokens = C.ones[:, :] if l == LV + 2 else sums[:, l, :]
                            last = nc.tensor.matmul(ps[:, 5 + b % 2, j * I:(j + 1) * I], tokens, dt[:, t, :],
                                                    start=True, stop=True)
                        last.then_inc(*PE("decay", t, b))

                decays(0)
                decays(1)
                for t in range(NT):
                    pe.wait_ge(*w(V, "re", t))
                    pe.wait_ge(*w(G, "gm", t))
                    for l in range(LV):
                        if t >= 1 and l % 2 == 0:
                            pe.wait_ge(*w(V, "tmp", t - 1, l // 2))
                        level = nc.tensor.matmul(ps[:, l // 2, l % 2 * I:(l % 2 + 1) * I], gm[:, t % 2, l, :],
                                                 rr[:, t % 2, l, :], start=True, stop=True)
                        if l % 2 == 1:
                            level.then_inc(*PE("Y", t, l // 2))
                    pe.wait_ge(*w(V, "state" if t else "state_zero", *([t - 1] if t else [])))
                    nc.tensor.matmul(ps[:, 3, I:2 * I], cT[:, t * P:(t + 1) * P], state[:, :], start=True,
                                     stop=True).then_inc(*PE("Y", t, 3))
                    nc.tensor.matmul(ps[:, 4, 0:I], gm[:, t % 2, LV, :], dtx[:, t, :], start=True,
                                     stop=True).then_inc(*PE("Y_diagonal", t))
                    nc.tensor.matmul(ps[0:N, 4, I:2 * I], bk[:, t, :], re[:, t % 2, :], start=True,
                                     stop=True).then_inc(*PE("Y", t, 4))
                    if t + 2 < NT:
                        decays(t + 2)
                    pe.wait_ge(*w(V, "yt", t))
                    if t >= 1:
                        pe.wait_ge(*w(V, "gT", t - 1, 1))
                    for c in range(CH):
                        last = nc.tensor.transpose(ps[:, 7, c * P:(c + 1) * P], yt[:, c * P:(c + 1) * P], C.ident[:, :])
                    last.then_inc(*PE("yT", t))
                pe.wait_ge(*w(V, "g"))
                pe_rows(nc, C, w, 5, [gT[:, c, :] for c in range(CH)],
                        [w_out[:, c, :] for c in range(CH)]).then_inc(*PE("out"))
    S.close()



def stage_l2_ffn(nc, C, plan):
    EX, F, CH, TOP = 8, 2 * D, 2, 2
    d = C.d
    S = Stage(nc, "l2ffn", plan)
    PE, A, V, G = S.PE, S.ACT, S.DVE, S.POOL
    ps = C.ps
    wg, bg = S.sb("wg", [P, EX]), S.sb("bg", [P, EX])
    w1, b1 = S.sb("w1", [P, EX, F]), S.sb("b1", [P, EX, CH])
    w2, b2 = S.sb("w2", [P, EX, CH, D]), S.sb("b2", [EX, D])
    gains, before = S.sb("gains", [P, 2, D]), S.sb("before", [P, EX, EX])
    hT, hT_next = S.sb("hT", [P, T]), S.sb("hT_next", [P, T])
    lg, top, ex, s = S.sb("lg", [P, NT, EX]), S.sb("top", [P, NT]), S.sb("ex", [P, NT, EX]), S.sb("s", [P, NT])
    gt, eq = S.sb("gt", [P, NT, EX, EX]), S.sb("eq", [P, NT, EX, EX])
    rank, coefT = S.sb("rank", [P, NT, EX]), S.sb("coefT", [EX, T])
    coef, coef_next = S.sb("coef", [P, NT, EX]), S.sb("coef_next", [P, NT, EX])
    hid, acc = S.sb("hid", [P, 2, CH, T]), S.sb("acc", [P, NT, D])

    with nc.Block() as block:
        @block.sync
        def _(sp):
            S.load(sp, wg[:, :], d["L2_ffn_Wg"])
            S.load(sp, bg[:, :], row(d["L2_ffn_bg"]).to_broadcast([P, EX]))
            S.load(sp, w1[:, :, :], d["L2_ffn_W1"].rearrange("e k n -> k e n"))
            S.load(sp, b1[:, :, :], d["L2_ffn_b1_turned"])
            S.load(sp, w2[:, :, :, :], d["L2_ffn_W2"].rearrange("e (c k) n -> k e c n", c=CH))
            S.load(sp, b2[:, :], d["L2_ffn_b2"])
            S.load(sp, gains[:, 0, :], row(d["L2_ffn_gamma"]).to_broadcast([P, D]))
            S.load(sp, gains[:, 1, :], row(d["L2_ffn_beta"]).to_broadcast([P, D]))
            S.load(sp, before[:, :, :], d["const_before"])
            sp.wait_ge(S.loaded, S.loads)

        @block.gpsimd
        def _(pool):
            S.once(pool, G)
            with S.loop(pool, G) as (i, w):
                pool_norm(nc, C, S, w, "norm_1")

        @block.scalar
        def _(act):
            w = S.once(act, A)
            act.wait_ge(S.loaded, S.loads)

            def keep_turned(w, *mark):
                act.wait_ge(*w(PE, *mark, "hT", NT - 1))
                nc.scalar.activation(hT_next[:, :], C.bank(0), ACT.Copy).then_inc(*A(*mark, "hT_next"))

            def keep_logits(w, *mark):
                act.wait_ge(*w(PE, *mark, "logits"))
                nc.scalar.activation(lg[:, :, :], ps[:, 1, 0:NT * EX].rearrange("p (t e) -> p t e", t=NT),
                                     ACT.Copy).then_inc(*A(*mark, "logits"))

            def exponents(w, *mark):
                act.wait_ge(*w(V, *mark, "centred"))
                nc.scalar.activation(ex[:, :, :], ex[:, :, :], ACT.Exp).then_inc(*A(*mark, "exp"))

            def keep_coefficients(w, *mark):
                act.wait_ge(*w(PE, *mark, "coefT"))
                nc.scalar.activation(coefT[:, :], C.bank(0, EX), ACT.Copy).then_inc(*A(*mark, "coefT"))

            nc.scalar.activation(C.xb[:, :, :], C.y[:, 0:NT, :], ACT.Copy).then_inc(*A("first", "xb"))
            for step in (keep_turned, keep_logits, exponents, keep_coefficients):
                step(w, "first")
            act.wait_ge(*w.own())
            nc.scalar.activation(hT[:, :], hT_next[:, :], ACT.Copy).then_inc(*A("first", "hT"))

            def turn(w, i, last=False):
                for e in range(EX):
                    act.wait_ge(*w(PE, "up", e, 0))
                    if e >= 2:
                        act.wait_ge(*w(PE, "down", e - 2))
                    nc.scalar.activation(hid[:, e % 2, 0, :], C.bank(2 + e % 2 * 2), ACT.Relu,
                                         bias=b1[:, e, 0:1]).then_inc(*A("hid", e))
                    if e == 1:
                        act.wait_ge(*w(V, "acc"))
                        nc.scalar.activation(C.xb[:, :, :], following(C.y, i, last), ACT.Copy).then_inc(*A("xb"))
                    if e in (2, 3, 5, 7):
                        {2: keep_turned, 3: keep_logits, 5: exponents, 7: keep_coefficients}[e](w)
                act.wait_ge(*w(PE, "up", EX - 1, 1))
                nc.scalar.activation(hT[:, :], hT_next[:, :], ACT.Copy).then_inc(*A("hT"))

            S.run(act, A, turn)

        @block.vector
        def _(dve):
            w = S.once(dve, V)
            dve.wait_ge(S.loaded, S.loads)

            def compare(w, *mark):
                dve.wait_ge(*w(A, *mark, "logits"))
                nc.vector.tensor_reduce(top[:, :], lg[:, :, :], AX, ALU.max).then_inc(*V(*mark, "top"))
                dve.wait_ge(*w.own())
                nc.vector.tensor_tensor(ex[:, :, :], lg[:, :, :], top[:, :].unsqueeze(2).to_broadcast([P, NT, EX]),
                                        ALU.subtract).then_inc(*V(*mark, "centred"))
                for t in range(NT):
                    mine = lg[:, t, :].unsqueeze(2).to_broadcast([P, EX, EX])
                    other = lg[:, t, :].unsqueeze(1).to_broadcast([P, EX, EX])
                    nc.vector.tensor_tensor(gt[:, t], other, mine, ALU.is_gt).then_inc(*V(*mark, "gt", t))
                    nc.vector.tensor_tensor(eq[:, t], other, mine, ALU.is_equal).then_inc(*V(*mark, "eq", t))

            def count_ahead(w, *mark):
                dve.wait_ge(*w.own())
                nc.vector.tensor_tensor(eq[:, :, :, :], eq[:, :, :, :], before[:, :, :].unsqueeze(1).to_broadcast(
                    [P, NT, EX, EX]), ALU.mult).then_inc(*V(*mark, "eq_before"))
                dve.wait_ge(*w.own())
                nc.vector.tensor_tensor(gt[:, :, :, :], gt[:, :, :, :], eq[:, :, :, :],
                                        ALU.add).then_inc(*V(*mark, "ahead"))
                dve.wait_ge(*w.own())
                nc.vector.tensor_reduce(rank[:, :, :], gt[:, :, :, :], AX, ALU.add).then_inc(*V(*mark, "rank"))

            def coefficients(w, *mark):
                dve.wait_ge(*w.own())
                dve.wait_ge(*w(A, *mark, "exp"))
                nc.vector.scalar_tensor_tensor(out=coef_next[:, :, :], in0=rank[:, :, :], scalar=float(TOP),
                                               in1=ex[:, :, :], op0=ALU.is_lt, op1=ALU.mult).then_inc(
                                                   *V(*mark, "chosen"))
                dve.wait_ge(*w.own())
                nc.vector.tensor_reduce(s[:, :], coef_next[:, :, :], AX, ALU.add).then_inc(*V(*mark, "sum"))
                dve.wait_ge(*w.own())
                nc.vector.reciprocal(s[:, :], s[:, :]).then_inc(*V(*mark, "rec"))
                dve.wait_ge(*w.own())
                nc.vector.tensor_tensor(coef_next[:, :, :], coef_next[:, :, :],
                                        s[:, :].unsqueeze(2).to_broadcast([P, NT, EX]),
                                        ALU.mult).then_inc(*V(*mark, "coef"))

            for step in (compare, count_ahead, coefficients):
                step(w, "first")
            dve.wait_ge(*w(PE, "first", "bias"))
            nc.vector.memset(s[:, :], 0.0).then_inc(*V("first", "end"))

            def turn(w, i, last=False):
                def hidden(e):
                    dve.wait_ge(*w(PE, "up", e, 1))
                    if e >= 2:
                        dve.wait_ge(*w(PE, "down", e - 2))
                    nc.vector.tensor_scalar(hid[:, e % 2, 1, :], C.bank(3 + e % 2 * 2), b1[:, e, 1:2], 0.0, ALU.add,
                                            ALU.max).then_inc(*V("hid", e))

                def weigh(e):
                    dve.wait_ge(*w(PE, "down", e))
                    dve.wait_ge(*w.own())
                    for t in range(NT):
                        nc.vector.scalar_tensor_tensor(out=acc[:, t, :], in0=ps[:, 6 + e % 2, t * P:(t + 1) * P],
                                                       scalar=coef[:, t, e:e + 1], in1=acc[:, t, :], op0=ALU.mult,
                                                       op1=ALU.add).then_inc(*V("acc", e, t))

                dve.wait_ge(*w(PE, "bias", back=1))
                nc.vector.tensor_tensor(acc[:, :, :], C.xb[:, :, :], C.bank(1).rearrange("p (t e) -> p t e", t=NT),
                                        ALU.add).then_inc(*V("acc"))
                nc.vector.tensor_copy(coef[:, :, :], coef_next[:, :, :]).then_inc(*V("coef_kept"))
                for e in range(EX):
                    hidden(e)
                    if e >= 1:
                        weigh(e - 1)
                    if e in (4, 5, 6):
                        {4: compare, 5: count_ahead, 6: coefficients}[e](w)
                weigh(EX - 1)
                dve.wait_ge(*w.own())
                dve_norm(nc, C, S, w, acc, C.nb, "norm_1")
                dve.wait_ge(*w.own())
                nc.vector.tensor_tensor(C.nb[:, :, :], C.nb[:, :, :], gains[:, 0, :].unsqueeze(1).to_broadcast(
                    [P, NT, D]), ALU.mult).then_inc(*V("gain"))
                dve.wait_ge(*w.own())
                nc.vector.tensor_tensor(C.y[:, bass.ds(i * NT, NT), :], C.nb[:, :, :],
                                        gains[:, 1, :].unsqueeze(1).to_broadcast([P, NT, D]),
                                        ALU.add).then_inc(*V("y"))

            S.run(dve, V, turn)

        @block.tensor
        def _(pe):
            w = S.once(pe, PE)
            pe.wait_ge(S.loaded, S.loads)

            def turn_x(w, *mark):
                pe.wait_ge(*w(A, *mark, "xb"))
                for t in range(NT):
                    nc.tensor.transpose(ps[:, 0, t * P:(t + 1) * P], C.xb[:, t, :],
                                        C.ident[:, :]).then_inc(*PE(*mark, "hT", t))

            def logits(w, *mark):
                pe.wait_ge(*w(A, *mark, "hT_next"))
                for t in range(NT):
                    o = ps[:, 1, t * EX:(t + 1) * EX]
                    nc.tensor.matmul(o, hT_next[:, t * P:(t + 1) * P], wg[:, :], start=True, stop=False)
                    product = nc.tensor.matmul(o, C.ident[:, :], bg[:, :], start=False, stop=True)
                product.then_inc(*PE(*mark, "logits"))

            def turn_coefficients(w, *mark):
                pe.wait_ge(*w(V, *mark, "coef"))
                for t in range(NT):
                    product = nc.tensor.transpose(ps[0:EX, 0, t * P:(t + 1) * P], coef_next[:, t, :], C.ident[:, :])
                product.then_inc(*PE(*mark, "coefT"))

            def weigh_biases(w, *mark):
                pe.wait_ge(*w(A, *mark, "coefT"))
                for t in range(NT):
                    product = nc.tensor.matmul(ps[:, 1, t * P:(t + 1) * P], coefT[:, t * P:(t + 1) * P], b2[:, :],
                                               start=True, stop=True)
                product.then_inc(*PE(*mark, "bias"))

            for step in (turn_x, logits, turn_coefficients, weigh_biases):
                step(w, "first")
            pe.wait_ge(*w(A, "first", "hT"))
            nc.tensor.transpose(ps[:, 2, 0:P], C.ident[:, :], C.ident[:, :]).then_inc(*PE("first", "end"))

            def turn(w, i, last=False):
                def up(e):
                    if e >= 2:
                        pe.wait_ge(*w(A, "hid", e - 2))
                        pe.wait_ge(*w(V, "hid", e - 2))
                    for c in range(CH):
                        nc.tensor.matmul(C.bank(2 + e % 2 * 2 + c), w1[:, e, c * P:(c + 1) * P], hT[:, :], start=True,
                                         stop=True).then_inc(*PE("up", e, c))

                def down(e):
                    pe.wait_ge(*w(A, "hid", e))
                    pe.wait_ge(*w(V, "hid", e))
                    if e >= 2:
                        pe.wait_ge(*w(V, "acc", e - 2, NT - 1))
                    pe_rows(nc, C, w, 6 + e % 2, [hid[:, e % 2, c, :] for c in range(CH)],
                            [w2[:, e, c, :] for c in range(CH)]).then_inc(*PE("down", e))

                pe.wait_ge(*w(A, "hT", back=1))
                up(0)
                up(1)
                for e in range(EX):
                    down(e)
                    if e + 2 < EX:
                        up(e + 2)
                    if e in (1, 2, 6, 7):
                        {1: turn_x, 2: logits, 6: turn_coefficients, 7: weigh_biases}[e](w)

            S.run(pe, PE, turn)
    S.close()



def stage_l3_attn(nc, C, plan):
    H, R, E = 16, 16, 8
    HALF_SCALE = float(np.float32(0.5) / np.sqrt(np.float32(E)))
    d = C.d
    S = Stage(nc, "l3attn", plan)
    PE, A, V, G = S.PE, S.ACT, S.DVE, S.POOL
    ps = C.ps
    wqk, wv = S.sb("wqk", [P, 4, D]), S.sb("wv", [P, D])
    wr, wrm = S.sb("wr", [P, 2, R]), S.sb("wrm", [P, 2, H, R])
    wgt, gb, dec = S.sb("wgt", [P, H * R]), S.sb("gb", [P, H]), S.sb("dec", [P, H])
    wrep = S.sb("wrep", [P, 2, H, P])
    wo, ob = S.sb("wo", [P, H, D]), S.sb("ob", [P, D])
    gains, headmask, rope = S.sb("gains", [P, 2, D]), S.sb("headmask", [P, H]), S.sb("rope", [P, 2, T])
    rrep = S.sb("rrep", [P, 2, H, P])
    hT, rot, tm = S.sb("hT", [P, T]), S.sb("rot", [P, 2, T]), S.sb("tm", [P, 2, T])
    hT_next, rot_next = S.sb("hT_next", [P, T]), S.sb("rot_next", [P, 2, T])
    th, u, st = S.sb("th", [P, 2, T]), S.sb("u", [P, 2, T]), S.sb("st", [P, 2, T])
    yv, hres = S.sb("yv", [P, 2, T]), S.sb("hres", [P, NT, D])

    with nc.Block() as block:
        @block.sync
        def _(sp):
            S.load(sp, wqk[:, :, :], d["L3_attn_qk_turned"])
            S.load(sp, wv[:, :], d["L3_attn_v_turned"])
            S.load(sp, wr[:, :, :], d["L3_attn_ranks"])
            S.load(sp, wgt[:, :], d["L3_attn_g_turned"])
            S.load(sp, gb[:, :], d["L3_attn_g_b_spread"])
            S.load(sp, dec[:, :], d["L3_attn_decay_spread"])
            for r in range(R):
                S.load(sp, wo[r * E:(r + 1) * E, :, :], d["L3_attn_out_turned"].rearrange("(h e) n -> e h n", h=H))
            S.load(sp, ob[:, :], row(d["L3_attn_out_b"]).to_broadcast([P, D]))
            S.load(sp, gains[:, 0, :], row(d["L3_attn_ln_g"]).to_broadcast([P, D]))
            S.load(sp, gains[:, 1, :], row(d["L3_attn_ln_b"]).to_broadcast([P, D]))
            S.load(sp, headmask[:, :], d["const_head_of_16"])
            S.load(sp, rope[:, :, :], d["const_l3_rope"])
            sp.wait_ge(S.loaded, S.loads)

        @block.gpsimd
        def _(pool):
            S.once(pool, G)
            with S.loop(pool, G) as (i, w):
                pool_norm(nc, C, S, w, "norm_1")

        @block.scalar
        def _(act):
            w = S.once(act, A)
            act.wait_ge(S.loaded, S.loads)
            nc.scalar.activation(dec[:, :], dec[:, :], ACT.Tanh, scale=0.5).then_inc(*A("dec"))
            nc.scalar.activation(gb[:, :], gb[:, :], ACT.Copy, scale=0.5).then_inc(*A("half_gb"))
            act.wait_ge(*w.own())

            def keep_turned(w, *mark):
                act.wait_ge(*w(PE, *mark, "hT", NT - 1))
                nc.scalar.activation(hT_next[:, :], C.bank(4), ACT.Copy).then_inc(*A(*mark, "hT_next"))

            def move_on(w, *mark):
                act.wait_ge(*w(V, *mark, "rot", 1))
                nc.scalar.activation(hT[:, :], hT_next[:, :], ACT.Copy).then_inc(*A(*mark, "hT"))
                nc.scalar.activation(rot[:, :, :], rot_next[:, :, :], ACT.Copy).then_inc(*A(*mark, "rot"))

            nc.scalar.activation(C.xb[:, :, :], C.y[:, 0:NT, :], ACT.Copy).then_inc(*A("first", "xb"))
            keep_turned(w, "first")
            act.wait_ge(*w.own())
            move_on(w, "first")

            def turn(w, i, last=False):
                act.wait_ge(*w(PE, "hT", NT - 1, back=1))
                nc.scalar.activation(C.xb[:, :, :], following(C.y, i, last), ACT.Copy).then_inc(*A("xb"))
                for h in range(H):
                    act.wait_ge(*w(PE, "g", h))
                    if h >= 2:
                        act.wait_ge(*w(V, "gk", h - 2))
                    nc.scalar.activation(th[:, h % 2, :], C.bank(2), ACT.Tanh, bias=gb[:, h:h + 1],
                                         scale=0.5).then_inc(*A("th", h))
                    if h == 2:
                        keep_turned(w)
                act.wait_ge(*w(PE, "q", H - 1))
                move_on(w)

            S.run(act, A, turn)

        @block.vector
        def _(dve):
            w = S.once(dve, V)
            dve.wait_ge(S.loaded, S.loads)
            dve.wait_ge(*w(A, "dec"))
            nc.vector.tensor_scalar(dec[:, :], dec[:, :], 0.5, 0.5, ALU.mult, ALU.add).then_inc(*V("dec"))
            for x in range(2):
                for j in range(H):
                    nc.vector.tensor_scalar(wrm[:, x, j, :], wr[:, x, :], headmask[:, j:j + 1], None,
                                            ALU.mult).then_inc(*V("wrm", x, j))
            dve.wait_ge(*w.own())
            for x in range(2):
                for j in range(H):
                    nc.vector.tensor_copy(rrep[:, x, j, :].rearrange("p (r e) -> p r e", r=R),
                                          wrm[:, x, j, :].unsqueeze(2).to_broadcast([P, R, E])).then_inc(
                                              *V("rrep", x, j))
            for h in range(H):
                nc.vector.tensor_copy(wrep[:, 0, h, :].rearrange("p (r e) -> p r e", r=R),
                                      wgt[:, h * R:(h + 1) * R].unsqueeze(2).to_broadcast([P, R, E])).then_inc(
                                          *V("wrep", 0, h))
                nc.vector.tensor_copy(wrep[:, 1, h, :].rearrange("p (r e) -> p r e", r=R),
                                      wv[:, h * E:(h + 1) * E].unsqueeze(1).to_broadcast([P, R, E])).then_inc(
                                          *V("wrep", 1, h))

            def rotate(w, x, j, *mark):
                dve.wait_ge(*w(PE, *mark, "qk", x, j))
                if j == 0:
                    dve.wait_ge(*w.own())
                nc.vector.tensor_tensor(tm[:, j, :], C.bank(4), rope[:, j, :], ALU.mult).then_inc(
                    *V(*mark, "sin" if j else "cos", x))
                if j:
                    dve.wait_ge(*w.own())
                    nc.vector.tensor_tensor(rot_next[:, x, :], tm[:, 0, :], tm[:, 1, :],
                                            ALU.add).then_inc(*V(*mark, "rot", x))

            for x, j in ((0, 0), (0, 1), (1, 0), (1, 1)):
                rotate(w, x, j, "first")
            dve.wait_ge(*w(A, "first", "rot"))
            nc.vector.memset(hres[:, :, :], 0.0).then_inc(*V("first", "end"))

            def turn(w, i, last=False):
                for h in range(H):
                    b = h % 2
                    dve.wait_ge(*w(A, "th", h))
                    dve.wait_ge(*w(PE, "k", h))
                    nc.vector.scalar_tensor_tensor(out=u[:, b, :], in0=th[:, b, :], scalar=1.0, in1=C.bank(b),
                                                   op0=ALU.add, op1=ALU.mult).then_inc(*V("gk", h))
                    dve.wait_ge(*w.own())
                    dve.wait_ge(*w(PE, "v", h))
                    nc.vector.scalar_tensor_tensor(out=u[:, b, :], in0=u[:, b, :], scalar=HALF_SCALE,
                                                   in1=C.bank(3), op0=ALU.mult, op1=ALU.mult).then_inc(
                                                       *V("gkv", h))
                    dve.wait_ge(*w.own())
                    nc.vector.tensor_tensor_scan(st[:, b, :], dec[:, h:h + 1].to_broadcast([P, T]), u[:, b, :], 0.0,
                                                 ALU.mult, ALU.add).then_inc(*V("memory", h))
                    dve.wait_ge(*w.own())
                    dve.wait_ge(*w(PE, "q", h))
                    if h >= 2:
                        dve.wait_ge(*w(PE, "y", h - 2))
                    nc.vector.tensor_tensor(yv[:, b, :], st[:, b, :], C.bank(5 + b), ALU.mult).then_inc(*V("yv", h))
                    if h in (4, 6, 8, 10):
                        rotate(w, (h - 4) // 4, h % 4 // 2)
                dve.wait_ge(*w(PE, "out"))
                nc.vector.tensor_tensor(hres[:, :, :], C.y[:, bass.ds(i * NT, NT), :],
                                        C.bank(7).rearrange("p (t e) -> p t e", t=NT), ALU.add).then_inc(*V("hres"))
                dve.wait_ge(*w.own())
                dve_norm(nc, C, S, w, hres, C.nb, "norm_1")
                dve.wait_ge(*w.own())
                nc.vector.tensor_tensor(C.nb[:, :, :], C.nb[:, :, :], gains[:, 0, :].unsqueeze(1).to_broadcast(
                    [P, NT, D]), ALU.mult).then_inc(*V("gain"))
                dve.wait_ge(*w.own())
                nc.vector.tensor_tensor(C.y[:, bass.ds(i * NT, NT), :], C.nb[:, :, :],
                                        gains[:, 1, :].unsqueeze(1).to_broadcast([P, NT, D]),
                                        ALU.add).then_inc(*V("y"))

            S.run(dve, V, turn)

        @block.tensor
        def _(pe):
            w = S.once(pe, PE)
            pe.wait_ge(S.loaded, S.loads)
            pe.wait_ge(*w(V, "wrep", 1, H - 1))

            def turn_x(w, *mark):
                pe.wait_ge(*w(A, *mark, "xb"))
                for t in range(NT):
                    nc.tensor.transpose(ps[:, 4, t * P:(t + 1) * P], C.xb[:, t, :],
                                        C.ident[:, :]).then_inc(*PE(*mark, "hT", t))

            def project(w, x, j, *mark):
                if j:
                    pe.wait_ge(*w(V, *mark, "cos", x))
                elif x:
                    pe.wait_ge(*w(V, *mark, "sin", 0))
                else:
                    pe.wait_ge(*w(A, *mark, "hT_next"))
                nc.tensor.matmul(C.bank(4), wqk[:, 2 * x + j, :], hT_next[:, :], start=True,
                                 stop=True).then_inc(*PE(*mark, "qk", x, j))

            turn_x(w, "first")
            for x, j in ((0, 0), (0, 1), (1, 0), (1, 1)):
                project(w, x, j, "first")
            pe.wait_ge(*w(A, "first", "rot"))
            nc.tensor.transpose(ps[:, 2, 0:P], C.ident[:, :], C.ident[:, :]).then_inc(*PE("first", "end"))

            def turn(w, i, last=False):
                pe.wait_ge(*w(A, "rot", back=1))

                def head(h):
                    b = h % 2
                    if h >= 1:
                        pe.wait_ge(*w(A, "th", h - 1))
                    nc.tensor.matmul(C.bank(2), wrep[:, 0, h, :], hT[:, :], start=True, stop=True).then_inc(*PE("g", h))
                    if h >= 2:
                        pe.wait_ge(*w(V, "gk", h - 2))
                    nc.tensor.matmul(C.bank(b), rrep[:, 1, h, :], rot[:, 1, :], start=True,
                                     stop=True).then_inc(*PE("k", h))
                    if h >= 1:
                        pe.wait_ge(*w(V, "gkv", h - 1))
                    nc.tensor.matmul(C.bank(3), wrep[:, 1, h, :], hT[:, :], start=True, stop=True).then_inc(
                        *PE("v", h))
                    if h >= 2:
                        pe.wait_ge(*w(V, "yv", h - 2))
                    nc.tensor.matmul(C.bank(5 + b), rrep[:, 0, h, :], rot[:, 0, :], start=True,
                                     stop=True).then_inc(*PE("q", h))

                def add_out(h):
                    pe.wait_ge(*w(V, "yv", h))
                    for t in range(NT):
                        product = nc.tensor.matmul(ps[:, 7, t * P:(t + 1) * P], yv[:, h % 2, t * P:(t + 1) * P],
                                                wo[:, h, :], start=(h == 0 and t == 0), stop=False,
                                                skip_group_check=True)
                    product.then_inc(*PE("y", h))

                for h in range(H + 1):
                    if h < H:
                        head(h)
                    if h == 1:
                        pe.wait_ge(*w(V, "hres", back=1))
                    if h >= 1:
                        add_out(h - 1)
                    if h == 1:
                        turn_x(w)
                    if h in (4, 6, 8, 10):
                        project(w, (h - 4) // 4, h % 4 // 2)
                for t in range(NT):
                    product = nc.tensor.matmul(ps[:, 7, t * P:(t + 1) * P], C.ident[:, :], ob[:, :], start=False,
                                            stop=True, skip_group_check=True)
                product.then_inc(*PE("out"))

            S.run(pe, PE, turn)
    S.close()



def stage_l3_ffn(nc, C, plan):
    I, BL = 352, 16
    CH = -(-I // P)
    rows_of = [min(P, I - c * P) for c in range(CH)]
    d = C.d
    S = Stage(nc, "l3ffn", plan)
    PE, A, V, G = S.PE, S.ACT, S.DVE, S.POOL
    ps = C.ps
    wgu, wd = S.sb("wgu", [P, 2, CH, D]), S.sb("wd", [P, I])
    wguT, wdT = S.sb("wguT", [P, 2, I]), S.sb("wdT", [P, CH, D])
    xqT, sg = S.sb("xqT", [P, T]), S.sb("sg", [P, 2, I])
    h, hqT = S.sb("h", [P, NT, I]), S.sb("hqT", [P, CH, T])
    WIDE = NT * I
    NB = WIDE // BL
    ab, sign, u = S.sb("ab", [P, WIDE]), S.sb("sign", [P, WIDE]), S.sb("u", [P, WIDE])
    am, rs = S.sb("am", [P, NB]), S.sb("rs", [P, NB])
    wide = ab, sign, u, am, rs
    small = tuple(S.sb(f"{n}_x", [P, m]) for n, m in (("ab", T), ("sign", T), ("u", T), ("am", T // BL), ("rs", T // BL)))

    def act_quantise(w, bufs, src, n, *name):
        ab, sign, _, _, _ = bufs
        nc.scalar.activation(ab[:, 0:n], src, ACT.Abs).then_inc(*A(*name, "abs"))
        nc.scalar.activation(sign[:, 0:n], src, ACT.Sign).then_inc(*A(*name, "sign"))

    def dve_quantise(w, bufs, dst, n, *name):
        ab, sign, u, am, rs = bufs
        nb = n // BL
        blocks = lambda x: x[:, 0:n].rearrange("p (b k) -> p b k", k=BL)
        each = lambda x: x[:, 0:nb].unsqueeze(2).to_broadcast([P, nb, BL])
        nc.vector.wait_ge(*w(A, *name, "abs"))
        nc.vector.tensor_reduce(am[:, 0:nb], blocks(ab), AX, ALU.max).then_inc(*V(*name, "max"))
        nc.vector.wait_ge(*w.own())
        nc.vector.tensor_scalar(am[:, 0:nb], am[:, 0:nb], 1.0 / 6.0, 1e-12, ALU.mult, ALU.max).then_inc(
            *V(*name, "scale"))
        nc.vector.wait_ge(*w.own())
        nc.vector.reciprocal(rs[:, 0:nb], am[:, 0:nb]).then_inc(*V(*name, "rec"))
        nc.vector.wait_ge(*w.own())
        nc.vector.tensor_tensor(blocks(ab), blocks(ab), each(rs), ALU.mult).then_inc(*V(*name, "norm"))
        nc.vector.wait_ge(*w.own())
        nc.vector.tensor_scalar(u[:, 0:n], ab[:, 0:n], 5.0, 2.0, ALU.is_gt, ALU.mult).then_inc(*V(*name, 5.0))
        for mid in (3.5, 2.5):
            nc.vector.wait_ge(*w.own())
            nc.vector.scalar_tensor_tensor(out=u[:, 0:n], in0=ab[:, 0:n], scalar=mid, in1=u[:, 0:n], op0=ALU.is_gt,
                                           op1=ALU.add).then_inc(*V(*name, mid))
        nc.vector.wait_ge(*w.own())
        nc.vector.tensor_scalar(u[:, 0:n], u[:, 0:n], 2.0, None, ALU.mult).then_inc(*V(*name, "double"))
        for mid in (1.75, 1.25, 0.75, 0.25):
            nc.vector.wait_ge(*w.own())
            nc.vector.scalar_tensor_tensor(out=u[:, 0:n], in0=ab[:, 0:n], scalar=mid, in1=u[:, 0:n], op0=ALU.is_gt,
                                           op1=ALU.add).then_inc(*V(*name, mid))
        nc.vector.wait_ge(*w(A, *name, "sign"))
        nc.vector.wait_ge(*w.own())
        nc.vector.scalar_tensor_tensor(out=u[:, 0:n], in0=u[:, 0:n], scalar=0.5, in1=sign[:, 0:n], op0=ALU.mult,
                                       op1=ALU.mult).then_inc(*V(*name, "signed"))
        nc.vector.wait_ge(*w.own())
        nc.vector.tensor_tensor(dst.rearrange("p (b k) -> p b k", k=BL), blocks(u), each(am),
                                ALU.mult).then_inc(*V(*name))

    with nc.Block() as block:
        @block.sync
        def _(sp):
            w = Waits(sp, None)
            sp.wait_ge(*w(G, "wgu_pad"))
            for x, n in enumerate(("w_gate", "w_up")):
                for c in range(CH):
                    m = rows_of[c]
                    S.load(sp, wgu[0:m, x, c, :], d["L3_ffn_" + n][c * P:c * P + m, :])
            S.load(sp, wd[:, :], d["L3_ffn_w_down"])
            sp.wait_ge(S.loaded, S.loads)

        @block.gpsimd
        def _(pool):
            w = S.once(pool, G)
            nc.gpsimd.memset(wgu[64:P, :, CH - 1, :], 0.0).then_inc(*G("wgu_pad"))

        @block.scalar
        def _(act):
            w = S.once(act, A)
            act.wait_ge(S.loaded, S.loads)
            act_quantise(w, wide, wgu[:, :, :, :].rearrange("p x c n -> p (x c n)"), 2 * CH * D, "qgu")
            act.wait_ge(*w(V, "qgu"))
            act_quantise(w, wide, wd[:, :], I, "qd")
            for x in range(2):
                act.wait_ge(*w(PE, "wT", x))
                nc.scalar.activation(wguT[:, x, :], ps[:, x, 0:I], ACT.Copy).then_inc(*A("wT", x))
            act.wait_ge(*w(PE, "wT", 2))
            for c in range(CH):
                m = rows_of[c]
                nc.scalar.activation(wdT[0:m, c, :], ps[0:m, 2, c * P:(c + 1) * P], ACT.Copy).then_inc(*A("wT", 2, c))

            def magnitudes(w, y, *mark):
                nc.scalar.activation(C.xb[:, :, :], y, ACT.Copy).then_inc(*A(*mark, "xb"))
                act.wait_ge(*w.own())
                act_quantise(w, small, C.xb[:, :, :].rearrange("p t e -> p (t e)"), T, *mark, "qx")

            def keep_x(w, *mark):
                act.wait_ge(*w(PE, *mark, "xqT", NT - 1))
                nc.scalar.activation(xqT[:, :], C.bank(1), ACT.Copy).then_inc(*A(*mark, "xqT"))

            magnitudes(w, C.y[:, 0:NT, :], "first")
            keep_x(w, "first")

            def turn(w, i, last=False):
                for t in range(NT):
                    act.wait_ge(*w(PE, "gate", t))
                    if t >= 2:
                        act.wait_ge(*w(V, "h", t - 2))
                    nc.scalar.activation(sg[:, t % 2, :], ps[:, 1 + t % 2, 0:I], ACT.Silu).then_inc(*A("silu", t))
                act.wait_ge(*w(V, "h", NT - 1))
                act_quantise(w, wide, h[:, :, :].rearrange("p t e -> p (t e)"), WIDE, "qh")
                act.wait_ge(*w(PE, "xqT", NT - 1, back=1))
                magnitudes(w, following(C.y, i, last))
                for c in range(CH):
                    m = rows_of[c]
                    act.wait_ge(*w(PE, "hqT", c))
                    nc.scalar.activation(hqT[0:m, c, :], C.bank(5 + c, m), ACT.Copy).then_inc(*A("hqT", c))
                keep_x(w)

            S.run(act, A, turn)

        @block.vector
        def _(dve):
            w = S.once(dve, V)
            dve.wait_ge(S.loaded, S.loads)
            dve_quantise(w, wide, wgu[:, :, :, :].rearrange("p x c n -> p (x c n)"), 2 * CH * D, "qgu")
            dve_quantise(w, wide, wd[:, :], I, "qd")

            def quantise_x(w, *mark):
                dve_quantise(w, small, C.xb[:, :, :].rearrange("p t e -> p (t e)"), T, *mark, "qx")

            quantise_x(w, "first")

            def turn(w, i, last=False):
                for t in range(NT):
                    dve.wait_ge(*w(A, "silu", t))
                    dve.wait_ge(*w(PE, "up", t))
                    nc.vector.tensor_tensor(h[:, t, :], sg[:, t % 2, :], ps[:, 3 + t % 2, 0:I],
                                            ALU.mult).then_inc(*V("h", t))
                dve_quantise(w, wide, h[:, :, :].rearrange("p t e -> p (t e)"), WIDE, "qh")
                quantise_x(w)
                dve.wait_ge(*w(PE, "out"))
                nc.vector.tensor_copy(C.y[:, bass.ds(i * NT, NT), :],
                                      C.bank(0).rearrange("p (t e) -> p t e", t=NT)).then_inc(*V("y"))

            S.run(dve, V, turn)

        @block.tensor
        def _(pe):
            w = S.once(pe, PE)
            pe.wait_ge(*w(V, "qd"))
            for x in range(2):
                for c in range(CH):
                    m = rows_of[c]
                    last = nc.tensor.transpose(ps[:, x, c * P:c * P + m], wgu[0:m, x, c, :], C.ident[0:m, 0:m])
                last.then_inc(*PE("wT", x))
            for c in range(CH):
                m = rows_of[c]
                last = nc.tensor.transpose(ps[0:m, 2, c * P:(c + 1) * P], wd[:, c * P:c * P + m], C.ident[:, :])
            last.then_inc(*PE("wT", 2))
            pe.wait_ge(*w(A, "wT", 2, CH - 1))

            def turn_x(w, *mark):
                pe.wait_ge(*w(V, *mark, "qx"))
                for t in range(NT):
                    nc.tensor.transpose(ps[:, 1, t * P:(t + 1) * P], C.xb[:, t, :],
                                        C.ident[:, :]).then_inc(*PE(*mark, "xqT", t))

            turn_x(w, "first")
            pe.wait_ge(*w(A, "first", "xqT"))
            nc.tensor.transpose(ps[:, 0, 0:P], C.ident[:, :], C.ident[:, :]).then_inc(*PE("first", "end"))

            def turn(w, i, last=False):
                pe.wait_ge(*w(A, "xqT", back=1))
                for t in range(NT):
                    for x, name in enumerate(("gate", "up")):
                        if t >= 2:
                            pe.wait_ge(*w(V, "h", t - 2))
                        nc.tensor.matmul(ps[:, 1 + 2 * x + t % 2, 0:I], xqT[:, t * P:(t + 1) * P], wguT[:, x, :],
                                         start=True, stop=True).then_inc(*PE(name, t))
                pe.wait_ge(*w(V, "qh"))
                for c in range(CH):
                    m = rows_of[c]
                    for t in range(NT):
                        product = nc.tensor.transpose(ps[0:m, 5 + c, t * P:(t + 1) * P], h[:, t, c * P:c * P + m],
                                                      C.ident[:, :])
                    product.then_inc(*PE("hqT", c))
                pe.wait_ge(*w(A, "hqT", CH - 1))
                pe.wait_ge(*w(V, "y", back=1))
                pe_rows(nc, C, w, 0, [hqT[0:rows_of[c], c, :] for c in range(CH)],
                        [wdT[0:rows_of[c], c, :] for c in range(CH)]).then_inc(*PE("out"))
                turn_x(w)

            S.run(pe, PE, turn)
    S.close()



def position_tables():
    import numpy as np

    p = np.arange(P)
    c = {f"const_head_of_{h}": (p[:, None] // (P // h) == np.arange(h)[None, :]).astype(np.float32) for h in (8, 16)}
    j = np.arange(2 * P)
    seen = (j[None, :] > p[:, None]) & (j[None, :] <= p[:, None] + P)
    both = np.stack([seen & (j >= P)[None, :], seen], 1)
    c["const_l0_mask"] = np.ascontiguousarray(
        np.repeat(np.where(both, 0.0, NEG).astype(np.float32)[:, :, None, :], 2, 2))
    for name, win in (("l0ffn", 32), ("l1ffn", 64)):
        j, r = np.arange(P)[None, :], p[:, None]
        seen = (j >= r) & (j <= r + win)
        both = np.where(np.stack([seen & (j >= win), seen], 1), 0.0, NEG).astype(np.float32)
        c[f"const_{name}_mask"] = np.ascontiguousarray(np.repeat(both[:, :, None, :], 4, 2))
        c[f"const_{name}_tables"] = rotary(win)
    shift = np.zeros((P, 2, P), np.float32)
    shift[p[:-1], 0, p[1:]] = 1.0
    shift[P - 1, 1, 0] = 1.0
    c["const_shift"] = shift
    sums, pairs = np.zeros((P, 9, P), np.float32), np.zeros((P, 8, P), np.float32)
    r, x = p[:, None], p[None, :]
    for l in range(7):
        mid = (x >> (l + 1) << (l + 1)) + (1 << l)
        sums[:, l, :] = np.where(x < mid, (r > x) & (r < mid), (r >= mid) & (r <= x))
        pairs[:, l, :] = (r >> (l + 1) == x >> (l + 1)) & (r < mid) & (x >= mid)
    sums[:, 7, :], sums[:, 8, :] = r <= x, r > x
    pairs[:, 7, :] = r == x
    c["const_l2_sums"], c["const_l2_pairs"] = sums, pairs
    e = np.arange(8)
    c["const_before"] = np.ascontiguousarray(np.tile((e[None, :] < e[:, None]).astype(np.float32), (P, 1, 1)))
    f = np.float32
    inv_freq = f(1.0) / np.power(f(10000.0), np.arange(4, dtype=f) / f(4), dtype=f)
    freqs = (np.arange(T, dtype=f)[None, :] * inv_freq[p % 8 // 2][:, None]).astype(f).astype(np.float64)
    sign = np.where(p % 2 == 0, -1.0, 1.0)[:, None]
    c["const_l3_rope"] = np.stack([np.cos(freqs), sign * np.sin(freqs)], 1).astype(f)
    return c


def rotary(win, head=64):
    import numpy as np

    f = np.float32
    half = np.arange(0, head, 2, dtype=f)
    inv_freq = f(1.0) / np.power(f(10000.0), half / f(head), dtype=f)
    t = np.arange(T, dtype=f)
    freqs = (t[:, None] * inv_freq[None, :]).astype(f)
    base = ((half + f(0.4 * head)) / f(1.4 * head)).astype(f)
    power = (t - f(T // 2)) / f(win // 2)
    scale = np.power(base[None, :].astype(np.float64), power[:, None].astype(np.float64)).astype(f)
    cos, sin = np.cos(freqs.astype(np.float64)), np.sin(freqs.astype(np.float64))
    parts = []
    for s in (scale.astype(np.float64), 1.0 / scale.astype(np.float64)):
        parts += [np.concatenate([cos * s, cos * s], 1), np.concatenate([-sin * s, sin * s], 1)]
    x = np.stack(parts, 0).astype(f).reshape(4, NT, P, head)
    return np.ascontiguousarray(x.transpose(2, 0, 1, 3))


def lay_out(inputs):
    import numpy as np

    a = {n: np.ascontiguousarray(x) for n, x in inputs.items()}
    q, k, v, g, o = (a.pop("L3_attn_" + n) for n in ("q_w", "k_w", "v_w", "g_w", "out_w"))
    partner = np.arange(D) ^ 1
    a["L3_attn_qk_turned"] = np.ascontiguousarray(np.stack([q, q[partner], k, k[partner]]).transpose(2, 0, 1))
    a["L3_attn_v_turned"] = np.ascontiguousarray(v.transpose())
    a["L3_attn_g_turned"] = np.ascontiguousarray(g.transpose())
    a["L3_attn_out_turned"] = np.ascontiguousarray(o.transpose())
    ranks = np.stack([a.pop("L3_attn_Wq"), a.pop("L3_attn_Wk")])
    a["L3_attn_ranks"] = np.ascontiguousarray(ranks.transpose(1, 3, 0, 2).reshape(D, 2, 16))
    for name, x in (("g_b_spread", a.pop("L3_attn_g_b").reshape(16, 16)),
                    ("decay_spread", a.pop("L3_attn_base_decay_logits"))):
        a["L3_attn_" + name] = np.ascontiguousarray(np.repeat(x.transpose(), 8, 0))
    for n in a:
        if n.startswith(("L0_ffn_", "L1_ffn_")):
            a[n] = np.concatenate([a[n], a[n][:1]])
    b1 = a.pop("L2_ffn_b1")
    a["L2_ffn_b1_turned"] = np.ascontiguousarray(b1.reshape(8, 2, P).transpose(2, 0, 1))
    a.update(position_tables())
    return a


BLOCKS = [stage_l0_attn, stage_l0_ffn, stage_l1_attn, stage_l1_ffn, stage_l2_attn, stage_l2_ffn, stage_l3_attn,
          stage_l3_ffn]


def build(nc, d, out, plan, blocks):
    C = Common(nc, d)
    setup(nc, C, d["L0_attn_x"])
    stage_norms(nc, C, plan, "norms_first", add=False)
    for n, block in enumerate(blocks):
        block(nc, C, plan)
        stage_norms(nc, C, plan, f"norms_{n}", then=n + 1 < len(blocks))
    stored = nc.alloc_semaphore("out_stored")
    with nc.Block() as block:
        @block.sync
        def _(sp):
            sp.dma_start(out.rearrange("b (t p) d -> p (b t) d", p=P), C.x[:, :, :]).then_inc(stored, 16)
            sp.wait_ge(stored, 16)


def program(bacc, shapes, blocks=None):
    plan = {}
    for _ in range(2):
        nc = bacc.Bacc("TRN2", target_bir_lowering=False, num_devices=1)
        d = {n: nc.dram_tensor(f"in_{n}_dram", s, F32, kind="ExternalInput").ap() for n, s in shapes.items()}
        out = nc.dram_tensor("out_0_dram", (B, T, D), F32, kind="ExternalOutput").ap()
        build(nc, d, out, plan, BLOCKS if blocks is None else blocks)
    return nc



def kernel(**inputs):
    import concourse.bacc as _bacc
    from concourse.bass_utils import run_bass_kernel_spmd as _run

    arrays = lay_out(inputs)
    nc = program(_bacc, {n: a.shape for n, a in arrays.items()})
    r = _run(nc, [{f"in_{n}_dram": a for n, a in arrays.items()}], core_ids=[0])
    return r.results[0]["out_0_dram"]
```
